# Optimizing a Trainium2 kernel written in Bass

```python
import numpy as np
import jax
import jax.numpy as jnp

def _softmax(x, axis=-1):
    return jax.nn.softmax(x, axis=axis)

def _gelu(x):
    return jax.nn.gelu(x, approximate=True)

def _silu(x):
    return jax.nn.silu(x)

def _sigmoid(x):
    return jax.nn.sigmoid(x)

def _layernorm(x, axis=-1, eps=1e-05):
    m = jnp.mean(x, axis=axis, keepdims=True)
    v = jnp.var(x, axis=axis, keepdims=True)
    return (x - m) / jnp.sqrt(v + eps)

def _scatter_add(tgt, idx, src, axis=0):
    return tgt.at[idx].add(src)

def _segment_sum(src, seg, n):
    return jax.ops.segment_sum(src, seg, n)
kernel_name = 'mk_early_fusion_d4_tok_img256_r4_585b4f'

def setup_inputs(seed: int=0):
    np.random.seed(seed)
    _w = jnp.asarray

    def _rec_inputs():
        import jax
        import jax.numpy as jnp
        _rk = jax.random.key(seed)
        x = 7.22013e-05 + 1.00017 * jax.random.normal(jax.random.fold_in(_rk, 1), (4, 1, 64, 64), jnp.float32)
        txt = 0.000424648 + 0.582507 * jax.random.normal(jax.random.fold_in(_rk, 2), (4, 512, 64), jnp.float32)
        return (x, txt)
    x, txt = _rec_inputs()

    def _L0_tok_setup():
        import jax, jax.numpy as jnp
        import numpy as np
        P = 8
        C = 1
        D = 64
        key = jax.random.key(seed)
        k1, k2, k3 = jax.random.split(key, 3)
        x = jax.random.normal(k1, (128, C, 64, 64), dtype=jnp.float32)
        patch_dim = P * P * C
        bound = 1.0 / np.sqrt(patch_dim)
        W = jax.random.uniform(k2, (D, patch_dim), dtype=jnp.float32, minval=-bound, maxval=bound)
        b = jax.random.uniform(k3, (D,), dtype=jnp.float32, minval=-bound, maxval=bound)
        return {'x': x, 'W': W, 'b': b}
    _L0_tok_all = _L0_tok_setup()
    _L0_tok_in = {k: v for k, v in _L0_tok_all.items() if k in ('W', 'b')}
    del _L0_tok_all

    def _L0_attn_setup():
        import jax, jax.numpy as jnp
        import numpy as np
        B, T, D = (2, 512, 64)

        def _layernorm(x, g, b, eps=1e-05):
            mu = jnp.mean(x, axis=-1, keepdims=True)
            var = jnp.var(x, axis=-1, keepdims=True)
            return (x - mu) * jax.lax.rsqrt(var + eps) * g + b
        key = jax.random.key(seed)
        ks = jax.random.split(key, 8)
        s = 0.02
        return {'x': jax.random.normal(ks[0], (B, T, D), jnp.float32), 'qkv_w': jax.random.normal(ks[1], (D, 3 * D), jnp.float32) * s, 'qkv_b': jnp.zeros((3 * D,), jnp.float32), 'proj_w': jax.random.normal(ks[2], (D, D), jnp.float32) * s, 'proj_b': jnp.zeros((D,), jnp.float32), 'ln1_g': jnp.ones((D,), jnp.float32), 'ln1_b': jnp.zeros((D,), jnp.float32), 'w1': jax.random.normal(ks[3], (D, 4 * D), jnp.float32) * s, 'b1': jnp.zeros((4 * D,), jnp.float32), 'w2': jax.random.normal(ks[4], (4 * D, D), jnp.float32) * s, 'b2': jnp.zeros((D,), jnp.float32), 'ln2_g': jnp.ones((D,), jnp.float32), 'ln2_b': jnp.zeros((D,), jnp.float32)}
    _L0_attn_all = _L0_attn_setup()
    _L0_attn_in = {k: v for k, v in _L0_attn_all.items() if k in ('qkv_w', 'qkv_b', 'proj_w', 'proj_b', 'ln1_g', 'ln1_b', 'w1', 'b1', 'w2', 'b2', 'ln2_g', 'ln2_b')}
    del _L0_attn_all

    def _L0_ffn_setup():
        import jax, jax.numpy as jnp
        import numpy as np
        DIM = 64
        HEADS = 8
        NUM_KEYS = 64
        NUM_KV = NUM_KEYS ** 2
        PK_TOPK = 16
        FINAL_TOPK = 16
        DIM_KEY = DIM // 2
        P = 2

        def _pk(x, Wq_pk, pk_keys):
            b, n, _ = x.shape
            q = (x @ Wq_pk).reshape(b, n, P, HEADS, DIM_KEY).transpose(2, 0, 1, 3, 4)
            sim = jnp.einsum('pbnhd,pkhd->pbnhk', q, pk_keys)
            scores, idx = jax.lax.top_k(sim, PK_TOPK)
            idx0 = idx[0]
            idx1 = idx[1] * NUM_KEYS
            index = (idx0[..., :, None] + idx1[..., None, :]).reshape(b, n, HEADS, PK_TOPK * PK_TOPK)
            score = (scores[0][..., :, None] + scores[1][..., None, :]).reshape(b, n, HEADS, PK_TOPK * PK_TOPK)
            final_scores, pk_idx = jax.lax.top_k(score, FINAL_TOPK)
            final_indices = jnp.take_along_axis(index, pk_idx, axis=-1)
            final_scores = jax.nn.softmax(final_scores, axis=-1)
            return (final_scores, final_indices)
        key = jax.random.key(seed)
        ks = jax.random.split(key, 7)
        b, n = (2, 256)
        std = 0.02
        x = jax.random.normal(ks[0], (b, n, DIM), dtype=jnp.float32)
        Wq_pk = jax.random.normal(ks[1], (DIM, P * HEADS * DIM_KEY), dtype=jnp.float32) * std
        pk_keys = jax.random.normal(ks[2], (P, NUM_KEYS, HEADS, DIM_KEY), dtype=jnp.float32) * std
        Wq = jax.random.normal(ks[3], (DIM, HEADS * DIM), dtype=jnp.float32) * std
        keys_table = jax.random.normal(ks[4], (NUM_KV * HEADS, DIM), dtype=jnp.float32) * std
        values_table = jax.random.normal(ks[5], (NUM_KV * HEADS, DIM), dtype=jnp.float32) * std
        Wo = jax.random.normal(ks[6], (DIM * HEADS, DIM), dtype=jnp.float32) * std
        return {'x': x, 'Wq_pk': Wq_pk, 'pk_keys': pk_keys, 'Wq': Wq, 'keys_table': keys_table, 'values_table': values_table, 'Wo': Wo}
    _L0_ffn_all = _L0_ffn_setup()
    _L0_ffn_in = {k: v for k, v in _L0_ffn_all.items() if k in ('Wq_pk', 'pk_keys', 'Wq', 'keys_table', 'values_table', 'Wo')}
    del _L0_ffn_all

    def _L1_attn_setup():
        import jax, jax.numpy as jnp
        import numpy as np
        B, N, E, H = (4, 1024, 64, 8)
        EXP = 3
        D1 = EXP * E // H * H
        HD = D1 // H
        RPE = int(min(E / 8, 32))
        LAYERS = 3
        EPS = 1e-08

        def _srms(x, d):
            rms = jnp.linalg.norm(x, axis=-1, keepdims=True) * d ** (-0.5)
            return x / (rms + EPS)

        def _rpe(idx, pos_w, pos_b, rpe_lw, rpe_lb, out_w, out_b):
            h = idx @ pos_w.T + pos_b
            for i in range(LAYERS):
                h = jax.nn.relu(_srms(h, RPE)) @ rpe_lw[i].T + rpe_lb[i]
            return jax.nn.relu(_srms(h, RPE)) @ out_w.T + out_b
        key = jax.random.key(seed)
        ks = jax.random.split(key, 9)
        s = lambda k, shape, fan: jax.random.normal(k, shape, jnp.float32) * fan ** (-0.5)
        return {'x': jax.random.normal(ks[0], (B, N, E), jnp.float32), 'u_w': s(ks[1], (D1, E), E), 'u_b': jnp.zeros((D1,), jnp.float32), 'v_w': s(ks[2], (D1, E), E), 'v_b': jnp.zeros((D1,), jnp.float32), 'o_w': s(ks[3], (E, D1), D1), 'o_b': jnp.zeros((E,), jnp.float32), 't_w': s(ks[4], (E, E), E), 't_b': jnp.zeros((E,), jnp.float32), 'pos_w': s(ks[5], (RPE, 1), 1), 'pos_b': jnp.zeros((RPE,), jnp.float32), 'rpe_lw': s(ks[6], (LAYERS, RPE, RPE), RPE), 'rpe_lb': jnp.zeros((LAYERS, RPE), jnp.float32), 'out_w': s(ks[7], (H * HD, RPE), RPE), 'out_b': jnp.zeros((H * HD,), jnp.float32)}
    _L1_attn_all = _L1_attn_setup()
    _L1_attn_in = {k: v for k, v in _L1_attn_all.items() if k in ('u_w', 'u_b', 'v_w', 'v_b', 'o_w', 'o_b', 't_w', 't_b', 'pos_w', 'pos_b', 'rpe_lw', 'rpe_lb', 'out_w', 'out_b')}
    del _L1_attn_all

    def _L1_ffn_setup():
        import jax, jax.numpy as jnp
        import numpy as np
        B, T, C = (64, 96, 64)
        NH, NKV = (4, 2)
        HD = C // NH
        NREP = NH // NKV
        NE, TOPK = (8, 2)
        HID = int(8 / 3 * C)
        EPS_RMS = 1e-06

        def _rope_tables(t_len):
            inv_freq = 1.0 / 10000.0 ** (np.arange(0, HD, 2, dtype=np.float32) / HD)
            t = np.arange(t_len, dtype=np.float32)
            freqs = np.outer(t, inv_freq)
            emb = np.concatenate([freqs, freqs], axis=-1)
            return (jnp.asarray(np.cos(emb)), jnp.asarray(np.sin(emb)))

        def _rotate_half(x):
            h = x.shape[-1] // 2
            return jnp.concatenate([-x[..., h:], x[..., :h]], axis=-1)

        def _rmsnorm(v, w):
            return v * jax.lax.rsqrt(jnp.mean(v * v, axis=-1, keepdims=True) + EPS_RMS) * w
        key = jax.random.key(seed)
        ks = jax.random.split(key, 10)
        s = lambda k, shape: jax.random.normal(k, shape, jnp.float32) * 0.02
        return {'x': jax.random.normal(ks[0], (B, T, C), jnp.float32), 'ln1_w': jnp.ones((C,), jnp.float32), 'ln2_w': jnp.ones((C,), jnp.float32), 'wq': s(ks[1], (NH * HD, C)), 'wk': s(ks[2], (NKV * HD, C)), 'wv': s(ks[3], (NKV * HD, C)), 'wo': s(ks[4], (C, C)), 'router_w': s(ks[5], (NE, C)), 'w1': s(ks[6], (NE, HID, C)), 'w2': s(ks[7], (NE, C, HID)), 'w3': s(ks[8], (NE, HID, C))}
    _L1_ffn_all = _L1_ffn_setup()
    _L1_ffn_in = {k: v for k, v in _L1_ffn_all.items() if k in ('ln1_w', 'ln2_w', 'wq', 'wk', 'wv', 'wo', 'router_w', 'w1', 'w2', 'w3')}
    del _L1_ffn_all

    def _L2_attn_setup():
        import jax, jax.numpy as jnp
        import numpy as np
        B, S, D, H = (4, 512, 64, 8)
        SPARSITY = 0.1
        key = jax.random.key(seed)
        ks = jax.random.split(key, 6)
        s = 0.02
        return {'x': jax.random.normal(ks[0], (B, S, D), jnp.float32), 'w_in': jax.random.normal(ks[1], (3 * D, D), jnp.float32) * s, 'b_in': jnp.zeros((3 * D,), jnp.float32), 'w_out': jax.random.normal(ks[2], (D, D), jnp.float32) * s, 'b_out': jnp.zeros((D,), jnp.float32), 'gate_w1': jax.random.normal(ks[3], (D // 4, D), jnp.float32) * s, 'gate_b1': jnp.zeros((D // 4,), jnp.float32), 'gate_w2': jax.random.normal(ks[4], (1, D // 4), jnp.float32) * s, 'gate_b2': jnp.zeros((1,), jnp.float32)}
    _L2_attn_all = _L2_attn_setup()
    _L2_attn_in = {k: v for k, v in _L2_attn_all.items() if k in ('w_in', 'b_in', 'w_out', 'b_out', 'gate_w1', 'gate_b1', 'gate_w2', 'gate_b2')}
    del _L2_attn_all

    def _L2_ffn_setup():
        import jax, jax.numpy as jnp
        import numpy as np
        INPUT_WIDTH = 64
        DEPTH = 7
        OUTPUT_WIDTH = 64
        N_NODES = 2 ** (DEPTH + 1) - 1
        key = jax.random.key(seed)
        k_x, k_w1, k_w2 = jax.random.split(key, 3)
        init1 = 1.0 / np.sqrt(INPUT_WIDTH)
        x = jax.random.normal(k_x, (2, 256, INPUT_WIDTH), dtype=jnp.float32)
        w1s = jax.random.uniform(k_w1, (N_NODES, INPUT_WIDTH), jnp.float32, -init1, init1)
        b1s = jnp.zeros((N_NODES,), jnp.float32)
        w2s = jax.random.uniform(k_w2, (N_NODES, INPUT_WIDTH, OUTPUT_WIDTH), jnp.float32, -init1, init1)
        b2s = jnp.zeros((N_NODES, OUTPUT_WIDTH), jnp.float32)
        return {'x': x, 'w1s': w1s, 'b1s': b1s, 'w2s': w2s, 'b2s': b2s}
    _L2_ffn_all = _L2_ffn_setup()
    _L2_ffn_in = {k: v for k, v in _L2_ffn_all.items() if k in ('w1s', 'b1s', 'w2s', 'b2s')}
    del _L2_ffn_all

    def _L3_attn_setup():
        import jax, jax.numpy as jnp
        import numpy as np
        key = jax.random.key(seed)
        k1, k2 = jax.random.split(key)
        B, N, D = (4, 1024, 64)
        inp = jax.random.normal(k1, (B, N, D), dtype=jnp.float32)
        q_weight = jax.random.normal(k2, (D, D), dtype=jnp.float32)
        return {'input': inp, 'q_weight': q_weight}
    _L3_attn_all = _L3_attn_setup()
    _L3_attn_in = {k: v for k, v in _L3_attn_all.items() if k in ('q_weight',)}
    del _L3_attn_all

    def _L3_ffn_setup():
        import jax, jax.numpy as jnp
        import numpy as np
        B, A = (1024, 8)
        IN, OUT = (64, 64)
        SH1, SH2 = (64, 128)
        EH1, EH2 = (128, 64)
        E, TOPK = (4, 2)

        def _shared_mlp(x, W1, b1, W2, b2, W3, b3):
            h = jax.nn.relu(x @ W1 + b1)
            h = jax.nn.relu(h @ W2 + b2)
            return h @ W3 + b3

        def _experts_mlp(x, eW1, eb1, eW2, eb2, eW3, eb3):
            h = jax.nn.relu(jnp.einsum('baf,efh->ebah', x, eW1) + eb1[:, None, None, :])
            h = jax.nn.relu(jnp.einsum('ebah,ehg->ebag', h, eW2) + eb2[:, None, None, :])
            o = jnp.einsum('ebag,ego->ebao', h, eW3) + eb3[:, None, None, :]
            return jnp.moveaxis(o, 0, -1)
        key = jax.random.key(seed)
        ks = jax.random.split(key, 16)
        s = 0.05
        return {'x': jax.random.normal(ks[0], (B, A, IN), jnp.float32), 'sW1': jax.random.normal(ks[1], (IN, SH1), jnp.float32) * s, 'sb1': jnp.zeros((SH1,), jnp.float32), 'sW2': jax.random.normal(ks[2], (SH1, SH2), jnp.float32) * s, 'sb2': jnp.zeros((SH2,), jnp.float32), 'sW3': jax.random.normal(ks[3], (SH2, OUT), jnp.float32) * s, 'sb3': jnp.zeros((OUT,), jnp.float32), 'eW1': jax.random.normal(ks[4], (E, IN, EH1), jnp.float32) * s, 'eb1': jnp.zeros((E, EH1), jnp.float32), 'eW2': jax.random.normal(ks[5], (E, EH1, EH2), jnp.float32) * s, 'eb2': jnp.zeros((E, EH2), jnp.float32), 'eW3': jax.random.normal(ks[6], (E, EH2, OUT), jnp.float32) * s, 'eb3': jnp.zeros((E, OUT), jnp.float32), 'gW': jax.random.normal(ks[7], (IN, E), jnp.float32) * s, 'gb': jnp.zeros((E,), jnp.float32)}
    _L3_ffn_all = _L3_ffn_setup()
    _L3_ffn_in = {k: v for k, v in _L3_ffn_all.items() if k in ('sW1', 'sb1', 'sW2', 'sb2', 'sW3', 'sb3', 'eW1', 'eb1', 'eW2', 'eb2', 'eW3', 'eb3', 'gW', 'gb')}
    del _L3_ffn_all
    return {'x': x, 'txt': txt, 'L0_tok_W': _L0_tok_in['W'], 'L0_tok_b': _L0_tok_in['b'], 'L0_attn_qkv_w': _L0_attn_in['qkv_w'], 'L0_attn_qkv_b': _L0_attn_in['qkv_b'], 'L0_attn_proj_w': _L0_attn_in['proj_w'], 'L0_attn_proj_b': _L0_attn_in['proj_b'], 'L0_attn_ln1_g': _L0_attn_in['ln1_g'], 'L0_attn_ln1_b': _L0_attn_in['ln1_b'], 'L0_attn_w1': _L0_attn_in['w1'], 'L0_attn_b1': _L0_attn_in['b1'], 'L0_attn_w2': _L0_attn_in['w2'], 'L0_attn_b2': _L0_attn_in['b2'], 'L0_attn_ln2_g': _L0_attn_in['ln2_g'], 'L0_attn_ln2_b': _L0_attn_in['ln2_b'], 'L0_ffn_Wq_pk': _L0_ffn_in['Wq_pk'], 'L0_ffn_pk_keys': _L0_ffn_in['pk_keys'], 'L0_ffn_Wq': _L0_ffn_in['Wq'], 'L0_ffn_keys_table': _L0_ffn_in['keys_table'], 'L0_ffn_values_table': _L0_ffn_in['values_table'], 'L0_ffn_Wo': _L0_ffn_in['Wo'], 'L1_attn_u_w': _L1_attn_in['u_w'], 'L1_attn_u_b': _L1_attn_in['u_b'], 'L1_attn_v_w': _L1_attn_in['v_w'], 'L1_attn_v_b': _L1_attn_in['v_b'], 'L1_attn_o_w': _L1_attn_in['o_w'], 'L1_attn_o_b': _L1_attn_in['o_b'], 'L1_attn_t_w': _L1_attn_in['t_w'], 'L1_attn_t_b': _L1_attn_in['t_b'], 'L1_attn_pos_w': _L1_attn_in['pos_w'], 'L1_attn_pos_b': _L1_attn_in['pos_b'], 'L1_attn_rpe_lw': _L1_attn_in['rpe_lw'], 'L1_attn_rpe_lb': _L1_attn_in['rpe_lb'], 'L1_attn_out_w': _L1_attn_in['out_w'], 'L1_attn_out_b': _L1_attn_in['out_b'], 'L1_ffn_ln1_w': _L1_ffn_in['ln1_w'], 'L1_ffn_ln2_w': _L1_ffn_in['ln2_w'], 'L1_ffn_wq': _L1_ffn_in['wq'], 'L1_ffn_wk': _L1_ffn_in['wk'], 'L1_ffn_wv': _L1_ffn_in['wv'], 'L1_ffn_wo': _L1_ffn_in['wo'], 'L1_ffn_router_w': _L1_ffn_in['router_w'], 'L1_ffn_w1': _L1_ffn_in['w1'], 'L1_ffn_w2': _L1_ffn_in['w2'], 'L1_ffn_w3': _L1_ffn_in['w3'], 'L2_attn_w_in': _L2_attn_in['w_in'], 'L2_attn_b_in': _L2_attn_in['b_in'], 'L2_attn_w_out': _L2_attn_in['w_out'], 'L2_attn_b_out': _L2_attn_in['b_out'], 'L2_attn_gate_w1': _L2_attn_in['gate_w1'], 'L2_attn_gate_b1': _L2_attn_in['gate_b1'], 'L2_attn_gate_w2': _L2_attn_in['gate_w2'], 'L2_attn_gate_b2': _L2_attn_in['gate_b2'], 'L2_ffn_w1s': _L2_ffn_in['w1s'], 'L2_ffn_b1s': _L2_ffn_in['b1s'], 'L2_ffn_w2s': _L2_ffn_in['w2s'], 'L2_ffn_b2s': _L2_ffn_in['b2s'], 'L3_attn_q_weight': _L3_attn_in['q_weight'], 'L3_ffn_sW1': _L3_ffn_in['sW1'], 'L3_ffn_sb1': _L3_ffn_in['sb1'], 'L3_ffn_sW2': _L3_ffn_in['sW2'], 'L3_ffn_sb2': _L3_ffn_in['sb2'], 'L3_ffn_sW3': _L3_ffn_in['sW3'], 'L3_ffn_sb3': _L3_ffn_in['sb3'], 'L3_ffn_eW1': _L3_ffn_in['eW1'], 'L3_ffn_eb1': _L3_ffn_in['eb1'], 'L3_ffn_eW2': _L3_ffn_in['eW2'], 'L3_ffn_eb2': _L3_ffn_in['eb2'], 'L3_ffn_eW3': _L3_ffn_in['eW3'], 'L3_ffn_eb3': _L3_ffn_in['eb3'], 'L3_ffn_gW': _L3_ffn_in['gW'], 'L3_ffn_gb': _L3_ffn_in['gb']}

def reference(x, txt, L0_tok_W, L0_tok_b, L0_attn_qkv_w, L0_attn_qkv_b, L0_attn_proj_w, L0_attn_proj_b, L0_attn_ln1_g, L0_attn_ln1_b, L0_attn_w1, L0_attn_b1, L0_attn_w2, L0_attn_b2, L0_attn_ln2_g, L0_attn_ln2_b, L0_ffn_Wq_pk, L0_ffn_pk_keys, L0_ffn_Wq, L0_ffn_keys_table, L0_ffn_values_table, L0_ffn_Wo, L1_attn_u_w, L1_attn_u_b, L1_attn_v_w, L1_attn_v_b, L1_attn_o_w, L1_attn_o_b, L1_attn_t_w, L1_attn_t_b, L1_attn_pos_w, L1_attn_pos_b, L1_attn_rpe_lw, L1_attn_rpe_lb, L1_attn_out_w, L1_attn_out_b, L1_ffn_ln1_w, L1_ffn_ln2_w, L1_ffn_wq, L1_ffn_wk, L1_ffn_wv, L1_ffn_wo, L1_ffn_router_w, L1_ffn_w1, L1_ffn_w2, L1_ffn_w3, L2_attn_w_in, L2_attn_b_in, L2_attn_w_out, L2_attn_b_out, L2_attn_gate_w1, L2_attn_gate_b1, L2_attn_gate_w2, L2_attn_gate_b2, L2_ffn_w1s, L2_ffn_b1s, L2_ffn_w2s, L2_ffn_b2s, L3_attn_q_weight, L3_ffn_sW1, L3_ffn_sb1, L3_ffn_sW2, L3_ffn_sb2, L3_ffn_sW3, L3_ffn_sb3, L3_ffn_eW1, L3_ffn_eb1, L3_ffn_eW2, L3_ffn_eb2, L3_ffn_eW3, L3_ffn_eb3, L3_ffn_gW, L3_ffn_gb):
    import jax
    import jax.numpy as jnp

    def _L0_tok_ref(x, W, b):
        import jax, jax.numpy as jnp
        import numpy as np
        P = 8
        C = 1
        D = 64
        B, c, h, w = x.shape
        p = P
        xp = x.reshape(B, c, h // p, p, w // p, p)
        xp = jnp.transpose(xp, (0, 2, 4, 3, 5, 1))
        xp = xp.reshape(B, h // p * (w // p), p * p * c)
        return jnp.einsum('bnk,dk->bnd', xp, W) + b

    def _L0_attn_ref(x, qkv_w, qkv_b, proj_w, proj_b, ln1_g, ln1_b, w1, b1, w2, b2, ln2_g, ln2_b):
        import jax, jax.numpy as jnp
        import numpy as np
        B, T, D = (2, 512, 64)

        def _layernorm(x, g, b, eps=1e-05):
            mu = jnp.mean(x, axis=-1, keepdims=True)
            var = jnp.var(x, axis=-1, keepdims=True)
            return (x - mu) * jax.lax.rsqrt(var + eps) * g + b
        scale = float(D) ** 0.5
        x_f32 = x.astype(jnp.float32)
        qkv = x_f32 @ qkv_w + qkv_b
        q, k, v = jnp.split(qkv, 3, axis=-1)
        q = q / scale
        k = k / scale
        q = q / jnp.maximum(jnp.linalg.norm(q, axis=-1, keepdims=True), 1e-12)
        k = k / jnp.maximum(jnp.linalg.norm(k, axis=-1, keepdims=True), 1e-12)
        q = jax.nn.softplus(q) + 1e-06
        k = jax.nn.softplus(k) + 1e-06
        kv = jnp.einsum('btd,bte->btde', k, v)
        kv_sum = jnp.cumsum(kv, axis=1)
        k_sum = jnp.cumsum(k, axis=1)
        num = jnp.einsum('btd,btde->bte', q, kv_sum)
        den = jnp.maximum(jnp.einsum('btd,btd->bt', q, k_sum)[..., None], 1e-06)
        num = jnp.clip(num, -10000.0, 10000.0)
        attn_out = num / den
        x_attn = _layernorm(x_f32 + attn_out @ proj_w + proj_b, ln1_g, ln1_b)
        h = jax.nn.gelu(x_attn @ w1 + b1, approximate=False)
        out = _layernorm(x_attn + h @ w2 + b2, ln2_g, ln2_b)
        return out.astype(x.dtype)

    def _L0_ffn_ref(x, Wq_pk, pk_keys, Wq, keys_table, values_table, Wo):
        import jax, jax.numpy as jnp
        import numpy as np
        DIM = 64
        HEADS = 8
        NUM_KEYS = 64
        NUM_KV = NUM_KEYS ** 2
        PK_TOPK = 16
        FINAL_TOPK = 16
        DIM_KEY = DIM // 2
        P = 2

        def _pk(x, Wq_pk, pk_keys):
            b, n, _ = x.shape
            q = (x @ Wq_pk).reshape(b, n, P, HEADS, DIM_KEY).transpose(2, 0, 1, 3, 4)
            sim = jnp.einsum('pbnhd,pkhd->pbnhk', q, pk_keys)
            scores, idx = jax.lax.top_k(sim, PK_TOPK)
            idx0 = idx[0]
            idx1 = idx[1] * NUM_KEYS
            index = (idx0[..., :, None] + idx1[..., None, :]).reshape(b, n, HEADS, PK_TOPK * PK_TOPK)
            score = (scores[0][..., :, None] + scores[1][..., None, :]).reshape(b, n, HEADS, PK_TOPK * PK_TOPK)
            final_scores, pk_idx = jax.lax.top_k(score, FINAL_TOPK)
            final_indices = jnp.take_along_axis(index, pk_idx, axis=-1)
            final_scores = jax.nn.softmax(final_scores, axis=-1)
            return (final_scores, final_indices)
        b, n, d = x.shape
        q = (x @ Wq).reshape(b, n, HEADS, DIM) * DIM ** (-0.5)
        kv_scores, indices = _pk(x, Wq_pk, pk_keys)
        offsets = jnp.arange(HEADS, dtype=indices.dtype) * NUM_KV
        ind = indices + offsets[None, None, :, None]
        k = jnp.einsum('bnhk,bnhkd->bnhd', kv_scores, keys_table[ind])
        v = jnp.einsum('bnhk,bnhkd->bnhd', kv_scores, values_table[ind])
        sim = jnp.einsum('bihd,bjhd->bhij', q, k)
        neg = -jnp.finfo(sim.dtype).max
        causal = jnp.tril(jnp.ones((n, n), dtype=bool))
        sim = jnp.where(causal, sim, neg)
        attn = jax.nn.softmax(sim, axis=-1)
        out = jnp.einsum('bhij,bjhd->bhid', attn, v)
        out = out.transpose(0, 2, 1, 3).reshape(b, n, HEADS * DIM)
        return out @ Wo

    def _L1_attn_ref(x, u_w, u_b, v_w, v_b, o_w, o_b, t_w, t_b, pos_w, pos_b, rpe_lw, rpe_lb, out_w, out_b):
        import jax, jax.numpy as jnp
        import numpy as np
        B, N, E, H = (4, 1024, 64, 8)
        EXP = 3
        D1 = EXP * E // H * H
        HD = D1 // H
        RPE = int(min(E / 8, 32))
        LAYERS = 3
        EPS = 1e-08

        def _srms(x, d):
            rms = jnp.linalg.norm(x, axis=-1, keepdims=True) * d ** (-0.5)
            return x / (rms + EPS)

        def _rpe(idx, pos_w, pos_b, rpe_lw, rpe_lb, out_w, out_b):
            h = idx @ pos_w.T + pos_b
            for i in range(LAYERS):
                h = jax.nn.relu(_srms(h, RPE)) @ rpe_lw[i].T + rpe_lb[i]
            return jax.nn.relu(_srms(h, RPE)) @ out_w.T + out_b
        b, n, _ = x.shape
        u = jax.nn.silu(x @ u_w.T + u_b)
        v = jax.nn.silu(x @ v_w.T + v_b)
        v = v.reshape(b, n, H, HD).transpose(0, 2, 1, 3)
        pos_idx = jnp.arange(1, n, dtype=jnp.float32)
        idx = jnp.concatenate([jnp.zeros((1,), jnp.float32), pos_idx, jnp.zeros((1,), jnp.float32), -pos_idx[::-1]])[:, None]
        a = _rpe(idx, pos_w, pos_b, rpe_lw, rpe_lb, out_w, out_b)
        a = a.reshape(2 * n, H, HD).transpose(1, 0, 2)
        yf = jnp.fft.rfft(v, 2 * n, axis=-2)
        af = jnp.fft.rfft(a, 2 * n, axis=-2)[None]
        out = jnp.fft.irfft(af * yf, 2 * n, axis=-2)[:, :, :n, :]
        out = out.transpose(0, 2, 1, 3).reshape(b, n, D1)
        out = u * out @ o_w.T + o_b
        x_r = jax.nn.silu(_srms((x - out) @ t_w.T + t_b, D1))
        return x + x_r

    def _L1_ffn_ref(x, ln1_w, ln2_w, wq, wk, wv, wo, router_w, w1, w2, w3):
        import jax, jax.numpy as jnp
        import numpy as np
        B, T, C = (64, 96, 64)
        NH, NKV = (4, 2)
        HD = C // NH
        NREP = NH // NKV
        NE, TOPK = (8, 2)
        HID = int(8 / 3 * C)
        EPS_RMS = 1e-06

        def _rope_tables(t_len):
            inv_freq = 1.0 / 10000.0 ** (np.arange(0, HD, 2, dtype=np.float32) / HD)
            t = np.arange(t_len, dtype=np.float32)
            freqs = np.outer(t, inv_freq)
            emb = np.concatenate([freqs, freqs], axis=-1)
            return (jnp.asarray(np.cos(emb)), jnp.asarray(np.sin(emb)))

        def _rotate_half(x):
            h = x.shape[-1] // 2
            return jnp.concatenate([-x[..., h:], x[..., :h]], axis=-1)

        def _rmsnorm(v, w):
            return v * jax.lax.rsqrt(jnp.mean(v * v, axis=-1, keepdims=True) + EPS_RMS) * w
        Bx, Tx, Cx = x.shape
        h = _rmsnorm(x, ln1_w)
        q = (h @ wq.T).reshape(Bx, Tx, NH, HD).transpose(0, 2, 1, 3)
        k = (h @ wk.T).reshape(Bx, Tx, NKV, HD).transpose(0, 2, 1, 3)
        v = (h @ wv.T).reshape(Bx, Tx, NKV, HD).transpose(0, 2, 1, 3)
        cos, sin = _rope_tables(Tx)
        cos, sin = (cos[None, None], sin[None, None])
        q = q * cos + _rotate_half(q) * sin
        k = k * cos + _rotate_half(k) * sin
        k = jnp.repeat(k, NREP, axis=1)
        v = jnp.repeat(v, NREP, axis=1)
        scores = jnp.einsum('bhtd,bhsd->bhts', q, k) / jnp.sqrt(jnp.float32(HD))
        causal = jnp.tril(jnp.ones((Tx, Tx), dtype=bool))
        scores = jnp.where(causal[None, None], scores, jnp.float32(-1e+30))
        att = jax.nn.softmax(scores, axis=-1)
        y = jnp.einsum('bhts,bhsd->bhtd', att, v).transpose(0, 2, 1, 3).reshape(Bx, Tx, Cx)
        x = x + y @ wo.T
        flat = _rmsnorm(x, ln2_w).reshape(-1, Cx)
        probs = jax.nn.softmax(flat @ router_w.T, axis=-1)
        tp, ti = jax.lax.top_k(probs, TOPK)
        tp = tp / (jnp.sum(tp, axis=-1, keepdims=True) + 1e-09)
        weights = jnp.sum(tp[..., None] * jax.nn.one_hot(ti, NE, dtype=flat.dtype), axis=1)
        out = jnp.zeros_like(flat)
        for e in range(NE):
            hh = jax.nn.silu(flat @ w1[e].T) * (flat @ w3[e].T)
            out = out + weights[:, e:e + 1] * (hh @ w2[e].T)
        return x + out.reshape(Bx, Tx, Cx)

    def _L2_attn_ref(x, w_in, b_in, w_out, b_out, gate_w1, gate_b1, gate_w2, gate_b2):
        import jax, jax.numpy as jnp
        import numpy as np
        B, S, D, H = (4, 512, 64, 8)
        SPARSITY = 0.1
        b, s, d = x.shape
        hd = d // H
        h = jax.nn.relu(jnp.einsum('bsd,fd->bsf', x, gate_w1) + gate_b1)
        importance = jax.nn.sigmoid(jnp.einsum('bsf,of->bso', h, gate_w2) + gate_b2)[..., 0]
        k = max(1, int(s * SPARSITY))
        _, top_idx = jax.lax.top_k(importance, k)
        keep = jnp.zeros((b, s), dtype=bool).at[jnp.arange(b)[:, None], top_idx].set(True)
        qkv = jnp.einsum('bsd,ed->bse', x, w_in) + b_in
        q, kk, v = jnp.split(qkv, 3, axis=-1)
        split_heads = lambda t: t.reshape(b, s, H, hd).transpose(0, 2, 1, 3)
        q, kk, v = (split_heads(q), split_heads(kk), split_heads(v))
        scores = jnp.einsum('bhqd,bhkd->bhqk', q, kk) / jnp.sqrt(jnp.asarray(hd, x.dtype))
        neg = jnp.finfo(scores.dtype).min
        scores = jnp.where(keep[:, None, None, :], scores, neg)
        attn = jax.nn.softmax(scores, axis=-1)
        out = jnp.einsum('bhqk,bhkd->bhqd', attn, v)
        out = out.transpose(0, 2, 1, 3).reshape(b, s, d)
        return jnp.einsum('bsd,od->bso', out, w_out) + b_out

    def _L2_ffn_ref(x, w1s, b1s, w2s, b2s):
        import jax, jax.numpy as jnp
        import numpy as np
        INPUT_WIDTH = 64
        DEPTH = 7
        OUTPUT_WIDTH = 64
        N_NODES = 2 ** (DEPTH + 1) - 1
        B, S, D = x.shape
        flat_x = x.reshape(B * S, D)
        T = flat_x.shape[0]
        current = jnp.zeros((T,), dtype=jnp.int32)
        all_nodes = []
        all_logits = []
        for _ in range(DEPTH + 1):
            all_nodes.append(current)
            score = jnp.einsum('td,td->t', flat_x, w1s[current]) + b1s[current]
            all_logits.append(score)
            choice = ((jnp.sign(score) + 1.0) / 2.0).astype(jnp.int32)
            current = current * 2 + choice + 1
        logits = jnp.stack(all_logits, axis=1)
        path_weights = jax.nn.gelu(jnp.abs(logits), approximate=False)
        out = jnp.zeros((T, OUTPUT_WIDTH), dtype=x.dtype)
        for i in range(DEPTH + 1):
            nodes_i = all_nodes[i]
            t_i = jnp.einsum('td,tdo->to', flat_x, w2s[nodes_i]) + b2s[nodes_i]
            out = out + t_i * path_weights[:, i][:, None]
        return out.reshape(B, S, OUTPUT_WIDTH)

    def _L3_attn_ref(input, q_weight):
        import jax, jax.numpy as jnp
        import numpy as np
        query = jnp.einsum('bnd,de->bne', input, q_weight)
        att = jax.nn.sigmoid(jnp.einsum('bnd,bmd->bnm', query, input))
        value = jnp.einsum('bnm,bmd->bnd', att, input)
        return value

    def _L3_ffn_ref(x, sW1, sb1, sW2, sb2, sW3, sb3, eW1, eb1, eW2, eb2, eW3, eb3, gW, gb):
        import jax, jax.numpy as jnp
        import numpy as np
        B, A = (1024, 8)
        IN, OUT = (64, 64)
        SH1, SH2 = (64, 128)
        EH1, EH2 = (128, 64)
        E, TOPK = (4, 2)

        def _shared_mlp(x, W1, b1, W2, b2, W3, b3):
            h = jax.nn.relu(x @ W1 + b1)
            h = jax.nn.relu(h @ W2 + b2)
            return h @ W3 + b3

        def _experts_mlp(x, eW1, eb1, eW2, eb2, eW3, eb3):
            h = jax.nn.relu(jnp.einsum('baf,efh->ebah', x, eW1) + eb1[:, None, None, :])
            h = jax.nn.relu(jnp.einsum('ebah,ehg->ebag', h, eW2) + eb2[:, None, None, :])
            o = jnp.einsum('ebag,ego->ebao', h, eW3) + eb3[:, None, None, :]
            return jnp.moveaxis(o, 0, -1)
        all_out = _experts_mlp(x, eW1, eb1, eW2, eb2, eW3, eb3)
        shared = _shared_mlp(x, sW1, sb1, sW2, sb2, sW3, sb3)
        gates = jax.nn.softmax(x @ gW + gb, axis=-1)
        topv, topi = jax.lax.top_k(gates, TOPK)
        topw = jax.nn.softmax(topv, axis=-1)
        sel = jnp.take_along_axis(all_out, topi[:, :, None, :], axis=-1)
        gated = jnp.sum(sel * topw[:, :, None, :], axis=-1)
        return shared + gated
    h = _L0_tok_ref(x, L0_tok_W, L0_tok_b)
    h = jnp.concatenate([h, txt], axis=1)
    h = h + _L0_attn_ref(_layernorm(h, axis=-1), L0_attn_qkv_w, L0_attn_qkv_b, L0_attn_proj_w, L0_attn_proj_b, L0_attn_ln1_g, L0_attn_ln1_b, L0_attn_w1, L0_attn_b1, L0_attn_w2, L0_attn_b2, L0_attn_ln2_g, L0_attn_ln2_b)
    h = h + _L0_ffn_ref(_layernorm(h, axis=-1), L0_ffn_Wq_pk, L0_ffn_pk_keys, L0_ffn_Wq, L0_ffn_keys_table, L0_ffn_values_table, L0_ffn_Wo)
    h = h + _L1_attn_ref(_layernorm(h, axis=-1), L1_attn_u_w, L1_attn_u_b, L1_attn_v_w, L1_attn_v_b, L1_attn_o_w, L1_attn_o_b, L1_attn_t_w, L1_attn_t_b, L1_attn_pos_w, L1_attn_pos_b, L1_attn_rpe_lw, L1_attn_rpe_lb, L1_attn_out_w, L1_attn_out_b)
    h = h + _L1_ffn_ref(_layernorm(h, axis=-1), L1_ffn_ln1_w, L1_ffn_ln2_w, L1_ffn_wq, L1_ffn_wk, L1_ffn_wv, L1_ffn_wo, L1_ffn_router_w, L1_ffn_w1, L1_ffn_w2, L1_ffn_w3)
    h = h + _L2_attn_ref(_layernorm(h, axis=-1), L2_attn_w_in, L2_attn_b_in, L2_attn_w_out, L2_attn_b_out, L2_attn_gate_w1, L2_attn_gate_b1, L2_attn_gate_w2, L2_attn_gate_b2)
    h = h + _L2_ffn_ref(_layernorm(h, axis=-1), L2_ffn_w1s, L2_ffn_b1s, L2_ffn_w2s, L2_ffn_b2s)
    h = h + _L3_attn_ref(_layernorm(h, axis=-1), L3_attn_q_weight)
    h = h + _L3_ffn_ref(_layernorm(h, axis=-1), L3_ffn_sW1, L3_ffn_sb1, L3_ffn_sW2, L3_ffn_sb2, L3_ffn_sW3, L3_ffn_sb3, L3_ffn_eW1, L3_ffn_eb1, L3_ffn_eW2, L3_ffn_eb2, L3_ffn_eW3, L3_ffn_eb3, L3_ffn_gW, L3_ffn_gb)
    return h

_drawn_inputs = setup_inputs


def setup_inputs(seed=0):
    import zlib

    import numpy as np

    out = dict(_drawn_inputs(seed))
    spreads = {'L0_attn_qkv_b': (0.0, 0.1),
     'L0_attn_proj_b': (0.0, 0.1),
     'L0_attn_ln1_g': (1.0, 0.2),
     'L0_attn_ln1_b': (0.0, 0.1),
     'L0_attn_b1': (0.0, 0.1),
     'L0_attn_b2': (0.0, 0.1),
     'L0_attn_ln2_g': (1.0, 0.2),
     'L0_attn_ln2_b': (0.0, 0.1),
     'L1_attn_u_b': (0.0, 0.1),
     'L1_attn_v_b': (0.0, 0.1),
     'L1_attn_o_b': (0.0, 0.8),
     'L1_attn_t_b': (0.0, 0.8),
     'L1_attn_pos_b': (0.0, 2.0),
     'L1_attn_rpe_lb': (0.0, 0.1),
     'L1_attn_out_b': (0.0, 0.1),
     'L1_ffn_ln1_w': (1.0, 0.6),
     'L1_ffn_ln2_w': (1.0, 0.6),
     'L2_attn_b_in': (0.0, 0.289),
     'L2_attn_b_out': (0.0, 0.1),
     'L2_attn_gate_b1': (0.0, 0.607),
     'L2_ffn_b1s': (0.0, 0.1),
     'L2_ffn_b2s': (0.0, 0.1),
     'L3_ffn_sb1': (0.0, 0.8),
     'L3_ffn_sb2': (0.0, 0.8),
     'L3_ffn_sb3': (0.0, 2.0),
     'L3_ffn_eb1': (0.0, 0.8),
     'L3_ffn_eb2': (0.0, 2.0),
     'L3_ffn_eb3': (0.0, 2.0),
     'L3_ffn_gb': (0.0, 0.8)}
    factors = {'L0_attn_qkv_w': 5.34,
     'L0_ffn_Wq_pk': 8.0,
     'L0_ffn_pk_keys': 8.0,
     'L0_ffn_Wq': 25.354,
     'L0_ffn_keys_table': 25.946,
     'L0_ffn_values_table': 8.0,
     'L0_ffn_Wo': 8.0,
     'L1_ffn_wq': 8.0,
     'L1_ffn_wk': 8.0,
     'L1_ffn_wv': 6.341,
     'L1_ffn_wo': 6.594,
     'L1_ffn_router_w': 8.0,
     'L1_ffn_w1': 8.0,
     'L1_ffn_w2': 8.0,
     'L1_ffn_w3': 8.0,
     'L2_attn_w_in': 4.483,
     'L2_attn_gate_w1': 4.713,
     'L2_attn_gate_w2': 4.479,
     'L3_ffn_sW1': 8.0,
     'L3_ffn_sW2': 8.0,
     'L3_ffn_sW3': 8.0,
     'L3_ffn_eW1': 8.0,
     'L3_ffn_eW2': 8.0,
     'L3_ffn_eW3': 8.0,
     'L3_ffn_gW': 8.0}
    for name, (base, spread) in spreads.items():
        noise = np.random.default_rng([zlib.crc32(name.encode()), seed]).standard_normal(out[name].shape)
        drawn = base * np.exp(spread * noise) if base else spread * noise
        out[name] = jnp.asarray(drawn.astype(out[name].dtype))
    for name, factor in factors.items():
        out[name] = (out[name] * factor).astype(out[name].dtype)
    return out
```

```python
from contextlib import ExitStack

import numpy as np

import concourse.bass as bass
from concourse import mybir
from concourse.alu_op_type import AluOpType as ALU

F32 = mybir.dt.float32
U32 = mybir.dt.uint32
ACT = mybir.ActivationFunctionType
AX = mybir.AxisListType

P = 128
B = 4
PATCHES = 64
TEXT = 512
SEQ = PATCHES + TEXT
D = 64
CH = 5
PAD = CH * P
TAIL = SEQ - 4 * P
T = B * CH
COLS = T * P
BANK = 512
GROUPS = COLS // BANK
LN_EPS = 1e-5
NEG = -1e30


class Steps:

    def __init__(self, engine, semaphore):
        self.engine, self.semaphore, self.before, self.count = engine, semaphore, 0, 0

    def add(self, instruction):
        instruction.then_inc(self.semaphore, 1)
        self.count += 1

    def settle(self, apart=None):
        self.engine.wait_ge(self.semaphore, self.before + self.count)
        if apart is not None:
            wait_apart(self.engine, apart)

    def do(self, instruction):
        self.add(instruction)
        self.settle()

    def enter_loop(self, turn, per_turn):
        self.outside = self.before + self.count
        self.before, self.count, self.per_turn = turn * per_turn + self.outside, 0, per_turn

    def leave_loop(self, turns):
        assert self.count == self.per_turn, (self.count, self.per_turn)
        self.before, self.count = self.outside + turns * self.per_turn, 0


def wait_apart(engine, passed):
    engine.sem_inc(passed, 1)


class Stage:

    SPENT_MAX = 90
    spent = []

    def __init__(self, nc, name):
        self.nc, self.name, self.sems = nc, name, []

    def __enter__(self):
        self.stack = ExitStack()
        return self

    def __exit__(self, *problem):
        self.stack.close()
        Stage.spent += self.sems
        if not problem[0] and len(Stage.spent) >= self.SPENT_MAX:
            self.nc.clear_and_free_semaphores(Stage.spent)
            Stage.spent.clear()
            self.nc.all_engine_barrier()

    def sb(self, name, shape, dtype=F32):
        return self.stack.enter_context(self.nc.sbuf_tensor(f"{self.name}_{name}", shape, dtype))

    def sem(self, name):
        s = self.nc.alloc_semaphore(f"{self.name}_{name}")
        self.sems.append(s)
        return s


class Core:
    pass


START = 1


def start_loop(nc, semaphores):
    with nc.Block() as block:
        @block.sync
        def _(sp):
            for s in semaphores:
                sp.sem_inc(s, START)


def over(ap, n):
    return ap.unsqueeze(len(ap.shape)).to_broadcast([*ap.shape, n])


def rows_of(ap, n):
    return ap.unsqueeze(1).to_broadcast([ap.shape[0], n, *ap.shape[1:]])


def load_stage(nc, name, loads):
    with Stage(nc, name) as st:
        landed = st.sem("landed")
        with nc.Block() as block:
            @block.sync
            def _(sp):
                for to, of in loads:
                    sp.dma_start(to, of).then_inc(landed, 16)
                sp.wait_ge(landed, 16 * len(loads))


def embed_stage(nc, core, x_patches, txt, w_patch):
    with Stage(nc, "embed") as st:
        pixels = st.sb("pixels", [D + 1, B * PATCHES])
        weights = st.sb("weights", [D + 1, D])
        ones_set, landed, products, text_landed, copied = (
            st.sem(n) for n in ("ones_set", "landed", "products", "text_landed", "copied"))
        h_b = core.h[:, :, :].rearrange("p (b c) d -> p b c d", c=CH)
        with nc.Block() as block:
            @block.sync
            def _(sp):
                sp.wait_ge(ones_set, 2)
                sp.dma_start(pixels[0:D, :], x_patches).then_inc(landed, 16)
                sp.dma_start(weights[:, :], w_patch).then_inc(landed, 16)
                for b in range(B):
                    sp.dma_start(h_b[PATCHES:P, b, 0, :], txt[b, 0:P - PATCHES, :]).then_inc(text_landed, 16)
                    sp.dma_start(h_b[:, b, 1:CH - 1, :],
                                 txt[b, P - PATCHES:TEXT - TAIL, :].rearrange("(c p) d -> p c d", p=P)
                                 ).then_inc(text_landed, 16)
                    sp.dma_start(h_b[0:TAIL, b, CH - 1, :], txt[b, TEXT - TAIL:TEXT, :]).then_inc(text_landed, 16)
                sp.wait_ge(text_landed, 16 * 3 * B)

            @block.gpsimd
            def _(pool):
                nc.gpsimd.memset(pixels[:, :], 1.0).then_inc(ones_set, 1)
                nc.gpsimd.memset(core.h[:, :, :], 0.0).then_inc(ones_set, 1)
                nc.gpsimd.memset(core.xnT[:, :], 1.0).then_inc(ones_set, 1)
                nc.gpsimd.memset(core.ident[:, :], 0.0).then_inc(ones_set, 1)
                pool.wait_ge(ones_set, 4)
                nc.gpsimd.affine_select(out=core.ident[:, :], in_=core.ident[:, :], compare_op=ALU.not_equal,
                                        fill=1.0, base=0, pattern=[[-1, P]], channel_multiplier=1)

            @block.tensor
            def _(pe):
                pe.wait_ge(landed, 32)
                for b in range(B):
                    last = nc.tensor.matmul(core.psum[0:PATCHES, 0, b * D:(b + 1) * D],
                                            pixels[:, b * PATCHES:(b + 1) * PATCHES], weights[:, :],
                                            start=True, stop=True)
                last.then_inc(products, 1)

            @block.vector
            def _(dve):
                dve.wait_ge(products, 1)
                dve.wait_ge(ones_set, 4)
                nc.vector.tensor_copy(h_b[0:PATCHES, :, 0, :],
                                      core.psum[0:PATCHES, 0, 0:B * D].rearrange("p (b d) -> p b d", d=D)
                                      ).then_inc(copied, 1)


def norm_steps(nc, steps, dve, x, out, sq, stat, std_ready, var_ready, eps, use_mean=True, by=None):
    width = x.shape[-1]
    if use_mean:
        steps.do(nc.vector.tensor_reduce(stat[:, 0, :], x, AX.X, ALU.add))
        steps.do(nc.vector.tensor_scalar(stat[:, 0, :], stat[:, 0, :], 1.0 / width, None, ALU.mult))
        steps.do(nc.vector.tensor_tensor(out, x, over(stat[:, 0, :], width), ALU.subtract))
        x = out
    steps.do(nc.vector.tensor_tensor(sq, x, x, ALU.mult))
    steps.do(nc.vector.tensor_reduce(stat[:, 1, :], sq, AX.X, ALU.add))
    nc.vector.tensor_scalar(stat[:, 1, :], stat[:, 1, :], 1.0 / width, eps, ALU.mult, ALU.add).then_inc(var_ready, 1)
    dve.wait_ge(std_ready, 1)
    steps.do(nc.vector.reciprocal(stat[:, 3, :], stat[:, 2, :]))
    steps.do(nc.vector.tensor_tensor(out, x, over(stat[:, 3, :], width), ALU.mult))


def norm_stage(nc, core, name, src, eps=LN_EPS, use_mean=True, gain=None, shift=None, first=None,
               dst=None, turn=True):
    dst = core.xn if dst is None else dst
    with Stage(nc, name) as st:
        sq = st.sb("sq", [P, T, D])
        stat = st.sb("stat", [P, 4, T])
        stat2 = st.sb("stat2", [P, 4, T])
        rows = st.sb("rows", [P, 2, D])
        vec, var, std, var2, std2, ready, turned, drained, landed = (
            st.sem(n) for n in ("vector_steps", "var_ready", "std_ready", "var2_ready", "std2_ready",
                                "dst_ready", "turned", "drained", "rows_landed"))
        vecs = [v for v in (gain, shift) if v is not None]
        with nc.Block() as block:
            @block.sync
            def _(sp):
                for k, v in enumerate(vecs):
                    sp.dma_start(rows[:, k, :], v.partition_broadcast(P)).then_inc(landed, 16)

            @block.vector
            def _(dve):
                steps = Steps(dve, vec)
                if first is None:
                    norm_steps(nc, steps, dve, src[:, :, :], dst[:, :, :], sq[:, :, :], stat, std, var, eps, use_mean)
                else:
                    norm_steps(nc, steps, dve, src[:, :, :], first[:, :, :], sq[:, :, :], stat, std, var, LN_EPS)
                    norm_steps(nc, steps, dve, first[:, :, :], dst[:, :, :], sq[:, :, :], stat2, std2, var2, eps, use_mean)
                if vecs:
                    dve.wait_ge(landed, 16 * len(vecs))
                    steps.do(nc.vector.tensor_tensor(dst[:, :, :], dst[:, :, :], rows_of(rows[:, 0, :], T), ALU.mult))
                    if shift is not None:
                        steps.do(nc.vector.tensor_tensor(dst[:, :, :], dst[:, :, :], rows_of(rows[:, 1, :], T), ALU.add))
                dve.sem_inc(ready, 1)

            @block.scalar
            def _(act):
                act.wait_ge(var, 1)
                nc.scalar.activation(stat[:, 2, :], stat[:, 1, :], ACT.Sqrt).then_inc(std, 1)
                if first is not None:
                    act.wait_ge(var2, 1)
                    nc.scalar.activation(stat2[:, 2, :], stat2[:, 1, :], ACT.Sqrt).then_inc(std2, 1)
                if turn:
                    for g in range(GROUPS):
                        act.wait_ge(turned, g + 1)
                        nc.scalar.activation(core.xnT[0:D, g * BANK:(g + 1) * BANK], core.psum[0:D, g, :],
                                             ACT.Copy).then_inc(drained, 1)

            @block.tensor
            def _(pe):
                if turn:
                    pe.wait_ge(ready, 1)
                    for t in range(T):
                        last = nc.tensor.transpose(core.psum[0:D, t // 4, t % 4 * P:(t % 4 + 1) * P],
                                                   dst[:, t, :], core.ident[:, :])
                        if t % 4 == 3:
                            last.then_inc(turned, 1)


def turn_stage(nc, core, name, jobs):
    with Stage(nc, name) as st:
        turned, by_scalar, by_vector = st.sem("turned"), st.sem("drained_scalar"), st.sem("drained_vector")
        banks = [(job, g) for job in jobs for g in range(GROUPS)]
        with nc.Block() as block:
            @block.tensor
            def _(pe):
                for n, ((_, width, src), g) in enumerate(banks):
                    if n >= 8:
                        pe.wait_ge(by_vector if n % 2 else by_scalar, (n - 8) // 2 + 1)
                    for k in range(4):
                        last = nc.tensor.transpose(core.psum[0:width, n % 8, k * P:(k + 1) * P],
                                                   src(4 * g + k), core.ident[:, :])
                    last.then_inc(turned, 1)

            @block.scalar
            def _(act):
                for n, ((dst, width, _), g) in enumerate(banks):
                    if n % 2 == 0:
                        act.wait_ge(turned, n + 1)
                        nc.scalar.activation(dst[0:width, g * BANK:(g + 1) * BANK], core.psum[0:width, n % 8, :],
                                             ACT.Copy).then_inc(by_scalar, 1)

            @block.vector
            def _(dve):
                for n, ((dst, width, _), g) in enumerate(banks):
                    if n % 2 == 1:
                        dve.wait_ge(turned, n + 1)
                        nc.vector.tensor_copy(dst[0:width, g * BANK:(g + 1) * BANK], core.psum[0:width, n % 8, :]
                                              ).then_inc(by_vector, 1)


def product_stage(nc, core, name, terms, width, use, engine="vector", tiles=T):
    per = min(BANK // width, 8)
    batches = [(t0, min(t0 + per, tiles)) for t0 in range(0, tiles, per)]
    with Stage(nc, name) as st:
        made, used = st.sem("made"), st.sem("used")
        with nc.Block() as block:
            @block.tensor
            def _(pe):
                for n, (t0, t1) in enumerate(batches):
                    if n >= 8:
                        pe.wait_ge(used, n - 7)
                    for t in range(t0, t1):
                        for k, (lhsT_of, rhs) in enumerate(terms):
                            last = nc.tensor.matmul(core.psum[:, n % 8, (t - t0) * width:(t - t0 + 1) * width],
                                                    lhsT_of(t), rhs, start=(k == 0), stop=(k == len(terms) - 1))
                    last.then_inc(made, 1)

            def take(eng):
                for n, (t0, t1) in enumerate(batches):
                    eng.wait_ge(made, n + 1)
                    view = core.psum[:, n % 8, 0:(t1 - t0) * width].rearrange("p (t w) -> p t w", w=width)
                    use(t0, t1, view).then_inc(used, 1)

            (block.vector if engine == "vector" else block.scalar)(take)


def wide_product_stage(nc, core, name, outputs, use, engine="scalar"):
    jobs = [(g, o) for g in range(GROUPS) for o in range(len(outputs))]
    with Stage(nc, name) as st:
        made, used = st.sem("made"), st.sem("used")
        with nc.Block() as block:
            @block.tensor
            def _(pe):
                for n, (g, o) in enumerate(jobs):
                    if n >= 8:
                        pe.wait_ge(used, n - 7)
                    rows, terms = outputs[o]
                    for k, (lhsT, rhs) in enumerate(terms):
                        last = nc.tensor.matmul(core.psum[0:rows, n % 8, :], lhsT, rhs(g * BANK, (g + 1) * BANK),
                                                start=(k == 0), stop=(k == len(terms) - 1))
                    last.then_inc(made, 1)

            def take(eng):
                for n, (g, o) in enumerate(jobs):
                    eng.wait_ge(made, n + 1)
                    use(g * BANK, (g + 1) * BANK, o, core.psum[0:outputs[o][0], n % 8, :]).then_inc(used, 1)

            (block.vector if engine == "vector" else block.scalar)(take)


def add_stage(nc, core, name, *sums):
    with Stage(nc, name) as st:
        vec = st.sem("vector_steps")
        with nc.Block() as block:
            @block.vector
            def _(dve):
                steps = Steps(dve, vec)
                for out, a, b in sums:
                    steps.do(nc.vector.tensor_tensor(out, a, b, ALU.add))


def linear_attention_stage(nc, core, I):
    with Stage(nc, "lin") as st:
        w_qkv = st.sb("w_qkv", [D + 1, 3 * D])
        qkv = st.sb("qkv", [P, T, 3 * D + 1])
        qk, v1 = qkv[:, :, 0:2 * D], qkv[:, :, 2 * D:3 * D + 1]
        sq = st.sb("sq", [P, T, 2 * D])
        stat = st.sb("stat", [P, 3, 2 * T])
        qT = st.sb("qT", [D, COLS])
        kT = st.sb("kT", [D, COLS])
        upper = st.sb("upper", [P, P])
        scores = st.sb("scores", [P, 2, CH, PAD])
        attn = st.sb("attn", [P, T, D])
        den = st.sb("den", [P, T])
        load_stage(nc, "lin_load", [(w_qkv[:, :], I["qkv_aug"])])
        projected, copied, copied_v, vec, act_steps, norm_ready, root_ready, feats, turned, drained, consts = (
            st.sem(n) for n in ("projected", "copied", "copied_by_vector", "vector_steps", "scalar_steps", "norm_ready",
                                "root_ready", "features_ready", "turned", "drained", "consts"))
        ps = core.psum
        with nc.Block() as block:
            @block.gpsimd
            def _(pool):
                nc.gpsimd.memset(qkv[:, :, 3 * D:3 * D + 1], 1.0).then_inc(consts, 1)
                nc.gpsimd.memset(upper[:, :], 1.0).then_inc(consts, 1)
                pool.wait_ge(consts, 2)
                nc.gpsimd.affine_select(out=upper[:, :], in_=upper[:, :], compare_op=ALU.is_ge, fill=0.0,
                                        base=0, pattern=[[1, P]], channel_multiplier=-1)

            @block.tensor
            def _(pe):
                for t in range(T):
                    if t >= 8:
                        pe.wait_ge(copied_v if t % 2 else copied, (t - 8) // 2 + 1)
                    nc.tensor.matmul(ps[:, t % 8, 0:3 * D], core.xnT[:, t * P:(t + 1) * P], w_qkv[:, :],
                                     start=True, stop=True).then_inc(projected, 1)
                pe.wait_ge(feats, 1)
                for part in range(2):
                    for t in range(T):
                        g = part * GROUPS + t // 4
                        if t % 4 == 0 and g >= 8:
                            pe.wait_ge(drained, g - 7)
                        last = nc.tensor.transpose(ps[0:D, g % 8, t % 4 * P:(t % 4 + 1) * P],
                                                   qk[:, t, part * D:(part + 1) * D], core.ident[:, :])
                        if t % 4 == 3:
                            last.then_inc(turned, 1)

            @block.scalar
            def _(act):
                steps = Steps(act, act_steps)
                for t in range(0, T, 2):
                    act.wait_ge(projected, t + 1)
                    nc.scalar.activation(qkv[:, t, 0:3 * D], ps[:, t % 8, 0:3 * D], ACT.Copy).then_inc(copied, 1)
                act.wait_ge(norm_ready, 1)
                nc.scalar.activation(stat[:, 1, :], stat[:, 0, :], ACT.Sqrt).then_inc(root_ready, 1)
                act.wait_ge(norm_ready, 2)
                steps.do(nc.scalar.activation(qk[:, :, :], qk[:, :, :], ACT.Exp))
                nc.scalar.activation(qk[:, :, :], qk[:, :, :], ACT.Ln, bias=1.0).then_inc(root_ready, 1)
                for g in range(2 * GROUPS):
                    act.wait_ge(turned, g + 1)
                    to = (qT if g < GROUPS else kT)[:, g % GROUPS * BANK:(g % GROUPS + 1) * BANK]
                    nc.scalar.activation(to, ps[0:D, g % 8, :], ACT.Copy).then_inc(drained, 1)

            @block.vector
            def _(dve):
                steps = Steps(dve, vec)
                for t in range(1, T, 2):
                    dve.wait_ge(projected, t + 1)
                    nc.vector.tensor_copy(qkv[:, t, 0:3 * D], ps[:, t % 8, 0:3 * D]).then_inc(copied_v, 1)
                dve.wait_ge(copied, T // 2)
                dve.wait_ge(copied_v, T // 2)
                steps.do(nc.vector.tensor_tensor(sq[:, :, :], qk[:, :, :], qk[:, :, :], ALU.mult))
                nc.vector.tensor_reduce(stat[:, 0, :], sq[:, :, :].rearrange("p t (s d) -> p (t s) d", s=2),
                                        AX.X, ALU.add).then_inc(norm_ready, 1)
                dve.wait_ge(root_ready, 1)
                steps.do(nc.vector.tensor_scalar(stat[:, 1, :], stat[:, 1, :], 0.125, 1e-12, ALU.mult, ALU.max))
                steps.do(nc.vector.reciprocal(stat[:, 2, :], stat[:, 1, :]))
                steps.do(nc.vector.tensor_scalar(stat[:, 2, :], stat[:, 2, :], 0.125, None, ALU.mult))
                view = qk.rearrange("p t (s d) -> p t s d", s=2)
                scale = stat[:, 2, :].rearrange("p (t s) -> p t s", s=2)
                nc.vector.tensor_tensor(view, view, over(scale, D), ALU.mult).then_inc(norm_ready, 1)
                dve.wait_ge(root_ready, 2)
                nc.vector.tensor_scalar(qk[:, :, :], qk[:, :, :], 1e-6, None, ALU.add).then_inc(feats, 1)

        scored, scored_rest, kept, kept_rest, weighed, divided = (
            st.sem(n) for n in ("scored_diagonal", "scored_rest", "kept_diagonal", "kept_rest", "weighed", "divided"))
        with nc.Block() as block:
            @block.tensor
            def _(pe):
                n = rest = 0
                for b in range(B):
                    for c in range(CH):
                        keys = kT[:, b * PAD + c * P:b * PAD + (c + 1) * P]
                        if n >= 2:
                            pe.wait_ge(kept, n - 1)
                        nc.tensor.matmul(ps[:, n % 2, 0:P], keys, qT[:, b * PAD + c * P:b * PAD + (c + 1) * P],
                                         start=True, stop=True).then_inc(scored, 1)
                        n += 1
                        if c < CH - 1:
                            if rest >= 2:
                                pe.wait_ge(kept_rest, rest - 1)
                            nc.tensor.matmul(ps[:, 2 + rest % 2, 0:PAD - (c + 1) * P], keys,
                                             qT[:, b * PAD + (c + 1) * P:(b + 1) * PAD],
                                             start=True, stop=True).then_inc(scored_rest, 1)
                            rest += 1
                    pe.wait_ge(kept, n)
                    pe.wait_ge(kept_rest, rest)
                    if b >= 1:
                        pe.wait_ge(divided, 2 * b)
                    for c in range(CH):
                        for m in range(c + 1):
                            rows = TAIL if m == CH - 1 else P
                            last = nc.tensor.matmul(ps[:, 6, c * (D + 1):(c + 1) * (D + 1)],
                                                    scores[0:rows, b % 2, m, c * P:(c + 1) * P],
                                                    v1[0:rows, b * CH + m, :], start=(m == 0), stop=(m == c))
                    last.then_inc(weighed, 1)

            @block.scalar
            def _(act):
                for b in range(B):
                    if b >= 2:
                        act.wait_ge(weighed, b - 1)
                    for c in range(CH - 1):
                        rest = b * (CH - 1) + c
                        act.wait_ge(scored_rest, rest + 1)
                        nc.scalar.activation(scores[:, b % 2, c, (c + 1) * P:PAD],
                                             ps[:, 2 + rest % 2, 0:PAD - (c + 1) * P], ACT.Copy
                                             ).then_inc(kept_rest, 1)

            @block.vector
            def _(dve):
                for b in range(B):
                    for c in range(CH):
                        n = b * CH + c
                        dve.wait_ge(scored, n + 1)
                        if b >= 2:
                            dve.wait_ge(weighed, b - 1)
                        nc.vector.tensor_tensor(scores[:, b % 2, c, c * P:(c + 1) * P], ps[:, n % 2, 0:P],
                                                upper[:, :], ALU.mult).then_inc(kept, 1)
                    dve.wait_ge(weighed, b + 1)
                    out = ps[:, 6, 0:CH * (D + 1)].rearrange("p (c e) -> p c e", e=D + 1)
                    nc.vector.tensor_scalar(attn[:, b * CH:(b + 1) * CH, :], out[:, :, 0:D], 1e4, -1e4, ALU.min, ALU.max
                                            ).then_inc(divided, 1)
                    nc.vector.tensor_scalar(den[:, b * CH:(b + 1) * CH], out[:, :, D], 1e-6, None, ALU.max
                                            ).then_inc(divided, 1)
                dve.wait_ge(divided, 2 * B)
                nc.vector.reciprocal(den[:, :], den[:, :]).then_inc(divided, 1)
                dve.wait_ge(divided, 2 * B + 1)
                nc.vector.tensor_tensor(attn[:, :, :], attn[:, :, :], over(den[:, :], D), ALU.mult)

        aT = st.sb("aT", [D + 1, COLS])
        w_proj = st.sb("w_proj", [D + 1, D])
        set_stage(nc, "lin_one", [(aT[:, :], 1.0)])
        load_stage(nc, "proj_load", [(w_proj[:, :], I["proj_aug"])])
        turn_stage(nc, core, "lin_turn", [(aT, D, lambda t: attn[:, t, :])])
        product_stage(nc, core, "lin_proj", [(lambda t: aT[:, t * P:(t + 1) * P], w_proj[:, :])], D,
                      lambda t0, t1, made: nc.vector.tensor_tensor(core.xn[:, t0:t1, :], core.xn[:, t0:t1, :], made, ALU.add))
    norm_stage(nc, core, "lin_ln1", core.xn, gain=I["ln1_g"], shift=I["ln1_b"])
    with Stage(nc, "gelu") as st:
        w1 = st.sb("w1", [D + 1, 4 * D])
        w2 = st.sb("w2", [P, 2, D])
        b2 = st.sb("b2", [1, D])
        hT = st.sb("hT", [P, 2, COLS])
        load_stage(nc, "gelu_load", [(w1[:, :], I["w1_aug"]), (w2[:, :, :], I["w2"].rearrange("(k p) d -> p k d", p=P)), (b2[:, :], I["b2"].unsqueeze(0))])
        wide_product_stage(nc, core, "gelu_up", [(P, [(w1[:, k * P:(k + 1) * P], lambda c0, c1: core.xnT[:, c0:c1])])
                                                 for k in range(2)],
                           lambda c0, c1, k, made: nc.scalar.activation(hT[:, k, c0:c1], made, ACT.Gelu))
        product_stage(nc, core, "gelu_down",
                      [(lambda t: hT[:, 0, t * P:(t + 1) * P], w2[:, 0, :]),
                       (lambda t: hT[:, 1, t * P:(t + 1) * P], w2[:, 1, :]),
                       (lambda t: core.ones[0:1, :], b2[:, :])], D,
                      lambda t0, t1, made: nc.vector.tensor_tensor(core.xn[:, t0:t1, :], core.xn[:, t0:t1, :], made, ALU.add))
    norm_stage(nc, core, "lin_ln2", core.xn, gain=I["ln2_g"], shift=I["ln2_b"], turn=False)
    add_stage(nc, core, "lin_residual", (core.h[:, :, :], core.h[:, :, :], core.xn[:, :, :]))


def set_stage(nc, name, fills):
    with nc.Block() as block:
        @block.gpsimd
        def _(pool):
            for ap, value in fills:
                nc.gpsimd.memset(ap, value)


def causal_attention_stage(nc, core, name, sources, heads, d, scale, w_out, yT):
    with Stage(nc, name) as st:
        q1, k1, v1 = (st.sb(n, [P, CH, d]) for n in ("q1", "k1", "v1"))
        wo1 = st.sb("wo1", [d, D])
        qT, kT = st.sb("qT", [d, PAD]), st.sb("kT", [d, PAD])
        mask = st.sb("mask", [P, 2 * PAD - P])
        probs = st.sb("probs", [P, 2, PAD])
        pT = st.sb("pT", [P, 2, CH, P])
        oT = st.sb("oT", [d, PAD])
        stat = st.sb("stat", [P, 2, 4])
        passed, passed_v = st.sem("passed"), st.sem("passed_by_vector")
        (masked, fetched, turned, turned_copied, scored, peaked, exped, normed, p_turned, p_copied, weighed, o_copied,
         projected, summed, vec, mask_set) = (st.sem(n) for n in (
            "masked", "fetched", "turned", "turned_copied", "scored", "peaked", "exped", "normed", "p_turned",
            "p_copied", "weighed", "o_copied", "projected", "summed", "vector_steps", "mask_set"))
        start_loop(nc, [fetched, turned, turned_copied, scored, peaked, exped, normed, p_turned, p_copied,
                        weighed, o_copied, projected, summed, masked])
        ps = core.psum
        width = [P * (c + 1) if c < CH - 1 else SEQ for c in range(CH)]
        rows = [P] * (CH - 1) + [TAIL]
        flat = ps[:, :, :].rearrange("p b n -> p (b n)")
        with nc.Block() as block:
            @block.gpsimd
            def _(pool):
                nc.gpsimd.memset(mask[:, :], 0.0).then_inc(mask_set, 1)
                nc.gpsimd.memset(yT[:, :], 0.0).then_inc(mask_set, 1)
                pool.wait_ge(mask_set, 1)
                nc.gpsimd.affine_select(out=mask[:, :], in_=mask[:, :], compare_op=ALU.is_ge, fill=NEG,
                                        base=PAD - P, pattern=[[-1, 2 * PAD - P]], channel_multiplier=1
                                        ).then_inc(mask_set, 1)
        with nc.Block() as block:
            @block.gpsimd
            def _(pool):
                with pool.Fori(0, B) as b:
                    with pool.Fori(0, heads) as h:
                        n = b * heads + h
                        pool.wait_ge(summed, START + n)
                        for to, (of, stride, start) in zip((q1, k1, v1), sources):
                            nc.gpsimd.tensor_copy(to[:, :, :], of[:, bass.ds(b * CH, CH), bass.ds(h * stride + start, d)]
                                                  ).then_inc(fetched, 1)
                        nc.gpsimd.tensor_copy(wo1[:, :], w_out[:, bass.ds(h * D, D)]).then_inc(fetched, 1)

            @block.tensor
            def _(pe):
                with pe.Fori(0, B) as b:
                    with pe.Fori(0, heads) as h:
                        n = b * heads + h
                        pe.wait_ge(fetched, START + 4 * n + 4)
                        wait_apart(pe, passed)
                        for bank, src in ((0, q1), (2, k1)):
                            for c in range(CH):
                                last = nc.tensor.transpose(flat[0:d, bank * BANK + c * P:bank * BANK + (c + 1) * P],
                                                           src[:, c, :], core.ident[:, :])
                            last.then_inc(turned, 1)

                        def score(c):
                            if c >= 2:
                                pe.wait_ge(peaked, START + CH * n + c - 1)
                                wait_apart(pe, passed)
                            at = 4 if c % 2 == 0 else 6
                            last = nc.tensor.matmul(ps[:, at, 0:min(width[c], BANK)], qT[:, c * P:(c + 1) * P],
                                                    kT[:, 0:min(width[c], BANK)], start=True, stop=True)
                            if width[c] > BANK:
                                last = nc.tensor.matmul(ps[:, at + 1, 0:width[c] - BANK], qT[:, c * P:(c + 1) * P],
                                                        kT[:, BANK:width[c]], start=True, stop=True)
                            last.then_inc(scored, 1)

                        pe.wait_ge(turned_copied, START + 2 * n + 2)
                        wait_apart(pe, passed)
                        score(0)
                        for c in range(CH):
                            if c + 1 < CH:
                                score(c + 1)
                            pe.wait_ge(normed, START + CH * n + c + 1)
                            if c >= 1:
                                pe.wait_ge(p_copied, START + CH * n + c)
                            wait_apart(pe, passed)
                            for m in range(c + 1):
                                last = nc.tensor.transpose(flat[0:rows[m], m * P:(m + 1) * P],
                                                           probs[:, c % 2, m * P:m * P + rows[m]], core.ident[:, :])
                            last.then_inc(p_turned, 1)
                            pe.wait_ge(p_copied, START + CH * n + c + 1)
                            wait_apart(pe, passed)
                            out = ps[0:d, 7, c * P:(c + 1) * P] if c < CH - 1 else ps[0:d, 3, 0:P]
                            for m in range(c + 1):
                                last = nc.tensor.matmul(out, v1[0:rows[m], m, :], pT[0:rows[m], c % 2, m, :],
                                                        start=(m == 0), stop=(m == c))
                            last.then_inc(weighed, 1)
                        pe.wait_ge(o_copied, START + 2 * n + 2)
                        wait_apart(pe, passed)
                        for lo, hi, bank in ((0, BANK, 0), (BANK, PAD, 1)):
                            last = nc.tensor.matmul(ps[0:D, bank, 0:hi - lo], wo1[:, :], oT[:, lo:hi],
                                                    start=True, stop=True)
                        last.then_inc(projected, 1)

            @block.scalar
            def _(act):
                with act.Fori(0, B) as b:
                    with act.Fori(0, heads) as h:
                        n = b * heads + h
                        for part, (to, bank) in enumerate(((qT, 0), (kT, 2))):
                            act.wait_ge(turned, START + 2 * n + part + 1)
                            nc.scalar.activation(to[:, :], flat[0:d, bank * BANK:bank * BANK + PAD], ACT.Copy
                                                 ).then_inc(turned_copied, 1)
                        for c in range(CH):
                            act.wait_ge(peaked, START + CH * n + c + 1)
                            nc.scalar.activation(probs[:, c % 2, 0:width[c]], probs[:, c % 2, 0:width[c]], ACT.Exp,
                                                 bias=stat[:, c % 2, 1:2], scale=scale, accum_out=stat[:, c % 2, 2:3]
                                                 ).then_inc(exped, 1)
                            act.wait_ge(p_turned, START + CH * n + c + 1)
                            full = c if c == CH - 1 else c + 1
                            last = nc.scalar.activation(
                                pT[:, c % 2, 0:full, :],
                                flat[:, 0:full * P].rearrange("p (m q) -> p m q", q=P), ACT.Copy)
                            if full < c + 1:
                                last.then_inc(masked, 1)
                                last = nc.scalar.activation(pT[0:TAIL, c % 2, c, :], flat[0:TAIL, c * P:(c + 1) * P], ACT.Copy)
                                act.wait_ge(masked, START + n + 1)
                            last.then_inc(p_copied, 1)
                        act.wait_ge(weighed, START + CH * n + CH)
                        nc.scalar.activation(oT[:, 0:BANK], ps[0:d, 7, :], ACT.Copy).then_inc(o_copied, 1)
                        nc.scalar.activation(oT[:, BANK:PAD], ps[0:d, 3, 0:P], ACT.Copy).then_inc(o_copied, 1)

            @block.vector
            def _(dve):
                steps = Steps(dve, vec)
                dve.wait_ge(mask_set, 3)
                with dve.Fori(0, B) as b:
                    with dve.Fori(0, heads) as h:
                        n = b * heads + h
                        steps.enter_loop(n, 2 * CH)
                        for c in range(CH):
                            dve.wait_ge(scored, START + CH * n + c + 1)
                            if c >= 2:
                                dve.wait_ge(p_turned, START + CH * n + c - 1)
                            at = (4 if c % 2 == 0 else 6) * BANK
                            w = width[c]
                            wait_apart(dve, passed_v)
                            steps.do(nc.vector.tensor_tensor_reduce(
                                probs[:, c % 2, 0:w], flat[:, at:at + w], mask[:, PAD - P - c * P:PAD - P - c * P + w],
                                1.0, -3e38, ALU.add, ALU.max, stat[:, c % 2, 0:1]))
                            nc.vector.tensor_scalar(stat[:, c % 2, 1:2], stat[:, c % 2, 0:1], -scale, None, ALU.mult
                                                    ).then_inc(peaked, 1)
                            dve.wait_ge(exped, START + CH * n + c + 1)
                            steps.do(nc.vector.reciprocal(stat[:, c % 2, 3:4], stat[:, c % 2, 2:3]))
                            nc.vector.tensor_scalar(probs[:, c % 2, 0:w], probs[:, c % 2, 0:w],
                                                    stat[:, c % 2, 3:4], None, ALU.mult).then_inc(normed, 1)
                        dve.wait_ge(projected, START + n + 1)
                        nc.vector.tensor_tensor(yT[:, bass.ds(b * PAD, PAD)], flat[0:D, 0:PAD],
                                                yT[:, bass.ds(b * PAD, PAD)], ALU.add).then_inc(summed, 1)


def add_turned_stage(nc, core, name, yT, out):
    with Stage(nc, name) as st:
        turned, added = st.sem("turned"), st.sem("added")
        with nc.Block() as block:
            @block.tensor
            def _(pe):
                for t in range(T):
                    last = nc.tensor.transpose(core.psum[:, t // 8, t % 8 * D:(t % 8 + 1) * D],
                                               yT[:, t * P:(t + 1) * P], core.ident[0:D, 0:D])
                    if t % 8 == 7 or t == T - 1:
                        last.then_inc(turned, 1)

            @block.vector
            def _(dve):
                for g, t0 in enumerate(range(0, T, 8)):
                    t1 = min(t0 + 8, T)
                    dve.wait_ge(turned, g + 1)
                    nc.vector.tensor_tensor(out[:, t0:t1, :], out[:, t0:t1, :],
                                            core.psum[:, g, 0:(t1 - t0) * D].rearrange("p (t d) -> p t d", d=D),
                                            ALU.add).then_inc(added, 1)


KEYS = 64
HEADS = 8
TOP = 16
SLOTS = 4
LOWEST = -3e38


def retrieval_stage(nc, core, I):
    with Stage(nc, "peer") as st:
        KV = st.sb("KV", [P, T, HEADS * 2 * D])
        Q = st.sb("Q", [P, T, HEADS * D])
        with Stage(nc, "pk") as at:
            w_pk = at.sb("w_pk", [D, 2 * HEADS * D // 2])
            keys = at.sb("keys", [P, 4, 4 * KEYS])
            w_q = at.sb("w_q", [D, HEADS * D])
            load_stage(nc, "pk_load", [(w_pk[:, :], I["w_pk"]), (keys[:, :, :], I["pk_blocks"]), (w_q[:, :], I["w_q"])])
            xt = at.sb("xt", [D, P])
            pkT = at.sb("pkT", [P, 4, P])
            sim = at.sb("sim", [P, 2 * HEADS, KEYS])
            vals = at.sb("vals", [P, 2 * HEADS, TOP])
            ids = at.sb("ids", [P, 2 * HEADS, TOP], U32)
            idf = at.sb("idf", [P, 2 * HEADS, TOP])
            cand = at.sb("cand", [P, HEADS, TOP * TOP])
            fvals = at.sb("fvals", [P, HEADS, TOP])
            fids = at.sb("fids", [P, HEADS * TOP], U32)
            half = at.sb("half", [P, HEADS * TOP], U32)
            halff = at.sb("halff", [P, HEADS * TOP])
            found = at.sb("found", [P, 2, HEADS * TOP])
            index = at.sb("index", [P, 2, HEADS * TOP], U32)
            weight = at.sb("weight", [P, 2, HEADS, TOP])
            sums = at.sb("sums", [P, 2, HEADS])
            count16 = at.sb("count16", [P, TOP])
            base = at.sb("base", [P, HEADS, TOP])
            rows = at.sb("rows", [P, SLOTS, TOP, 2 * D])
            (consts, fetched, pk_made, pk_copied, sims_made, sims_copied, q_made, q_copied, sim_used, shifted, exped,
             index_ready, weighed, vec) = (at.sem(n) for n in (
                "consts", "fetched", "pk_made", "pk_copied", "sims_made", "sims_copied", "q_made", "q_copied",
                "sim_used", "shifted", "exped", "index_ready", "weighed", "vector_steps"))
            passed, passed_pool = at.sem("passed"), at.sem("passed_by_pool")
            gathered = [at.sem(f"gathered{s}") for s in range(SLOTS)]
            start_loop(nc, [fetched, pk_made, pk_copied, sims_made, sims_copied, q_made, q_copied, sim_used, shifted,
                            exped, index_ready])
            ps = core.psum
            PAIRS = T // 2 - 1

            def walk(engine, tile_step, steps=None, per_turn=0):
                with engine.Fori(0, PAIRS) as j:
                    if steps:
                        steps.enter_loop(j, per_turn)
                    for u in range(2):
                        tile_step(2 * j + u, u, True)
                if steps:
                    steps.leave_loop(PAIRS)
                for t in (T - 2, T - 1):
                    tile_step(t, t % 2, t < T - 1)

            with nc.Block() as block:
                @block.gpsimd
                def _(pool):
                    nc.gpsimd.iota(count16[:, :], [[1, TOP]], base=0, channel_multiplier=0,
                                   allow_small_or_imprecise_dtypes=True).then_inc(consts, 1)
                    nc.gpsimd.iota(base[:, :, :], [[KEYS * KEYS // 2, HEADS], [0, TOP]], base=0, channel_multiplier=0,
                                   allow_small_or_imprecise_dtypes=True).then_inc(consts, 1)

                    def gather(t, u, _):
                        pool.wait_ge(index_ready, START + t + 1)
                        for h in range(HEADS):
                            pool.wait_ge(weighed, HEADS * t + h + 1)
                            wait_apart(pool, passed_pool)
                            for k in range(TOP):
                                pool.indirect_dma_start(
                                    out=rows[:, h % SLOTS, k, :], out_offset=None, in_=I["table"],
                                    in_offset=bass.IndirectOffsetOnAxis(
                                        ap=index[:, u, h * TOP + k:h * TOP + k + 1], axis=0)
                                ).then_inc(gathered[h % SLOTS], 16)

                    walk(pool, gather)

                @block.tensor
                def _(pe):
                    def project(t):
                        pe.wait_ge(fetched, START + t + 1)
                        pe.wait_ge(pk_copied, START + t)
                        for c in range(4):
                            last = nc.tensor.matmul(ps[:, 0, c * P:(c + 1) * P], w_pk[:, c * P:(c + 1) * P], xt[:, :],
                                                    start=True, stop=True)
                        last.then_inc(pk_made, 1)
                        pe.wait_ge(q_copied, START + t)
                        nc.tensor.matmul(ps[:, 3, :], xt[:, :], w_q[:, :], start=True, stop=True).then_inc(q_made, 1)
                        pe.wait_ge(pk_copied, START + t + 1)
                        pe.wait_ge(sims_copied, START + t)
                        for c in range(4):
                            last = nc.tensor.matmul(ps[:, 1 + c // 2, c % 2 * 256:(c % 2 + 1) * 256], pkT[:, c, :],
                                                    keys[:, c, :], start=True, stop=True)
                        last.then_inc(sims_made, 1)

                    with pe.Fori(0, T) as t:
                        project(t)

                @block.scalar
                def _(act):
                    def prepare(t):
                        act.wait_ge(q_made, START + t)
                        nc.scalar.activation(xt[:, :], core.xnT[0:D, bass.ds(t * P, P)], ACT.Copy).then_inc(fetched, 1)
                        act.wait_ge(pk_made, START + t + 1)
                        act.wait_ge(sims_made, START + t)
                        nc.scalar.activation(pkT[:, :, :], ps[:, 0, :].rearrange("p (c n) -> p c n", n=P), ACT.Copy
                                             ).then_inc(pk_copied, 1)
                        act.wait_ge(q_made, START + t + 1)
                        nc.scalar.activation(Q[:, bass.ds(t, 1), :], ps[:, 3, :].unsqueeze(1), ACT.Copy, scale=0.125
                                             ).then_inc(q_copied, 1)
                        act.wait_ge(sims_made, START + t + 1)
                        act.wait_ge(sim_used, START + t)
                        nc.scalar.activation(sim[:, :, :], ps[:, 1:3, :].rearrange("p b (q n) -> p (b q) n", n=KEYS),
                                             ACT.Copy).then_inc(sims_copied, 1)
                        act.wait_ge(shifted, START + t + 1)
                        nc.scalar.activation(fvals[:, :, :], fvals[:, :, :], ACT.Exp).then_inc(exped, 1)

                    with act.Fori(0, T) as t:
                        prepare(t)

                @block.vector
                def _(dve):
                    steps = Steps(dve, vec)

                    def select(t, u):
                        dve.wait_ge(sims_copied, START + t + 1)
                        wait_apart(dve, passed)
                        for lo in (0, 8):
                            for q in range(2 * HEADS):
                                steps.add(nc.vector.max(vals[:, q, lo:lo + 8], sim[:, q, :]))
                            steps.settle(passed)
                            for q in range(2 * HEADS):
                                steps.add(nc.vector.max_index(ids[:, q, lo:lo + 8], vals[:, q, lo:lo + 8], sim[:, q, :]))
                            steps.settle(passed)
                            if lo == 0:
                                for q in range(2 * HEADS):
                                    steps.add(nc.vector.match_replace(sim[:, q, :], vals[:, q, 0:8], sim[:, q, :], LOWEST))
                                steps.settle(passed)
                        nc.vector.tensor_copy(idf[:, :, :], ids[:, :, :]).then_inc(sim_used, 1)
                        dve.wait_ge(sim_used, START + t + 1)
                        steps.add(nc.vector.tensor_scalar(idf[:, HEADS:, :], idf[:, HEADS:, :], float(KEYS), None, ALU.mult))
                        steps.add(nc.vector.scalar_tensor_tensor(idf[:, 0:HEADS, :], base[:, :, :], 2.0, idf[:, 0:HEADS, :],
                                                                 ALU.mult, ALU.add))
                        steps.do(nc.vector.tensor_tensor(
                            cand[:, :, :].rearrange("p h (a b) -> p h a b", a=TOP),
                            vals[:, 0:HEADS, :].unsqueeze(3).to_broadcast([P, HEADS, TOP, TOP]),
                            vals[:, HEADS:, :].unsqueeze(2).to_broadcast([P, HEADS, TOP, TOP]), ALU.add))
                        wait_apart(dve, passed)
                        for lo in (0, 8):
                            for h in range(HEADS):
                                steps.add(nc.vector.max(fvals[:, h, lo:lo + 8], cand[:, h, :]))
                            steps.settle(passed)
                            for h in range(HEADS):
                                steps.add(nc.vector.max_index(fids[:, h * TOP + lo:h * TOP + lo + 8],
                                                              fvals[:, h, lo:lo + 8], cand[:, h, :]))
                            steps.settle(passed)
                            if lo == 0:
                                for h in range(HEADS):
                                    steps.add(nc.vector.match_replace(cand[:, h, :], fvals[:, h, 0:8], cand[:, h, :], LOWEST))
                                steps.settle(passed)
                        onehot = cand[:, :, :].rearrange("p h (k a) -> p h k a", a=TOP)
                        for part, (op, by) in enumerate(((ALU.logical_shift_right, 4), (ALU.bitwise_and, 15))):
                            steps.do(nc.vector.tensor_scalar(half[:, :], fids[:, :], by, None, op))
                            steps.do(nc.vector.tensor_copy(halff[:, :], half[:, :]))
                            steps.do(nc.vector.tensor_tensor(cand[:, :, :].rearrange("p h (k a) -> p (h k) a", a=TOP),
                                                             over(halff[:, :], TOP), rows_of(count16[:, :], HEADS * TOP),
                                                             ALU.is_equal))
                            steps.do(nc.vector.tensor_tensor(
                                onehot, onehot,
                                idf[:, part * HEADS:(part + 1) * HEADS, :].unsqueeze(2).to_broadcast([P, HEADS, TOP, TOP]),
                                ALU.mult))
                            steps.do(nc.vector.tensor_reduce(found[:, part, :],
                                                             cand[:, :, :].rearrange("p h (k a) -> p (h k) a", a=TOP),
                                                             AX.X, ALU.add))
                        steps.add(nc.vector.tensor_copy(sums[:, 0, :], fvals[:, :, 0]))
                        nc.vector.tensor_tensor(index[:, u, :], found[:, 0, :], found[:, 1, :], ALU.add
                                                ).then_inc(index_ready, 1)
                        steps.settle()
                        nc.vector.tensor_tensor(fvals[:, :, :], fvals[:, :, :], over(sums[:, 0, :], TOP), ALU.subtract
                                                ).then_inc(shifted, 1)
                        dve.wait_ge(exped, START + t + 1)
                        steps.do(nc.vector.tensor_reduce(sums[:, 1, :], fvals[:, :, :], AX.X, ALU.add))
                        steps.do(nc.vector.reciprocal(sums[:, 0, :], sums[:, 1, :]))
                        steps.do(nc.vector.tensor_tensor(weight[:, u, :, :], fvals[:, :, :], over(sums[:, 0, :], TOP), ALU.mult))

                    def weigh(t, u):
                        for h in range(HEADS):
                            slot = h % SLOTS
                            uses = HEADS // SLOTS
                            dve.wait_ge(gathered[slot], 16 * TOP * (uses * t + h // SLOTS + 1))
                            steps.do(nc.vector.tensor_tensor(rows[:, slot, :, :], rows[:, slot, :, :],
                                                             over(weight[:, u, h, :], 2 * D), ALU.mult))
                            nc.vector.tensor_reduce(KV[:, bass.ds(t, 1), h * 2 * D:(h + 1) * 2 * D],
                                                    rows[:, slot, :, :].rearrange("p k d -> p d k"), AX.X, ALU.add
                                                    ).then_inc(weighed, 1)

                    def both(t, u, more):
                        if more:
                            select(t + 1, 1 - u)
                        weigh(t, u)

                    dve.sem_inc(weighed, SLOTS)
                    dve.wait_ge(consts, 2)
                    select(0, 0)
                    per_select = steps.count
                    walk(dve, both, steps, 2 * (per_select + HEADS))
        with Stage(nc, "peer_out") as at:
            w_o = at.sb("w_o", [D, HEADS * D])
            yT = at.sb("yT", [D, COLS])
            load_stage(nc, "peer_out_load", [(w_o[:, :].rearrange("p (h n) -> p h n", n=D),
                                              I["w_o"].rearrange("(h p) n -> p h n", p=D))])
            causal_attention_stage(nc, core, "peer_attn", [(Q, D, 0), (KV, 2 * D, 0), (KV, 2 * D, D)], HEADS, D, 1.0, w_o, yT)
            add_turned_stage(nc, core, "peer_add", yT, core.h)


CHANNELS = 3 * D
RPE = 8
RPE_LAYERS = 3
SPAN = 2 * SEQ
LAGS = SPAN // P
FREQ = SEQ + 1
FCH = (FREQ + P - 1) // P
FREQ_ROWS = [min(P, FREQ - P * k) for k in range(FCH)]
TOKEN_ROWS = [min(P, SEQ - P * c) for c in range(CH)]


def root_stage(nc, core, name, x, sq, stat, scale, eps, ones=None):
    with Stage(nc, name) as st:
        vec, squared, rooted = st.sem("vector_steps"), st.sem("squared"), st.sem("rooted")
        with nc.Block() as block:
            @block.vector
            def _(dve):
                steps = Steps(dve, vec)
                steps.do(nc.vector.tensor_tensor(sq, x, x, ALU.mult))
                nc.vector.tensor_reduce(stat[:, 0, :], sq, AX.X, ALU.add).then_inc(squared, 1)
                dve.wait_ge(rooted, 1)
                steps.do(nc.vector.tensor_scalar(stat[:, 0, :], stat[:, 0, :], scale, eps, ALU.mult, ALU.add))
                steps.do(nc.vector.reciprocal(stat[:, 1, :], stat[:, 0, :]))
                steps.do(nc.vector.tensor_tensor(x, x, over(stat[:, 1, :], D), ALU.mult))

            @block.scalar
            def _(act):
                act.wait_ge(squared, 1)
                nc.scalar.activation(stat[:, 0, :], stat[:, 0, :], ACT.Sqrt).then_inc(rooted, 1)


def lag_network_stage(nc, core, I, a):
    with Stage(nc, "rpe") as st:
        lags = st.sb("lags", [2, SPAN])
        w_pos = st.sb("w_pos", [2, RPE])
        w_mid = st.sb("w_mid", [RPE + 1, RPE_LAYERS, RPE])
        w_out = st.sb("w_out", [RPE + 1, CHANNELS])
        ones8 = st.sb("ones8", [RPE, RPE])
        x, sq, root = (st.sb(n, [RPE, 3, SPAN // 3]) for n in ("x", "sq", "root"))
        act_in = st.sb("act_in", [RPE + 1, SPAN])
        load_stage(nc, "rpe_load", [(lags[:, :], I["lags"]), (w_pos[:, :], I["pos_aug"]),
                                    (w_mid[:, :, :], I["rpe_aug"]), (w_out[:, :], I["out_aug"])])
        set_stage(nc, "rpe_ones", [(ones8[:, :], 1.0), (act_in[:, :], 1.0)])
        made, squared, summed, rooted, ready, vec, copied = (
            st.sem(n) for n in ("made", "squared", "summed", "rooted", "ready", "vector_steps", "copied"))
        ps, third = core.psum, SPAN // 3
        rounds = RPE_LAYERS + 1
        with nc.Block() as block:
            @block.tensor
            def _(pe):
                for r in range(rounds):
                    if r:
                        pe.wait_ge(ready, r)
                    for k in range(3):
                        weights = w_pos[:, :] if r == 0 else w_mid[:, r - 1, :]
                        moving = lags if r == 0 else act_in
                        last = nc.tensor.matmul(ps[0:RPE, k, 0:third], weights, moving[:, k * third:(k + 1) * third],
                                                start=True, stop=True)
                    last.then_inc(made, 1)
                    pe.wait_ge(squared, r + 1)
                    for k in range(3):
                        last = nc.tensor.matmul(ps[0:RPE, 3 + k, 0:third], ones8[:, :], sq[:, k, :],
                                                start=True, stop=True)
                    last.then_inc(summed, 1)
                pe.wait_ge(ready, rounds)
                for t in range(LAGS):
                    if t == 6:
                        pe.wait_ge(copied, 1)
                    nc.tensor.matmul(ps[:, t % 6, 0:CHANNELS], act_in[:, t * P:(t + 1) * P], w_out[:, :],
                                     start=True, stop=True).then_inc(made, 1)

            @block.vector
            def _(dve):
                steps = Steps(dve, vec)
                for r in range(rounds):
                    dve.wait_ge(made, r + 1)
                    steps.do(nc.vector.tensor_copy(x[:, :, :], ps[0:RPE, 0:3, 0:third]))
                    nc.vector.tensor_tensor(sq[:, :, :], x[:, :, :], x[:, :, :], ALU.mult).then_inc(squared, 1)
                    dve.wait_ge(rooted, r + 1)
                    steps.do(nc.vector.tensor_scalar(root[:, :, :], root[:, :, :], RPE ** -0.5, 1e-8, ALU.mult, ALU.add))
                    steps.do(nc.vector.reciprocal(root[:, :, :], root[:, :, :]))
                    steps.do(nc.vector.tensor_tensor(x[:, :, :], x[:, :, :], root[:, :, :], ALU.mult))
                    nc.vector.tensor_scalar(act_in[0:RPE, :].rearrange("p (k n) -> p k n", k=3), x[:, :, :],
                                            0.0, None, ALU.max).then_inc(ready, 1)
                for lo, hi in ((0, 6), (6, LAGS)):
                    dve.wait_ge(made, rounds + hi)
                    nc.vector.tensor_copy(a[:, lo:hi, :], ps[:, 0:hi - lo, 0:CHANNELS]).then_inc(copied, 1)

            @block.scalar
            def _(act):
                for r in range(rounds):
                    act.wait_ge(summed, r + 1)
                    nc.scalar.activation(root[:, :, :], ps[0:RPE, 3:6, 0:third], ACT.Sqrt).then_inc(rooted, 1)


def toeplitz_stage(nc, core, I):
    with Stage(nc, "tnn") as st:
        w_uv = st.sb("w_uv", [D + 1, 2 * CHANNELS])
        uv = st.sb("uv", [P, T, 2 * CHANNELS])
        load_stage(nc, "tnn_load", [(w_uv[:, :], I["uv_aug"])])
        product_stage(nc, core, "tnn_uv", [(lambda t: core.xnT[:, t * P:(t + 1) * P], w_uv[:, :])], 2 * CHANNELS,
                      lambda t0, t1, made: nc.scalar.activation(uv[:, t0:t1, :], made, ACT.Silu), engine="scalar")
        uv_b = uv[:, :, :].rearrange("p (b c) w -> p b c w", c=CH)
        with Stage(nc, "dft") as at:
            a = at.sb("a", [P, LAGS, CHANNELS])
            cos, sin = at.sb("cos", [P, LAGS, FREQ]), at.sb("sin", [P, LAGS, FREQ])
            icos, isin = at.sb("icos", [P, FCH, SEQ]), at.sb("isin", [P, FCH, SEQ])
            af = at.sb("af", [P, 2, CHANNELS])
            vf = at.sb("vf", [P, 2, B, CHANNELS])
            t1, t2, t3, t4 = (at.sb(f"t{k}", [P, B, CHANNELS]) for k in range(4))
            y = at.sb("y", [P, FCH, 2, B, CHANNELS])
            loads = [(to[:, :, :], I[n].rearrange("(k p) f -> p k f", p=P)) for to, n in ((cos, "cos"), (sin, "sin"))]
            for to, n in ((icos, "icos"), (isin, "isin")):
                loads += [(to[:, 0:FCH - 1, :], I[n][0:(FCH - 1) * P, :].rearrange("(k p) f -> p k f", p=P)),
                          (to[0:FREQ_ROWS[-1], FCH - 1, :], I[n][(FCH - 1) * P:FREQ, :])]
            load_stage(nc, "dft_load", loads)
            lag_network_stage(nc, core, I, a)
            made, copied, multiplied, vec, gps, crossed = (
                at.sem(n) for n in ("made", "copied", "multiplied", "vector_steps", "pool_steps", "crossed"))
            ps = core.psum
            with nc.Block() as block:
                @block.tensor
                def _(pe):
                    for f in range(FCH):
                        m = FREQ_ROWS[f]
                        if f:
                            pe.wait_ge(copied, f)
                        for part, table in enumerate((cos, sin)):
                            for k in range(LAGS):
                                nc.tensor.matmul(ps[0:m, part, 0:CHANNELS], table[:, k, f * P:f * P + m], a[:, k, :],
                                                 start=(k == 0), stop=(k == LAGS - 1))
                            for pair in range(2):
                                for c in range(CH):
                                    r = TOKEN_ROWS[c]
                                    last = nc.tensor.matmul(
                                        ps[0:m, 2 + 2 * part + pair, 0:2 * CHANNELS].rearrange("p (b w) -> p b w", b=2),
                                        table[0:r, c, f * P:f * P + m],
                                        uv_b[0:r, 2 * pair:2 * pair + 2, c, CHANNELS:2 * CHANNELS],
                                        start=(c == 0), stop=(c == CH - 1))
                        last.then_inc(made, 1)

                @block.scalar
                def _(act):
                    for f in range(FCH):
                        m = FREQ_ROWS[f]
                        act.wait_ge(made, f + 1)
                        if f:
                            act.wait_ge(multiplied, f)
                            act.wait_ge(crossed, f)
                        nc.scalar.activation(af[0:m, :, :], ps[0:m, 0:2, 0:CHANNELS], ACT.Copy)
                        nc.scalar.activation(
                            vf[0:m, :, :, :].rearrange("p s (q b) w -> p (s q) (b w)", b=2),
                            ps[0:m, 2:6, 0:2 * CHANNELS], ACT.Copy).then_inc(copied, 1)

                def cross(eng, engine, steps, f, out, parts, temps, op, done):
                    m = FREQ_ROWS[f]
                    for k in range(2):
                        steps.add(engine.tensor_tensor(temps[k][0:m, :, :], vf[0:m, parts[2 * k], :, :],
                                                       rows_of(af[0:m, parts[2 * k + 1], :], B), ALU.mult))
                    steps.settle()
                    engine.tensor_tensor(out[0:m, :, :], temps[0][0:m, :, :], temps[1][0:m, :, :], op).then_inc(done, 1)

                @block.vector
                def _(dve):
                    steps = Steps(dve, vec)
                    for f in range(FCH):
                        dve.wait_ge(copied, f + 1)
                        if f:
                            dve.wait_ge(multiplied, f)
                        cross(dve, nc.vector, steps, f, y[:, f, 0, :, :], (0, 0, 1, 1), (t1, t2), ALU.subtract, multiplied)

                @block.gpsimd
                def _(pool):
                    steps = Steps(pool, gps)
                    for f in range(FCH):
                        pool.wait_ge(copied, f + 1)
                        if f:
                            pool.wait_ge(crossed, f)
                        cross(pool, nc.gpsimd, steps, f, y[:, f, 1, :, :], (1, 0, 0, 1), (t3, t4), ALU.add, crossed)

            jobs = [(c, pair) for c in range(CH) for pair in range(2)]
            inverted, gated = at.sem("inverted"), at.sem("gated")
            with nc.Block() as block:
                @block.tensor
                def _(pe):
                    for n, (c, pair) in enumerate(jobs):
                        if n >= 8:
                            pe.wait_ge(gated, n - 7)
                        m = TOKEN_ROWS[c]
                        for k in range(2 * FCH):
                            f, part = k // 2, k % 2
                            r = FREQ_ROWS[f]
                            last = nc.tensor.matmul(
                                ps[0:m, n % 8, 0:2 * CHANNELS].rearrange("p (b w) -> p b w", b=2),
                                (icos, isin)[part][0:r, f, c * P:c * P + m], y[0:r, f, part, 2 * pair:2 * pair + 2, :],
                                start=(k == 0), stop=(k == 2 * FCH - 1))
                        last.then_inc(inverted, 1)

                @block.vector
                def _(dve):
                    for n, (c, pair) in enumerate(jobs):
                        m = TOKEN_ROWS[c]
                        dve.wait_ge(inverted, n + 1)
                        u = uv_b[0:m, 2 * pair:2 * pair + 2, c, 0:CHANNELS]
                        nc.vector.tensor_tensor(u, u, ps[0:m, n % 8, 0:2 * CHANNELS].rearrange("p (b w) -> p b w", b=2),
                                                ALU.mult).then_inc(gated, 1)
        with Stage(nc, "tnn_out") as at:
            g0, g1 = at.sb("g0", [P, COLS]), at.sb("g1", [D + 1, COLS])
            w_o0, w_o1, w_t = at.sb("w_o0", [P, D]), at.sb("w_o1", [D + 1, D]), at.sb("w_t", [D + 1, D])
            r = at.sb("r", [P, T, D])
            sq, stat = at.sb("sq", [P, T, D]), at.sb("stat", [P, 2, T])
            set_stage(nc, "g1_ones", [(g1[:, :], 1.0)])
            load_stage(nc, "tnn_out_load", [(w_o0[:, :], I["o_aug"][0:P, :]), (w_o1[:, :], I["o_aug"][P:CHANNELS + 1, :]),
                                            (w_t[:, :], I["t_aug"])])
            turn_stage(nc, core, "tnn_turn", [(g0, P, lambda t: uv[:, t, 0:P]), (g1, D, lambda t: uv[:, t, P:CHANNELS])])
            product_stage(nc, core, "tnn_o", [(lambda t: g0[:, t * P:(t + 1) * P], w_o0[:, :]),
                                              (lambda t: g1[:, t * P:(t + 1) * P], w_o1[:, :])], D,
                          lambda t0, t1, made: nc.vector.tensor_tensor(r[:, t0:t1, :], core.xn[:, t0:t1, :], made, ALU.subtract))
            turn_stage(nc, core, "tnn_turn_r", [(core.xnT, D, lambda t: r[:, t, :])])
            product_stage(nc, core, "tnn_t", [(lambda t: core.xnT[:, t * P:(t + 1) * P], w_t[:, :])], D,
                          lambda t0, t1, made: nc.vector.tensor_copy(r[:, t0:t1, :], made))
            root_stage(nc, core, "tnn_root", r[:, :, :], sq[:, :, :], stat, CHANNELS ** -0.5, 1e-8)
            silu_stage(nc, core, "tnn_silu", r[:, :, :])
            add_stage(nc, core, "tnn_add", (core.h[:, :, :], core.h[:, :, :], core.xn[:, :, :]),
                      (core.h[:, :, :], core.h[:, :, :], r[:, :, :]))


def silu_stage(nc, core, name, x):
    with nc.Block() as block:
        @block.scalar
        def _(act):
            nc.scalar.activation(x, x, ACT.Silu)


def top_two_stage(nc, core, name, scores, weight, experts, renorm):
    E = experts
    with Stage(nc, name) as st:
        peak, total = st.sb("peak", [P, T]), st.sb("total", [P, T])
        above = st.sb("above", [P, T, E, E])
        same = st.sb("same", [P, T, E, E])
        before = st.sb("before", [P, E, E])
        rank = st.sb("rank", [P, T, E])
        vec, shifted, exped, consts = (st.sem(n) for n in ("vector_steps", "shifted", "exped", "consts"))
        with nc.Block() as block:
            @block.gpsimd
            def _(pool):
                nc.gpsimd.memset(before[:, :, :], 1.0).then_inc(consts, 1)
                pool.wait_ge(consts, 1)
                nc.gpsimd.affine_select(out=before[:, :, :], in_=before[:, :, :], compare_op=ALU.is_gt, fill=0.0,
                                        base=0, pattern=[[1, E], [-1, E]], channel_multiplier=0).then_inc(consts, 1)

            @block.scalar
            def _(act):
                act.wait_ge(shifted, 1)
                nc.scalar.activation(scores, scores, ACT.Exp).then_inc(exped, 1)
                if renorm == "softmax":
                    act.wait_ge(shifted, 2)
                    nc.scalar.activation(weight, weight, ACT.Exp).then_inc(exped, 1)

            @block.vector
            def _(dve):
                steps = Steps(dve, vec)
                steps.do(nc.vector.tensor_reduce(peak[:, :], scores, AX.X, ALU.max))
                nc.vector.tensor_tensor(scores, scores, over(peak[:, :], E), ALU.subtract).then_inc(shifted, 1)
                dve.wait_ge(exped, 1)
                steps.do(nc.vector.tensor_reduce(total[:, :], scores, AX.X, ALU.add))
                steps.do(nc.vector.reciprocal(total[:, :], total[:, :]))
                steps.do(nc.vector.tensor_tensor(scores, scores, over(total[:, :], E), ALU.mult))
                of_f = scores.unsqueeze(2).to_broadcast([P, T, E, E])
                of_e = scores.unsqueeze(3).to_broadcast([P, T, E, E])
                steps.add(nc.vector.tensor_tensor(above[:, :, :, :], of_f, of_e, ALU.is_gt))
                steps.do(nc.vector.tensor_tensor(same[:, :, :, :], of_f, of_e, ALU.is_equal))
                dve.wait_ge(consts, 2)
                flat = lambda a: a[:, :, :, :].rearrange("p t e f -> p t (e f)")
                steps.do(nc.vector.tensor_tensor(flat(same), flat(same),
                                                 rows_of(before[:, :, :].rearrange("p e f -> p (e f)"), T), ALU.mult))
                steps.do(nc.vector.tensor_tensor(flat(above), flat(above), flat(same), ALU.add))
                steps.do(nc.vector.tensor_reduce(rank[:, :, :], above[:, :, :, :], AX.X, ALU.add))
                steps.do(nc.vector.tensor_scalar(rank[:, :, :], rank[:, :, :], 2.0, None, ALU.is_lt))
                if renorm == "softmax":
                    steps.do(nc.vector.tensor_reduce(peak[:, :], scores, AX.X, ALU.max))
                    nc.vector.tensor_tensor(weight, scores, over(peak[:, :], E), ALU.subtract).then_inc(shifted, 1)
                    dve.wait_ge(exped, 2)
                    steps.do(nc.vector.tensor_tensor(weight, weight, rank[:, :, :], ALU.mult))
                else:
                    steps.do(nc.vector.tensor_tensor(weight, scores, rank[:, :, :], ALU.mult))
                steps.do(nc.vector.tensor_reduce(total[:, :], weight, AX.X, ALU.add))
                if renorm != "softmax":
                    steps.do(nc.vector.tensor_scalar(total[:, :], total[:, :], 1e-9, None, ALU.add))
                steps.do(nc.vector.reciprocal(total[:, :], total[:, :]))
                steps.do(nc.vector.tensor_tensor(weight, weight, over(total[:, :], E), ALU.mult))


Q_HEADS = 4
HD = D // Q_HEADS
EXPERTS = 8
HIDDEN = 170
HALF = HIDDEN // 2


def gated_experts_stage(nc, core, I, weight, acc):
    with Stage(nc, "moe") as st:
        w1, w3 = st.sb("w1", [D, EXPERTS * HIDDEN]), st.sb("w3", [D, EXPERTS * HIDDEN])
        w2 = st.sb("w2", [HALF, 2 * EXPERTS, D])
        act1 = st.sb("act1", [HALF, 2, BANK])
        hid = st.sb("hid", [HALF, 4, BANK])
        part = st.sb("part", [P, 2, 4, D])
        load_stage(nc, "moe_load", [(w1[:, :], I["moe_w1"]), (w3[:, :], I["moe_w3"]),
                                    (w2[:, :, :], I["moe_w2"].rearrange("(u p) d -> p u d", p=HALF))])
        raised, activated, gated, lowered, scaled, added, passed = (
            st.sem(n) for n in ("raised", "activated", "gated", "lowered", "scaled", "added", "passed"))
        start_loop(nc, [raised, activated, gated, lowered, scaled, added])
        ps = core.psum
        U = 2 * EXPERTS
        with nc.Block() as block:
            @block.tensor
            def _(pe):
                with pe.Fori(0, GROUPS) as g:
                    def raise_(e):
                        for u in (2 * e, 2 * e + 1):
                            if u >= 2:
                                pe.wait_ge(gated, START + U * g + u - 1)
                            else:
                                pe.wait_ge(gated, START + U * g)
                            wait_apart(pe, passed)
                            cols = core.xnT[0:D, bass.ds(g * BANK, BANK)]
                            nc.tensor.matmul(ps[0:HALF, u % 2, :], w1[:, u * HALF:(u + 1) * HALF], cols, start=True, stop=True)
                            nc.tensor.matmul(ps[0:HALF, 2 + u % 2, :], w3[:, u * HALF:(u + 1) * HALF], cols,
                                             start=True, stop=True).then_inc(raised, 1)

                    raise_(0)
                    for e in range(EXPERTS):
                        if e + 1 < EXPERTS:
                            raise_(e + 1)
                        pe.wait_ge(gated, START + U * g + 2 * e + 2)
                        pe.wait_ge(scaled, START + EXPERTS * g + max(e - 1, 0))
                        wait_apart(pe, passed)
                        for k in range(4):
                            for half in range(2):
                                last = nc.tensor.matmul(ps[:, 4 + e % 2, k * D:(k + 1) * D],
                                                        hid[:, (2 * e + half) % 4, k * P:(k + 1) * P], w2[:, 2 * e + half, :],
                                                        start=(half == 0), stop=(half == 1))
                        last.then_inc(lowered, 1)

            @block.scalar
            def _(act):
                with act.Fori(0, GROUPS) as g:
                    for u in range(U):
                        act.wait_ge(raised, START + U * g + u + 1)
                        act.wait_ge(gated, START + U * g + max(u - 1, 0))
                        nc.scalar.activation(act1[:, u % 2, :], ps[0:HALF, u % 2, :], ACT.Silu).then_inc(activated, 1)

            @block.vector
            def _(dve):
                with dve.Fori(0, GROUPS) as g:
                    def gate(e):
                        for u in (2 * e, 2 * e + 1):
                            dve.wait_ge(activated, START + U * g + u + 1)
                            dve.wait_ge(lowered, START + EXPERTS * g + max(e - 1, 0))
                            nc.vector.tensor_tensor(hid[:, u % 4, :], act1[:, u % 2, :], ps[0:HALF, 2 + u % 2, :],
                                                    ALU.mult).then_inc(gated, 1)

                    gate(0)
                    for e in range(EXPERTS):
                        if e + 1 < EXPERTS:
                            gate(e + 1)
                        n = EXPERTS * g + e
                        dve.wait_ge(lowered, START + n + 1)
                        nc.vector.tensor_tensor(part[:, e % 2, :, :], ps[:, 4 + e % 2, 0:4 * D].rearrange("p (t d) -> p t d", d=D),
                                                over(weight[:, bass.ds(4 * g, 4), e], D), ALU.mult).then_inc(scaled, 1)
                        dve.wait_ge(scaled, START + n + 1)
                        dve.wait_ge(added, START + n)
                        nc.vector.tensor_tensor(acc[:, bass.ds(4 * g, 4), :], acc[:, bass.ds(4 * g, 4), :],
                                                part[:, e % 2, :, :], ALU.add).then_inc(added, 1)


def rotary_experts_stage(nc, core, I):
    with Stage(nc, "rot") as st:
        spare = st.sb("spare", [P, T, D])
        norm_stage(nc, core, "rot_rms1", core.xn, eps=1e-6, use_mean=False, gain=I["rms1_w"], dst=spare)
        with Stage(nc, "rot_attn") as at:
            width = 5 * D
            w_in = at.sb("w_in", [D, width])
            w_out = at.sb("w_out", [HD, Q_HEADS * D])
            cos, sin = at.sb("cos", [P, CH, HD]), at.sb("sin", [P, CH, HD])
            qkv = at.sb("qkv", [P, T, width])
            yT = at.sb("yT", [D, COLS])
            load_stage(nc, "rot_load", [(w_in[:, :], I["rot_in"]), (w_out[:, :], I["rot_out"]),
                                        (cos[:, :, :], I["rot_cos"].rearrange("(c p) d -> p c d", p=P)),
                                        (sin[:, :, :], I["rot_sin"].rearrange("(c p) d -> p c d", p=P))])
            product_stage(nc, core, "rot_qkv", [(lambda t: core.xnT[0:D, t * P:(t + 1) * P], w_in[:, :])], width,
                          lambda t0, t1, made: nc.scalar.activation(qkv[:, t0:t1, :], made, ACT.Copy), engine="scalar")
            with Stage(nc, "rope") as rt:
                vec = rt.sem("vector_steps")
                with nc.Block() as block:
                    @block.vector
                    def _(dve):
                        steps = Steps(dve, vec)
                        parts = [(lo, table) for lo, table in ((0, cos), (2 * D, sin))]
                        view = lambda b, lo: qkv[:, b * CH:(b + 1) * CH, lo:lo + 2 * D].rearrange("p c (h d) -> p c h d", d=HD)
                        for b in range(B):
                            for lo, table in parts:
                                steps.add(nc.vector.tensor_tensor(
                                    view(b, lo), view(b, lo),
                                    table[:, :, :].unsqueeze(2).to_broadcast([P, CH, 2 * Q_HEADS, HD]), ALU.mult))
                        steps.settle()
                        steps.do(nc.vector.tensor_tensor(qkv[:, :, 0:2 * D], qkv[:, :, 0:2 * D], qkv[:, :, 2 * D:4 * D], ALU.add))
            causal_attention_stage(nc, core, "rot_soft", [(qkv, HD, 0), (qkv, HD, D), (qkv, HD, 4 * D)], Q_HEADS, HD,
                                   HD ** -0.5, w_out, yT)
            add_turned_stage(nc, core, "rot_add", yT, core.xn)
        norm_stage(nc, core, "rot_rms2", core.xn, eps=1e-6, use_mean=False, gain=I["rms2_w"], dst=spare)
        router, weight = st.sb("router", [P, T, EXPERTS]), st.sb("weight", [P, T, EXPERTS])
        w_r = st.sb("w_r", [D, EXPERTS])
        load_stage(nc, "router_load", [(w_r[:, :], I["router"])])
        product_stage(nc, core, "router_p", [(lambda t: core.xnT[0:D, t * P:(t + 1) * P], w_r[:, :])], EXPERTS,
                      lambda t0, t1, made: nc.vector.tensor_copy(router[:, t0:t1, :], made))
        top_two_stage(nc, core, "router_top", router[:, :, :], weight[:, :, :], EXPERTS, "sum")
        gated_experts_stage(nc, core, I, weight, core.xn)
        add_stage(nc, core, "rot_residual", (core.h[:, :, :], core.h[:, :, :], core.xn[:, :, :]))


KEEP = SEQ // 10
SLOT = 64
S_HEADS = 8
S_HD = D // S_HEADS


def sparse_attention_stage(nc, core, I):
    with Stage(nc, "sparse") as st:
        w_qkv, w_g1, w_g2, w_o = (st.sb(n, s) for n, s in (
            ("w_qkv", [D + 1, 3 * D]), ("w_g1", [D + 1, 16]), ("w_g2", [17, 1]), ("w_o", [D + 1, D])))
        qkv = st.sb("qkv", [P, T, 3 * D])
        gT = st.sb("gT", [17, COLS])
        imp = st.sb("imp", [P, T])
        diag = st.sb("diag", [P, T, P])
        row = st.sb("row", [P, COLS])
        square = st.sb("square", [P, P])
        earlier = st.sb("earlier", [P, 2 * PAD - P])
        junk = st.sb("junk", [P, 2, SEQ])
        col, larger, ties = st.sb("col", [P, T]), st.sb("larger", [P, T]), st.sb("ties", [P, T])
        slots = st.sb("slots", [P, SLOT])
        pick = st.sb("pick", [P, T, 2, SLOT])
        k_mask, v_mask = st.sb("k_mask", [D, S_HEADS]), st.sb("v_mask", [P, S_HEADS // 2, 2, S_HD])
        kB = st.sb("kB", [D, B, S_HEADS * SLOT])
        vB = st.sb("vB", [P, B, D])
        qT = st.sb("qT", [D, COLS])
        attn = st.sb("attn", [P, T, D])
        load_stage(nc, "sparse_load", [(w_qkv[:, :], I["s_qkv"]), (w_g1[:, :], I["s_g1"]), (w_g2[:, :], I["s_g2"]),
                                       (w_o[:, :], I["s_out"])])
        consts = st.sem("consts")
        with nc.Block() as block:
            @block.gpsimd
            def _(pool):
                steps = Steps(pool, consts)
                steps.do(nc.gpsimd.memset(gT[:, :], 1.0))
                steps.do(nc.gpsimd.memset(square[:, :], 1.0))
                steps.do(nc.gpsimd.memset(earlier[:, :], 1.0))
                steps.do(nc.gpsimd.memset(k_mask[:, :], 1.0))
                steps.do(nc.gpsimd.memset(v_mask[:, :, :, :], 0.0))
                steps.do(nc.gpsimd.iota(slots[:, :], [[1, SLOT]], base=0, channel_multiplier=0,
                                        allow_small_or_imprecise_dtypes=True))
                steps.do(nc.gpsimd.memset(slots[:, KEEP:SLOT], -1.0))
                steps.do(nc.gpsimd.memset(v_mask[0:D, :, 0, :], 1.0))
                steps.do(nc.gpsimd.memset(v_mask[D:P, :, 1, :], 1.0))
                steps.do(nc.gpsimd.affine_select(out=earlier[:, :], in_=earlier[:, :], compare_op=ALU.is_gt, fill=0.0,
                                                 base=PAD - P, pattern=[[-1, 2 * PAD - P]], channel_multiplier=1))
                steps.do(nc.gpsimd.affine_select(out=k_mask[:, :], in_=k_mask[:, :], compare_op=ALU.is_ge, fill=0.0,
                                                 base=0, pattern=[[-S_HD, S_HEADS]], channel_multiplier=1))
                steps.do(nc.gpsimd.affine_select(out=k_mask[:, :], in_=k_mask[:, :], compare_op=ALU.is_ge, fill=0.0,
                                                 base=S_HD - 1, pattern=[[S_HD, S_HEADS]], channel_multiplier=-1))
        product_stage(nc, core, "sparse_qkv", [(lambda t: core.xnT[:, t * P:(t + 1) * P], w_qkv[:, :])], 3 * D,
                      lambda t0, t1, made: nc.scalar.activation(qkv[:, t0:t1, :], made, ACT.Copy), engine="scalar")
        wide_product_stage(nc, core, "sparse_g1", [(16, [(w_g1[:, :], lambda c0, c1: core.xnT[:, c0:c1])])],
                           lambda c0, c1, _, made: nc.scalar.activation(gT[0:16, c0:c1], made, ACT.Relu))
        product_stage(nc, core, "sparse_g2", [(lambda t: gT[:, t * P:(t + 1) * P], w_g2[:, :])], 1,
                      lambda t0, t1, made: nc.scalar.activation(imp[:, t0:t1], made.rearrange("p t w -> p (t w)"), ACT.Sigmoid),
                      engine="scalar")
        ps = core.psum
        vec, dg, spread, rowed, picked, made, done = (
            st.sem(n) for n in ("vector_steps", "diag_ready", "spread", "rowed", "picked", "made", "done"))
        with nc.Block() as block:
            @block.tensor
            def _(pe):
                pe.wait_ge(dg, 1)
                for g in range(GROUPS):
                    nc.tensor.matmul(ps[:, g, :], square[:, :], diag[:, 4 * g:4 * g + 4, :].rearrange("p t n -> p (t n)"),
                                     start=True, stop=True).then_inc(spread, 1)
                pe.wait_ge(picked, 1)
                pe.wait_ge(rowed, GROUPS)
                for b in range(B):
                    for c in range(CH):
                        t, r = b * CH + c, TOKEN_ROWS[c]
                        nc.tensor.matmul(ps[0:D, b, 0:SLOT], qkv[0:r, t, D:2 * D], pick[0:r, t, 0, :],
                                         start=(c == 0), stop=(c == CH - 1))
                    for c in range(CH):
                        t, r = b * CH + c, TOKEN_ROWS[c]
                        last = nc.tensor.matmul(ps[:, 4 + b, 0:D], pick[0:r, t, :, :].rearrange("p s n -> p (s n)"),
                                                qkv[0:r, t, 2 * D:3 * D], start=(c == 0), stop=(c == CH - 1))
                    last.then_inc(made, 1)

            @block.scalar
            def _(act):
                for g in range(GROUPS):
                    act.wait_ge(spread, g + 1)
                    nc.scalar.activation(row[:, g * BANK:(g + 1) * BANK], ps[:, g, :], ACT.Copy).then_inc(rowed, 1)

            @block.vector
            def _(dve):
                steps = Steps(dve, vec)
                nc.vector.tensor_tensor(diag[:, :, :], rows_of(core.ident[:, :], T), over(imp[:, :], P), ALU.mult
                                        ).then_inc(dg, 1)
                dve.wait_ge(rowed, GROUPS)
                steps.do(nc.vector.tensor_tensor(diag[:, :, :], row[:, :].rearrange("p (t n) -> p t n", n=P),
                                                 rows_of(core.ident[:, :], T), ALU.mult))
                steps.do(nc.vector.tensor_reduce(col[:, :], diag[:, :, :], AX.X, ALU.add))
                for b in range(B):
                    for c in range(CH):
                        t = b * CH + c
                        seq = row[:, b * PAD:b * PAD + SEQ]
                        shift = PAD - P - c * P
                        steps.add(nc.vector.tensor_scalar(junk[:, 0, :], seq, col[:, t:t + 1], 0.0, ALU.is_gt, ALU.add,
                                                          accum_out=larger[:, t:t + 1]))
                        steps.add(nc.vector.scalar_tensor_tensor(junk[:, 1, :], seq, col[:, t:t + 1], earlier[:, shift:shift + SEQ],
                                                                 ALU.is_equal, ALU.mult, accum_out=ties[:, t:t + 1]))
                        steps.settle()
                steps.do(nc.vector.tensor_tensor(larger[:, :], larger[:, :], ties[:, :], ALU.add))
                for s in range(2):
                    steps.add(nc.vector.tensor_tensor(pick[:, :, s, :], over(larger[:, :], SLOT), rows_of(slots[:, :], T),
                                                      ALU.is_equal))
                steps.settle()
                dve.sem_inc(picked, 1)
                for b in range(B):
                    dve.wait_ge(made, b + 1)
                    nc.vector.tensor_tensor(kB[:, b, :].rearrange("p (h s) -> p h s", s=SLOT),
                                            ps[0:D, b, 0:SLOT].unsqueeze(1).to_broadcast([D, S_HEADS, SLOT]),
                                            over(k_mask[:, :], SLOT), ALU.mult).then_inc(done, 1)
                    nc.vector.tensor_tensor(vB[:, b, :], ps[:, 4 + b, 0:D],
                                            v_mask[:, :, :, :].rearrange("p a s d -> p (a s d)"), ALU.mult).then_inc(done, 1)
        turn_stage(nc, core, "sparse_turn_q", [(qT, D, lambda t: qkv[:, t, 0:D])])
        with Stage(nc, "sparse_soft") as at:
            qt = at.sb("qt", [D, P])
            probs = at.sb("probs", [P, S_HEADS, SLOT])
            pT = at.sb("pT", [P, 4, P])
            stat = at.sb("stat", [P, 3, S_HEADS])
            (fetched, scored, shifted, exped, normed, turned, copied, weighed, kept, vec, zeroed, passed) = (
                at.sem(n) for n in ("fetched", "scored", "shifted", "exped", "normed", "turned", "copied", "weighed",
                                    "kept", "vector_steps", "zeroed", "passed"))
            start_loop(nc, [fetched, scored, shifted, exped, normed, turned, copied, weighed, kept])
            kB_flat, vB_flat = kB[:, :, :].rearrange("p b n -> p (b n)"), vB[:, :, :].rearrange("p b n -> p (b n)")
            real = lambda x: x[:, :, 0:KEEP]
            with nc.Block() as block:
                @block.tensor
                def _(pe):
                    with pe.Fori(0, B) as b:
                        with pe.Fori(0, CH) as c:
                            t = b * CH + c
                            pe.wait_ge(fetched, START + t + 1)
                            pe.wait_ge(shifted, START + t)
                            wait_apart(pe, passed)
                            nc.tensor.matmul(ps[:, 0, :], qt[:, :], kB_flat[:, bass.ds(b * S_HEADS * SLOT, BANK)],
                                             start=True, stop=True).then_inc(scored, 1)
                            pe.wait_ge(normed, START + t + 1)
                            pe.wait_ge(copied, START + t)
                            wait_apart(pe, passed)
                            for k in range(4):
                                last = nc.tensor.transpose(ps[:, 1, k * P:(k + 1) * P],
                                                           probs[:, 2 * k:2 * k + 2, :].rearrange("p h s -> p (h s)"),
                                                           core.ident[:, :])
                            last.then_inc(turned, 1)
                            pe.wait_ge(copied, START + t + 1)
                            pe.wait_ge(kept, START + t)
                            wait_apart(pe, passed)
                            for k in range(4):
                                last = nc.tensor.matmul(ps[:, 2, k * 2 * S_HD:(k + 1) * 2 * S_HD], pT[:, k, :],
                                                        vB_flat[:, bass.ds(b * D + k * 2 * S_HD, 2 * S_HD)],
                                                        start=True, stop=True)
                            last.then_inc(weighed, 1)

                @block.scalar
                def _(act):
                    with act.Fori(0, T) as t:
                        act.wait_ge(scored, START + t)
                        nc.scalar.activation(qt[:, :], qT[:, bass.ds(t * P, P)], ACT.Copy).then_inc(fetched, 1)
                        act.wait_ge(shifted, START + t + 1)
                        nc.scalar.activation(real(probs), real(probs), ACT.Exp, scale=S_HD ** -0.5).then_inc(exped, 1)
                        act.wait_ge(turned, START + t + 1)
                        act.wait_ge(weighed, START + t)
                        nc.scalar.activation(pT[:, :, :], ps[:, 1, :].rearrange("p (k n) -> p k n", n=P), ACT.Copy
                                             ).then_inc(copied, 1)
                        act.wait_ge(weighed, START + t + 1)
                        nc.scalar.activation(attn[:, bass.ds(t, 1), :], ps[:, 2, 0:D].unsqueeze(1), ACT.Copy).then_inc(kept, 1)

                @block.vector
                def _(dve):
                    steps = Steps(dve, vec)
                    steps.do(nc.vector.memset(probs[:, :, :], 0.0))
                    with dve.Fori(0, T) as t:
                        steps.enter_loop(t, 3)
                        s = ps[:, 0, :].rearrange("p (h s) -> p h s", s=SLOT)
                        dve.wait_ge(scored, START + t + 1)
                        steps.do(nc.vector.tensor_reduce(stat[:, 0, :], real(s), AX.X, ALU.max))
                        dve.wait_ge(turned, START + t)
                        nc.vector.tensor_tensor(real(probs), real(s), over(stat[:, 0, :], KEEP), ALU.subtract
                                                ).then_inc(shifted, 1)
                        dve.wait_ge(exped, START + t + 1)
                        steps.do(nc.vector.tensor_reduce(stat[:, 1, :], real(probs), AX.X, ALU.add))
                        steps.do(nc.vector.reciprocal(stat[:, 2, :], stat[:, 1, :]))
                        nc.vector.tensor_tensor(real(probs), real(probs), over(stat[:, 2, :], KEEP), ALU.mult
                                                ).then_inc(normed, 1)
        turn_stage(nc, core, "sparse_turn_o", [(core.xnT, D, lambda t: attn[:, t, :])])
        product_stage(nc, core, "sparse_out", [(lambda t: core.xnT[:, t * P:(t + 1) * P], w_o[:, :])], D,
                      lambda t0, t1, made: nc.vector.tensor_tensor(core.h[:, t0:t1, :], core.h[:, t0:t1, :], made, ALU.add))


DEPTH = 7
NODES = 2 ** (DEPTH + 1)
CHUNK = BANK // D
LEVELS = DEPTH + 1 - 3


def tree_stage(nc, core, I):
    with Stage(nc, "tree") as st:
        w_n = st.sb("w_n", [D + 1, NODES])
        w_v = st.sb("w_v", [P, NODES // 2 * D])
        w_b = st.sb("w_b", [P, 2, D])
        logit = st.sb("logit", [P, T, NODES])
        on = st.sb("on", [P, T, NODES])
        right = st.sb("right", [P, T, NODES])
        gate = st.sb("gate", [P, T, DEPTH + 1])
        twice = st.sb("twice", [P, T, 2, D])
        xT2 = st.sb("xT2", [P, COLS])
        load_stage(nc, "tree_load", [(w_n[:, :], I["tree_w1"]), (w_v[:, :], I["tree_w2"]),
                                     (w_b[:, :, :], I["tree_b2"].rearrange("(k p) d -> p k d", p=P))])
        product_stage(nc, core, "tree_logits", [(lambda t: core.xnT[:, t * P:(t + 1) * P], w_n[:, :])], NODES,
                      lambda t0, t1, made: nc.scalar.activation(logit[:, t0:t1, :], made, ACT.Copy), engine="scalar")
        vec, pol, gelu, absed, doubled = (st.sem(n) for n in ("vector_steps", "pool_steps", "gelu", "absed", "doubled"))
        with nc.Block() as block:
            @block.gpsimd
            def _(pool):
                for s in range(2):
                    nc.gpsimd.tensor_copy(twice[:, :, s, :], core.xn[:, :, :])

            @block.vector
            def _(dve):
                steps = Steps(dve, vec)
                steps.add(nc.vector.tensor_scalar(right[:, :, :], logit[:, :, :], 0.0, None, ALU.is_gt))
                steps.add(nc.vector.memset(on[:, :, 0:1], 0.0))
                steps.do(nc.vector.memset(on[:, :, 1:2], 1.0))
                dve.sem_inc(absed, 1)
                for level in range(DEPTH):
                    lo, n = 2 ** level, 2 ** level
                    child = on[:, :, 2 * lo:4 * lo].rearrange("p t (n s) -> p t n s", s=2)
                    steps.do(nc.vector.tensor_tensor(child[:, :, :, 1], on[:, :, lo:lo + n], right[:, :, lo:lo + n], ALU.mult))
                    steps.do(nc.vector.tensor_tensor(child[:, :, :, 0], on[:, :, lo:lo + n], child[:, :, :, 1], ALU.subtract))
                dve.wait_ge(gelu, 2)
                steps.do(nc.vector.tensor_tensor(logit[:, :, :], logit[:, :, :], on[:, :, :], ALU.mult))
                for level in range(DEPTH + 1):
                    lo = 2 ** level
                    steps.add(nc.vector.tensor_reduce(gate[:, :, level], logit[:, :, lo:2 * lo], AX.X, ALU.add))

            @block.scalar
            def _(act):
                act.wait_ge(absed, 1)
                nc.scalar.activation(logit[:, :, :], logit[:, :, :], ACT.Abs).then_inc(gelu, 1)
                act.wait_ge(gelu, 1)
                nc.scalar.activation(logit[:, :, :], logit[:, :, :], ACT.Gelu).then_inc(gelu, 1)
        turn_stage(nc, core, "tree_turn", [(xT2, P, lambda t: twice[:, t, :, :].rearrange("p s d -> p (s d)"))])
        tree_sum_stage(nc, core, logit, on, gate, xT2, w_v, w_b)


def tree_sum_stage(nc, core, weight, on, gate, xT2, w_v, w_b):
    with Stage(nc, "leaf") as st:
        xs = st.sb("xs", [P, P])
        ws = st.sb("ws", [P, NODES])
        path = st.sb("path", [P, NODES])
        wT = st.sb("wT", [P, 2, P])
        acc = st.sb("acc", [P, LEVELS + 1, CHUNK, D])
        total = st.sb("total", [P, 2, D])
        masked, passed_v = st.sem("masked"), st.sem("passed_by_vector")
        fetched, made, taken, turned, turned_copied, biased, scaled, vec, freed, passed, added = (
            st.sem(n) for n in ("fetched", "made", "taken", "turned", "turned_copied", "biased", "scaled",
                                "vector_steps", "freed", "passed", "added"))
        start_loop(nc, [fetched, masked, made, taken, turned, turned_copied, biased, scaled, added])
        ps = core.psum
        half = NODES // CHUNK // 2
        first = {2 ** (3 + k) // CHUNK: k for k in range(LEVELS)}
        order = [c for pair in zip(range(half), range(half, 2 * half)) for c in pair]
        with nc.Block() as block:
            @block.tensor
            def _(pe):
                with pe.Fori(0, T) as t:
                    pe.wait_ge(fetched, START + 2 * t + 2)
                    for n, c in enumerate(order):
                        lower = c < half
                        if n == 0:
                            pe.wait_ge(taken, START + 2 * half * t)
                        elif n >= 6:
                            pe.wait_ge(taken, START + 2 * half * t + n - 5)
                        wait_apart(pe, passed)
                        rows = slice(0, D) if lower else slice(D, P)
                        at = (c % half) * BANK
                        nc.tensor.matmul(ps[:, n % 6, :], xs[rows, :], w_v[rows, at:at + BANK],
                                         start=True, stop=True).then_inc(made, 1)
                    pe.wait_ge(turned_copied, START + t)
                    wait_apart(pe, passed)
                    for k in range(2):
                        last = nc.tensor.transpose(ps[:, 6, k * P:(k + 1) * P], ws[:, k * P:(k + 1) * P], core.ident[:, :])
                    last.then_inc(turned, 1)
                    pe.wait_ge(turned_copied, START + t + 1)
                    pe.wait_ge(added, START + t)
                    wait_apart(pe, passed)
                    for k in range(2):
                        last = nc.tensor.matmul(ps[:, 7, 0:D], wT[:, k, :], w_b[:, k, :], start=(k == 0), stop=(k == 1))
                    last.then_inc(biased, 1)

            @block.scalar
            def _(act):
                with act.Fori(0, T) as t:
                    act.wait_ge(made, START + 2 * half * t)
                    act.wait_ge(turned, START + t)
                    nc.scalar.activation(xs[:, :], xT2[:, bass.ds(t * P, P)], ACT.Copy).then_inc(fetched, 1)
                    nc.scalar.activation(ws[:, :].unsqueeze(1), weight[:, bass.ds(t, 1), :], ACT.Copy).then_inc(fetched, 1)
                    act.wait_ge(taken, START + 2 * half * t)
                    nc.scalar.activation(path[:, :].unsqueeze(1), on[:, bass.ds(t, 1), :], ACT.Copy).then_inc(masked, 1)
                    act.wait_ge(turned, START + t + 1)
                    act.wait_ge(biased, START + t)
                    nc.scalar.activation(wT[:, :, :], ps[:, 6, 0:2 * P].rearrange("p (k n) -> p k n", n=P), ACT.Copy
                                         ).then_inc(turned_copied, 1)

            @block.gpsimd
            def _(pool):
                with pool.Fori(0, T) as t:
                    pool.wait_ge(taken, START + 2 * half * (t + 1))
                    for k in range(LEVELS):
                        last = nc.gpsimd.tensor_tensor(
                            acc[:, k + 1, :, :].rearrange("p c d -> p (c d)"), acc[:, k + 1, :, :].rearrange("p c d -> p (c d)"),
                            gate[:, bass.ds(t, 1), k + 3].to_broadcast([P, CHUNK * D]), ALU.mult)
                        last.then_inc(scaled, 1)

            @block.vector
            def _(dve):
                steps = Steps(dve, vec)
                with dve.Fori(0, T) as t:
                    steps.enter_loop(t, 2)
                    dve.wait_ge(masked, START + t + 1)
                    for n, c in enumerate(order):
                        dve.wait_ge(made, START + 2 * half * t + n + 1)
                        if n >= 2:
                            dve.wait_ge(taken, START + 2 * half * t + n - 1)
                        wait_apart(dve, passed_v)
                        bank = ps[:, n % 6, :].rearrange("p (c d) -> p c d", d=D)
                        if c == 0:
                            ins = nc.vector.tensor_tensor(acc[:, 0, :, :], bank,
                                                          over(weight[:, bass.ds(t, 1), 0:CHUNK].rearrange("p t n -> p (t n)"), D), ALU.mult)
                        else:
                            level = max(k for f, k in first.items() if f <= c)
                            mask = path[:, c * CHUNK:(c + 1) * CHUNK]
                            if c in first:
                                ins = nc.vector.tensor_tensor(acc[:, level + 1, :, :], bank, over(mask, D), ALU.mult)
                            else:
                                ins = nc.vector.copy_predicated(acc[:, level + 1, :, :], over(mask.bitcast(U32), D), bank)
                        ins.then_inc(taken, 1)
                    dve.wait_ge(scaled, START + LEVELS * (t + 1))
                    steps.do(nc.vector.tensor_reduce(total[:, 0, :], acc[:, :, :, :].rearrange("p l c d -> p d (l c)"),
                                                     AX.X, ALU.add))
                    dve.wait_ge(biased, START + t + 1)
                    steps.do(nc.vector.tensor_tensor(total[:, 1, :], ps[:, 7, 0:D], total[:, 0, :], ALU.add))
                    nc.vector.tensor_tensor(core.h[:, bass.ds(t, 1), :], core.h[:, bass.ds(t, 1), :],
                                            total[:, 1, :].unsqueeze(1), ALU.add).then_inc(added, 1)


def sigmoid_attention_stage(nc, core, I):
    with Stage(nc, "sig") as st:
        w = st.sb("w", [D, D])
        qT = st.sb("qT", [D, COLS])
        keys = st.sb("keys", [D, PAD])
        att = st.sb("att", [P, CH, PAD])
        load_stage(nc, "sig_load", [(w[:, :], I["sig_w"])])
        wide_product_stage(nc, core, "sig_q", [(D, [(w[:, :], lambda c0, c1: core.xnT[0:D, c0:c1])])],
                           lambda c0, c1, _, made: nc.scalar.activation(qT[:, c0:c1], made, ACT.Copy))
        set_stage(nc, "att_zero", [(att[:, :, :], 0.0)])
        fetched, scored, attended, weighed, added, passed = (
            st.sem(n) for n in ("fetched", "scored", "attended", "weighed", "added", "passed"))
        start_loop(nc, [fetched, scored, attended, weighed, added])
        ps = core.psum
        side = SEQ // 2
        with nc.Block() as block:
            @block.tensor
            def _(pe):
                with pe.Fori(0, B) as b:
                    pe.wait_ge(fetched, START + b + 1)
                    for m in range(CH):
                        if m >= 2:
                            pe.wait_ge(attended, START + CH * b + m - 1)
                        else:
                            pe.wait_ge(attended, START + CH * b)
                        wait_apart(pe, passed)
                        for s in range(2):
                            last = nc.tensor.matmul(ps[:, 2 * (m % 2) + s, 0:side], keys[:, m * P:(m + 1) * P],
                                                    qT[:, bass.ds(b * PAD + s * side, side)], start=True, stop=True)
                        last.then_inc(scored, 1)
                    pe.wait_ge(attended, START + CH * b + CH)
                    pe.wait_ge(added, START + b)
                    wait_apart(pe, passed)
                    for c in range(CH):
                        for m in range(CH):
                            r = TOKEN_ROWS[m]
                            last = nc.tensor.matmul(ps[:, 4, c * D:(c + 1) * D], att[0:r, m, c * P:(c + 1) * P],
                                                    core.xn[0:r, bass.ds(b * CH + m, 1), :].rearrange("p t d -> p (t d)"),
                                                    start=(m == 0), stop=(m == CH - 1))
                    last.then_inc(weighed, 1)

            @block.scalar
            def _(act):
                with act.Fori(0, B) as b:
                    act.wait_ge(scored, START + CH * b)
                    nc.scalar.activation(keys[:, :], core.xnT[0:D, bass.ds(b * PAD, PAD)], ACT.Copy).then_inc(fetched, 1)
                    act.wait_ge(weighed, START + b)
                    for m in range(CH):
                        r = TOKEN_ROWS[m]
                        act.wait_ge(scored, START + CH * b + m + 1)
                        nc.scalar.activation(att[0:r, m, 0:SEQ].rearrange("p (s n) -> p s n", s=2),
                                             ps[0:r, 2 * (m % 2):2 * (m % 2) + 2, 0:side], ACT.Sigmoid).then_inc(attended, 1)

            @block.vector
            def _(dve):
                with dve.Fori(0, B) as b:
                    dve.wait_ge(weighed, START + b + 1)
                    full = core.h[:, bass.ds(b * CH, CH - 1), :]
                    nc.vector.tensor_tensor(full, full, ps[:, 4, 0:(CH - 1) * D].rearrange("p (c d) -> p c d", d=D), ALU.add)
                    tail = core.h[0:TAIL, bass.ds(b * CH + CH - 1, 1), :]
                    nc.vector.tensor_tensor(tail, tail, ps[0:TAIL, 4, (CH - 1) * D:CH * D].unsqueeze(1), ALU.add
                                            ).then_inc(added, 1)


R_EXPERTS = 4


def relu_experts_stage(nc, core, I):
    with Stage(nc, "mlp") as st:
        E = R_EXPERTS
        w_g = st.sb("w_g", [D + 1, E])
        router, weight = st.sb("router", [P, T, E]), st.sb("weight", [P, T, E])
        s1, s2, s3 = st.sb("s1", [D + 1, D]), st.sb("s2", [D + 1, P]), st.sb("s3", [P, D])
        s3b = st.sb("s3b", [1, D])
        e1, e2, e3 = st.sb("e1", [D + 1, E, P]), st.sb("e2", [P, E, D]), st.sb("e3", [D + 1, E, D])
        e2b = st.sb("e2b", [D, E])
        h1, h2 = st.sb("h1", [P, 2, BANK]), st.sb("h2", [P, 2, BANK])
        g1, g2 = st.sb("g1", [D + 1, BANK]), st.sb("g2", [P, BANK])
        part = st.sb("part", [P, 2, 4, D])
        load_stage(nc, "mlp_load", [(w_g[:, :], I["m_gate"]), (s1[:, :], I["m_s1"]), (s2[:, :], I["m_s2"]),
                                    (s3[:, :], I["m_s3"]), (s3b[:, :], I["m_s3b"]), (e1[:, :, :], I["m_e1"]),
                                    (e2[:, :, :], I["m_e2"]), (e3[:, :, :], I["m_e3"]), (e2b[:, :], I["m_e2b"])])
        set_stage(nc, "mlp_ones", [(h2[:, :, :], 1.0), (g1[:, :], 1.0)])
        product_stage(nc, core, "mlp_gate", [(lambda t: core.xnT[:, t * P:(t + 1) * P], w_g[:, :])], E,
                      lambda t0, t1, made: nc.vector.tensor_copy(router[:, t0:t1, :], made))
        top_two_stage(nc, core, "mlp_top", router[:, :, :], weight[:, :, :], E, "softmax")
        up1, act1, up2, act2, down, taken, added, passed = (
            st.sem(n) for n in ("up1", "act1", "up2", "act2", "down", "taken", "added", "passed"))
        start_loop(nc, [up1, act1, up2, act2, down, taken, added])
        ps = core.psum
        N = E + 1
        with nc.Block() as block:
            @block.tensor
            def _(pe):
                with pe.Fori(0, GROUPS) as g:
                    cols = core.xnT[:, bass.ds(g * BANK, BANK)]

                    def first_layer(e):
                        pe.wait_ge(act1, START + N * g + max(e - 1, 0))
                        wait_apart(pe, passed)
                        rows = P if e < E else D
                        nc.tensor.matmul(ps[0:rows, e % 2, :], e1[:, e, :] if e < E else s1[:, :], cols,
                                         start=True, stop=True).then_inc(up1, 1)

                    first_layer(0)
                    for e in range(N):
                        n = N * g + e
                        if e + 1 < N:
                            first_layer(e + 1)
                        pe.wait_ge(act1, START + n + 1)
                        pe.wait_ge(act2, START + N * g + max(e - 1, 0))
                        wait_apart(pe, passed)
                        if e < E:
                            last = nc.tensor.matmul(ps[0:D, 2 + e % 2, :], e2[:, e, :], h1[:, e % 2, :], start=True, stop=True)
                        else:
                            last = nc.tensor.matmul(ps[:, 2 + e % 2, :], s2[:, :], g1[:, :], start=True, stop=True)
                        last.then_inc(up2, 1)
                        pe.wait_ge(act2, START + n + 1)
                        pe.wait_ge(taken, START + N * g + max(e - 1, 0))
                        wait_apart(pe, passed)
                        for k in range(4):
                            out = ps[:, 4 + e % 2, k * D:(k + 1) * D]
                            if e < E:
                                last = nc.tensor.matmul(out, h2[0:D + 1, e % 2, k * P:(k + 1) * P], e3[:, e, :],
                                                        start=True, stop=True)
                            else:
                                nc.tensor.matmul(out, g2[:, k * P:(k + 1) * P], s3[:, :], start=True, stop=False)
                                last = nc.tensor.matmul(out, core.ones[:, :], s3b[:, :], start=False, stop=True)
                        last.then_inc(down, 1)

            @block.scalar
            def _(act):
                with act.Fori(0, GROUPS) as g:
                    for e in range(N):
                        n = N * g + e
                        act.wait_ge(up1, START + n + 1)
                        act.wait_ge(up2, START + N * g + max(e - 1, 0))
                        if e < E:
                            ins = nc.scalar.activation(h1[:, e % 2, :], ps[:, e % 2, :], ACT.Relu)
                        else:
                            ins = nc.scalar.activation(g1[0:D, :], ps[0:D, e % 2, :], ACT.Relu)
                        ins.then_inc(act1, 1)
                        act.wait_ge(up2, START + n + 1)
                        act.wait_ge(down, START + N * g + max(e - 1, 0))
                        if e < E:
                            ins = nc.scalar.activation(h2[0:D, e % 2, :], ps[0:D, 2 + e % 2, :], ACT.Relu, bias=e2b[:, e:e + 1])
                        else:
                            ins = nc.scalar.activation(g2[:, :], ps[:, 2 + e % 2, :], ACT.Relu)
                        ins.then_inc(act2, 1)

            @block.vector
            def _(dve):
                with dve.Fori(0, GROUPS) as g:
                    tiles = core.h[:, bass.ds(4 * g, 4), :]
                    for e in range(N):
                        n = N * g + e
                        dve.wait_ge(down, START + n + 1)
                        dve.wait_ge(added, START + N * g + max(e - 1, 0))
                        made = ps[:, 4 + e % 2, 0:4 * D].rearrange("p (t d) -> p t d", d=D)
                        if e < E:
                            ins = nc.vector.tensor_tensor(part[:, e % 2, :, :], made,
                                                          over(weight[:, bass.ds(4 * g, 4), e], D), ALU.mult)
                        else:
                            ins = nc.vector.tensor_copy(part[:, e % 2, :, :], made)
                        ins.then_inc(taken, 1)
                        dve.wait_ge(taken, START + n + 1)
                        dve.wait_ge(added, START + n)
                        nc.vector.tensor_tensor(tiles, tiles, part[:, e % 2, :, :], ALU.add).then_inc(added, 1)


def store_stage(nc, core, out):
    with Stage(nc, "store") as st:
        stored = st.sem("stored")
        h_b = core.h[:, :, :].rearrange("p (b c) d -> p b c d", c=CH)
        with nc.Block() as block:
            @block.sync
            def _(sp):
                for b in range(B):
                    sp.dma_start(out[b, 0:4 * P, :].rearrange("(c p) d -> p c d", p=P), h_b[:, b, 0:4, :]).then_inc(stored, 16)
                    sp.dma_start(out[b, 4 * P:SEQ, :], h_b[0:TAIL, b, 4, :]).then_inc(stored, 16)
                sp.wait_ge(stored, 16 * 2 * B)


def build(nc, I, out):
    core = Core()
    Stage.spent.clear()
    with ExitStack() as stack:
        sb = lambda name, shape: stack.enter_context(nc.sbuf_tensor(name, shape, F32))
        core.h = sb("h", [P, T, D])
        core.xn = sb("xn", [P, T, D])
        core.xnT = sb("xnT", [D + 1, COLS])
        core.ident = sb("ident", [P, P])
        core.ones = sb("ones", [1, P])
        core.psum = stack.enter_context(nc.psum_tensor("psum", [P, 8, BANK], F32))
        set_stage(nc, "ones", [(core.ones[:, :], 1.0)])
        embed_stage(nc, core, I["x_patches"], I["txt"], I["tok_aug"])
        layers = [linear_attention_stage, retrieval_stage, toeplitz_stage, rotary_experts_stage,
                  sparse_attention_stage, tree_stage, sigmoid_attention_stage, relu_experts_stage]
        for n, layer in enumerate(layers):
            norm_stage(nc, core, f"norm{n}", core.h)
            layer(nc, core, I)
        store_stage(nc, core, out)


def transform_tables():
    lag = np.concatenate([np.arange(SEQ), [0], np.arange(1 - SEQ, 0)]).astype(np.float32)
    n, f = np.arange(SPAN), np.arange(FREQ)
    angle = 2 * np.pi * (np.outer(n, f) % SPAN) / SPAN
    twice = np.where((f == 0) | (f == SEQ), 1.0, 2.0)[:, None] / SPAN
    back = angle[:SEQ].T
    tables = {"cos": np.cos(angle), "sin": -np.sin(angle), "icos": twice * np.cos(back), "isin": -twice * np.sin(back)}
    return {"lags": np.stack([lag, np.ones_like(lag)]), **{k: v.astype(np.float32) for k, v in tables.items()}}


def rotary_weights(wq, wk, wv):
    q = wq.T.reshape(D, Q_HEADS, HD)
    k, v = (w.T.reshape(D, Q_HEADS // 2, HD).repeat(2, axis=1) for w in (wk, wv))
    swap = np.roll(np.arange(HD), HD // 2)
    return np.concatenate([q, k, q[:, :, swap], k[:, :, swap], v], axis=1).reshape(D, 5 * D)


def rotary_tables():
    frequency = 1.0 / 10000.0 ** (np.arange(0, HD, 2, dtype=np.float32) / HD)
    angle = np.outer(np.arange(PAD, dtype=np.float32), frequency)
    angle = np.concatenate([angle, angle], axis=-1)
    sign = np.where(np.arange(HD) < HD // 2, -1.0, 1.0)
    return {"rot_cos": np.cos(angle).astype(np.float32), "rot_sin": (np.sin(angle) * sign).astype(np.float32)}


def tree_weights(w1, b1, w2, b2):
    first = lambda a: np.concatenate([np.zeros_like(a[:1]), a], axis=0)
    w1, b1, w2, b2 = (first(a) for a in (w1, b1, w2, b2))
    v = w2.reshape(2, NODES // 2, D, D).transpose(0, 2, 1, 3).reshape(P, NODES // 2 * D)
    return {"tree_w1": np.concatenate([w1.T, b1[None]], axis=0), "tree_w2": v, "tree_b2": b2}


def pk_blocks(keys):
    k = keys.reshape(2, KEYS, 2, 4, D // 2)
    blocks = np.zeros((4, D // 2, 2, 2, 4, KEYS), keys.dtype)
    for h in range(4):
        blocks[h, :, :, :, h, :] = k[:, :, :, h, :].transpose(3, 0, 2, 1)
    return blocks.reshape(P, 4, 4 * KEYS)


def lay_out(a):
    g = {k: np.asarray(v) for k, v in a.items()}
    join = lambda w, b: np.concatenate([w, b.reshape(1, -1)], axis=0)
    x = g["x"].reshape(B, 8, 8, 8, 8)
    return {
        "x_patches": x.transpose(2, 4, 0, 1, 3).reshape(D, B * PATCHES),
        "txt": g["txt"],
        "tok_aug": join(g["L0_tok_W"].T, g["L0_tok_b"]),
        "qkv_aug": join(g["L0_attn_qkv_w"], g["L0_attn_qkv_b"]),
        "proj_aug": join(g["L0_attn_proj_w"], g["L0_attn_proj_b"]),
        "ln1_g": g["L0_attn_ln1_g"], "ln1_b": g["L0_attn_ln1_b"],
        "ln2_g": g["L0_attn_ln2_g"], "ln2_b": g["L0_attn_ln2_b"],
        "w1_aug": join(g["L0_attn_w1"], g["L0_attn_b1"]),
        "w2": g["L0_attn_w2"], "b2": g["L0_attn_b2"],
        "uv_aug": np.concatenate([join(g["L1_attn_u_w"].T, g["L1_attn_u_b"]), join(g["L1_attn_v_w"].T, g["L1_attn_v_b"])], axis=1),
        "o_aug": join(g["L1_attn_o_w"].T, g["L1_attn_o_b"]),
        "t_aug": join(g["L1_attn_t_w"].T, g["L1_attn_t_b"]),
        "pos_aug": join(g["L1_attn_pos_w"].T, g["L1_attn_pos_b"]),
        "rpe_aug": np.concatenate([g["L1_attn_rpe_lw"].transpose(2, 0, 1), g["L1_attn_rpe_lb"][None]], axis=0),
        "out_aug": join(g["L1_attn_out_w"].T, g["L1_attn_out_b"]),
        **transform_tables(),
        "rms1_w": g["L1_ffn_ln1_w"], "rms2_w": g["L1_ffn_ln2_w"],
        "rot_in": rotary_weights(g["L1_ffn_wq"], g["L1_ffn_wk"], g["L1_ffn_wv"]),
        "rot_out": g["L1_ffn_wo"].T.reshape(Q_HEADS, HD, D).transpose(1, 0, 2).reshape(HD, Q_HEADS * D),
        **rotary_tables(),
        "router": g["L1_ffn_router_w"].T,
        "moe_w1": g["L1_ffn_w1"].reshape(EXPERTS * HIDDEN, D).T, "moe_w3": g["L1_ffn_w3"].reshape(EXPERTS * HIDDEN, D).T,
        "moe_w2": g["L1_ffn_w2"].transpose(0, 2, 1).reshape(EXPERTS * HIDDEN, D),
        "s_qkv": join(g["L2_attn_w_in"].T, g["L2_attn_b_in"]),
        "s_g1": join(g["L2_attn_gate_w1"].T, g["L2_attn_gate_b1"]),
        "s_g2": join(g["L2_attn_gate_w2"].T, g["L2_attn_gate_b2"]),
        "s_out": join(g["L2_attn_w_out"].T, g["L2_attn_b_out"]),
        **tree_weights(g["L2_ffn_w1s"], g["L2_ffn_b1s"], g["L2_ffn_w2s"], g["L2_ffn_b2s"]),
        "sig_w": g["L3_attn_q_weight"],
        "m_gate": join(g["L3_ffn_gW"], g["L3_ffn_gb"]),
        "m_s1": join(g["L3_ffn_sW1"], g["L3_ffn_sb1"]), "m_s2": join(g["L3_ffn_sW2"], g["L3_ffn_sb2"]),
        "m_s3": g["L3_ffn_sW3"], "m_s3b": g["L3_ffn_sb3"].reshape(1, D),
        "m_e1": np.concatenate([g["L3_ffn_eW1"].transpose(1, 0, 2), g["L3_ffn_eb1"][None]], axis=0),
        "m_e2": g["L3_ffn_eW2"].transpose(1, 0, 2), "m_e2b": g["L3_ffn_eb2"].T,
        "m_e3": np.concatenate([g["L3_ffn_eW3"].transpose(1, 0, 2), g["L3_ffn_eb3"][None]], axis=0),
        "w_pk": g["L0_ffn_Wq_pk"], "w_q": g["L0_ffn_Wq"], "w_o": g["L0_ffn_Wo"],
        "pk_blocks": pk_blocks(g["L0_ffn_pk_keys"]),
        "table": np.concatenate([g["L0_ffn_keys_table"], g["L0_ffn_values_table"]], axis=1),
    }


def kernel(**inputs):
    import concourse.bacc as _bacc
    from concourse.bass_utils import run_bass_kernel_spmd as _run

    nc = _bacc.Bacc("TRN2", target_bir_lowering=False, num_devices=1)
    arrays = {f"in_{k}": np.ascontiguousarray(v) for k, v in lay_out(inputs).items()}
    I = {k[3:]: nc.dram_tensor(k, v.shape, mybir.dt.from_np(v.dtype), kind="ExternalInput").ap() for k, v in arrays.items()}
    out = nc.dram_tensor("out", (B, SEQ, D), F32, kind="ExternalOutput").ap()
    build(nc, I, out)
    return _run(nc, [arrays], core_ids=[0]).results[0]["out"]
```

```python
from contextlib import ExitStack

import numpy as np

import concourse.bass as bass
from concourse import mybir
from concourse.alu_op_type import AluOpType as ALU

F32 = mybir.dt.float32
U32 = mybir.dt.uint32
BF16 = mybir.dt.bfloat16
ACT = mybir.ActivationFunctionType
AX = mybir.AxisListType

P = 128
B = 4
PATCHES = 64
TEXT = 512
SEQ = PATCHES + TEXT
D = 64
CH = 5
PAD = CH * P
TAIL = SEQ - 4 * P
T = B * CH
COLS = T * P
BANK = 512
GROUPS = COLS // BANK
LN_EPS = 1e-5
NEG = -1e30


class Steps:

    def __init__(self, engine, semaphore):
        self.engine, self.semaphore, self.before, self.count = engine, semaphore, 0, 0

    def add(self, instruction):
        instruction.then_inc(self.semaphore, 1)
        self.count += 1

    def settle(self, apart=None):
        self.engine.wait_ge(self.semaphore, self.before + self.count)
        if apart is not None:
            wait_apart(self.engine, apart)

    def do(self, instruction):
        self.add(instruction)
        self.settle()

    def enter_loop(self, turn, per_turn):
        self.outside = self.before + self.count
        self.before, self.count, self.per_turn = turn * per_turn + self.outside, 0, per_turn

    def leave_loop(self, turns):
        assert self.count == self.per_turn, (self.count, self.per_turn)
        self.before, self.count = self.outside + turns * self.per_turn, 0


def wait_apart(engine, passed):
    engine.sem_inc(passed, 1)


class Stage:

    SPENT_MAX = 90
    spent = []

    def __init__(self, nc, name):
        self.nc, self.name, self.sems = nc, name, []

    def __enter__(self):
        self.stack = ExitStack()
        return self

    def __exit__(self, *problem):
        self.stack.close()
        Stage.spent += self.sems
        if not problem[0] and len(Stage.spent) >= self.SPENT_MAX:
            self.nc.clear_and_free_semaphores(Stage.spent)
            Stage.spent.clear()
            self.nc.all_engine_barrier()

    def sb(self, name, shape, dtype=F32):
        return self.stack.enter_context(self.nc.sbuf_tensor(f"{self.name}_{name}", shape, dtype))

    def sem(self, name):
        s = self.nc.alloc_semaphore(f"{self.name}_{name}")
        self.sems.append(s)
        return s


class Core:
    pass


START = 1


def start_loop(nc, semaphores):
    with nc.Block() as block:
        @block.sync
        def _(sp):
            for s in semaphores:
                sp.sem_inc(s, START)


def over(ap, n):
    return ap.unsqueeze(len(ap.shape)).to_broadcast([*ap.shape, n])


def rows_of(ap, n):
    return ap.unsqueeze(1).to_broadcast([ap.shape[0], n, *ap.shape[1:]])


def load_stage(nc, name, loads):
    with Stage(nc, name) as st:
        landed = st.sem("landed")
        with nc.Block() as block:
            @block.sync
            def _(sp):
                for to, of in loads:
                    sp.dma_start(to, of).then_inc(landed, 16)
                sp.wait_ge(landed, 16 * len(loads))


def embed_stage(nc, core, x_patches, txt, w_patch):
    with Stage(nc, "embed") as st:
        pixels = st.sb("pixels", [D + 1, B * PATCHES])
        weights = st.sb("weights", [D + 1, D])
        ones_set, landed, products, text_landed, copied = (
            st.sem(n) for n in ("ones_set", "landed", "products", "text_landed", "copied"))
        h_b = core.h[:, :, :].rearrange("p (b c) d -> p b c d", c=CH)
        with nc.Block() as block:
            @block.sync
            def _(sp):
                sp.wait_ge(ones_set, 2)
                sp.dma_start(pixels[0:D, :], x_patches).then_inc(landed, 16)
                sp.dma_start(weights[:, :], w_patch).then_inc(landed, 16)
                for b in range(B):
                    sp.dma_start(h_b[PATCHES:P, b, 0, :], txt[b, 0:P - PATCHES, :]).then_inc(text_landed, 16)
                    sp.dma_start(h_b[:, b, 1:CH - 1, :],
                                 txt[b, P - PATCHES:TEXT - TAIL, :].rearrange("(c p) d -> p c d", p=P)
                                 ).then_inc(text_landed, 16)
                    sp.dma_start(h_b[0:TAIL, b, CH - 1, :], txt[b, TEXT - TAIL:TEXT, :]).then_inc(text_landed, 16)
                sp.wait_ge(text_landed, 16 * 3 * B)

            @block.gpsimd
            def _(pool):
                nc.gpsimd.memset(pixels[:, :], 1.0).then_inc(ones_set, 1)
                nc.gpsimd.memset(core.h[:, :, :], 0.0).then_inc(ones_set, 1)
                nc.gpsimd.memset(core.xnT[:, :], 1.0).then_inc(ones_set, 1)
                nc.gpsimd.memset(core.ident[:, :], 0.0).then_inc(ones_set, 1)
                pool.wait_ge(ones_set, 4)
                nc.gpsimd.affine_select(out=core.ident[:, :], in_=core.ident[:, :], compare_op=ALU.not_equal,
                                        fill=1.0, base=0, pattern=[[-1, P]], channel_multiplier=1)

            @block.tensor
            def _(pe):
                pe.wait_ge(landed, 32)
                for b in range(B):
                    last = nc.tensor.matmul(core.psum[0:PATCHES, 0, b * D:(b + 1) * D],
                                            pixels[:, b * PATCHES:(b + 1) * PATCHES], weights[:, :],
                                            start=True, stop=True)
                last.then_inc(products, 1)

            @block.vector
            def _(dve):
                dve.wait_ge(products, 1)
                dve.wait_ge(ones_set, 4)
                nc.vector.tensor_copy(h_b[0:PATCHES, :, 0, :],
                                      core.psum[0:PATCHES, 0, 0:B * D].rearrange("p (b d) -> p b d", d=D)
                                      ).then_inc(copied, 1)


def norm_steps(nc, steps, dve, x, out, sq, stat, std_ready, var_ready, eps, use_mean=True, by=None):
    width = x.shape[-1]
    if use_mean:
        steps.do(nc.vector.tensor_reduce(stat[:, 0, :], x, AX.X, ALU.add))
        steps.do(nc.vector.tensor_scalar(stat[:, 0, :], stat[:, 0, :], 1.0 / width, None, ALU.mult))
        steps.do(nc.vector.tensor_tensor(out, x, over(stat[:, 0, :], width), ALU.subtract))
        x = out
    steps.do(nc.vector.tensor_tensor(sq, x, x, ALU.mult))
    steps.do(nc.vector.tensor_reduce(stat[:, 1, :], sq, AX.X, ALU.add))
    nc.vector.tensor_scalar(stat[:, 1, :], stat[:, 1, :], 1.0 / width, eps, ALU.mult, ALU.add).then_inc(var_ready, 1)
    dve.wait_ge(std_ready, 1)
    steps.do(nc.vector.reciprocal(stat[:, 3, :], stat[:, 2, :]))
    steps.do(nc.vector.tensor_tensor(out, x, over(stat[:, 3, :], width), ALU.mult))


def norm_stage(nc, core, name, src, eps=LN_EPS, use_mean=True, gain=None, shift=None, first=None,
               dst=None, turn=True):
    dst = core.xn if dst is None else dst
    with Stage(nc, name) as st:
        sq = st.sb("sq", [P, T, D])
        stat = st.sb("stat", [P, 4, T])
        stat2 = st.sb("stat2", [P, 4, T])
        rows = st.sb("rows", [P, 2, D])
        vec, var, std, var2, std2, ready, turned, drained, landed = (
            st.sem(n) for n in ("vector_steps", "var_ready", "std_ready", "var2_ready", "std2_ready",
                                "dst_ready", "turned", "drained", "rows_landed"))
        vecs = [v for v in (gain, shift) if v is not None]
        with nc.Block() as block:
            @block.sync
            def _(sp):
                for k, v in enumerate(vecs):
                    sp.dma_start(rows[:, k, :], v.partition_broadcast(P)).then_inc(landed, 16)

            @block.vector
            def _(dve):
                steps = Steps(dve, vec)
                if first is None:
                    norm_steps(nc, steps, dve, src[:, :, :], dst[:, :, :], sq[:, :, :], stat, std, var, eps, use_mean)
                else:
                    norm_steps(nc, steps, dve, src[:, :, :], first[:, :, :], sq[:, :, :], stat, std, var, LN_EPS)
                    norm_steps(nc, steps, dve, first[:, :, :], dst[:, :, :], sq[:, :, :], stat2, std2, var2, eps, use_mean)
                if vecs:
                    dve.wait_ge(landed, 16 * len(vecs))
                    steps.do(nc.vector.tensor_tensor(dst[:, :, :], dst[:, :, :], rows_of(rows[:, 0, :], T), ALU.mult))
                    if shift is not None:
                        steps.do(nc.vector.tensor_tensor(dst[:, :, :], dst[:, :, :], rows_of(rows[:, 1, :], T), ALU.add))
                dve.sem_inc(ready, 1)

            @block.scalar
            def _(act):
                act.wait_ge(var, 1)
                nc.scalar.activation(stat[:, 2, :], stat[:, 1, :], ACT.Sqrt).then_inc(std, 1)
                if first is not None:
                    act.wait_ge(var2, 1)
                    nc.scalar.activation(stat2[:, 2, :], stat2[:, 1, :], ACT.Sqrt).then_inc(std2, 1)
                if turn:
                    for g in range(GROUPS):
                        act.wait_ge(turned, g + 1)
                        nc.scalar.activation(core.xnT[0:D, g * BANK:(g + 1) * BANK], core.psum[0:D, g, :],
                                             ACT.Copy).then_inc(drained, 1)

            @block.tensor
            def _(pe):
                if turn:
                    pe.wait_ge(ready, 1)
                    for t in range(T):
                        last = nc.tensor.transpose(core.psum[0:D, t // 4, t % 4 * P:(t % 4 + 1) * P],
                                                   dst[:, t, :], core.ident[:, :])
                        if t % 4 == 3:
                            last.then_inc(turned, 1)


def turn_stage(nc, core, name, jobs):
    with Stage(nc, name) as st:
        turned, by_scalar, by_vector = st.sem("turned"), st.sem("drained_scalar"), st.sem("drained_vector")
        banks = [(job, g) for job in jobs for g in range(GROUPS)]
        with nc.Block() as block:
            @block.tensor
            def _(pe):
                for n, ((_, width, src), g) in enumerate(banks):
                    if n >= 8:
                        pe.wait_ge(by_vector if n % 2 else by_scalar, (n - 8) // 2 + 1)
                    for k in range(4):
                        last = nc.tensor.transpose(core.psum[0:width, n % 8, k * P:(k + 1) * P],
                                                   src(4 * g + k), core.ident[:, :])
                    last.then_inc(turned, 1)

            @block.scalar
            def _(act):
                for n, ((dst, width, _), g) in enumerate(banks):
                    if n % 2 == 0:
                        act.wait_ge(turned, n + 1)
                        nc.scalar.activation(dst[0:width, g * BANK:(g + 1) * BANK], core.psum[0:width, n % 8, :],
                                             ACT.Copy).then_inc(by_scalar, 1)

            @block.vector
            def _(dve):
                for n, ((dst, width, _), g) in enumerate(banks):
                    if n % 2 == 1:
                        dve.wait_ge(turned, n + 1)
                        nc.vector.tensor_copy(dst[0:width, g * BANK:(g + 1) * BANK], core.psum[0:width, n % 8, :]
                                              ).then_inc(by_vector, 1)


def product_stage(nc, core, name, terms, width, use, engine="vector", tiles=T):
    per = min(BANK // width, 8)
    batches = [(t0, min(t0 + per, tiles)) for t0 in range(0, tiles, per)]
    with Stage(nc, name) as st:
        made, used = st.sem("made"), st.sem("used")
        with nc.Block() as block:
            @block.tensor
            def _(pe):
                for n, (t0, t1) in enumerate(batches):
                    if n >= 8:
                        pe.wait_ge(used, n - 7)
                    for t in range(t0, t1):
                        for k, (lhsT_of, rhs) in enumerate(terms):
                            last = nc.tensor.matmul(core.psum[:, n % 8, (t - t0) * width:(t - t0 + 1) * width],
                                                    lhsT_of(t), rhs, start=(k == 0), stop=(k == len(terms) - 1))
                    last.then_inc(made, 1)

            def take(eng):
                for n, (t0, t1) in enumerate(batches):
                    eng.wait_ge(made, n + 1)
                    view = core.psum[:, n % 8, 0:(t1 - t0) * width].rearrange("p (t w) -> p t w", w=width)
                    use(t0, t1, view).then_inc(used, 1)

            (block.vector if engine == "vector" else block.scalar)(take)


def wide_product_stage(nc, core, name, outputs, use, engine="scalar"):
    jobs = [(g, o) for g in range(GROUPS) for o in range(len(outputs))]
    with Stage(nc, name) as st:
        made, used = st.sem("made"), st.sem("used")
        with nc.Block() as block:
            @block.tensor
            def _(pe):
                for n, (g, o) in enumerate(jobs):
                    if n >= 8:
                        pe.wait_ge(used, n - 7)
                    rows, terms = outputs[o]
                    for k, (lhsT, rhs) in enumerate(terms):
                        last = nc.tensor.matmul(core.psum[0:rows, n % 8, :], lhsT, rhs(g * BANK, (g + 1) * BANK),
                                                start=(k == 0), stop=(k == len(terms) - 1))
                    last.then_inc(made, 1)

            def take(eng):
                for n, (g, o) in enumerate(jobs):
                    eng.wait_ge(made, n + 1)
                    use(g * BANK, (g + 1) * BANK, o, core.psum[0:outputs[o][0], n % 8, :]).then_inc(used, 1)

            (block.vector if engine == "vector" else block.scalar)(take)



def split_tokens_stage(nc, name, x, s12, s13):
    with Stage(nc, name) as st:
        part1 = st.sb("part1", [P, x.shape[1]], BF16)
        part2 = st.sb("part2", [P, x.shape[1]], BF16)
        cast, less = st.sem("cast"), st.sem("less")
        with nc.Block() as block:
            @block.scalar
            def _(act):
                nc.scalar.activation(part1[:, :], x, ACT.Copy).then_inc(cast, 1)
                act.wait_ge(less, 1)
                nc.scalar.activation(part2[:, :], x, ACT.Copy).then_inc(cast, 1)
                nc.scalar.activation(s12[0:D, :], part1[0:D, :], ACT.Copy)
                nc.scalar.activation(s13[0:D, :], part1[0:D, :], ACT.Copy)
                act.wait_ge(cast, 2)
                nc.scalar.activation(s12[D:P, :], part2[D:P, :], ACT.Copy)

            @block.vector
            def _(dve):
                dve.wait_ge(cast, 1)
                nc.vector.tensor_tensor(x, x, part1[:, :], ALU.subtract).then_inc(less, 1)
                dve.wait_ge(cast, 2)
                dve.wait_ge(less, 1)
                nc.vector.tensor_tensor(s13[D:P, :], x[D:P, :], part2[D:P, :], ALU.subtract)


def split_weights_stage(nc, name, source, s11, s22, s31, chunk):
    pieces = source.shape[1] // chunk
    with Stage(nc, name) as st:
        x = st.sb("x", [P, 2, chunk])
        landed = [st.sem(f"landed{b}") for b in range(2)]
        first, less, second, third = (st.sem(n) for n in ("first", "less", "second", "third"))
        with nc.Block() as block:
            @block.sync
            def _(sp):
                for i in range(pieces):
                    if i >= 2:
                        sp.wait_ge(third, i - 1)
                        sp.wait_ge(second, i - 1)
                    for half in range(2):
                        sp.dma_start(x[half * D:(half + 1) * D, i % 2, :], source[:, i * chunk:(i + 1) * chunk]
                                     ).then_inc(landed[i % 2], 16)

            @block.scalar
            def _(act):
                def second_part(i):
                    at = slice(i * chunk, (i + 1) * chunk)
                    act.wait_ge(less, i + 1)
                    nc.scalar.activation(s22[:, at], x[:, i % 2, :], ACT.Copy).then_inc(second, 1)

                for i in range(pieces):
                    at = slice(i * chunk, (i + 1) * chunk)
                    act.wait_ge(landed[i % 2], 32 * (i // 2 + 1))
                    nc.scalar.activation(s11[:, at], x[:, i % 2, :], ACT.Copy).then_inc(first, 1)
                    if i >= 1:
                        second_part(i - 1)
                    act.wait_ge(first, i + 1)
                    nc.scalar.activation(s31[D:P, at], s11[D:P, at], ACT.Copy)
                second_part(pieces - 1)

            @block.vector
            def _(dve):
                def third_part(i):
                    at = slice(i * chunk, (i + 1) * chunk)
                    dve.wait_ge(second, i + 1)
                    dve.wait_ge(less, i + 1)
                    nc.vector.tensor_tensor(s31[0:D, at], x[0:D, i % 2, :], s22[0:D, at], ALU.subtract).then_inc(third, 1)

                for i in range(pieces):
                    dve.wait_ge(first, i + 1)
                    nc.vector.tensor_tensor(x[:, i % 2, :], x[:, i % 2, :], s11[:, i * chunk:(i + 1) * chunk], ALU.subtract
                                            ).then_inc(less, 1)
                    if i >= 1:
                        third_part(i - 1)
                third_part(pieces - 1)


def add_stage(nc, core, name, *sums):
    with Stage(nc, name) as st:
        vec = st.sem("vector_steps")
        with nc.Block() as block:
            @block.vector
            def _(dve):
                steps = Steps(dve, vec)
                for out, a, b in sums:
                    steps.do(nc.vector.tensor_tensor(out, a, b, ALU.add))


def linear_attention_stage(nc, core, I):
    with Stage(nc, "lin") as st:
        w_qkv = st.sb("w_qkv", [D + 1, 3 * D])
        qkv = st.sb("qkv", [P, T, 3 * D + 1])
        qk, v1 = qkv[:, :, 0:2 * D], qkv[:, :, 2 * D:3 * D + 1]
        sq = st.sb("sq", [P, T, 2 * D])
        stat = st.sb("stat", [P, 3, 2 * T])
        qT = st.sb("qT", [D, COLS])
        kT = st.sb("kT", [D, COLS])
        upper = st.sb("upper", [P, P])
        scores = st.sb("scores", [P, 2, CH, PAD])
        attn = st.sb("attn", [P, T, D])
        den = st.sb("den", [P, T])
        load_stage(nc, "lin_load", [(w_qkv[:, :], I["qkv_aug"])])
        projected, copied, copied_v, vec, act_steps, norm_ready, root_ready, feats, turned, drained, consts = (
            st.sem(n) for n in ("projected", "copied", "copied_by_vector", "vector_steps", "scalar_steps", "norm_ready",
                                "root_ready", "features_ready", "turned", "drained", "consts"))
        ps = core.psum
        with nc.Block() as block:
            @block.gpsimd
            def _(pool):
                nc.gpsimd.memset(qkv[:, :, 3 * D:3 * D + 1], 1.0).then_inc(consts, 1)
                nc.gpsimd.memset(upper[:, :], 1.0).then_inc(consts, 1)
                pool.wait_ge(consts, 2)
                nc.gpsimd.affine_select(out=upper[:, :], in_=upper[:, :], compare_op=ALU.is_ge, fill=0.0,
                                        base=0, pattern=[[1, P]], channel_multiplier=-1)

            @block.tensor
            def _(pe):
                for t in range(T):
                    if t >= 8:
                        pe.wait_ge(copied_v if t % 2 else copied, (t - 8) // 2 + 1)
                    nc.tensor.matmul(ps[:, t % 8, 0:3 * D], core.xnT[:, t * P:(t + 1) * P], w_qkv[:, :],
                                     start=True, stop=True).then_inc(projected, 1)
                pe.wait_ge(feats, 1)
                for part in range(2):
                    for t in range(T):
                        g = part * GROUPS + t // 4
                        if t % 4 == 0 and g >= 8:
                            pe.wait_ge(drained, g - 7)
                        last = nc.tensor.transpose(ps[0:D, g % 8, t % 4 * P:(t % 4 + 1) * P],
                                                   qk[:, t, part * D:(part + 1) * D], core.ident[:, :])
                        if t % 4 == 3:
                            last.then_inc(turned, 1)

            @block.scalar
            def _(act):
                steps = Steps(act, act_steps)
                for t in range(0, T, 2):
                    act.wait_ge(projected, t + 1)
                    nc.scalar.activation(qkv[:, t, 0:3 * D], ps[:, t % 8, 0:3 * D], ACT.Copy).then_inc(copied, 1)
                act.wait_ge(norm_ready, 1)
                nc.scalar.activation(stat[:, 1, :], stat[:, 0, :], ACT.Sqrt).then_inc(root_ready, 1)
                act.wait_ge(norm_ready, 2)
                steps.do(nc.scalar.activation(qk[:, :, :], qk[:, :, :], ACT.Exp))
                nc.scalar.activation(qk[:, :, :], qk[:, :, :], ACT.Ln, bias=1.0).then_inc(root_ready, 1)
                for g in range(2 * GROUPS):
                    act.wait_ge(turned, g + 1)
                    to = (qT if g < GROUPS else kT)[:, g % GROUPS * BANK:(g % GROUPS + 1) * BANK]
                    nc.scalar.activation(to, ps[0:D, g % 8, :], ACT.Copy).then_inc(drained, 1)

            @block.vector
            def _(dve):
                steps = Steps(dve, vec)
                for t in range(1, T, 2):
                    dve.wait_ge(projected, t + 1)
                    nc.vector.tensor_copy(qkv[:, t, 0:3 * D], ps[:, t % 8, 0:3 * D]).then_inc(copied_v, 1)
                dve.wait_ge(copied, T // 2)
                dve.wait_ge(copied_v, T // 2)
                steps.do(nc.vector.tensor_tensor(sq[:, :, :], qk[:, :, :], qk[:, :, :], ALU.mult))
                nc.vector.tensor_reduce(stat[:, 0, :], sq[:, :, :].rearrange("p t (s d) -> p (t s) d", s=2),
                                        AX.X, ALU.add).then_inc(norm_ready, 1)
                dve.wait_ge(root_ready, 1)
                steps.do(nc.vector.tensor_scalar(stat[:, 1, :], stat[:, 1, :], 0.125, 1e-12, ALU.mult, ALU.max))
                steps.do(nc.vector.reciprocal(stat[:, 2, :], stat[:, 1, :]))
                steps.do(nc.vector.tensor_scalar(stat[:, 2, :], stat[:, 2, :], 0.125, None, ALU.mult))
                view = qk.rearrange("p t (s d) -> p t s d", s=2)
                scale = stat[:, 2, :].rearrange("p (t s) -> p t s", s=2)
                nc.vector.tensor_tensor(view, view, over(scale, D), ALU.mult).then_inc(norm_ready, 1)
                dve.wait_ge(root_ready, 2)
                nc.vector.tensor_scalar(qk[:, :, :], qk[:, :, :], 1e-6, None, ALU.add).then_inc(feats, 1)

        scored, scored_rest, kept, kept_rest, weighed, divided = (
            st.sem(n) for n in ("scored_diagonal", "scored_rest", "kept_diagonal", "kept_rest", "weighed", "divided"))
        with nc.Block() as block:
            @block.tensor
            def _(pe):
                n = rest = 0
                for b in range(B):
                    for c in range(CH):
                        keys = kT[:, b * PAD + c * P:b * PAD + (c + 1) * P]
                        if n >= 2:
                            pe.wait_ge(kept, n - 1)
                        nc.tensor.matmul(ps[:, n % 2, 0:P], keys, qT[:, b * PAD + c * P:b * PAD + (c + 1) * P],
                                         start=True, stop=True).then_inc(scored, 1)
                        n += 1
                        if c < CH - 1:
                            if rest >= 2:
                                pe.wait_ge(kept_rest, rest - 1)
                            nc.tensor.matmul(ps[:, 2 + rest % 2, 0:PAD - (c + 1) * P], keys,
                                             qT[:, b * PAD + (c + 1) * P:(b + 1) * PAD],
                                             start=True, stop=True).then_inc(scored_rest, 1)
                            rest += 1
                    pe.wait_ge(kept, n)
                    pe.wait_ge(kept_rest, rest)
                    if b >= 1:
                        pe.wait_ge(divided, 2 * b)
                    for c in range(CH):
                        for m in range(c + 1):
                            rows = TAIL if m == CH - 1 else P
                            last = nc.tensor.matmul(ps[:, 6, c * (D + 1):(c + 1) * (D + 1)],
                                                    scores[0:rows, b % 2, m, c * P:(c + 1) * P],
                                                    v1[0:rows, b * CH + m, :], start=(m == 0), stop=(m == c))
                    last.then_inc(weighed, 1)

            @block.scalar
            def _(act):
                for b in range(B):
                    if b >= 2:
                        act.wait_ge(weighed, b - 1)
                    for c in range(CH - 1):
                        rest = b * (CH - 1) + c
                        act.wait_ge(scored_rest, rest + 1)
                        nc.scalar.activation(scores[:, b % 2, c, (c + 1) * P:PAD],
                                             ps[:, 2 + rest % 2, 0:PAD - (c + 1) * P], ACT.Copy
                                             ).then_inc(kept_rest, 1)

            @block.vector
            def _(dve):
                for b in range(B):
                    for c in range(CH):
                        n = b * CH + c
                        dve.wait_ge(scored, n + 1)
                        if b >= 2:
                            dve.wait_ge(weighed, b - 1)
                        nc.vector.tensor_tensor(scores[:, b % 2, c, c * P:(c + 1) * P], ps[:, n % 2, 0:P],
                                                upper[:, :], ALU.mult).then_inc(kept, 1)
                    dve.wait_ge(weighed, b + 1)
                    out = ps[:, 6, 0:CH * (D + 1)].rearrange("p (c e) -> p c e", e=D + 1)
                    nc.vector.tensor_scalar(attn[:, b * CH:(b + 1) * CH, :], out[:, :, 0:D], 1e4, -1e4, ALU.min, ALU.max
                                            ).then_inc(divided, 1)
                    nc.vector.tensor_scalar(den[:, b * CH:(b + 1) * CH], out[:, :, D], 1e-6, None, ALU.max
                                            ).then_inc(divided, 1)
                dve.wait_ge(divided, 2 * B)
                nc.vector.reciprocal(den[:, :], den[:, :]).then_inc(divided, 1)
                dve.wait_ge(divided, 2 * B + 1)
                nc.vector.tensor_tensor(attn[:, :, :], attn[:, :, :], over(den[:, :], D), ALU.mult)

        aT = st.sb("aT", [D + 1, COLS])
        w_proj = st.sb("w_proj", [D + 1, D])
        set_stage(nc, "lin_one", [(aT[:, :], 1.0)])
        load_stage(nc, "proj_load", [(w_proj[:, :], I["proj_aug"])])
        turn_stage(nc, core, "lin_turn", [(aT, D, lambda t: attn[:, t, :])])
        product_stage(nc, core, "lin_proj", [(lambda t: aT[:, t * P:(t + 1) * P], w_proj[:, :])], D,
                      lambda t0, t1, made: nc.vector.tensor_tensor(core.xn[:, t0:t1, :], core.xn[:, t0:t1, :], made, ALU.add))
    norm_stage(nc, core, "lin_ln1", core.xn, gain=I["ln1_g"], shift=I["ln1_b"])
    with Stage(nc, "gelu") as st:
        w1 = st.sb("w1", [D + 1, 4 * D])
        w2 = st.sb("w2", [P, 2, D])
        b2 = st.sb("b2", [1, D])
        hT = st.sb("hT", [P, 2, COLS])
        load_stage(nc, "gelu_load", [(w1[:, :], I["w1_aug"]), (w2[:, :, :], I["w2"].rearrange("(k p) d -> p k d", p=P)), (b2[:, :], I["b2"].unsqueeze(0))])
        wide_product_stage(nc, core, "gelu_up", [(P, [(w1[:, k * P:(k + 1) * P], lambda c0, c1: core.xnT[:, c0:c1])])
                                                 for k in range(2)],
                           lambda c0, c1, k, made: nc.scalar.activation(hT[:, k, c0:c1], made, ACT.Gelu))
        product_stage(nc, core, "gelu_down",
                      [(lambda t: hT[:, 0, t * P:(t + 1) * P], w2[:, 0, :]),
                       (lambda t: hT[:, 1, t * P:(t + 1) * P], w2[:, 1, :]),
                       (lambda t: core.ones[0:1, :], b2[:, :])], D,
                      lambda t0, t1, made: nc.vector.tensor_tensor(core.xn[:, t0:t1, :], core.xn[:, t0:t1, :], made, ALU.add))
    norm_stage(nc, core, "lin_ln2", core.xn, gain=I["ln2_g"], shift=I["ln2_b"], turn=False)
    add_stage(nc, core, "lin_residual", (core.h[:, :, :], core.h[:, :, :], core.xn[:, :, :]))


def set_stage(nc, name, fills):
    with nc.Block() as block:
        @block.gpsimd
        def _(pool):
            for ap, value in fills:
                nc.gpsimd.memset(ap, value)


class CausalAttention:

    BEGIN = 6
    SCORE_BANK = (2, 3, 2, 3, 4)
    TURN_BANK = (6, 7, 6, 7, 6)

    def __init__(self, nc, core, st, d, scale, fetches=(2, 1)):
        self.nc, self.core, self.d, self.scale, self.fetches = nc, core, d, scale, fetches
        self.width = [P * (c + 1) for c in range(CH - 1)] + [SEQ]
        self.rows = [P] * (CH - 1) + [TAIL]
        self.prob_at = [sum(self.width[:c]) for c in range(CH)]
        self.pT_at = [0, 3 * P, 0, 3 * P, 7 * P]
        self.k_at = max(d, 32)
        self.qk1 = st.sb("qk1", [P, 2, CH, self.k_at + d])
        self.v1 = st.sb("v1", [P, 2, CH, d])
        self.qT, self.kT = st.sb("qT", [d, 2, SEQ]), st.sb("kT", [d, 2, SEQ])
        self.mask = st.sb("mask", [P, 2 * PAD - P])
        self.probs = st.sb("probs", [P, sum(self.width)])
        self.pT = st.sb("pT", [P, 7 * P + CH * TAIL])
        self.stat = st.sb("stat", [P, 2, CH, 4])
        self.fetched = [st.sem(f"head_fetched{u}") for u in range(2)]
        self.v_fetched = [st.sem(f"head_v_fetched{u}") for u in range(2)]
        names = ("turned", "qk_copied", "scored", "peaked", "exped", "p_turned", "p_copied",
                 "weighed", "normed", "masked")
        (self.turned, self.qk_copied, self.scored, self.peaked, self.exped,
         self.p_turned, self.p_copied, self.weighed, self.normed, self.own) = self.semaphores = [st.sem(f"head_{x}") for x in names]
        self.passed_pe, self.passed_dve = st.sem("passed_by_tensor"), st.sem("passed_by_vector")
        self.set = st.sem("mask_set")

    def begin(self):
        nc, mask = self.nc, self.mask
        with nc.Block() as block:
            @block.sync
            def _(sp):
                for s in self.semaphores:
                    sp.sem_inc(s, self.BEGIN)

            @block.gpsimd
            def _(pool):
                nc.gpsimd.memset(mask[:, :], 0.0).then_inc(self.set, 1)
                nc.gpsimd.memset(self.qk1[:, :, :, :], 0.0)
                pool.wait_ge(self.set, 1)
                nc.gpsimd.affine_select(out=mask[:, :], in_=mask[:, :], compare_op=ALU.is_ge, fill=NEG,
                                        base=PAD - P, pattern=[[-1, 2 * PAD - P]], channel_multiplier=1)

    def act_fetch(self, act, n, u, q, k, v):
        nc, d = self.nc, self.d
        act.wait_ge(self.turned, self.BEGIN + 2 * n - 2)
        nc.scalar.activation(self.qk1[:, u, :, 0:d], q, ACT.Copy).then_inc(self.fetched[u], 1)
        nc.scalar.activation(self.qk1[:, u, :, self.k_at:self.k_at + d], k, ACT.Copy).then_inc(self.fetched[u], 1)
        act.wait_ge(self.weighed, self.BEGIN + CH * n - CH)
        nc.scalar.activation(self.v1[:, u, :, :], v, ACT.Copy).then_inc(self.v_fetched[u], 1)

    def pe_turn(self, pe, m, u, tail):
        nc, ps = self.nc, self.core.psum
        rows, n = self.k_at + self.d, 2 * m + u
        pe.wait_ge(self.fetched[u], self.fetches[0] * (m + 1))
        pe.wait_ge(self.qk_copied, self.BEGIN + 4 * n + (2 if tail else 0))
        wait_apart(pe, self.passed_pe)
        if tail:
            last = nc.tensor.transpose(ps[0:rows, 0, 0:TAIL], self.qk1[0:TAIL, u, CH - 1, :], self.core.ident[0:TAIL, 0:TAIL])
        else:
            for c in range(CH - 1):
                last = nc.tensor.transpose(ps[0:rows, 0, c * P:(c + 1) * P], self.qk1[:, u, c, :], self.core.ident[:, :])
        last.then_inc(self.turned, 1)

    def dve_turn(self, dve, n, u, tail):
        nc, ps = self.nc, self.core.psum
        lo, hi = (BANK, SEQ) if tail else (0, BANK)
        dve.wait_ge(self.turned, self.BEGIN + 2 * n + (2 if tail else 1))
        for to, at in ((self.qT, 0), (self.kT, self.k_at)):
            nc.vector.tensor_copy(to[:, u, lo:hi], ps[at:at + self.d, 0, 0:hi - lo]).then_inc(self.qk_copied, 1)

    def pe_score(self, pe, n, u, c):
        nc, ps, w, r = self.nc, self.core.psum, self.width[c], self.rows[c]
        if c == 0:
            pe.wait_ge(self.qk_copied, self.BEGIN + 4 * n + 4)
        pe.wait_ge(self.peaked, self.BEGIN + CH * n + (-2, -1, 1, 2, 0)[c])
        wait_apart(pe, self.passed_pe)
        bank, q = self.SCORE_BANK[c], self.qT[:, u, c * P:c * P + r]
        last = nc.tensor.matmul(ps[0:r, bank, 0:min(w, BANK)], q, self.kT[:, u, 0:min(w, BANK)], start=True, stop=True)
        if w > BANK:
            last = nc.tensor.matmul(ps[0:r, bank + 1, 0:w - BANK], q, self.kT[:, u, BANK:w], start=True, stop=True)
        last.then_inc(self.scored, 1)

    def pe_turn_probs(self, pe, n, c):
        nc, ps = self.nc, self.core.psum
        pe.wait_ge(self.exped, self.BEGIN + CH * n + c + 1)
        pe.wait_ge(self.p_copied, self.BEGIN + CH * n + (0, 0, 1, 2, 3)[c])
        wait_apart(pe, self.passed_pe)
        r = self.rows[c]
        for m in range(c + 1):
            last = nc.tensor.transpose(ps[0:self.rows[m], self.TURN_BANK[c], m * r:(m + 1) * r],
                                       self.probs[0:r, self.prob_at[c] + m * P:self.prob_at[c] + m * P + self.rows[m]], self.core.ident[0:r, 0:r])
        last.then_inc(self.p_turned, 1)

    def pe_weigh(self, pe, m, u, c):
        nc, ps, d, r, n = self.nc, self.core.psum, self.d, self.rows[c], 2 * m + u
        if c == 0:
            pe.wait_ge(self.v_fetched[u], self.fetches[1] * (m + 1))
        pe.wait_ge(self.p_copied, self.BEGIN + CH * n + c + 1)
        pe.wait_ge(self.normed, self.BEGIN + CH * n + c)
        wait_apart(pe, self.passed_pe)
        for m in range(c + 1):
            k = self.rows[m]
            last = nc.tensor.matmul(ps[0:r, 1, c * d:(c + 1) * d], self.pT[0:k, self.pT_at[c] + m * r:self.pT_at[c] + (m + 1) * r], self.v1[0:k, u, m, :],
                                    start=(m == 0), stop=(m == c))
        last.then_inc(self.weighed, 1)

    def pe_start(self, pe, m, u):
        for tail in (False, True):
            self.pe_turn(pe, m, u, tail)
        self.pe_score(pe, 2 * m + u, u, 0)
        self.pe_score(pe, 2 * m + u, u, 1)

    def pe_head(self, pe, m, u, more):
        n = 2 * m + u
        for c in range(CH):
            if c + 2 < CH:
                self.pe_score(pe, n, u, c + 2)
            if more and c in (1, 2):
                self.pe_turn(pe, m + u, 1 - u, c == 2)
            if more and c == 3:
                self.pe_score(pe, n + 1, 1 - u, 0)
            self.pe_turn_probs(pe, n, c)
            if c >= 1:
                self.pe_weigh(pe, m, u, c - 1)
        if more:
            self.pe_score(pe, n + 1, 1 - u, 1)
        self.pe_weigh(pe, m, u, CH - 1)

    def act_head(self, act, n, u, more, following=None):
        nc, ps, stat = self.nc, self.core.psum, self.stat

        def copy(c):
            act.wait_ge(self.p_turned, self.BEGIN + CH * n + c + 1)
            act.wait_ge(self.weighed, self.BEGIN + CH * n + (-2, -1, 1, 2, 0)[c])
            r, bank = self.rows[c], self.TURN_BANK[c]
            full = min(c + 1, CH - 1)
            at = self.pT_at[c]
            last = nc.scalar.activation(self.pT[:, at:at + full * r], ps[:, bank, 0:full * r], ACT.Copy)
            if full < c + 1:
                last.then_inc(self.own, 1)
                last = nc.scalar.activation(self.pT[0:TAIL, at + c * r:at + (c + 1) * r], ps[0:TAIL, bank, c * r:(c + 1) * r], ACT.Copy)
                act.wait_ge(self.own, self.BEGIN + n + 1)
            last.then_inc(self.p_copied, 1)

        for c in range(CH):
            r, w = self.rows[c], self.width[c]
            act.wait_ge(self.peaked, self.BEGIN + CH * n + c + 1)
            nc.scalar.activation(self.probs[0:r, self.prob_at[c]:self.prob_at[c] + w], self.probs[0:r, self.prob_at[c]:self.prob_at[c] + w], ACT.Exp, bias=stat[0:r, u, c, 1:2],
                                 scale=self.scale, accum_out=stat[0:r, u, c, 2:3]).then_inc(self.exped, 1)
            if more and c == 0:
                self.act_fetch(act, n + 1, 1 - u, *following)
            if c >= 1:
                copy(c - 1)
        copy(CH - 1)

    def dve_norm(self, dve, steps, n, u, c, out_of):
        nc, ps, d, r = self.nc, self.core.psum, self.d, self.rows[c]
        dve.wait_ge(self.weighed, self.BEGIN + CH * n + c + 1)
        steps.do(nc.vector.reciprocal(self.stat[0:r, u, c, 3:4], self.stat[0:r, u, c, 2:3]))
        nc.vector.tensor_scalar(out_of(c, r), ps[0:r, 1, c * d:(c + 1) * d].unsqueeze(1),
                                self.stat[0:r, u, c, 3:4], None, ALU.mult).then_inc(self.normed, 1)

    STEPS = 2 * CH

    def dve_start(self, dve, n, u):
        for tail in (False, True):
            self.dve_turn(dve, n, u, tail)

    def dve_head(self, dve, steps, n, u, more, carry, out_of, out_before=None):
        nc, ps, stat = self.nc, self.core.psum, self.stat
        flat = ps[:, :, :].rearrange("p b n -> p (b n)")
        for c in range(CH):
            r, w, at = self.rows[c], self.width[c], self.SCORE_BANK[c] * BANK
            dve.wait_ge(self.scored, self.BEGIN + CH * n + c + 1)
            dve.wait_ge(self.p_turned, self.BEGIN + CH * n + c - CH + 1)
            wait_apart(dve, self.passed_dve)
            steps.do(nc.vector.tensor_tensor_reduce(
                self.probs[0:r, self.prob_at[c]:self.prob_at[c] + w], flat[0:r, at:at + w], self.mask[0:r, PAD - P - c * P:PAD - P - c * P + w],
                1.0, -3e38, ALU.add, ALU.max, stat[0:r, u, c, 0:1]))
            nc.vector.tensor_scalar(stat[0:r, u, c, 1:2], stat[0:r, u, c, 0:1], -self.scale, None, ALU.mult
                                    ).then_inc(self.peaked, 1)
            if c >= 2:
                self.dve_norm(dve, steps, n, u, c - 2, out_of)
            elif carry:
                self.dve_norm(dve, steps, n - 1, 1 - u, CH - 2 + c, out_before)
            if more and c in (1, 2):
                self.dve_turn(dve, n + 1, 1 - u, c == 2)
        if not more:
            for c in (CH - 2, CH - 1):
                self.dve_norm(dve, steps, n, u, c, out_of)


def causal_attention_stage(nc, core, name, sources, out, heads, d, scale):
    with Stage(nc, name) as st:
        A = CausalAttention(nc, core, st, d, scale)
        vec = st.sem("vector_steps")
        A.begin()
        pairs = heads // 2
        views = lambda b, h: [of[:, bass.ds(b * CH, CH), bass.ds(h * stride + start, d)] for of, stride, start in sources]
        out_of = lambda b, h: (lambda c, r: out[0:r, bass.ds(b * CH + c, 1), bass.ds(h * d, d)])

        def walk(engine, pair):
            with engine.Fori(0, B) as b:
                pair(b, 0, True, pairs == 1)
                if pairs > 2:
                    with engine.Fori(1, pairs - 1) as j:
                        pair(b, j, False, False)
                if pairs > 1:
                    pair(b, pairs - 1, False, True)

        with nc.Block() as block:
            @block.tensor
            def _(pe):
                def pair(b, j, first, last):
                    m = b * pairs + j
                    if first:
                        A.pe_start(pe, m, 0)
                    A.pe_head(pe, m, 0, True)
                    A.pe_head(pe, m, 1, not last)

                walk(pe, pair)

            @block.scalar
            def _(act):
                def pair(b, j, first, last):
                    n, h = b * heads + j * 2, j * 2
                    if first:
                        A.act_fetch(act, n, 0, *views(b, h))
                    A.act_head(act, n, 0, True, views(b, h + 1))
                    A.act_head(act, n + 1, 1, not last, None if last else views(b, h + 2))

                walk(act, pair)

            @block.vector
            def _(dve):
                steps = Steps(dve, vec)

                def pair(b, j, first, last):
                    n, h = b * heads + j * 2, j * 2
                    steps.before, steps.count = 2 * CH * n - (0 if first else 2), 0
                    if first:
                        A.dve_start(dve, n, 0)
                    A.dve_head(dve, steps, n, 0, True, not first, out_of(b, h), None if first else out_of(b, h - 1))
                    A.dve_head(dve, steps, n + 1, 1, not last, True, out_of(b, h + 1), out_of(b, h))

                walk(dve, pair)


def add_turned_stage(nc, core, name, yT, out):
    with Stage(nc, name) as st:
        turned, added = st.sem("turned"), st.sem("added")
        with nc.Block() as block:
            @block.tensor
            def _(pe):
                for t in range(T):
                    last = nc.tensor.transpose(core.psum[:, t // 8, t % 8 * D:(t % 8 + 1) * D],
                                               yT[:, t * P:(t + 1) * P], core.ident[0:D, 0:D])
                    if t % 8 == 7 or t == T - 1:
                        last.then_inc(turned, 1)

            @block.vector
            def _(dve):
                for g, t0 in enumerate(range(0, T, 8)):
                    t1 = min(t0 + 8, T)
                    dve.wait_ge(turned, g + 1)
                    nc.vector.tensor_tensor(out[:, t0:t1, :], out[:, t0:t1, :],
                                            core.psum[:, g, 0:(t1 - t0) * D].rearrange("p (t d) -> p t d", d=D),
                                            ALU.add).then_inc(added, 1)


KEYS = 64
HEADS = 8
TOP = 16
SLOTS = 4
LOWEST = -3e38


def retrieval_stage(nc, core, I):
    with Stage(nc, "peer") as st:
        O = st.sb("O", [P, T, HEADS * D])
        with Stage(nc, "pk") as at:
            w_pk = at.sb("w_pk", [D, 2 * HEADS * D // 2])
            keys = at.sb("keys", [P, 4, 4 * KEYS])
            w_q = at.sb("w_q", [D, HEADS * D])
            load_stage(nc, "pk_load", [(w_pk[:, :], I["w_pk"]), (keys[:, :, :], I["pk_blocks"]), (w_q[:, :], I["w_q"])])
            xt = at.sb("xt", [D, P])
            pkT = at.sb("pkT", [P, 4, P])
            sim = at.sb("sim", [P, 2 * HEADS, KEYS])
            vals = at.sb("vals", [P, 2 * HEADS, TOP])
            ids = at.sb("ids", [P, 2 * HEADS, TOP], U32)
            idf = at.sb("idf", [P, 2 * HEADS, TOP])
            cand = at.sb("cand", [P, HEADS, TOP * TOP])
            fvals = at.sb("fvals", [P, HEADS, TOP])
            fids = at.sb("fids", [P, HEADS * TOP], U32)
            half = at.sb("half", [P, HEADS * TOP], U32)
            halff = at.sb("halff", [P, HEADS * TOP])
            found = at.sb("found", [P, 2, HEADS * TOP])
            index = at.sb("index", [P, 2, HEADS * TOP], U32)
            weight = at.sb("weight", [P, 2, HEADS, TOP])
            sums = at.sb("sums", [P, 2, HEADS])
            count16 = at.sb("count16", [P, TOP])
            base = at.sb("base", [P, HEADS, TOP])
            rows = at.sb("rows", [P, SLOTS, TOP, 2 * D])
            made_tile = at.sb("made_tile", [P, 2, HEADS, 3 * D])
            kept = nc.dram_tensor("peer_kept", (T, P, HEADS, 3 * D), F32, kind="Internal").ap()
            (consts, fetched, pk_made, pk_copied, sims_made, sims_copied, q_made, q_copied, sim_used, shifted, exped,
             index_ready, weighed, vec, attn_vec) = (at.sem(n) for n in (
                "consts", "fetched", "pk_made", "pk_copied", "sims_made", "sims_copied", "q_made", "q_copied",
                "sim_used", "shifted", "exped", "index_ready", "weighed", "vector_steps", "attention_steps"))
            passed, passed_pool, passed_sp = at.sem("passed"), at.sem("passed_by_pool"), at.sem("passed_by_sync")
            gathered = [at.sem(f"gathered{s}") for s in range(SLOTS)]
            stored = [at.sem(f"stored{u}") for u in range(2)]
            start_loop(nc, [fetched, pk_made, pk_copied, sims_made, sims_copied, q_made, q_copied, sim_used, shifted,
                            exped, index_ready])
            A = CausalAttention(nc, core, at, D, 1.0, fetches=(32, 32))
            A.begin()
            ps = core.psum
            TAILS = B // 2
            TILES = TAILS + 4 * B
            PAIRS = HEADS // 2

            class Step:

                def __init__(self, t, u, round_, tails=None, tile=None, following=None, b=None, j=None):
                    self.t, self.u, self.round, self.tails, self.tile, self.next = t, u, round_, tails, tile, following
                    self.b, self.j = b, j
                    self.m = None if b is None else b * PAIRS + j

            def turn(s, half, attend, last=False):
                for i in range(2):
                    b, j = (s - 1, 2 * half + i) if attend else (None, None)
                    following = None if last and i else ("tile", s * CH + 2 * half + 1 if i == 0 else s * CH + 2 + 3 * half)
                    yield Step(TAILS + 4 * s + 2 * half + i, i, 1 + 2 * s + half, tile=s * CH + 2 * half + i,
                               following=following, b=b, j=j)

            def walk(engine, step):
                step(Step(0, 0, 0, tails=0, following=("tails", 1)))
                step(Step(1, 1, 0, tails=1, following=("tile", 0)))
                with engine.Fori(0, 2) as half:
                    for x in turn(0, half, False):
                        step(x)
                with engine.Fori(1, B - 1) as s:
                    with engine.Fori(0, 2) as half:
                        for x in turn(s, half, True):
                            step(x)
                for half in range(2):
                    for x in turn(B - 1, half, True, last=half == 1):
                        step(x)

            def finish(engine, pair):
                pair(0, True, False)
                with engine.Fori(1, PAIRS - 1) as j:
                    pair(j, False, False)
                pair(PAIRS - 1, False, True)

            out_of = lambda b, h: (lambda c, r: O[0:r, bass.ds(b * CH + c, 1), bass.ds(h * D, D)])

            with nc.Block() as block:
                @block.sync
                def _(sp):
                    def load(m, u, b, h):
                        n = 2 * m + u
                        for sem, to, lo, hi, free, at_least in (
                                (A.fetched[u], A.qk1, 0, 2 * D, A.turned, A.BEGIN + 2 * n - 2),
                                (A.v_fetched[u], A.v1, 2 * D, 3 * D, A.weighed, A.BEGIN + CH * n - CH)):
                            sp.wait_ge(free, at_least)
                            wait_apart(sp, passed_sp)
                            sp.dma_start(to[:, u, 0:CH - 1, :].unsqueeze(2),
                                         kept.rearrange("t p h f -> p t h f")[:, bass.ds(b * CH, CH - 1), bass.ds(h, 1), lo:hi]
                                         ).then_inc(sem, 16)
                            sp.dma_start(to[0:TAIL, u, CH - 1, :].unsqueeze(1).unsqueeze(1),
                                         kept.rearrange("t p h f -> p t h f")[0:TAIL, bass.ds(b * CH + CH - 1, 1), bass.ds(h, 1), lo:hi]
                                         ).then_inc(sem, 16)

                    def step(x):
                        if x.m is not None:
                            sp.wait_ge(stored[0], 16 * (x.round + 1 + x.u))
                            wait_apart(sp, passed_sp)
                            sp.wait_ge(stored[1], 16 * (x.round + 1))
                            wait_apart(sp, passed_sp)
                            for u in range(2):
                                load(x.m, u, x.b, 2 * x.j + u)
                        sp.wait_ge(weighed, SLOTS + HEADS * (x.t + 1))
                        wait_apart(sp, passed_sp)
                        sp.wait_ge(q_copied, START + x.t + 1)
                        wait_apart(sp, passed_sp)
                        if x.tails is None:
                            sp.dma_start(kept[bass.ds(x.tile, 1), :, :, :].rearrange("o p h f -> p (o h) f"), made_tile[:, x.u, :, :]
                                         ).then_inc(stored[x.u], 16)
                        else:
                            for k in range(2):
                                sp.dma_start(kept[(2 * x.tails + k) * CH + CH - 1, 0:TAIL, :, :],
                                             made_tile[k * TAIL:(k + 1) * TAIL, x.u, :, :]).then_inc(stored[x.u], 16)

                    walk(sp, step)
                    for u in range(2):
                        sp.wait_ge(stored[u], 16 * (TILES // 2 + 1))
                    finish(sp, lambda j, first, last: [load((B - 1) * PAIRS + j, u, B - 1, 2 * j + u) for u in range(2)])

                @block.gpsimd
                def _(pool):
                    nc.gpsimd.iota(count16[:, :], [[1, TOP]], base=0, channel_multiplier=0,
                                   allow_small_or_imprecise_dtypes=True).then_inc(consts, 1)
                    nc.gpsimd.iota(base[:, :, :], [[KEYS * KEYS // 2, HEADS], [0, TOP]], base=0, channel_multiplier=0,
                                   allow_small_or_imprecise_dtypes=True).then_inc(consts, 1)

                    def gather(x):
                        pool.wait_ge(index_ready, START + x.t + 1)
                        for h in range(HEADS):
                            pool.wait_ge(weighed, HEADS * x.t + h + 1)
                            wait_apart(pool, passed_pool)
                            for k in range(TOP):
                                pool.indirect_dma_start(
                                    out=rows[:, h % SLOTS, k, :], out_offset=None, in_=I["table"],
                                    in_offset=bass.IndirectOffsetOnAxis(
                                        ap=index[:, x.u, h * TOP + k:h * TOP + k + 1], axis=0)
                                ).then_inc(gathered[h % SLOTS], 16)

                    walk(pool, gather)

                @block.tensor
                def _(pe):
                    def project(t):
                        pe.wait_ge(fetched, START + t + 1)
                        pe.wait_ge(pk_copied, START + t)
                        for c in range(4):
                            last = nc.tensor.matmul(ps[:, 0, c * P:(c + 1) * P], w_pk[:, c * P:(c + 1) * P], xt[:, :],
                                                    start=True, stop=True)
                        last.then_inc(pk_made, 1)
                        pe.wait_ge(q_copied, START + t)
                        nc.tensor.matmul(ps[:, 3, :], xt[:, :], w_q[:, :], start=True, stop=True).then_inc(q_made, 1)
                        pe.wait_ge(pk_copied, START + t + 1)
                        pe.wait_ge(sims_copied, START + t)
                        for c in range(4):
                            last = nc.tensor.matmul(ps[:, 1 + c // 2, c % 2 * 256:(c % 2 + 1) * 256], pkT[:, c, :],
                                                    keys[:, c, :], start=True, stop=True)
                        last.then_inc(sims_made, 1)

                    def attend(x):
                        for copied in (pk_copied, q_copied, sims_copied):
                            pe.wait_ge(copied, START + x.t + 1 + (x.next is not None))
                        wait_apart(pe, A.passed_pe)
                        A.pe_start(pe, x.m, 0)
                        A.pe_head(pe, x.m, 0, True)
                        A.pe_head(pe, x.m, 1, False)
                        pe.wait_ge(A.normed, A.BEGIN + CH * (2 * x.m + 2))
                        wait_apart(pe, A.passed_pe)

                    def step(x):
                        if x.next is not None:
                            project(x.t + 1)
                        if x.m is not None:
                            attend(x)

                    project(0)
                    walk(pe, step)

                    def pair(j, first, last):
                        m = (B - 1) * PAIRS + j
                        if first:
                            A.pe_start(pe, m, 0)
                        A.pe_head(pe, m, 0, True)
                        A.pe_head(pe, m, 1, not last)

                    finish(pe, pair)

                @block.scalar
                def _(act):
                    def prepare(t, u, tile, stores):
                        act.wait_ge(q_made, START + t)
                        if tile[0] == "tails":
                            lo = (2 * tile[1] + 1) * CH - 1
                            tails = core.xnT[0:D, :].rearrange("d (t n) -> d t n", n=P)[:, lo:lo + CH + 1:CH, 0:TAIL]
                            nc.scalar.activation(xt[:, :].rearrange("d (t n) -> d t n", n=TAIL), tails, ACT.Copy
                                                 ).then_inc(fetched, 1)
                        else:
                            nc.scalar.activation(xt[:, :], core.xnT[0:D, bass.ds(tile[1] * P, P)], ACT.Copy).then_inc(fetched, 1)
                        act.wait_ge(pk_made, START + t + 1)
                        act.wait_ge(sims_made, START + t)
                        nc.scalar.activation(pkT[:, :, :], ps[:, 0, :].rearrange("p (c n) -> p c n", n=P), ACT.Copy
                                             ).then_inc(pk_copied, 1)
                        act.wait_ge(q_made, START + t + 1)
                        if stores is not None:
                            act.wait_ge(stored[u], stores)
                        nc.scalar.activation(made_tile[:, u, :, 0:D], ps[:, 3, :].rearrange("p (h d) -> p h d", d=D),
                                             ACT.Copy, scale=0.125).then_inc(q_copied, 1)
                        act.wait_ge(sims_made, START + t + 1)
                        act.wait_ge(sim_used, START + t)
                        nc.scalar.activation(sim[:, :, :], ps[:, 1:3, :].rearrange("p b (q n) -> p (b q) n", n=KEYS),
                                             ACT.Copy).then_inc(sims_copied, 1)
                        act.wait_ge(shifted, START + t + 1)
                        nc.scalar.activation(fvals[:, :, :], fvals[:, :, :], ACT.Exp).then_inc(exped, 1)

                    def step(x):
                        if x.next is not None:
                            first = isinstance(x.t, int) and x.t == 0
                            prepare(x.t + 1, 1 - x.u, x.next, None if first else 16 * (x.round + 1 + x.u))
                        if x.m is not None:
                            A.act_head(act, 2 * x.m, 0, False)
                            A.act_head(act, 2 * x.m + 1, 1, False)

                    prepare(0, 0, ("tails", 0), None)
                    walk(act, step)

                    def pair(j, first, last):
                        n = 2 * ((B - 1) * PAIRS + j)
                        A.act_head(act, n, 0, False)
                        A.act_head(act, n + 1, 1, False)

                    finish(act, pair)

                @block.vector
                def _(dve):
                    steps, attn_steps = Steps(dve, vec), Steps(dve, attn_vec)

                    def select(t, u):
                        dve.wait_ge(sims_copied, START + t + 1)
                        wait_apart(dve, passed)
                        for lo in (0, 8):
                            for q in range(2 * HEADS):
                                steps.add(nc.vector.max(vals[:, q, lo:lo + 8], sim[:, q, :]))
                            steps.settle(passed)
                            for q in range(2 * HEADS):
                                steps.add(nc.vector.max_index(ids[:, q, lo:lo + 8], vals[:, q, lo:lo + 8], sim[:, q, :]))
                            steps.settle(passed)
                            if lo == 0:
                                for q in range(2 * HEADS):
                                    steps.add(nc.vector.match_replace(sim[:, q, :], vals[:, q, 0:8], sim[:, q, :], LOWEST))
                                steps.settle(passed)
                        nc.vector.tensor_copy(idf[:, :, :], ids[:, :, :]).then_inc(sim_used, 1)
                        dve.wait_ge(sim_used, START + t + 1)
                        steps.add(nc.vector.tensor_scalar(idf[:, HEADS:, :], idf[:, HEADS:, :], float(KEYS), None, ALU.mult))
                        steps.add(nc.vector.scalar_tensor_tensor(idf[:, 0:HEADS, :], base[:, :, :], 2.0, idf[:, 0:HEADS, :],
                                                                 ALU.mult, ALU.add))
                        steps.do(nc.vector.tensor_tensor(
                            cand[:, :, :].rearrange("p h (a b) -> p h a b", a=TOP),
                            vals[:, 0:HEADS, :].unsqueeze(3).to_broadcast([P, HEADS, TOP, TOP]),
                            vals[:, HEADS:, :].unsqueeze(2).to_broadcast([P, HEADS, TOP, TOP]), ALU.add))
                        wait_apart(dve, passed)
                        for lo in (0, 8):
                            for h in range(HEADS):
                                steps.add(nc.vector.max(fvals[:, h, lo:lo + 8], cand[:, h, :]))
                            steps.settle(passed)
                            for h in range(HEADS):
                                steps.add(nc.vector.max_index(fids[:, h * TOP + lo:h * TOP + lo + 8],
                                                              fvals[:, h, lo:lo + 8], cand[:, h, :]))
                            steps.settle(passed)
                            if lo == 0:
                                for h in range(HEADS):
                                    steps.add(nc.vector.match_replace(cand[:, h, :], fvals[:, h, 0:8], cand[:, h, :], LOWEST))
                                steps.settle(passed)
                        onehot = cand[:, :, :].rearrange("p h (k a) -> p h k a", a=TOP)
                        for part, (op, by) in enumerate(((ALU.logical_shift_right, 4), (ALU.bitwise_and, 15))):
                            steps.do(nc.vector.tensor_scalar(half[:, :], fids[:, :], by, None, op))
                            steps.do(nc.vector.tensor_copy(halff[:, :], half[:, :]))
                            steps.do(nc.vector.tensor_tensor(cand[:, :, :].rearrange("p h (k a) -> p (h k) a", a=TOP),
                                                             over(halff[:, :], TOP), rows_of(count16[:, :], HEADS * TOP),
                                                             ALU.is_equal))
                            steps.do(nc.vector.tensor_tensor(
                                onehot, onehot,
                                idf[:, part * HEADS:(part + 1) * HEADS, :].unsqueeze(2).to_broadcast([P, HEADS, TOP, TOP]),
                                ALU.mult))
                            steps.do(nc.vector.tensor_reduce(found[:, part, :],
                                                             cand[:, :, :].rearrange("p h (k a) -> p (h k) a", a=TOP),
                                                             AX.X, ALU.add))
                        steps.add(nc.vector.tensor_copy(sums[:, 0, :], fvals[:, :, 0]))
                        nc.vector.tensor_tensor(index[:, u, :], found[:, 0, :], found[:, 1, :], ALU.add
                                                ).then_inc(index_ready, 1)
                        steps.settle()
                        nc.vector.tensor_tensor(fvals[:, :, :], fvals[:, :, :], over(sums[:, 0, :], TOP), ALU.subtract
                                                ).then_inc(shifted, 1)
                        dve.wait_ge(exped, START + t + 1)
                        steps.do(nc.vector.tensor_reduce(sums[:, 1, :], fvals[:, :, :], AX.X, ALU.add))
                        steps.do(nc.vector.reciprocal(sums[:, 0, :], sums[:, 1, :]))
                        steps.do(nc.vector.tensor_tensor(weight[:, u, :, :], fvals[:, :, :], over(sums[:, 0, :], TOP), ALU.mult))

                    def weigh(x, heads):
                        for h in heads:
                            slot = h % SLOTS
                            uses = HEADS // SLOTS
                            dve.wait_ge(gathered[slot], 16 * TOP * (uses * x.t + h // SLOTS + 1))
                            steps.do(nc.vector.tensor_tensor(rows[:, slot, :, :], rows[:, slot, :, :],
                                                             over(weight[:, x.u, h, :], 2 * D), ALU.mult))
                            nc.vector.tensor_reduce(made_tile[:, x.u, h, D:3 * D],
                                                    rows[:, slot, :, :].rearrange("p k d -> p d k"), AX.X, ALU.add
                                                    ).then_inc(weighed, 1)

                    dve.sem_inc(weighed, SLOTS)
                    dve.wait_ge(consts, 2)
                    select(0, 0)
                    per_select = steps.count

                    def step(x):
                        steps.before, steps.count = per_select * (x.t + 1) + HEADS * x.t, 0
                        if x.next is not None:
                            select(x.t + 1, 1 - x.u)
                        if x.tails is None:
                            dve.wait_ge(stored[x.u], 16 * (x.round + 1))
                            wait_apart(dve, passed)
                        attn_steps.before, attn_steps.count = (0 if x.m is None else 4 * CH * x.m), 0
                        weigh(x, range(0, 2))
                        if x.m is not None:
                            A.dve_start(dve, 2 * x.m, 0)
                            A.dve_head(dve, attn_steps, 2 * x.m, 0, True, False, out_of(x.b, 2 * x.j))
                        weigh(x, range(2, 5))
                        if x.m is not None:
                            A.dve_head(dve, attn_steps, 2 * x.m + 1, 1, False, True, out_of(x.b, 2 * x.j + 1), out_of(x.b, 2 * x.j))
                        weigh(x, range(5, HEADS))

                    walk(dve, step)

                    def pair(j, first, last):
                        n, b, h = 2 * ((B - 1) * PAIRS + j), B - 1, 2 * j
                        attn_steps.before, attn_steps.count = 2 * CH * n - (0 if first else 2), 0
                        if first:
                            A.dve_start(dve, n, 0)
                        A.dve_head(dve, attn_steps, n, 0, True, not first, out_of(b, h), None if first else out_of(b, h - 1))
                        A.dve_head(dve, attn_steps, n + 1, 1, not last, True, out_of(b, h + 1), out_of(b, h))

                    finish(dve, pair)
        with Stage(nc, "peer_out") as at:
            TERMS = HEADS * D // P
            w_o = at.sb("w_o", [P, TERMS, D])
            oT = at.sb("oT", [P, TERMS, COLS])
            load_stage(nc, "peer_out_load", [(w_o[:, :, :], I["w_o"].rearrange("(k p) n -> p k n", p=P))])
            set_stage(nc, "peer_padding", [(O[TAIL:P, CH - 1::CH, :], 0.0)])
            turn_stage(nc, core, "peer_turn", [(oT[:, k, :], P, lambda t, k=k: O[:, t, k * P:(k + 1) * P]) for k in range(TERMS)])
            product_stage(nc, core, "peer_proj",
                          [(lambda t, k=k: oT[:, k, t * P:(t + 1) * P], w_o[:, k, :]) for k in range(TERMS)], D,
                          lambda t0, t1, made: nc.vector.tensor_tensor(core.h[:, t0:t1, :], core.h[:, t0:t1, :], made, ALU.add))


CHANNELS = 3 * D
RPE = 8
RPE_LAYERS = 3
SPAN = 2 * SEQ
LAGS = SPAN // P
FREQ = SEQ + 1
FCH = (FREQ + P - 1) // P
FREQ_ROWS = [min(P, FREQ - P * k) for k in range(FCH)]
TOKEN_ROWS = [min(P, SEQ - P * c) for c in range(CH)]


def root_stage(nc, core, name, x, sq, stat, scale, eps, ones=None):
    with Stage(nc, name) as st:
        vec, squared, rooted = st.sem("vector_steps"), st.sem("squared"), st.sem("rooted")
        with nc.Block() as block:
            @block.vector
            def _(dve):
                steps = Steps(dve, vec)
                steps.do(nc.vector.tensor_tensor(sq, x, x, ALU.mult))
                nc.vector.tensor_reduce(stat[:, 0, :], sq, AX.X, ALU.add).then_inc(squared, 1)
                dve.wait_ge(rooted, 1)
                steps.do(nc.vector.tensor_scalar(stat[:, 0, :], stat[:, 0, :], scale, eps, ALU.mult, ALU.add))
                steps.do(nc.vector.reciprocal(stat[:, 1, :], stat[:, 0, :]))
                steps.do(nc.vector.tensor_tensor(x, x, over(stat[:, 1, :], D), ALU.mult))

            @block.scalar
            def _(act):
                act.wait_ge(squared, 1)
                nc.scalar.activation(stat[:, 0, :], stat[:, 0, :], ACT.Sqrt).then_inc(rooted, 1)


def lag_network_stage(nc, core, I, a):
    with Stage(nc, "rpe") as st:
        lags = st.sb("lags", [2, SPAN])
        w_pos = st.sb("w_pos", [2, RPE])
        w_mid = st.sb("w_mid", [RPE + 1, RPE_LAYERS, RPE])
        w_out = st.sb("w_out", [RPE + 1, CHANNELS])
        ones8 = st.sb("ones8", [RPE, RPE])
        x, sq, root = (st.sb(n, [RPE, 3, SPAN // 3]) for n in ("x", "sq", "root"))
        act_in = st.sb("act_in", [RPE + 1, SPAN])
        load_stage(nc, "rpe_load", [(lags[:, :], I["lags"]), (w_pos[:, :], I["pos_aug"]),
                                    (w_mid[:, :, :], I["rpe_aug"]), (w_out[:, :], I["out_aug"])])
        set_stage(nc, "rpe_ones", [(ones8[:, :], 1.0), (act_in[:, :], 1.0)])
        made, squared, summed, rooted, ready, vec, copied = (
            st.sem(n) for n in ("made", "squared", "summed", "rooted", "ready", "vector_steps", "copied"))
        ps, third = core.psum, SPAN // 3
        rounds = RPE_LAYERS + 1
        with nc.Block() as block:
            @block.tensor
            def _(pe):
                for r in range(rounds):
                    if r:
                        pe.wait_ge(ready, r)
                    for k in range(3):
                        weights = w_pos[:, :] if r == 0 else w_mid[:, r - 1, :]
                        moving = lags if r == 0 else act_in
                        last = nc.tensor.matmul(ps[0:RPE, k, 0:third], weights, moving[:, k * third:(k + 1) * third],
                                                start=True, stop=True)
                    last.then_inc(made, 1)
                    pe.wait_ge(squared, r + 1)
                    for k in range(3):
                        last = nc.tensor.matmul(ps[0:RPE, 3 + k, 0:third], ones8[:, :], sq[:, k, :],
                                                start=True, stop=True)
                    last.then_inc(summed, 1)
                pe.wait_ge(ready, rounds)
                for t in range(LAGS):
                    if t == 6:
                        pe.wait_ge(copied, 1)
                    nc.tensor.matmul(ps[:, t % 6, 0:CHANNELS], act_in[:, t * P:(t + 1) * P], w_out[:, :],
                                     start=True, stop=True).then_inc(made, 1)

            @block.vector
            def _(dve):
                steps = Steps(dve, vec)
                for r in range(rounds):
                    dve.wait_ge(made, r + 1)
                    steps.do(nc.vector.tensor_copy(x[:, :, :], ps[0:RPE, 0:3, 0:third]))
                    nc.vector.tensor_tensor(sq[:, :, :], x[:, :, :], x[:, :, :], ALU.mult).then_inc(squared, 1)
                    dve.wait_ge(rooted, r + 1)
                    steps.do(nc.vector.tensor_scalar(root[:, :, :], root[:, :, :], RPE ** -0.5, 1e-8, ALU.mult, ALU.add))
                    steps.do(nc.vector.reciprocal(root[:, :, :], root[:, :, :]))
                    steps.do(nc.vector.tensor_tensor(x[:, :, :], x[:, :, :], root[:, :, :], ALU.mult))
                    nc.vector.tensor_scalar(act_in[0:RPE, :].rearrange("p (k n) -> p k n", k=3), x[:, :, :],
                                            0.0, None, ALU.max).then_inc(ready, 1)
                for lo, hi in ((0, 6), (6, LAGS)):
                    dve.wait_ge(made, rounds + hi)
                    nc.vector.tensor_copy(a[:, lo:hi, :], ps[:, 0:hi - lo, 0:CHANNELS]).then_inc(copied, 1)

            @block.scalar
            def _(act):
                for r in range(rounds):
                    act.wait_ge(summed, r + 1)
                    nc.scalar.activation(root[:, :, :], ps[0:RPE, 3:6, 0:third], ACT.Sqrt).then_inc(rooted, 1)


def toeplitz_stage(nc, core, I):
    with Stage(nc, "tnn") as st:
        w_uv = st.sb("w_uv", [D + 1, 2 * CHANNELS])
        uv = st.sb("uv", [P, T, 2 * CHANNELS])
        load_stage(nc, "tnn_load", [(w_uv[:, :], I["uv_aug"])])
        product_stage(nc, core, "tnn_uv", [(lambda t: core.xnT[:, t * P:(t + 1) * P], w_uv[:, :])], 2 * CHANNELS,
                      lambda t0, t1, made: nc.scalar.activation(uv[:, t0:t1, :], made, ACT.Silu), engine="scalar")
        uv_b = uv[:, :, :].rearrange("p (b c) w -> p b c w", c=CH)
        with Stage(nc, "dft") as at:
            a = at.sb("a", [P, LAGS, CHANNELS])
            cos, sin = at.sb("cos", [P, LAGS, FREQ]), at.sb("sin", [P, LAGS, FREQ])
            icos, isin = at.sb("icos", [P, FCH, SEQ]), at.sb("isin", [P, FCH, SEQ])
            af = at.sb("af", [P, 2, CHANNELS])
            vf = at.sb("vf", [P, 2, B, CHANNELS])
            t1, t2, t3, t4 = (at.sb(f"t{k}", [P, B, CHANNELS]) for k in range(4))
            y = at.sb("y", [P, FCH, 2, B, CHANNELS])
            loads = [(to[:, :, :], I[n].rearrange("(k p) f -> p k f", p=P)) for to, n in ((cos, "cos"), (sin, "sin"))]
            for to, n in ((icos, "icos"), (isin, "isin")):
                loads += [(to[:, 0:FCH - 1, :], I[n][0:(FCH - 1) * P, :].rearrange("(k p) f -> p k f", p=P)),
                          (to[0:FREQ_ROWS[-1], FCH - 1, :], I[n][(FCH - 1) * P:FREQ, :])]
            load_stage(nc, "dft_load", loads)
            lag_network_stage(nc, core, I, a)
            made, copied, multiplied, vec, gps, crossed = (
                at.sem(n) for n in ("made", "copied", "multiplied", "vector_steps", "pool_steps", "crossed"))
            ps = core.psum
            with nc.Block() as block:
                @block.tensor
                def _(pe):
                    for f in range(FCH):
                        m = FREQ_ROWS[f]
                        if f:
                            pe.wait_ge(copied, f)
                        for part, table in enumerate((cos, sin)):
                            for k in range(LAGS):
                                nc.tensor.matmul(ps[0:m, part, 0:CHANNELS], table[:, k, f * P:f * P + m], a[:, k, :],
                                                 start=(k == 0), stop=(k == LAGS - 1))
                            for pair in range(2):
                                for c in range(CH):
                                    r = TOKEN_ROWS[c]
                                    last = nc.tensor.matmul(
                                        ps[0:m, 2 + 2 * part + pair, 0:2 * CHANNELS].rearrange("p (b w) -> p b w", b=2),
                                        table[0:r, c, f * P:f * P + m],
                                        uv_b[0:r, 2 * pair:2 * pair + 2, c, CHANNELS:2 * CHANNELS],
                                        start=(c == 0), stop=(c == CH - 1))
                        last.then_inc(made, 1)

                @block.scalar
                def _(act):
                    for f in range(FCH):
                        m = FREQ_ROWS[f]
                        act.wait_ge(made, f + 1)
                        if f:
                            act.wait_ge(multiplied, f)
                            act.wait_ge(crossed, f)
                        nc.scalar.activation(af[0:m, :, :], ps[0:m, 0:2, 0:CHANNELS], ACT.Copy)
                        nc.scalar.activation(
                            vf[0:m, :, :, :].rearrange("p s (q b) w -> p (s q) (b w)", b=2),
                            ps[0:m, 2:6, 0:2 * CHANNELS], ACT.Copy).then_inc(copied, 1)

                def cross(eng, engine, steps, f, out, parts, temps, op, done):
                    m = FREQ_ROWS[f]
                    for k in range(2):
                        steps.add(engine.tensor_tensor(temps[k][0:m, :, :], vf[0:m, parts[2 * k], :, :],
                                                       rows_of(af[0:m, parts[2 * k + 1], :], B), ALU.mult))
                    steps.settle()
                    engine.tensor_tensor(out[0:m, :, :], temps[0][0:m, :, :], temps[1][0:m, :, :], op).then_inc(done, 1)

                @block.vector
                def _(dve):
                    steps = Steps(dve, vec)
                    for f in range(FCH):
                        dve.wait_ge(copied, f + 1)
                        if f:
                            dve.wait_ge(multiplied, f)
                        cross(dve, nc.vector, steps, f, y[:, f, 0, :, :], (0, 0, 1, 1), (t1, t2), ALU.subtract, multiplied)

                @block.gpsimd
                def _(pool):
                    steps = Steps(pool, gps)
                    for f in range(FCH):
                        pool.wait_ge(copied, f + 1)
                        if f:
                            pool.wait_ge(crossed, f)
                        cross(pool, nc.gpsimd, steps, f, y[:, f, 1, :, :], (1, 0, 0, 1), (t3, t4), ALU.add, crossed)

            jobs = [(c, pair) for c in range(CH) for pair in range(2)]
            inverted, gated = at.sem("inverted"), at.sem("gated")
            with nc.Block() as block:
                @block.tensor
                def _(pe):
                    for n, (c, pair) in enumerate(jobs):
                        if n >= 8:
                            pe.wait_ge(gated, n - 7)
                        m = TOKEN_ROWS[c]
                        for k in range(2 * FCH):
                            f, part = k // 2, k % 2
                            r = FREQ_ROWS[f]
                            last = nc.tensor.matmul(
                                ps[0:m, n % 8, 0:2 * CHANNELS].rearrange("p (b w) -> p b w", b=2),
                                (icos, isin)[part][0:r, f, c * P:c * P + m], y[0:r, f, part, 2 * pair:2 * pair + 2, :],
                                start=(k == 0), stop=(k == 2 * FCH - 1))
                        last.then_inc(inverted, 1)

                @block.vector
                def _(dve):
                    for n, (c, pair) in enumerate(jobs):
                        m = TOKEN_ROWS[c]
                        dve.wait_ge(inverted, n + 1)
                        u = uv_b[0:m, 2 * pair:2 * pair + 2, c, 0:CHANNELS]
                        nc.vector.tensor_tensor(u, u, ps[0:m, n % 8, 0:2 * CHANNELS].rearrange("p (b w) -> p b w", b=2),
                                                ALU.mult).then_inc(gated, 1)
        with Stage(nc, "tnn_out") as at:
            g0, g1 = at.sb("g0", [P, COLS]), at.sb("g1", [D + 1, COLS])
            w_o0, w_o1, w_t = at.sb("w_o0", [P, D]), at.sb("w_o1", [D + 1, D]), at.sb("w_t", [D + 1, D])
            r = at.sb("r", [P, T, D])
            sq, stat = at.sb("sq", [P, T, D]), at.sb("stat", [P, 2, T])
            set_stage(nc, "g1_ones", [(g1[:, :], 1.0)])
            load_stage(nc, "tnn_out_load", [(w_o0[:, :], I["o_aug"][0:P, :]), (w_o1[:, :], I["o_aug"][P:CHANNELS + 1, :]),
                                            (w_t[:, :], I["t_aug"])])
            turn_stage(nc, core, "tnn_turn", [(g0, P, lambda t: uv[:, t, 0:P]), (g1, D, lambda t: uv[:, t, P:CHANNELS])])
            product_stage(nc, core, "tnn_o", [(lambda t: g0[:, t * P:(t + 1) * P], w_o0[:, :]),
                                              (lambda t: g1[:, t * P:(t + 1) * P], w_o1[:, :])], D,
                          lambda t0, t1, made: nc.vector.tensor_tensor(r[:, t0:t1, :], core.xn[:, t0:t1, :], made, ALU.subtract))
            turn_stage(nc, core, "tnn_turn_r", [(core.xnT, D, lambda t: r[:, t, :])])
            product_stage(nc, core, "tnn_t", [(lambda t: core.xnT[:, t * P:(t + 1) * P], w_t[:, :])], D,
                          lambda t0, t1, made: nc.vector.tensor_copy(r[:, t0:t1, :], made))
            root_stage(nc, core, "tnn_root", r[:, :, :], sq[:, :, :], stat, CHANNELS ** -0.5, 1e-8)
            silu_stage(nc, core, "tnn_silu", r[:, :, :])
            add_stage(nc, core, "tnn_add", (core.h[:, :, :], core.h[:, :, :], core.xn[:, :, :]),
                      (core.h[:, :, :], core.h[:, :, :], r[:, :, :]))


def silu_stage(nc, core, name, x):
    with nc.Block() as block:
        @block.scalar
        def _(act):
            nc.scalar.activation(x, x, ACT.Silu)


def top_two_stage(nc, core, name, scores, weight, experts, renorm):
    E = experts
    with Stage(nc, name) as st:
        peak, total = st.sb("peak", [P, T]), st.sb("total", [P, T])
        above = st.sb("above", [P, T, E, E])
        same = st.sb("same", [P, T, E, E])
        before = st.sb("before", [P, E, E])
        rank = st.sb("rank", [P, T, E])
        vec, shifted, exped, consts = (st.sem(n) for n in ("vector_steps", "shifted", "exped", "consts"))
        with nc.Block() as block:
            @block.gpsimd
            def _(pool):
                nc.gpsimd.memset(before[:, :, :], 1.0).then_inc(consts, 1)
                pool.wait_ge(consts, 1)
                nc.gpsimd.affine_select(out=before[:, :, :], in_=before[:, :, :], compare_op=ALU.is_gt, fill=0.0,
                                        base=0, pattern=[[1, E], [-1, E]], channel_multiplier=0).then_inc(consts, 1)

            @block.scalar
            def _(act):
                act.wait_ge(shifted, 1)
                nc.scalar.activation(scores, scores, ACT.Exp).then_inc(exped, 1)
                if renorm == "softmax":
                    act.wait_ge(shifted, 2)
                    nc.scalar.activation(weight, weight, ACT.Exp).then_inc(exped, 1)

            @block.vector
            def _(dve):
                steps = Steps(dve, vec)
                steps.do(nc.vector.tensor_reduce(peak[:, :], scores, AX.X, ALU.max))
                nc.vector.tensor_tensor(scores, scores, over(peak[:, :], E), ALU.subtract).then_inc(shifted, 1)
                dve.wait_ge(exped, 1)
                steps.do(nc.vector.tensor_reduce(total[:, :], scores, AX.X, ALU.add))
                steps.do(nc.vector.reciprocal(total[:, :], total[:, :]))
                steps.do(nc.vector.tensor_tensor(scores, scores, over(total[:, :], E), ALU.mult))
                of_f = scores.unsqueeze(2).to_broadcast([P, T, E, E])
                of_e = scores.unsqueeze(3).to_broadcast([P, T, E, E])
                steps.add(nc.vector.tensor_tensor(above[:, :, :, :], of_f, of_e, ALU.is_gt))
                steps.do(nc.vector.tensor_tensor(same[:, :, :, :], of_f, of_e, ALU.is_equal))
                dve.wait_ge(consts, 2)
                flat = lambda a: a[:, :, :, :].rearrange("p t e f -> p t (e f)")
                steps.do(nc.vector.tensor_tensor(flat(same), flat(same),
                                                 rows_of(before[:, :, :].rearrange("p e f -> p (e f)"), T), ALU.mult))
                steps.do(nc.vector.tensor_tensor(flat(above), flat(above), flat(same), ALU.add))
                steps.do(nc.vector.tensor_reduce(rank[:, :, :], above[:, :, :, :], AX.X, ALU.add))
                steps.do(nc.vector.tensor_scalar(rank[:, :, :], rank[:, :, :], 2.0, None, ALU.is_lt))
                if renorm == "softmax":
                    steps.do(nc.vector.tensor_reduce(peak[:, :], scores, AX.X, ALU.max))
                    nc.vector.tensor_tensor(weight, scores, over(peak[:, :], E), ALU.subtract).then_inc(shifted, 1)
                    dve.wait_ge(exped, 2)
                    steps.do(nc.vector.tensor_tensor(weight, weight, rank[:, :, :], ALU.mult))
                else:
                    steps.do(nc.vector.tensor_tensor(weight, scores, rank[:, :, :], ALU.mult))
                steps.do(nc.vector.tensor_reduce(total[:, :], weight, AX.X, ALU.add))
                if renorm != "softmax":
                    steps.do(nc.vector.tensor_scalar(total[:, :], total[:, :], 1e-9, None, ALU.add))
                steps.do(nc.vector.reciprocal(total[:, :], total[:, :]))
                steps.do(nc.vector.tensor_tensor(weight, weight, over(total[:, :], E), ALU.mult))


Q_HEADS = 4
HD = D // Q_HEADS
EXPERTS = 8
HIDDEN = 170
HALF = HIDDEN // 2


def gated_experts_stage(nc, core, I, weight, acc):
    with Stage(nc, "moe") as st:
        WIDE = EXPERTS * HIDDEN
        w11, w22, w31 = (st.sb(n, [P, 2 * WIDE], BF16) for n in ("w11", "w22", "w31"))
        x12, x13 = st.sb("x12", [P, COLS], BF16), st.sb("x13", [P, COLS], BF16)
        with Stage(nc, "moe_x") as at:
            x = at.sb("x", [P, COLS])
            load_stage(nc, "moe_twice", [(x[half * D:(half + 1) * D, :], core.xnT[0:D, :]) for half in range(2)])
            split_tokens_stage(nc, "moe_split", x[:, :], x12, x13)
        split_weights_stage(nc, "moe_weights", I["moe_w13"], w11, w22, w31, WIDE)
        products = ((w11, x12), (w22, x12), (w31, x13))
        w2 = st.sb("w2", [HALF, 2 * EXPERTS, D])
        act1 = st.sb("act1", [HALF, 2, BANK])
        hid = st.sb("hid", [HALF, 4, BANK])
        part = st.sb("part", [P, 2, 4, D])
        load_stage(nc, "moe_load", [(w2[:, :, :], I["moe_w2"].rearrange("(u p) d -> p u d", p=HALF))])
        raised, activated, gated, lowered, scaled, added, passed = (
            st.sem(n) for n in ("raised", "activated", "gated", "lowered", "scaled", "added", "passed"))
        start_loop(nc, [raised, activated, gated, lowered, scaled, added])
        ps = core.psum
        U = 2 * EXPERTS
        with nc.Block() as block:
            @block.tensor
            def _(pe):
                with pe.Fori(0, GROUPS) as g:
                    def raise_(e):
                        for u in (2 * e, 2 * e + 1):
                            if u >= 2:
                                pe.wait_ge(gated, START + U * g + u - 1)
                            else:
                                pe.wait_ge(gated, START + U * g)
                            wait_apart(pe, passed)
                            for which in range(2):
                                lo = which * WIDE + u * HALF
                                for k, (w, x) in enumerate(products):
                                    last = nc.tensor.matmul(ps[0:HALF, 2 * which + u % 2, :], w[:, lo:lo + HALF],
                                                            x[:, bass.ds(g * BANK, BANK)], start=(k == 0), stop=(k == 2))
                            last.then_inc(raised, 1)

                    raise_(0)
                    for e in range(EXPERTS):
                        if e + 1 < EXPERTS:
                            raise_(e + 1)
                        pe.wait_ge(gated, START + U * g + 2 * e + 2)
                        pe.wait_ge(scaled, START + EXPERTS * g + max(e - 1, 0))
                        wait_apart(pe, passed)
                        for k in range(4):
                            for half in range(2):
                                last = nc.tensor.matmul(ps[:, 4 + e % 2, k * D:(k + 1) * D],
                                                        hid[:, (2 * e + half) % 4, k * P:(k + 1) * P], w2[:, 2 * e + half, :],
                                                        start=(half == 0), stop=(half == 1))
                        last.then_inc(lowered, 1)

            @block.scalar
            def _(act):
                with act.Fori(0, GROUPS) as g:
                    for u in range(U):
                        act.wait_ge(raised, START + U * g + u + 1)
                        act.wait_ge(gated, START + U * g + max(u - 1, 0))
                        nc.scalar.activation(act1[:, u % 2, :], ps[0:HALF, u % 2, :], ACT.Silu).then_inc(activated, 1)

            @block.vector
            def _(dve):
                with dve.Fori(0, GROUPS) as g:
                    def gate(e):
                        for u in (2 * e, 2 * e + 1):
                            dve.wait_ge(activated, START + U * g + u + 1)
                            dve.wait_ge(lowered, START + EXPERTS * g + max(e - 1, 0))
                            nc.vector.tensor_tensor(hid[:, u % 4, :], act1[:, u % 2, :], ps[0:HALF, 2 + u % 2, :],
                                                    ALU.mult).then_inc(gated, 1)

                    gate(0)
                    for e in range(EXPERTS):
                        if e + 1 < EXPERTS:
                            gate(e + 1)
                        n = EXPERTS * g + e
                        dve.wait_ge(lowered, START + n + 1)
                        nc.vector.tensor_tensor(part[:, e % 2, :, :], ps[:, 4 + e % 2, 0:4 * D].rearrange("p (t d) -> p t d", d=D),
                                                over(weight[:, bass.ds(4 * g, 4), e], D), ALU.mult).then_inc(scaled, 1)
                        dve.wait_ge(scaled, START + n + 1)
                        dve.wait_ge(added, START + n)
                        nc.vector.tensor_tensor(acc[:, bass.ds(4 * g, 4), :], acc[:, bass.ds(4 * g, 4), :],
                                                part[:, e % 2, :, :], ALU.add).then_inc(added, 1)


def rotary_experts_stage(nc, core, I):
    with Stage(nc, "rot") as st:
        spare = st.sb("spare", [P, T, D])
        norm_stage(nc, core, "rot_rms1", core.xn, eps=1e-6, use_mean=False, gain=I["rms1_w"], dst=spare)
        with Stage(nc, "rot_attn") as at:
            width = 5 * D
            w_in = at.sb("w_in", [D, width])
            w_out = at.sb("w_out", [D, D])
            cos, sin = at.sb("cos", [P, CH, HD]), at.sb("sin", [P, CH, HD])
            qkv = at.sb("qkv", [P, T, width])
            yT = at.sb("yT", [D, COLS])
            load_stage(nc, "rot_load", [(w_in[:, :], I["rot_in"]), (w_out[:, :], I["rot_out"]),
                                        (cos[:, :, :], I["rot_cos"].rearrange("(c p) d -> p c d", p=P)),
                                        (sin[:, :, :], I["rot_sin"].rearrange("(c p) d -> p c d", p=P))])
            product_stage(nc, core, "rot_qkv", [(lambda t: core.xnT[0:D, t * P:(t + 1) * P], w_in[:, :])], width,
                          lambda t0, t1, made: nc.scalar.activation(qkv[:, t0:t1, :], made, ACT.Copy), engine="scalar")
            with Stage(nc, "rope") as rt:
                vec = rt.sem("vector_steps")
                with nc.Block() as block:
                    @block.vector
                    def _(dve):
                        steps = Steps(dve, vec)
                        parts = [(lo, table) for lo, table in ((0, cos), (2 * D, sin))]
                        view = lambda b, lo: qkv[:, b * CH:(b + 1) * CH, lo:lo + 2 * D].rearrange("p c (h d) -> p c h d", d=HD)
                        for b in range(B):
                            for lo, table in parts:
                                steps.add(nc.vector.tensor_tensor(
                                    view(b, lo), view(b, lo),
                                    table[:, :, :].unsqueeze(2).to_broadcast([P, CH, 2 * Q_HEADS, HD]), ALU.mult))
                        steps.settle()
                        steps.do(nc.vector.tensor_tensor(qkv[:, :, 0:2 * D], qkv[:, :, 0:2 * D], qkv[:, :, 2 * D:4 * D], ALU.add))
            causal_attention_stage(nc, core, "rot_soft", [(qkv, HD, 0), (qkv, HD, D), (qkv, HD, 4 * D)], qkv, Q_HEADS, HD,
                                   HD ** -0.5)
            turn_stage(nc, core, "rot_turn", [(yT, D, lambda t: qkv[:, t, 0:D])])
            product_stage(nc, core, "rot_proj", [(lambda t: yT[:, t * P:(t + 1) * P], w_out[:, :])], D,
                          lambda t0, t1, made: nc.vector.tensor_tensor(core.xn[:, t0:t1, :], core.xn[:, t0:t1, :], made, ALU.add))
        norm_stage(nc, core, "rot_rms2", core.xn, eps=1e-6, use_mean=False, gain=I["rms2_w"], dst=spare)
        router, weight = st.sb("router", [P, T, EXPERTS]), st.sb("weight", [P, T, EXPERTS])
        w_r = st.sb("w_r", [D, EXPERTS])
        load_stage(nc, "router_load", [(w_r[:, :], I["router"])])
        product_stage(nc, core, "router_p", [(lambda t: core.xnT[0:D, t * P:(t + 1) * P], w_r[:, :])], EXPERTS,
                      lambda t0, t1, made: nc.vector.tensor_copy(router[:, t0:t1, :], made))
        top_two_stage(nc, core, "router_top", router[:, :, :], weight[:, :, :], EXPERTS, "sum")
        gated_experts_stage(nc, core, I, weight, core.xn)
        add_stage(nc, core, "rot_residual", (core.h[:, :, :], core.h[:, :, :], core.xn[:, :, :]))


KEEP = SEQ // 10
SLOT = 64
S_HEADS = 8
S_HD = D // S_HEADS


def sparse_attention_stage(nc, core, I):
    with Stage(nc, "sparse") as st:
        w_qkv, w_g1, w_g2, w_o = (st.sb(n, s) for n, s in (
            ("w_qkv", [D + 1, 3 * D]), ("w_g1", [D + 1, 16]), ("w_g2", [17, 1]), ("w_o", [D + 1, D])))
        qkv = st.sb("qkv", [P, T, 3 * D])
        gT = st.sb("gT", [17, COLS])
        imp = st.sb("imp", [P, T])
        diag = st.sb("diag", [P, T, P])
        row = st.sb("row", [P, COLS])
        square = st.sb("square", [P, P])
        earlier = st.sb("earlier", [P, 2 * PAD - P])
        junk = st.sb("junk", [P, 2, SEQ])
        col, larger, ties = st.sb("col", [P, T]), st.sb("larger", [P, T]), st.sb("ties", [P, T])
        slots = st.sb("slots", [P, SLOT])
        pick = st.sb("pick", [P, T, 2, SLOT])
        k_mask, v_mask = st.sb("k_mask", [D, S_HEADS]), st.sb("v_mask", [P, S_HEADS // 2, 2, S_HD])
        kB = st.sb("kB", [D, B, S_HEADS * SLOT])
        vB = st.sb("vB", [P, B, D])
        qT = st.sb("qT", [D, COLS])
        attn = st.sb("attn", [P, T, D])
        load_stage(nc, "sparse_load", [(w_qkv[:, :], I["s_qkv"]), (w_g1[:, :], I["s_g1"]), (w_g2[:, :], I["s_g2"]),
                                       (w_o[:, :], I["s_out"])])
        consts = st.sem("consts")
        with nc.Block() as block:
            @block.gpsimd
            def _(pool):
                steps = Steps(pool, consts)
                steps.do(nc.gpsimd.memset(gT[:, :], 1.0))
                steps.do(nc.gpsimd.memset(square[:, :], 1.0))
                steps.do(nc.gpsimd.memset(earlier[:, :], 1.0))
                steps.do(nc.gpsimd.memset(k_mask[:, :], 1.0))
                steps.do(nc.gpsimd.memset(v_mask[:, :, :, :], 0.0))
                steps.do(nc.gpsimd.iota(slots[:, :], [[1, SLOT]], base=0, channel_multiplier=0,
                                        allow_small_or_imprecise_dtypes=True))
                steps.do(nc.gpsimd.memset(slots[:, KEEP:SLOT], -1.0))
                steps.do(nc.gpsimd.memset(v_mask[0:D, :, 0, :], 1.0))
                steps.do(nc.gpsimd.memset(v_mask[D:P, :, 1, :], 1.0))
                steps.do(nc.gpsimd.affine_select(out=earlier[:, :], in_=earlier[:, :], compare_op=ALU.is_gt, fill=0.0,
                                                 base=PAD - P, pattern=[[-1, 2 * PAD - P]], channel_multiplier=1))
                steps.do(nc.gpsimd.affine_select(out=k_mask[:, :], in_=k_mask[:, :], compare_op=ALU.is_ge, fill=0.0,
                                                 base=0, pattern=[[-S_HD, S_HEADS]], channel_multiplier=1))
                steps.do(nc.gpsimd.affine_select(out=k_mask[:, :], in_=k_mask[:, :], compare_op=ALU.is_ge, fill=0.0,
                                                 base=S_HD - 1, pattern=[[S_HD, S_HEADS]], channel_multiplier=-1))
        product_stage(nc, core, "sparse_qkv", [(lambda t: core.xnT[:, t * P:(t + 1) * P], w_qkv[:, :])], 3 * D,
                      lambda t0, t1, made: nc.scalar.activation(qkv[:, t0:t1, :], made, ACT.Copy), engine="scalar")
        wide_product_stage(nc, core, "sparse_g1", [(16, [(w_g1[:, :], lambda c0, c1: core.xnT[:, c0:c1])])],
                           lambda c0, c1, _, made: nc.scalar.activation(gT[0:16, c0:c1], made, ACT.Relu))
        product_stage(nc, core, "sparse_g2", [(lambda t: gT[:, t * P:(t + 1) * P], w_g2[:, :])], 1,
                      lambda t0, t1, made: nc.scalar.activation(imp[:, t0:t1], made.rearrange("p t w -> p (t w)"), ACT.Sigmoid),
                      engine="scalar")
        ps = core.psum
        vec, dg, spread, rowed, picked, made, done = (
            st.sem(n) for n in ("vector_steps", "diag_ready", "spread", "rowed", "picked", "made", "done"))
        with nc.Block() as block:
            @block.tensor
            def _(pe):
                pe.wait_ge(dg, 1)
                for g in range(GROUPS):
                    nc.tensor.matmul(ps[:, g, :], square[:, :], diag[:, 4 * g:4 * g + 4, :].rearrange("p t n -> p (t n)"),
                                     start=True, stop=True).then_inc(spread, 1)
                pe.wait_ge(picked, 1)
                pe.wait_ge(rowed, GROUPS)
                for b in range(B):
                    for c in range(CH):
                        t, r = b * CH + c, TOKEN_ROWS[c]
                        nc.tensor.matmul(ps[0:D, b, 0:SLOT], qkv[0:r, t, D:2 * D], pick[0:r, t, 0, :],
                                         start=(c == 0), stop=(c == CH - 1))
                    for c in range(CH):
                        t, r = b * CH + c, TOKEN_ROWS[c]
                        last = nc.tensor.matmul(ps[:, 4 + b, 0:D], pick[0:r, t, :, :].rearrange("p s n -> p (s n)"),
                                                qkv[0:r, t, 2 * D:3 * D], start=(c == 0), stop=(c == CH - 1))
                    last.then_inc(made, 1)

            @block.scalar
            def _(act):
                for g in range(GROUPS):
                    act.wait_ge(spread, g + 1)
                    nc.scalar.activation(row[:, g * BANK:(g + 1) * BANK], ps[:, g, :], ACT.Copy).then_inc(rowed, 1)

            @block.vector
            def _(dve):
                steps = Steps(dve, vec)
                nc.vector.tensor_tensor(diag[:, :, :], rows_of(core.ident[:, :], T), over(imp[:, :], P), ALU.mult
                                        ).then_inc(dg, 1)
                dve.wait_ge(rowed, GROUPS)
                steps.do(nc.vector.tensor_tensor(diag[:, :, :], row[:, :].rearrange("p (t n) -> p t n", n=P),
                                                 rows_of(core.ident[:, :], T), ALU.mult))
                steps.do(nc.vector.tensor_reduce(col[:, :], diag[:, :, :], AX.X, ALU.add))
                for b in range(B):
                    for c in range(CH):
                        t = b * CH + c
                        seq = row[:, b * PAD:b * PAD + SEQ]
                        shift = PAD - P - c * P
                        steps.add(nc.vector.tensor_scalar(junk[:, 0, :], seq, col[:, t:t + 1], 0.0, ALU.is_gt, ALU.add,
                                                          accum_out=larger[:, t:t + 1]))
                        steps.add(nc.vector.scalar_tensor_tensor(junk[:, 1, :], seq, col[:, t:t + 1], earlier[:, shift:shift + SEQ],
                                                                 ALU.is_equal, ALU.mult, accum_out=ties[:, t:t + 1]))
                        steps.settle()
                steps.do(nc.vector.tensor_tensor(larger[:, :], larger[:, :], ties[:, :], ALU.add))
                for s in range(2):
                    steps.add(nc.vector.tensor_tensor(pick[:, :, s, :], over(larger[:, :], SLOT), rows_of(slots[:, :], T),
                                                      ALU.is_equal))
                steps.settle()
                dve.sem_inc(picked, 1)
                for b in range(B):
                    dve.wait_ge(made, b + 1)
                    nc.vector.tensor_tensor(kB[:, b, :].rearrange("p (h s) -> p h s", s=SLOT),
                                            ps[0:D, b, 0:SLOT].unsqueeze(1).to_broadcast([D, S_HEADS, SLOT]),
                                            over(k_mask[:, :], SLOT), ALU.mult).then_inc(done, 1)
                    nc.vector.tensor_tensor(vB[:, b, :], ps[:, 4 + b, 0:D],
                                            v_mask[:, :, :, :].rearrange("p a s d -> p (a s d)"), ALU.mult).then_inc(done, 1)
        turn_stage(nc, core, "sparse_turn_q", [(qT, D, lambda t: qkv[:, t, 0:D])])
        with Stage(nc, "sparse_soft") as at:
            qt = at.sb("qt", [D, P])
            probs = at.sb("probs", [P, S_HEADS, SLOT])
            pT = at.sb("pT", [P, 4, P])
            stat = at.sb("stat", [P, 3, S_HEADS])
            (fetched, scored, shifted, exped, normed, turned, copied, weighed, kept, vec, zeroed, passed) = (
                at.sem(n) for n in ("fetched", "scored", "shifted", "exped", "normed", "turned", "copied", "weighed",
                                    "kept", "vector_steps", "zeroed", "passed"))
            start_loop(nc, [fetched, scored, shifted, exped, normed, turned, copied, weighed, kept])
            kB_flat, vB_flat = kB[:, :, :].rearrange("p b n -> p (b n)"), vB[:, :, :].rearrange("p b n -> p (b n)")
            real = lambda x: x[:, :, 0:KEEP]
            with nc.Block() as block:
                @block.tensor
                def _(pe):
                    with pe.Fori(0, B) as b:
                        with pe.Fori(0, CH) as c:
                            t = b * CH + c
                            pe.wait_ge(fetched, START + t + 1)
                            pe.wait_ge(shifted, START + t)
                            wait_apart(pe, passed)
                            nc.tensor.matmul(ps[:, 0, :], qt[:, :], kB_flat[:, bass.ds(b * S_HEADS * SLOT, BANK)],
                                             start=True, stop=True).then_inc(scored, 1)
                            pe.wait_ge(normed, START + t + 1)
                            pe.wait_ge(copied, START + t)
                            wait_apart(pe, passed)
                            for k in range(4):
                                last = nc.tensor.transpose(ps[:, 1, k * P:(k + 1) * P],
                                                           probs[:, 2 * k:2 * k + 2, :].rearrange("p h s -> p (h s)"),
                                                           core.ident[:, :])
                            last.then_inc(turned, 1)
                            pe.wait_ge(copied, START + t + 1)
                            pe.wait_ge(kept, START + t)
                            wait_apart(pe, passed)
                            for k in range(4):
                                last = nc.tensor.matmul(ps[:, 2, k * 2 * S_HD:(k + 1) * 2 * S_HD], pT[:, k, :],
                                                        vB_flat[:, bass.ds(b * D + k * 2 * S_HD, 2 * S_HD)],
                                                        start=True, stop=True)
                            last.then_inc(weighed, 1)

                @block.scalar
                def _(act):
                    with act.Fori(0, T) as t:
                        act.wait_ge(scored, START + t)
                        nc.scalar.activation(qt[:, :], qT[:, bass.ds(t * P, P)], ACT.Copy).then_inc(fetched, 1)
                        act.wait_ge(shifted, START + t + 1)
                        nc.scalar.activation(real(probs), real(probs), ACT.Exp, scale=S_HD ** -0.5).then_inc(exped, 1)
                        act.wait_ge(turned, START + t + 1)
                        act.wait_ge(weighed, START + t)
                        nc.scalar.activation(pT[:, :, :], ps[:, 1, :].rearrange("p (k n) -> p k n", n=P), ACT.Copy
                                             ).then_inc(copied, 1)
                        act.wait_ge(weighed, START + t + 1)
                        nc.scalar.activation(attn[:, bass.ds(t, 1), :], ps[:, 2, 0:D].unsqueeze(1), ACT.Copy).then_inc(kept, 1)

                @block.vector
                def _(dve):
                    steps = Steps(dve, vec)
                    steps.do(nc.vector.memset(probs[:, :, :], 0.0))
                    with dve.Fori(0, T) as t:
                        steps.enter_loop(t, 3)
                        s = ps[:, 0, :].rearrange("p (h s) -> p h s", s=SLOT)
                        dve.wait_ge(scored, START + t + 1)
                        steps.do(nc.vector.tensor_reduce(stat[:, 0, :], real(s), AX.X, ALU.max))
                        dve.wait_ge(turned, START + t)
                        nc.vector.tensor_tensor(real(probs), real(s), over(stat[:, 0, :], KEEP), ALU.subtract
                                                ).then_inc(shifted, 1)
                        dve.wait_ge(exped, START + t + 1)
                        steps.do(nc.vector.tensor_reduce(stat[:, 1, :], real(probs), AX.X, ALU.add))
                        steps.do(nc.vector.reciprocal(stat[:, 2, :], stat[:, 1, :]))
                        nc.vector.tensor_tensor(real(probs), real(probs), over(stat[:, 2, :], KEEP), ALU.mult
                                                ).then_inc(normed, 1)
        turn_stage(nc, core, "sparse_turn_o", [(core.xnT, D, lambda t: attn[:, t, :])])
        product_stage(nc, core, "sparse_out", [(lambda t: core.xnT[:, t * P:(t + 1) * P], w_o[:, :])], D,
                      lambda t0, t1, made: nc.vector.tensor_tensor(core.h[:, t0:t1, :], core.h[:, t0:t1, :], made, ALU.add))


DEPTH = 7
NODES = 2 ** (DEPTH + 1)
CHUNK = BANK // D
LEVELS = DEPTH + 1 - 3


def tree_stage(nc, core, I):
    with Stage(nc, "tree") as st:
        w_b = st.sb("w_b", [P, 2, D])
        logit = st.sb("logit", [P, T, NODES])
        on = st.sb("on", [P, T, NODES])
        gate = st.sb("gate", [P, T, DEPTH + 1])
        x12, x13 = st.sb("x12", [P, COLS], BF16), st.sb("x13", [P, COLS], BF16)
        with Stage(nc, "path") as at:
            w_n = at.sb("w_n", [D + 1, NODES])
            right = at.sb("right", [P, T, NODES])
            twice = at.sb("twice", [P, T, 2, D])
            xT2 = at.sb("xT2", [P, COLS])
            load_stage(nc, "tree_load", [(w_n[:, :], I["tree_w1"]),
                                         (w_b[:, :, :], I["tree_b2"].rearrange("(k p) d -> p k d", p=P))])
            product_stage(nc, core, "tree_logits", [(lambda t: core.xnT[:, t * P:(t + 1) * P], w_n[:, :])], NODES,
                          lambda t0, t1, made: nc.scalar.activation(logit[:, t0:t1, :], made, ACT.Copy), engine="scalar")
            vec, gelu, absed = (at.sem(n) for n in ("vector_steps", "gelu", "absed"))
            with nc.Block() as block:
                @block.gpsimd
                def _(pool):
                    for s in range(2):
                        nc.gpsimd.tensor_copy(twice[:, :, s, :], core.xn[:, :, :])

                @block.vector
                def _(dve):
                    steps = Steps(dve, vec)
                    steps.add(nc.vector.tensor_scalar(right[:, :, :], logit[:, :, :], 0.0, None, ALU.is_gt))
                    steps.add(nc.vector.memset(on[:, :, 0:1], 0.0))
                    steps.do(nc.vector.memset(on[:, :, 1:2], 1.0))
                    dve.sem_inc(absed, 1)
                    for level in range(DEPTH):
                        lo, n = 2 ** level, 2 ** level
                        child = on[:, :, 2 * lo:4 * lo].rearrange("p t (n s) -> p t n s", s=2)
                        steps.do(nc.vector.tensor_tensor(child[:, :, :, 1], on[:, :, lo:lo + n], right[:, :, lo:lo + n], ALU.mult))
                        steps.do(nc.vector.tensor_tensor(child[:, :, :, 0], on[:, :, lo:lo + n], child[:, :, :, 1], ALU.subtract))
                    dve.wait_ge(gelu, 2)
                    steps.do(nc.vector.tensor_tensor(logit[:, :, :], logit[:, :, :], on[:, :, :], ALU.mult))
                    for level in range(DEPTH + 1):
                        lo = 2 ** level
                        steps.add(nc.vector.tensor_reduce(gate[:, :, level], logit[:, :, lo:2 * lo], AX.X, ALU.add))

                @block.scalar
                def _(act):
                    act.wait_ge(absed, 1)
                    nc.scalar.activation(logit[:, :, :], logit[:, :, :], ACT.Abs).then_inc(gelu, 1)
                    act.wait_ge(gelu, 1)
                    nc.scalar.activation(logit[:, :, :], logit[:, :, :], ACT.Gelu).then_inc(gelu, 1)
            turn_stage(nc, core, "tree_turn", [(xT2, P, lambda t: twice[:, t, :, :].rearrange("p s d -> p (s d)"))])
            split_tokens_stage(nc, "tree_split", xT2[:, :], x12, x13)
        w11, w22, w31 = (st.sb(n, [P, NODES * D], BF16) for n in ("w11", "w22", "w31"))
        split_weights_stage(nc, "tree_weights", I["tree_w2"], w11, w22, w31, 4 * BANK)
        tree_sum_stage(nc, core, logit, on, gate, ((x12, w11), (x12, w22), (x13, w31)), w_b)


def tree_sum_stage(nc, core, weight, on, gate, products, w_b):
    with Stage(nc, "leaf") as st:
        ws = st.sb("ws", [P, NODES])
        path = st.sb("path", [P, 2, NODES])
        wT = st.sb("wT", [P, 2, P])
        acc = st.sb("acc", [P, 2, LEVELS + 1, CHUNK, D])
        total = st.sb("total", [P, 2, D])
        passed_v = st.sem("passed_by_vector")
        fetched, masked, made, taken, turned, turned_copied, biased, scaled, vec, passed, added = (
            st.sem(n) for n in ("fetched", "masked", "made", "taken", "turned", "turned_copied", "biased", "scaled",
                                "vector_steps", "passed", "added"))
        start_loop(nc, [fetched, masked, made, taken, turned, turned_copied, biased, scaled, added])
        ps = core.psum
        C = NODES // CHUNK
        BANKS = 6
        first = {2 ** (3 + k) // CHUNK: k for k in range(LEVELS)}
        with nc.Block() as block:
            @block.tensor
            def _(pe):
                def bias(t):
                    pe.wait_ge(turned_copied, START + t + 1)
                    pe.wait_ge(added, START + t)
                    wait_apart(pe, passed)
                    for k in range(2):
                        last = nc.tensor.matmul(ps[:, 7, 0:D], wT[:, k, :], w_b[:, k, :], start=(k == 0), stop=(k == 1))
                    last.then_inc(biased, 1)

                def tile(t, before):
                    for c in range(C):
                        pe.wait_ge(taken, START + C * t + c - BANKS + 1 if c >= BANKS else START + C * t)
                        wait_apart(pe, passed)
                        for k, (x, w) in enumerate(products):
                            last = nc.tensor.matmul(ps[:, c % BANKS, :], x[:, bass.ds(t * P, P)], w[:, c * BANK:(c + 1) * BANK],
                                                    start=(k == 0), stop=(k == len(products) - 1))
                        last.then_inc(made, 1)
                        if before and c == BANKS:
                            bias(t - 1)
                        if c == 2 * BANKS:
                            pe.wait_ge(fetched, START + t + 1)
                            pe.wait_ge(turned_copied, START + t)
                            wait_apart(pe, passed)
                            for k in range(2):
                                last = nc.tensor.transpose(ps[:, 6, k * P:(k + 1) * P], ws[:, k * P:(k + 1) * P], core.ident[:, :])
                            last.then_inc(turned, 1)

                tile(0, False)
                with pe.Fori(1, T) as t:
                    tile(t, True)
                bias(T - 1)

            @block.scalar
            def _(act):
                with act.Fori(0, T // 2) as j:
                    for u in range(2):
                        t = 2 * j + u
                        act.wait_ge(turned, START + t)
                        nc.scalar.activation(ws[:, :].unsqueeze(1), weight[:, bass.ds(t, 1), :], ACT.Copy).then_inc(fetched, 1)
                        act.wait_ge(taken, START + C * t)
                        nc.scalar.activation(path[:, u, :].unsqueeze(1), on[:, bass.ds(t, 1), :], ACT.Copy).then_inc(masked, 1)
                        act.wait_ge(turned, START + t + 1)
                        act.wait_ge(biased, START + t)
                        nc.scalar.activation(wT[:, :, :], ps[:, 6, 0:2 * P].rearrange("p (k n) -> p k n", n=P), ACT.Copy
                                             ).then_inc(turned_copied, 1)

            @block.gpsimd
            def _(pool):
                with pool.Fori(0, T // 2) as j:
                    for u in range(2):
                        t = 2 * j + u
                        pool.wait_ge(taken, START + C * (t + 1))
                        for k in range(LEVELS):
                            level = acc[:, u, k + 1, :, :].rearrange("p c d -> p (c d)")
                            nc.gpsimd.tensor_tensor(level, level, gate[:, bass.ds(t, 1), k + 3].to_broadcast([P, CHUNK * D]),
                                                    ALU.mult).then_inc(scaled, 1)

            @block.vector
            def _(dve):
                steps = Steps(dve, vec)

                def take(t, u):
                    dve.wait_ge(masked, START + t + 1)
                    for c in range(C):
                        dve.wait_ge(made, START + C * t + c + 1)
                        if c >= 1:
                            dve.wait_ge(taken, START + C * t + c)
                        wait_apart(dve, passed_v)
                        bank = ps[:, c % BANKS, :].rearrange("p (c d) -> p c d", d=D)
                        if c == 0:
                            ins = nc.vector.tensor_tensor(acc[:, u, 0, :, :], bank,
                                                          over(weight[:, bass.ds(t, 1), 0:CHUNK].rearrange("p t n -> p (t n)"), D), ALU.mult)
                        else:
                            level = max(k for f, k in first.items() if f <= c)
                            mask = path[:, u, c * CHUNK:(c + 1) * CHUNK]
                            if c in first:
                                ins = nc.vector.tensor_tensor(acc[:, u, level + 1, :, :], bank, over(mask, D), ALU.mult)
                            else:
                                ins = nc.vector.copy_predicated(acc[:, u, level + 1, :, :], over(mask.bitcast(U32), D), bank)
                        ins.then_inc(taken, 1)

                def finish(t, u):
                    steps.before, steps.count = 2 * t, 0
                    dve.wait_ge(scaled, START + LEVELS * (t + 1))
                    steps.do(nc.vector.tensor_reduce(total[:, 0, :], acc[:, u, :, :, :].rearrange("p l c d -> p d (l c)"),
                                                     AX.X, ALU.add))
                    dve.wait_ge(biased, START + t + 1)
                    steps.do(nc.vector.tensor_tensor(total[:, 1, :], ps[:, 7, 0:D], total[:, 0, :], ALU.add))
                    nc.vector.tensor_tensor(core.h[:, bass.ds(t, 1), :], core.h[:, bass.ds(t, 1), :],
                                            total[:, 1, :].unsqueeze(1), ALU.add).then_inc(added, 1)

                take(0, 0)
                take(1, 1)
                finish(0, 0)
                with dve.Fori(1, T // 2) as j:
                    take(2 * j, 0)
                    finish(2 * j - 1, 1)
                    take(2 * j + 1, 1)
                    finish(2 * j, 0)
                finish(T - 1, 1)


def sigmoid_attention_stage(nc, core, I):
    with Stage(nc, "sig") as st:
        w = st.sb("w", [D, D])
        qT = st.sb("qT", [D, COLS])
        keys = st.sb("keys", [D, PAD])
        att = st.sb("att", [P, CH, PAD])
        load_stage(nc, "sig_load", [(w[:, :], I["sig_w"])])
        wide_product_stage(nc, core, "sig_q", [(D, [(w[:, :], lambda c0, c1: core.xnT[0:D, c0:c1])])],
                           lambda c0, c1, _, made: nc.scalar.activation(qT[:, c0:c1], made, ACT.Copy))
        set_stage(nc, "att_zero", [(att[:, :, :], 0.0)])
        fetched, scored, attended, weighed, added, passed = (
            st.sem(n) for n in ("fetched", "scored", "attended", "weighed", "added", "passed"))
        start_loop(nc, [fetched, scored, attended, weighed, added])
        ps = core.psum
        side = SEQ // 2
        with nc.Block() as block:
            @block.tensor
            def _(pe):
                with pe.Fori(0, B) as b:
                    pe.wait_ge(fetched, START + b + 1)
                    for m in range(CH):
                        if m >= 2:
                            pe.wait_ge(attended, START + CH * b + m - 1)
                        else:
                            pe.wait_ge(attended, START + CH * b)
                        wait_apart(pe, passed)
                        for s in range(2):
                            last = nc.tensor.matmul(ps[:, 2 * (m % 2) + s, 0:side], keys[:, m * P:(m + 1) * P],
                                                    qT[:, bass.ds(b * PAD + s * side, side)], start=True, stop=True)
                        last.then_inc(scored, 1)
                    pe.wait_ge(attended, START + CH * b + CH)
                    pe.wait_ge(added, START + b)
                    wait_apart(pe, passed)
                    for c in range(CH):
                        for m in range(CH):
                            r = TOKEN_ROWS[m]
                            last = nc.tensor.matmul(ps[:, 4, c * D:(c + 1) * D], att[0:r, m, c * P:(c + 1) * P],
                                                    core.xn[0:r, bass.ds(b * CH + m, 1), :].rearrange("p t d -> p (t d)"),
                                                    start=(m == 0), stop=(m == CH - 1))
                    last.then_inc(weighed, 1)

            @block.scalar
            def _(act):
                with act.Fori(0, B) as b:
                    act.wait_ge(scored, START + CH * b)
                    nc.scalar.activation(keys[:, :], core.xnT[0:D, bass.ds(b * PAD, PAD)], ACT.Copy).then_inc(fetched, 1)
                    act.wait_ge(weighed, START + b)
                    for m in range(CH):
                        r = TOKEN_ROWS[m]
                        act.wait_ge(scored, START + CH * b + m + 1)
                        nc.scalar.activation(att[0:r, m, 0:SEQ].rearrange("p (s n) -> p s n", s=2),
                                             ps[0:r, 2 * (m % 2):2 * (m % 2) + 2, 0:side], ACT.Sigmoid).then_inc(attended, 1)

            @block.vector
            def _(dve):
                with dve.Fori(0, B) as b:
                    dve.wait_ge(weighed, START + b + 1)
                    full = core.h[:, bass.ds(b * CH, CH - 1), :]
                    nc.vector.tensor_tensor(full, full, ps[:, 4, 0:(CH - 1) * D].rearrange("p (c d) -> p c d", d=D), ALU.add)
                    tail = core.h[0:TAIL, bass.ds(b * CH + CH - 1, 1), :]
                    nc.vector.tensor_tensor(tail, tail, ps[0:TAIL, 4, (CH - 1) * D:CH * D].unsqueeze(1), ALU.add
                                            ).then_inc(added, 1)


R_EXPERTS = 4


def relu_experts_stage(nc, core, I):
    with Stage(nc, "mlp") as st:
        E = R_EXPERTS
        w_g = st.sb("w_g", [D + 1, E])
        router, weight = st.sb("router", [P, T, E]), st.sb("weight", [P, T, E])
        s1, s2, s3 = st.sb("s1", [D + 1, D]), st.sb("s2", [D + 1, P]), st.sb("s3", [P, D])
        s3b = st.sb("s3b", [1, D])
        e1, e2, e3 = st.sb("e1", [D + 1, E, P]), st.sb("e2", [P, E, D]), st.sb("e3", [D + 1, E, D])
        e2b = st.sb("e2b", [D, E])
        h1, h2 = st.sb("h1", [P, 2, BANK]), st.sb("h2", [P, 2, BANK])
        g1, g2 = st.sb("g1", [D + 1, BANK]), st.sb("g2", [P, BANK])
        part = st.sb("part", [P, 2, 4, D])
        load_stage(nc, "mlp_load", [(w_g[:, :], I["m_gate"]), (s1[:, :], I["m_s1"]), (s2[:, :], I["m_s2"]),
                                    (s3[:, :], I["m_s3"]), (s3b[:, :], I["m_s3b"]), (e1[:, :, :], I["m_e1"]),
                                    (e2[:, :, :], I["m_e2"]), (e3[:, :, :], I["m_e3"]), (e2b[:, :], I["m_e2b"])])
        set_stage(nc, "mlp_ones", [(h2[:, :, :], 1.0), (g1[:, :], 1.0)])
        product_stage(nc, core, "mlp_gate", [(lambda t: core.xnT[:, t * P:(t + 1) * P], w_g[:, :])], E,
                      lambda t0, t1, made: nc.vector.tensor_copy(router[:, t0:t1, :], made))
        top_two_stage(nc, core, "mlp_top", router[:, :, :], weight[:, :, :], E, "softmax")
        up1, act1, up2, act2, down, taken, added, passed = (
            st.sem(n) for n in ("up1", "act1", "up2", "act2", "down", "taken", "added", "passed"))
        start_loop(nc, [up1, act1, up2, act2, down, taken, added])
        ps = core.psum
        N = E + 1
        with nc.Block() as block:
            @block.tensor
            def _(pe):
                with pe.Fori(0, GROUPS) as g:
                    cols = core.xnT[:, bass.ds(g * BANK, BANK)]

                    def first_layer(e):
                        pe.wait_ge(act1, START + N * g + max(e - 1, 0))
                        wait_apart(pe, passed)
                        rows = P if e < E else D
                        nc.tensor.matmul(ps[0:rows, e % 2, :], e1[:, e, :] if e < E else s1[:, :], cols,
                                         start=True, stop=True).then_inc(up1, 1)

                    first_layer(0)
                    for e in range(N):
                        n = N * g + e
                        if e + 1 < N:
                            first_layer(e + 1)
                        pe.wait_ge(act1, START + n + 1)
                        pe.wait_ge(act2, START + N * g + max(e - 1, 0))
                        wait_apart(pe, passed)
                        if e < E:
                            last = nc.tensor.matmul(ps[0:D, 2 + e % 2, :], e2[:, e, :], h1[:, e % 2, :], start=True, stop=True)
                        else:
                            last = nc.tensor.matmul(ps[:, 2 + e % 2, :], s2[:, :], g1[:, :], start=True, stop=True)
                        last.then_inc(up2, 1)
                        pe.wait_ge(act2, START + n + 1)
                        pe.wait_ge(taken, START + N * g + max(e - 1, 0))
                        wait_apart(pe, passed)
                        for k in range(4):
                            out = ps[:, 4 + e % 2, k * D:(k + 1) * D]
                            if e < E:
                                last = nc.tensor.matmul(out, h2[0:D + 1, e % 2, k * P:(k + 1) * P], e3[:, e, :],
                                                        start=True, stop=True)
                            else:
                                nc.tensor.matmul(out, g2[:, k * P:(k + 1) * P], s3[:, :], start=True, stop=False)
                                last = nc.tensor.matmul(out, core.ones[:, :], s3b[:, :], start=False, stop=True)
                        last.then_inc(down, 1)

            @block.scalar
            def _(act):
                with act.Fori(0, GROUPS) as g:
                    for e in range(N):
                        n = N * g + e
                        act.wait_ge(up1, START + n + 1)
                        act.wait_ge(up2, START + N * g + max(e - 1, 0))
                        if e < E:
                            ins = nc.scalar.activation(h1[:, e % 2, :], ps[:, e % 2, :], ACT.Relu)
                        else:
                            ins = nc.scalar.activation(g1[0:D, :], ps[0:D, e % 2, :], ACT.Relu)
                        ins.then_inc(act1, 1)
                        act.wait_ge(up2, START + n + 1)
                        act.wait_ge(down, START + N * g + max(e - 1, 0))
                        if e < E:
                            ins = nc.scalar.activation(h2[0:D, e % 2, :], ps[0:D, 2 + e % 2, :], ACT.Relu, bias=e2b[:, e:e + 1])
                        else:
                            ins = nc.scalar.activation(g2[:, :], ps[:, 2 + e % 2, :], ACT.Relu)
                        ins.then_inc(act2, 1)

            @block.vector
            def _(dve):
                with dve.Fori(0, GROUPS) as g:
                    tiles = core.h[:, bass.ds(4 * g, 4), :]
                    for e in range(N):
                        n = N * g + e
                        dve.wait_ge(down, START + n + 1)
                        dve.wait_ge(added, START + N * g + max(e - 1, 0))
                        made = ps[:, 4 + e % 2, 0:4 * D].rearrange("p (t d) -> p t d", d=D)
                        if e < E:
                            ins = nc.vector.tensor_tensor(part[:, e % 2, :, :], made,
                                                          over(weight[:, bass.ds(4 * g, 4), e], D), ALU.mult)
                        else:
                            ins = nc.vector.tensor_copy(part[:, e % 2, :, :], made)
                        ins.then_inc(taken, 1)
                        dve.wait_ge(taken, START + n + 1)
                        dve.wait_ge(added, START + n)
                        nc.vector.tensor_tensor(tiles, tiles, part[:, e % 2, :, :], ALU.add).then_inc(added, 1)


def store_stage(nc, core, out):
    with Stage(nc, "store") as st:
        stored = st.sem("stored")
        h_b = core.h[:, :, :].rearrange("p (b c) d -> p b c d", c=CH)
        with nc.Block() as block:
            @block.sync
            def _(sp):
                for b in range(B):
                    sp.dma_start(out[b, 0:4 * P, :].rearrange("(c p) d -> p c d", p=P), h_b[:, b, 0:4, :]).then_inc(stored, 16)
                    sp.dma_start(out[b, 4 * P:SEQ, :], h_b[0:TAIL, b, 4, :]).then_inc(stored, 16)
                sp.wait_ge(stored, 16 * 2 * B)


def build(nc, I, out):
    core = Core()
    Stage.spent.clear()
    with ExitStack() as stack:
        sb = lambda name, shape: stack.enter_context(nc.sbuf_tensor(name, shape, F32))
        core.h = sb("h", [P, T, D])
        core.xn = sb("xn", [P, T, D])
        core.xnT = sb("xnT", [D + 1, COLS])
        core.ident = sb("ident", [P, P])
        core.ones = sb("ones", [1, P])
        core.psum = stack.enter_context(nc.psum_tensor("psum", [P, 8, BANK], F32))
        set_stage(nc, "ones", [(core.ones[:, :], 1.0)])
        embed_stage(nc, core, I["x_patches"], I["txt"], I["tok_aug"])
        layers = [linear_attention_stage, retrieval_stage, toeplitz_stage, rotary_experts_stage,
                  sparse_attention_stage, tree_stage, sigmoid_attention_stage, relu_experts_stage]
        for n, layer in enumerate(layers):
            norm_stage(nc, core, f"norm{n}", core.h)
            layer(nc, core, I)
        store_stage(nc, core, out)


def transform_tables():
    lag = np.concatenate([np.arange(SEQ), [0], np.arange(1 - SEQ, 0)]).astype(np.float32)
    n, f = np.arange(SPAN), np.arange(FREQ)
    angle = 2 * np.pi * (np.outer(n, f) % SPAN) / SPAN
    twice = np.where((f == 0) | (f == SEQ), 1.0, 2.0)[:, None] / SPAN
    back = angle[:SEQ].T
    tables = {"cos": np.cos(angle), "sin": -np.sin(angle), "icos": twice * np.cos(back), "isin": -twice * np.sin(back)}
    return {"lags": np.stack([lag, np.ones_like(lag)]), **{k: v.astype(np.float32) for k, v in tables.items()}}


def rotary_weights(wq, wk, wv):
    q = wq.T.reshape(D, Q_HEADS, HD)
    k, v = (w.T.reshape(D, Q_HEADS // 2, HD).repeat(2, axis=1) for w in (wk, wv))
    swap = np.roll(np.arange(HD), HD // 2)
    return np.concatenate([q, k, q[:, :, swap], k[:, :, swap], v], axis=1).reshape(D, 5 * D)


def rotary_tables():
    frequency = 1.0 / 10000.0 ** (np.arange(0, HD, 2, dtype=np.float32) / HD)
    angle = np.outer(np.arange(PAD, dtype=np.float32), frequency)
    angle = np.concatenate([angle, angle], axis=-1)
    sign = np.where(np.arange(HD) < HD // 2, -1.0, 1.0)
    return {"rot_cos": np.cos(angle).astype(np.float32), "rot_sin": (np.sin(angle) * sign).astype(np.float32)}


def tree_weights(w1, b1, w2, b2):
    first = lambda a: np.concatenate([np.zeros_like(a[:1]), a], axis=0)
    w1, b1, w2, b2 = (first(a) for a in (w1, b1, w2, b2))
    return {"tree_w1": np.concatenate([w1.T, b1[None]], axis=0), "tree_w2": w2.transpose(1, 0, 2).reshape(D, NODES * D),
            "tree_b2": b2}


def pk_blocks(keys):
    k = keys.reshape(2, KEYS, 2, 4, D // 2)
    blocks = np.zeros((4, D // 2, 2, 2, 4, KEYS), keys.dtype)
    for h in range(4):
        blocks[h, :, :, :, h, :] = k[:, :, :, h, :].transpose(3, 0, 2, 1)
    return blocks.reshape(P, 4, 4 * KEYS)


def lay_out(a):
    g = {k: np.asarray(v) for k, v in a.items()}
    join = lambda w, b: np.concatenate([w, b.reshape(1, -1)], axis=0)
    x = g["x"].reshape(B, 8, 8, 8, 8)
    return {
        "x_patches": x.transpose(2, 4, 0, 1, 3).reshape(D, B * PATCHES),
        "txt": g["txt"],
        "tok_aug": join(g["L0_tok_W"].T, g["L0_tok_b"]),
        "qkv_aug": join(g["L0_attn_qkv_w"], g["L0_attn_qkv_b"]),
        "proj_aug": join(g["L0_attn_proj_w"], g["L0_attn_proj_b"]),
        "ln1_g": g["L0_attn_ln1_g"], "ln1_b": g["L0_attn_ln1_b"],
        "ln2_g": g["L0_attn_ln2_g"], "ln2_b": g["L0_attn_ln2_b"],
        "w1_aug": join(g["L0_attn_w1"], g["L0_attn_b1"]),
        "w2": g["L0_attn_w2"], "b2": g["L0_attn_b2"],
        "uv_aug": np.concatenate([join(g["L1_attn_u_w"].T, g["L1_attn_u_b"]), join(g["L1_attn_v_w"].T, g["L1_attn_v_b"])], axis=1),
        "o_aug": join(g["L1_attn_o_w"].T, g["L1_attn_o_b"]),
        "t_aug": join(g["L1_attn_t_w"].T, g["L1_attn_t_b"]),
        "pos_aug": join(g["L1_attn_pos_w"].T, g["L1_attn_pos_b"]),
        "rpe_aug": np.concatenate([g["L1_attn_rpe_lw"].transpose(2, 0, 1), g["L1_attn_rpe_lb"][None]], axis=0),
        "out_aug": join(g["L1_attn_out_w"].T, g["L1_attn_out_b"]),
        **transform_tables(),
        "rms1_w": g["L1_ffn_ln1_w"], "rms2_w": g["L1_ffn_ln2_w"],
        "rot_in": rotary_weights(g["L1_ffn_wq"], g["L1_ffn_wk"], g["L1_ffn_wv"]),
        "rot_out": g["L1_ffn_wo"].T,
        **rotary_tables(),
        "router": g["L1_ffn_router_w"].T,
        "moe_w13": np.concatenate([g[k].reshape(EXPERTS * HIDDEN, D).T for k in ("L1_ffn_w1", "L1_ffn_w3")], axis=1),
        "moe_w2": g["L1_ffn_w2"].transpose(0, 2, 1).reshape(EXPERTS * HIDDEN, D),
        "s_qkv": join(g["L2_attn_w_in"].T, g["L2_attn_b_in"]),
        "s_g1": join(g["L2_attn_gate_w1"].T, g["L2_attn_gate_b1"]),
        "s_g2": join(g["L2_attn_gate_w2"].T, g["L2_attn_gate_b2"]),
        "s_out": join(g["L2_attn_w_out"].T, g["L2_attn_b_out"]),
        **tree_weights(g["L2_ffn_w1s"], g["L2_ffn_b1s"], g["L2_ffn_w2s"], g["L2_ffn_b2s"]),
        "sig_w": g["L3_attn_q_weight"],
        "m_gate": join(g["L3_ffn_gW"], g["L3_ffn_gb"]),
        "m_s1": join(g["L3_ffn_sW1"], g["L3_ffn_sb1"]), "m_s2": join(g["L3_ffn_sW2"], g["L3_ffn_sb2"]),
        "m_s3": g["L3_ffn_sW3"], "m_s3b": g["L3_ffn_sb3"].reshape(1, D),
        "m_e1": np.concatenate([g["L3_ffn_eW1"].transpose(1, 0, 2), g["L3_ffn_eb1"][None]], axis=0),
        "m_e2": g["L3_ffn_eW2"].transpose(1, 0, 2), "m_e2b": g["L3_ffn_eb2"].T,
        "m_e3": np.concatenate([g["L3_ffn_eW3"].transpose(1, 0, 2), g["L3_ffn_eb3"][None]], axis=0),
        "w_pk": g["L0_ffn_Wq_pk"], "w_q": g["L0_ffn_Wq"], "w_o": g["L0_ffn_Wo"],
        "pk_blocks": pk_blocks(g["L0_ffn_pk_keys"]),
        "table": np.concatenate([g["L0_ffn_keys_table"], g["L0_ffn_values_table"]], axis=1),
    }


def kernel(**inputs):
    import concourse.bacc as _bacc
    from concourse.bass_utils import run_bass_kernel_spmd as _run

    nc = _bacc.Bacc("TRN2", target_bir_lowering=False, num_devices=1)
    arrays = {f"in_{k}": np.ascontiguousarray(v) for k, v in lay_out(inputs).items()}
    I = {k[3:]: nc.dram_tensor(k, v.shape, mybir.dt.from_np(v.dtype), kind="ExternalInput").ap() for k, v in arrays.items()}
    out = nc.dram_tensor("out", (B, SEQ, D), F32, kind="ExternalOutput").ap()
    build(nc, I, out)
    return _run(nc, [arrays], core_ids=[0]).results[0]["out"]
```

```python
from contextlib import ExitStack

import numpy as np

import concourse.bass as bass
from concourse import mybir
from concourse.alu_op_type import AluOpType as ALU

F32 = mybir.dt.float32
U32 = mybir.dt.uint32
BF16 = mybir.dt.bfloat16
ACT = mybir.ActivationFunctionType
AX = mybir.AxisListType

P = 128
B = 4
PATCHES = 64
TEXT = 512
SEQ = PATCHES + TEXT
D = 64
CH = 5
PAD = CH * P
TAIL = SEQ - 4 * P
T = B * CH
COLS = T * P
BANK = 512
GROUPS = COLS // BANK
LN_EPS = 1e-5
NEG = -1e30


class Steps:

    def __init__(self, engine, semaphore):
        self.engine, self.semaphore, self.before, self.count = engine, semaphore, 0, 0

    def add(self, instruction):
        instruction.then_inc(self.semaphore, 1)
        self.count += 1

    def settle(self, apart=None):
        self.engine.wait_ge(self.semaphore, self.before + self.count)
        if apart is not None:
            wait_apart(self.engine, apart)

    def do(self, instruction):
        self.add(instruction)
        self.settle()

    def enter_loop(self, turn, per_turn):
        self.outside = self.before + self.count
        self.before, self.count, self.per_turn = turn * per_turn + self.outside, 0, per_turn

    def leave_loop(self, turns):
        assert self.count == self.per_turn, (self.count, self.per_turn)
        self.before, self.count = self.outside + turns * self.per_turn, 0


def wait_apart(engine, passed):
    engine.sem_inc(passed, 1)


class Stage:

    SPENT_MAX = 90
    spent = []

    def __init__(self, nc, name):
        self.nc, self.name, self.sems = nc, name, []

    def __enter__(self):
        self.stack = ExitStack()
        return self

    def __exit__(self, *problem):
        self.stack.close()
        Stage.spent += self.sems
        if not problem[0] and len(Stage.spent) >= self.SPENT_MAX:
            self.nc.clear_and_free_semaphores(Stage.spent)
            Stage.spent.clear()
            self.nc.all_engine_barrier()

    def sb(self, name, shape, dtype=F32):
        return self.stack.enter_context(self.nc.sbuf_tensor(f"{self.name}_{name}", shape, dtype))

    def sem(self, name):
        s = self.nc.alloc_semaphore(f"{self.name}_{name}")
        self.sems.append(s)
        return s


class Core:
    pass


START = 1


def start_loop(nc, semaphores, value=START):
    with nc.Block() as block:
        @block.sync
        def _(sp):
            for s in semaphores:
                sp.sem_inc(s, value)


def over(ap, n):
    return ap.unsqueeze(len(ap.shape)).to_broadcast([*ap.shape, n])


def rows_of(ap, n):
    return ap.unsqueeze(1).to_broadcast([ap.shape[0], n, *ap.shape[1:]])


def load_stage(nc, name, loads):
    with Stage(nc, name) as st:
        landed = st.sem("landed")
        with nc.Block() as block:
            @block.sync
            def _(sp):
                for to, of in loads:
                    sp.dma_start(to, of).then_inc(landed, 16)
                sp.wait_ge(landed, 16 * len(loads))


class Loads:

    def __init__(self, nc, st, name, loads):
        self.nc, self.total = nc, 16 * len(loads)
        self.landed = st.sem(name)
        with nc.Block() as block:
            @block.sync
            def _(sp):
                for to, of in loads:
                    sp.dma_start(to, of).then_inc(self.landed, 16)

    def arrive(self):
        with self.nc.Block() as block:
            @block.sync
            def _(sp):
                sp.wait_ge(self.landed, self.total)


def embed_stage(nc, core, x_patches, txt, w_patch):
    with Stage(nc, "embed") as st:
        pixels = st.sb("pixels", [D + 1, B * PATCHES])
        weights = st.sb("weights", [D + 1, D])
        ones_set, landed, products, text_landed, copied = (
            st.sem(n) for n in ("ones_set", "landed", "products", "text_landed", "copied"))
        h_b = core.h[:, :, :].rearrange("p (b c) d -> p b c d", c=CH)
        with nc.Block() as block:
            @block.sync
            def _(sp):
                sp.wait_ge(ones_set, 2)
                sp.dma_start(pixels[0:D, :], x_patches).then_inc(landed, 16)
                sp.dma_start(weights[:, :], w_patch).then_inc(landed, 16)
                for b in range(B):
                    sp.dma_start(h_b[PATCHES:P, b, 0, :], txt[b, 0:P - PATCHES, :]).then_inc(text_landed, 16)
                    sp.dma_start(h_b[:, b, 1:CH - 1, :],
                                 txt[b, P - PATCHES:TEXT - TAIL, :].rearrange("(c p) d -> p c d", p=P)
                                 ).then_inc(text_landed, 16)
                    sp.dma_start(h_b[0:TAIL, b, CH - 1, :], txt[b, TEXT - TAIL:TEXT, :]).then_inc(text_landed, 16)
                sp.wait_ge(text_landed, 16 * 3 * B)

            @block.gpsimd
            def _(pool):
                nc.gpsimd.memset(pixels[:, :], 1.0).then_inc(ones_set, 1)
                nc.gpsimd.memset(core.h[:, :, :], 0.0).then_inc(ones_set, 1)
                nc.gpsimd.memset(core.xnT[:, :], 1.0).then_inc(ones_set, 1)
                nc.gpsimd.memset(core.ident[:, :], 0.0).then_inc(ones_set, 1)
                pool.wait_ge(ones_set, 4)
                nc.gpsimd.affine_select(out=core.ident[:, :], in_=core.ident[:, :], compare_op=ALU.not_equal,
                                        fill=1.0, base=0, pattern=[[-1, P]], channel_multiplier=1)

            @block.tensor
            def _(pe):
                pe.wait_ge(landed, 32)
                for b in range(B):
                    last = nc.tensor.matmul(core.psum[0:PATCHES, 0, b * D:(b + 1) * D],
                                            pixels[:, b * PATCHES:(b + 1) * PATCHES], weights[:, :],
                                            start=True, stop=True)
                last.then_inc(products, 1)

            @block.vector
            def _(dve):
                dve.wait_ge(products, 1)
                dve.wait_ge(ones_set, 4)
                nc.vector.tensor_copy(h_b[0:PATCHES, :, 0, :],
                                      core.psum[0:PATCHES, 0, 0:B * D].rearrange("p (b d) -> p b d", d=D)
                                      ).then_inc(copied, 1)


def norm_steps(nc, steps, dve, x, out, sq, stat, std_ready, var_ready, eps, use_mean=True, groups=None):
    width = x.shape[-1]
    if use_mean:
        steps.do(nc.vector.tensor_reduce(stat[:, 0, :], x, AX.X, ALU.add))
        steps.do(nc.vector.tensor_scalar(stat[:, 0, :], stat[:, 0, :], 1.0 / width, None, ALU.mult))
        steps.do(nc.vector.tensor_tensor(out, x, over(stat[:, 0, :], width), ALU.subtract))
        x = out
    steps.do(nc.vector.tensor_tensor(sq, x, x, ALU.mult))
    steps.do(nc.vector.tensor_reduce(stat[:, 1, :], sq, AX.X, ALU.add))
    nc.vector.tensor_scalar(stat[:, 1, :], stat[:, 1, :], 1.0 / width, eps, ALU.mult, ALU.add).then_inc(var_ready, 1)
    dve.wait_ge(std_ready, 1)
    steps.do(nc.vector.reciprocal(stat[:, 3, :], stat[:, 2, :]))
    if groups is None:
        steps.do(nc.vector.tensor_tensor(out, x, over(stat[:, 3, :], width), ALU.mult))
    else:
        for lo in range(0, T, 4):
            hi = lo + 4
            steps.do(nc.vector.tensor_tensor(out[:, lo:hi, :], x[:, lo:hi, :], over(stat[:, 3, lo:hi], width), ALU.mult))
            groups(lo, hi)


def norm_stage(nc, core, name, src, eps=LN_EPS, use_mean=True, gain=None, shift=None, first=None,
               dst=None, turn=True):
    dst = core.xn if dst is None else dst
    with Stage(nc, name) as st:
        sq = st.sb("sq", [P, T, D])
        stat = st.sb("stat", [P, 4, T])
        stat2 = st.sb("stat2", [P, 4, T])
        rows = st.sb("rows", [P, 2, D])
        vec, var, std, var2, std2, ready, turned, drained, landed = (
            st.sem(n) for n in ("vector_steps", "var_ready", "std_ready", "var2_ready", "std2_ready",
                                "dst_ready", "turned", "drained", "rows_landed"))
        vecs = [v for v in (gain, shift) if v is not None]
        with nc.Block() as block:
            @block.sync
            def _(sp):
                for k, v in enumerate(vecs):
                    sp.dma_start(rows[:, k, :], v.partition_broadcast(P)).then_inc(landed, 16)

            @block.vector
            def _(dve):
                steps = Steps(dve, vec)

                if first is not None:
                    norm_steps(nc, steps, dve, src[:, :, :], first[:, :, :], sq[:, :, :], stat2, std2, var2, LN_EPS)
                norm_steps(nc, steps, dve, (src if first is None else first)[:, :, :], dst[:, :, :], sq[:, :, :], stat,
                           std, var, eps, use_mean, None if vecs else lambda lo, hi: dve.sem_inc(ready, 1))
                if vecs:
                    dve.wait_ge(landed, 16 * len(vecs))
                    for k, op in zip(range(len(vecs)), (ALU.mult, ALU.add)):
                        steps.do(nc.vector.tensor_tensor(dst[:, :, :], dst[:, :, :], rows_of(rows[:, k, :], T), op))
                    dve.sem_inc(ready, GROUPS)

            @block.scalar
            def _(act):
                if first is not None:
                    act.wait_ge(var2, 1)
                    nc.scalar.activation(stat2[:, 2, :], stat2[:, 1, :], ACT.Sqrt).then_inc(std2, 1)
                act.wait_ge(var, 1)
                nc.scalar.activation(stat[:, 2, :], stat[:, 1, :], ACT.Sqrt).then_inc(std, 1)
                if turn:
                    for g in range(GROUPS):
                        act.wait_ge(turned, g + 1)
                        nc.scalar.activation(core.xnT[0:D, g * BANK:(g + 1) * BANK], core.psum[0:D, g, :],
                                             ACT.Copy).then_inc(drained, 1)

            @block.tensor
            def _(pe):
                if turn:
                    for t in range(T):
                        if t % 4 == 0:
                            pe.wait_ge(ready, t // 4 + 1)
                        last = nc.tensor.transpose(core.psum[0:D, t // 4, t % 4 * P:(t % 4 + 1) * P],
                                                   dst[:, t, :], core.ident[:, :])
                        if t % 4 == 3:
                            last.then_inc(turned, 1)


def turn_stage(nc, core, name, jobs, tiles=T):
    with Stage(nc, name) as st:
        turned, by_scalar, by_vector = st.sem("turned"), st.sem("drained_scalar"), st.sem("drained_vector")
        banks = [(job, g) for job in jobs for g in range((tiles + 3) // 4)]
        full = lambda g: min(4, tiles - 4 * g)
        with nc.Block() as block:
            @block.tensor
            def _(pe):
                for n, ((_, width, src), g) in enumerate(banks):
                    if n >= 8:
                        pe.wait_ge(by_vector if n % 2 else by_scalar, (n - 8) // 2 + 1)
                    for k in range(full(g)):
                        last = nc.tensor.transpose(core.psum[0:width, n % 8, k * P:(k + 1) * P],
                                                   src(4 * g + k), core.ident[:, :])
                    last.then_inc(turned, 1)

            @block.scalar
            def _(act):
                for n, ((dst, width, _), g) in enumerate(banks):
                    if n % 2 == 0:
                        act.wait_ge(turned, n + 1)
                        nc.scalar.activation(dst[0:width, g * BANK:g * BANK + full(g) * P], core.psum[0:width, n % 8, 0:full(g) * P],
                                             ACT.Copy).then_inc(by_scalar, 1)

            @block.vector
            def _(dve):
                for n, ((dst, width, _), g) in enumerate(banks):
                    if n % 2 == 1:
                        dve.wait_ge(turned, n + 1)
                        nc.vector.tensor_copy(dst[0:width, g * BANK:g * BANK + full(g) * P], core.psum[0:width, n % 8, 0:full(g) * P]
                                              ).then_inc(by_vector, 1)


def product_stage(nc, core, name, terms, width, use, engine="vector", tiles=T, loads=None):
    per = min(BANK // width, 8)
    batches = [(t0, min(t0 + per, tiles)) for t0 in range(0, tiles, per)]
    with Stage(nc, name) as st:
        made, used = st.sem("made"), st.sem("used")
        with nc.Block() as block:
            @block.tensor
            def _(pe):
                if loads is not None:
                    pe.wait_ge(loads.landed, loads.total)
                for n, (t0, t1) in enumerate(batches):
                    if n >= 8:
                        pe.wait_ge(used, n - 7)
                    for t in range(t0, t1):
                        for k, (lhsT_of, rhs) in enumerate(terms):
                            last = nc.tensor.matmul(core.psum[:, n % 8, (t - t0) * width:(t - t0 + 1) * width],
                                                    lhsT_of(t), rhs, start=(k == 0), stop=(k == len(terms) - 1))
                    last.then_inc(made, 1)

            def take(eng):
                for n, (t0, t1) in enumerate(batches):
                    eng.wait_ge(made, n + 1)
                    view = core.psum[:, n % 8, 0:(t1 - t0) * width].rearrange("p (t w) -> p t w", w=width)
                    use(t0, t1, view).then_inc(used, 1)

            (block.vector if engine == "vector" else block.scalar)(take)


def wide_product_stage(nc, core, name, outputs, use, engine="scalar", loads=None):
    jobs = [(g, o) for g in range(GROUPS) for o in range(len(outputs))]
    with Stage(nc, name) as st:
        made, used = st.sem("made"), st.sem("used")
        with nc.Block() as block:
            @block.tensor
            def _(pe):
                if loads is not None:
                    pe.wait_ge(loads.landed, loads.total)
                for n, (g, o) in enumerate(jobs):
                    if n >= 8:
                        pe.wait_ge(used, n - 7)
                    rows, terms = outputs[o]
                    for k, (lhsT, rhs) in enumerate(terms):
                        last = nc.tensor.matmul(core.psum[0:rows, n % 8, :], lhsT, rhs(g * BANK, (g + 1) * BANK),
                                                start=(k == 0), stop=(k == len(terms) - 1))
                    last.then_inc(made, 1)

            def take(eng):
                for n, (g, o) in enumerate(jobs):
                    eng.wait_ge(made, n + 1)
                    use(g * BANK, (g + 1) * BANK, o, core.psum[0:outputs[o][0], n % 8, :]).then_inc(used, 1)

            (block.vector if engine == "vector" else block.scalar)(take)



def split_tokens_stage(nc, name, x, s12, s13):
    with Stage(nc, name) as st:
        part1 = st.sb("part1", [P, x.shape[1]], BF16)
        part2 = st.sb("part2", [P, x.shape[1]], BF16)
        cast, less = st.sem("cast"), st.sem("less")
        with nc.Block() as block:
            @block.scalar
            def _(act):
                nc.scalar.activation(part1[:, :], x, ACT.Copy).then_inc(cast, 1)
                act.wait_ge(less, 1)
                nc.scalar.activation(part2[:, :], x, ACT.Copy).then_inc(cast, 1)
                nc.scalar.activation(s12[0:D, :], part1[0:D, :], ACT.Copy)
                nc.scalar.activation(s13[0:D, :], part1[0:D, :], ACT.Copy)
                act.wait_ge(cast, 2)
                nc.scalar.activation(s12[D:P, :], part2[D:P, :], ACT.Copy)

            @block.vector
            def _(dve):
                dve.wait_ge(cast, 1)
                nc.vector.tensor_tensor(x, x, part1[:, :], ALU.subtract).then_inc(less, 1)
                dve.wait_ge(cast, 2)
                dve.wait_ge(less, 1)
                nc.vector.tensor_tensor(s13[D:P, :], x[D:P, :], part2[D:P, :], ALU.subtract)


def split_weights_stage(nc, name, source, s11, s22, s31, chunk):
    pieces, BUFFERS = source.shape[1] // chunk, 4
    with Stage(nc, name) as st:
        x = st.sb("x", [P, BUFFERS, chunk])
        landed = [st.sem(f"landed{b}") for b in range(BUFFERS)]
        first, less, second, third, moved = (st.sem(n) for n in ("first", "less", "second", "third", "moved"))
        with nc.Block() as block:
            @block.sync
            def _(sp):
                def copy_first(i):
                    at = slice(i * chunk, (i + 1) * chunk)
                    sp.wait_ge(first, i + 1)
                    sp.dma_start(s31[D:P, at], s11[D:P, at]).then_inc(moved, 16)

                for i in range(pieces):
                    if i >= BUFFERS:
                        sp.wait_ge(third, i - BUFFERS + 1)
                        sp.wait_ge(second, i - BUFFERS + 1)
                    for half in range(2):
                        sp.dma_start(x[half * D:(half + 1) * D, i % BUFFERS, :], source[:, i * chunk:(i + 1) * chunk]
                                     ).then_inc(landed[i % BUFFERS], 16)
                    if i >= BUFFERS:
                        copy_first(i - BUFFERS)
                for i in range(max(pieces - BUFFERS, 0), pieces):
                    copy_first(i)
                sp.wait_ge(moved, 16 * pieces)

            @block.scalar
            def _(act):
                def second_part(i):
                    at = slice(i * chunk, (i + 1) * chunk)
                    act.wait_ge(less, i + 1)
                    nc.scalar.activation(s22[:, at], x[:, i % BUFFERS, :], ACT.Copy).then_inc(second, 1)

                for i in range(pieces):
                    at = slice(i * chunk, (i + 1) * chunk)
                    act.wait_ge(landed[i % BUFFERS], 32 * (i // BUFFERS + 1))
                    nc.scalar.activation(s11[:, at], x[:, i % BUFFERS, :], ACT.Copy).then_inc(first, 1)
                    if i >= 1:
                        second_part(i - 1)
                second_part(pieces - 1)

            @block.vector
            def _(dve):
                def third_part(i):
                    at = slice(i * chunk, (i + 1) * chunk)
                    dve.wait_ge(second, i + 1)
                    dve.wait_ge(less, i + 1)
                    nc.vector.tensor_tensor(s31[0:D, at], x[0:D, i % BUFFERS, :], s22[0:D, at], ALU.subtract).then_inc(third, 1)

                for i in range(pieces):
                    dve.wait_ge(first, i + 1)
                    nc.vector.tensor_tensor(x[:, i % BUFFERS, :], x[:, i % BUFFERS, :], s11[:, i * chunk:(i + 1) * chunk], ALU.subtract
                                            ).then_inc(less, 1)
                    if i >= 1:
                        third_part(i - 1)
                third_part(pieces - 1)


def add_stage(nc, core, name, *sums):
    with Stage(nc, name) as st:
        vec = st.sem("vector_steps")
        with nc.Block() as block:
            @block.vector
            def _(dve):
                steps = Steps(dve, vec)
                for out, a, b in sums:
                    steps.do(nc.vector.tensor_tensor(out, a, b, ALU.add))


def linear_attention_stage(nc, core, I, norm):
    with Stage(nc, "lin") as st:
        w_qkv = st.sb("w_qkv", [D + 1, 3 * D])
        qkv = st.sb("qkv", [P, T, 3 * D + 1])
        qk, v1 = qkv[:, :, 0:2 * D], qkv[:, :, 2 * D:3 * D + 1]
        sq = st.sb("sq", [P, T, 2 * D])
        stat = st.sb("stat", [P, 3, 2 * T])
        qT = st.sb("qT", [D, COLS])
        kT = st.sb("kT", [D, COLS])
        upper = st.sb("upper", [P, P])
        scores = st.sb("scores", [P, 2, CH, PAD])
        attn = st.sb("attn", [P, T, D])
        den = st.sb("den", [P, T])
        loads = Loads(nc, st, "landed", [(w_qkv[:, :], I["qkv_aug"])])
        norm()
        loads.arrive()
        projected, copied, copied_v, vec, act_steps, norm_ready, root_ready, feats, turned, drained, consts = (
            st.sem(n) for n in ("projected", "copied", "copied_by_vector", "vector_steps", "scalar_steps", "norm_ready",
                                "root_ready", "features_ready", "turned", "drained", "consts"))
        ps = core.psum
        with nc.Block() as block:
            @block.gpsimd
            def _(pool):
                nc.gpsimd.memset(qkv[:, :, 3 * D:3 * D + 1], 1.0).then_inc(consts, 1)
                nc.gpsimd.memset(upper[:, :], 1.0).then_inc(consts, 1)
                pool.wait_ge(consts, 2)
                nc.gpsimd.affine_select(out=upper[:, :], in_=upper[:, :], compare_op=ALU.is_ge, fill=0.0,
                                        base=0, pattern=[[1, P]], channel_multiplier=-1)

            @block.tensor
            def _(pe):
                for t in range(T):
                    if t >= 8:
                        pe.wait_ge(copied_v if t % 2 else copied, (t - 8) // 2 + 1)
                    nc.tensor.matmul(ps[:, t % 8, 0:3 * D], core.xnT[:, t * P:(t + 1) * P], w_qkv[:, :],
                                     start=True, stop=True).then_inc(projected, 1)
                pe.wait_ge(feats, 1)
                for part in range(2):
                    for t in range(T):
                        g = part * GROUPS + t // 4
                        if t % 4 == 0 and g >= 8:
                            pe.wait_ge(drained, g - 7)
                        last = nc.tensor.transpose(ps[0:D, g % 8, t % 4 * P:(t % 4 + 1) * P],
                                                   qk[:, t, part * D:(part + 1) * D], core.ident[:, :])
                        if t % 4 == 3:
                            last.then_inc(turned, 1)

            @block.scalar
            def _(act):
                steps = Steps(act, act_steps)
                for t in range(0, T, 2):
                    act.wait_ge(projected, t + 1)
                    nc.scalar.activation(qkv[:, t, 0:3 * D], ps[:, t % 8, 0:3 * D], ACT.Copy).then_inc(copied, 1)
                act.wait_ge(norm_ready, 1)
                nc.scalar.activation(stat[:, 1, :], stat[:, 0, :], ACT.Sqrt).then_inc(root_ready, 1)
                act.wait_ge(norm_ready, 2)
                steps.do(nc.scalar.activation(qk[:, :, :], qk[:, :, :], ACT.Exp))
                nc.scalar.activation(qk[:, :, :], qk[:, :, :], ACT.Ln, bias=1.0).then_inc(root_ready, 1)
                for g in range(2 * GROUPS):
                    act.wait_ge(turned, g + 1)
                    to = (qT if g < GROUPS else kT)[:, g % GROUPS * BANK:(g % GROUPS + 1) * BANK]
                    nc.scalar.activation(to, ps[0:D, g % 8, :], ACT.Copy).then_inc(drained, 1)

            @block.vector
            def _(dve):
                steps = Steps(dve, vec)
                for t in range(1, T, 2):
                    dve.wait_ge(projected, t + 1)
                    nc.vector.tensor_copy(qkv[:, t, 0:3 * D], ps[:, t % 8, 0:3 * D]).then_inc(copied_v, 1)
                dve.wait_ge(copied, T // 2)
                dve.wait_ge(copied_v, T // 2)
                steps.do(nc.vector.tensor_tensor(sq[:, :, :], qk[:, :, :], qk[:, :, :], ALU.mult))
                nc.vector.tensor_reduce(stat[:, 0, :], sq[:, :, :].rearrange("p t (s d) -> p (t s) d", s=2),
                                        AX.X, ALU.add).then_inc(norm_ready, 1)
                dve.wait_ge(root_ready, 1)
                steps.do(nc.vector.tensor_scalar(stat[:, 1, :], stat[:, 1, :], 0.125, 1e-12, ALU.mult, ALU.max))
                steps.do(nc.vector.reciprocal(stat[:, 2, :], stat[:, 1, :]))
                steps.do(nc.vector.tensor_scalar(stat[:, 2, :], stat[:, 2, :], 0.125, None, ALU.mult))
                view = qk.rearrange("p t (s d) -> p t s d", s=2)
                scale = stat[:, 2, :].rearrange("p (t s) -> p t s", s=2)
                nc.vector.tensor_tensor(view, view, over(scale, D), ALU.mult).then_inc(norm_ready, 1)
                dve.wait_ge(root_ready, 2)
                nc.vector.tensor_scalar(qk[:, :, :], qk[:, :, :], 1e-6, None, ALU.add).then_inc(feats, 1)

        scored, scored_rest, kept, kept_rest, weighed, divided = (
            st.sem(n) for n in ("scored_diagonal", "scored_rest", "kept_diagonal", "kept_rest", "weighed", "divided"))
        with nc.Block() as block:
            @block.tensor
            def _(pe):
                n = rest = 0
                for b in range(B):
                    for c in range(CH):
                        keys = kT[:, b * PAD + c * P:b * PAD + (c + 1) * P]
                        if n >= 2:
                            pe.wait_ge(kept, n - 1)
                        nc.tensor.matmul(ps[:, n % 2, 0:P], keys, qT[:, b * PAD + c * P:b * PAD + (c + 1) * P],
                                         start=True, stop=True).then_inc(scored, 1)
                        n += 1
                        if c < CH - 1:
                            if rest >= 2:
                                pe.wait_ge(kept_rest, rest - 1)
                            nc.tensor.matmul(ps[:, 2 + rest % 2, 0:PAD - (c + 1) * P], keys,
                                             qT[:, b * PAD + (c + 1) * P:(b + 1) * PAD],
                                             start=True, stop=True).then_inc(scored_rest, 1)
                            rest += 1
                    pe.wait_ge(kept, n)
                    pe.wait_ge(kept_rest, rest)
                    if b >= 1:
                        pe.wait_ge(divided, 2 * b)
                    for c in range(CH):
                        for m in range(c + 1):
                            rows = TAIL if m == CH - 1 else P
                            last = nc.tensor.matmul(ps[:, 6, c * (D + 1):(c + 1) * (D + 1)],
                                                    scores[0:rows, b % 2, m, c * P:(c + 1) * P],
                                                    v1[0:rows, b * CH + m, :], start=(m == 0), stop=(m == c))
                    last.then_inc(weighed, 1)

            @block.scalar
            def _(act):
                for b in range(B):
                    if b >= 2:
                        act.wait_ge(weighed, b - 1)
                    for c in range(CH - 1):
                        rest = b * (CH - 1) + c
                        act.wait_ge(scored_rest, rest + 1)
                        nc.scalar.activation(scores[:, b % 2, c, (c + 1) * P:PAD],
                                             ps[:, 2 + rest % 2, 0:PAD - (c + 1) * P], ACT.Copy
                                             ).then_inc(kept_rest, 1)

            @block.vector
            def _(dve):
                for b in range(B):
                    for c in range(CH):
                        n = b * CH + c
                        dve.wait_ge(scored, n + 1)
                        if b >= 2:
                            dve.wait_ge(weighed, b - 1)
                        nc.vector.tensor_tensor(scores[:, b % 2, c, c * P:(c + 1) * P], ps[:, n % 2, 0:P],
                                                upper[:, :], ALU.mult).then_inc(kept, 1)
                    dve.wait_ge(weighed, b + 1)
                    out = ps[:, 6, 0:CH * (D + 1)].rearrange("p (c e) -> p c e", e=D + 1)
                    nc.vector.tensor_scalar(attn[:, b * CH:(b + 1) * CH, :], out[:, :, 0:D], 1e4, -1e4, ALU.min, ALU.max
                                            ).then_inc(divided, 1)
                    nc.vector.tensor_scalar(den[:, b * CH:(b + 1) * CH], out[:, :, D], 1e-6, None, ALU.max
                                            ).then_inc(divided, 1)
                dve.wait_ge(divided, 2 * B)
                nc.vector.reciprocal(den[:, :], den[:, :]).then_inc(divided, 1)
                dve.wait_ge(divided, 2 * B + 1)
                nc.vector.tensor_tensor(attn[:, :, :], attn[:, :, :], over(den[:, :], D), ALU.mult)

        aT = st.sb("aT", [D + 1, COLS])
        w_proj = st.sb("w_proj", [D + 1, D])
        loads = Loads(nc, st, "proj_landed", [(w_proj[:, :], I["proj_aug"])])
        set_stage(nc, "lin_one", [(aT[:, :], 1.0)])
        turn_stage(nc, core, "lin_turn", [(aT, D, lambda t: attn[:, t, :])])
        product_stage(nc, core, "lin_proj", [(lambda t: aT[:, t * P:(t + 1) * P], w_proj[:, :])], D,
                      lambda t0, t1, made: nc.vector.tensor_tensor(core.xn[:, t0:t1, :], core.xn[:, t0:t1, :], made, ALU.add), loads=loads)
    with Stage(nc, "gelu") as st:
        w1 = st.sb("w1", [D + 1, 4 * D])
        w2 = st.sb("w2", [P, 2, D])
        b2 = st.sb("b2", [1, D])
        hT = st.sb("hT", [P, 2, COLS])
        loads = Loads(nc, st, "landed", [(w1[:, :], I["w1_aug"]), (w2[:, :, :], I["w2"].rearrange("(k p) d -> p k d", p=P)),
                                         (b2[:, :], I["b2"].unsqueeze(0))])
        norm_stage(nc, core, "lin_ln1", core.xn, gain=I["ln1_g"], shift=I["ln1_b"])
        wide_product_stage(nc, core, "gelu_up", [(P, [(w1[:, k * P:(k + 1) * P], lambda c0, c1: core.xnT[:, c0:c1])])
                                                 for k in range(2)],
                           lambda c0, c1, k, made: nc.scalar.activation(hT[:, k, c0:c1], made, ACT.Gelu), loads=loads)
        product_stage(nc, core, "gelu_down",
                      [(lambda t: hT[:, 0, t * P:(t + 1) * P], w2[:, 0, :]),
                       (lambda t: hT[:, 1, t * P:(t + 1) * P], w2[:, 1, :]),
                       (lambda t: core.ones[0:1, :], b2[:, :])], D,
                      lambda t0, t1, made: nc.vector.tensor_tensor(core.xn[:, t0:t1, :], core.xn[:, t0:t1, :], made, ALU.add))
    norm_stage(nc, core, "lin_ln2", core.xn, gain=I["ln2_g"], shift=I["ln2_b"], turn=False)
    add_stage(nc, core, "lin_residual", (core.h[:, :, :], core.h[:, :, :], core.xn[:, :, :]))


def set_stage(nc, name, fills):
    with nc.Block() as block:
        @block.gpsimd
        def _(pool):
            for ap, value in fills:
                nc.gpsimd.memset(ap, value)


class CausalAttention:

    BEGIN = 6
    SCORE_BANK = (2, 3, 2, 3, 4)
    TURN_BANK = (6, 7, 6, 7, 6)

    def __init__(self, nc, core, st, d, scale, fetches=(2, 1), parts=None):
        self.nc, self.core, self.d, self.scale, self.fetches = nc, core, d, scale, fetches
        self.width = [P * (c + 1) for c in range(CH - 1)] + [SEQ]
        self.rows = [P] * (CH - 1) + [TAIL]
        self.prob_at = [sum(self.width[:c]) for c in range(CH)]
        self.pT_at = [0, 3 * P, 0, 3 * P, 7 * P]
        self.parts, self.dq = parts, parts or d
        self.k_at = parts or max(d, 32)
        kind = BF16 if parts else F32
        self.qk1 = st.sb("qk1", [P, 2, CH, self.k_at + self.dq], kind)
        if parts:
            self.ident16 = st.sb("ident16", [P, P], BF16)
        self.v1 = st.sb("v1", [P, 2, CH, d])
        self.qT, self.kT = st.sb("qT", [self.dq, 2, SEQ], kind), st.sb("kT", [self.dq, 2, SEQ], kind)
        self.mask = st.sb("mask", [P, 2 * PAD - P])
        self.probs = st.sb("probs", [P, sum(self.width)])
        self.pT = st.sb("pT", [P, 7 * P + CH * TAIL])
        self.stat = st.sb("stat", [P, 2, CH, 4])
        self.fetched = [st.sem(f"head_fetched{u}") for u in range(2)]
        self.v_fetched = [st.sem(f"head_v_fetched{u}") for u in range(2)]
        names = ("turned", "qk_copied", "scored", "peaked", "exped", "p_turned", "p_copied",
                 "weighed", "normed", "masked")
        (self.turned, self.qk_copied, self.scored, self.peaked, self.exped,
         self.p_turned, self.p_copied, self.weighed, self.normed, self.own) = self.semaphores = [st.sem(f"head_{x}") for x in names]
        self.passed_pe, self.passed_dve = st.sem("passed_by_tensor"), st.sem("passed_by_vector")
        self.set = st.sem("mask_set")

    def begin(self):
        nc, mask = self.nc, self.mask
        with nc.Block() as block:
            @block.sync
            def _(sp):
                for s in self.semaphores:
                    sp.sem_inc(s, self.BEGIN)

            if self.parts:
                @block.scalar
                def _(act):
                    nc.scalar.activation(self.ident16[:, :], self.core.ident[:, :], ACT.Copy)

            @block.gpsimd
            def _(pool):
                nc.gpsimd.memset(mask[:, :], 0.0).then_inc(self.set, 1)
                if not self.parts and self.k_at > self.dq:
                    nc.gpsimd.memset(self.qk1[:, :, :, :], 0.0)
                pool.wait_ge(self.set, 1)
                nc.gpsimd.affine_select(out=mask[:, :], in_=mask[:, :], compare_op=ALU.is_ge, fill=NEG,
                                        base=PAD - P, pattern=[[-1, 2 * PAD - P]], channel_multiplier=1)

    def pool_fetch(self, pool, n, u, q, k, v):
        nc = self.nc
        pool.wait_ge(self.turned, self.BEGIN + 2 * n - 2)
        nc.gpsimd.tensor_copy(self.qk1[:, u, :, 0:self.dq], q).then_inc(self.fetched[u], 1)
        nc.gpsimd.tensor_copy(self.qk1[:, u, :, self.k_at:self.k_at + self.dq], k).then_inc(self.fetched[u], 1)
        pool.wait_ge(self.weighed, self.BEGIN + CH * n - CH)
        nc.gpsimd.tensor_copy(self.v1[:, u, :, :], v).then_inc(self.v_fetched[u], 1)

    def pe_turn(self, pe, m, u, tail):
        nc, ps = self.nc, self.core.psum
        rows, n = self.k_at + self.dq, 2 * m + u
        pe.wait_ge(self.fetched[u], self.fetches[0] * (m + 1))
        pe.wait_ge(self.qk_copied, self.BEGIN + 4 * n + (2 if tail else 0))
        wait_apart(pe, self.passed_pe)
        r = TAIL if tail else P
        tiles = [CH - 1] if tail else range(CH - 1)
        if self.parts:
            bank = ps[:, 0, :].bitcast(BF16)
            for part in range(2):
                for i, c in enumerate(tiles):
                    at = (part * len(tiles) + i) * r
                    last = nc.tensor.transpose(bank[0:self.dq, at:at + r], self.qk1[0:r, u, c, part * self.k_at:part * self.k_at + self.dq],
                                               self.ident16[0:r, 0:r])
        else:
            for i, c in enumerate(tiles):
                last = nc.tensor.transpose(ps[0:rows, 0, i * r:(i + 1) * r], self.qk1[0:r, u, c, :], self.core.ident[0:r, 0:r])
        last.then_inc(self.turned, 1)

    def dve_turn(self, dve, n, u, tail):
        nc, ps = self.nc, self.core.psum
        lo, hi = (BANK, SEQ) if tail else (0, BANK)
        dve.wait_ge(self.turned, self.BEGIN + 2 * n + (2 if tail else 1))
        for part, to in enumerate((self.qT, self.kT)):
            if self.parts:
                of = ps[:, 0, :].bitcast(BF16)[0:self.dq, part * (hi - lo):(part + 1) * (hi - lo)]
            else:
                of = ps[part * self.k_at:part * self.k_at + self.d, 0, 0:hi - lo]
            nc.vector.tensor_copy(to[:, u, lo:hi], of).then_inc(self.qk_copied, 1)

    def pe_score(self, pe, n, u, c):
        nc, ps, w, r = self.nc, self.core.psum, self.width[c], self.rows[c]
        if c == 0:
            pe.wait_ge(self.qk_copied, self.BEGIN + 4 * n + 4)
        pe.wait_ge(self.peaked, self.BEGIN + CH * n + (-2, -1, 1, 2, 0)[c])
        wait_apart(pe, self.passed_pe)
        bank, q = self.SCORE_BANK[c], self.qT[:, u, c * P:c * P + r]
        last = nc.tensor.matmul(ps[0:r, bank, 0:min(w, BANK)], q, self.kT[:, u, 0:min(w, BANK)], start=True, stop=True)
        if w > BANK:
            last = nc.tensor.matmul(ps[0:r, bank + 1, 0:w - BANK], q, self.kT[:, u, BANK:w], start=True, stop=True)
        last.then_inc(self.scored, 1)

    def pe_turn_probs(self, pe, n, c):
        nc, ps = self.nc, self.core.psum
        pe.wait_ge(self.exped, self.BEGIN + CH * n + c + 1)
        pe.wait_ge(self.p_copied, self.BEGIN + CH * n + (0, 0, 1, 2, 3)[c])
        wait_apart(pe, self.passed_pe)
        r = self.rows[c]
        for m in range(c + 1):
            last = nc.tensor.transpose(ps[0:self.rows[m], self.TURN_BANK[c], m * r:(m + 1) * r],
                                       self.probs[0:r, self.prob_at[c] + m * P:self.prob_at[c] + m * P + self.rows[m]], self.core.ident[0:r, 0:r])
        last.then_inc(self.p_turned, 1)

    def pe_weigh(self, pe, m, u, c):
        nc, ps, d, r, n = self.nc, self.core.psum, self.d, self.rows[c], 2 * m + u
        if c == 0:
            pe.wait_ge(self.v_fetched[u], self.fetches[1] * (m + 1))
            pe.wait_ge(self.normed, self.BEGIN + 2 * n)
        pe.wait_ge(self.p_copied, self.BEGIN + CH * n + c + 1)
        wait_apart(pe, self.passed_pe)
        for m in range(c + 1):
            k = self.rows[m]
            last = nc.tensor.matmul(ps[0:r, 1, c * d:(c + 1) * d], self.pT[0:k, self.pT_at[c] + m * r:self.pT_at[c] + (m + 1) * r], self.v1[0:k, u, m, :],
                                    start=(m == 0), stop=(m == c))
        last.then_inc(self.weighed, 1)

    def pe_start(self, pe, m, u):
        for tail in (False, True):
            self.pe_turn(pe, m, u, tail)
        self.pe_score(pe, 2 * m + u, u, 0)
        self.pe_score(pe, 2 * m + u, u, 1)

    def pe_head(self, pe, m, u, more):
        n = 2 * m + u
        for c in range(CH):
            if c + 2 < CH:
                self.pe_score(pe, n, u, c + 2)
            if more and c in (1, 2):
                self.pe_turn(pe, m + u, 1 - u, c == 2)
            if more and c == 3:
                self.pe_score(pe, n + 1, 1 - u, 0)
            self.pe_turn_probs(pe, n, c)
            if c >= 1:
                self.pe_weigh(pe, m, u, c - 1)
        if more:
            self.pe_score(pe, n + 1, 1 - u, 1)
        self.pe_weigh(pe, m, u, CH - 1)

    def act_head(self, act, n, u):
        nc, ps, stat = self.nc, self.core.psum, self.stat

        def copy(c):
            act.wait_ge(self.p_turned, self.BEGIN + CH * n + c + 1)
            act.wait_ge(self.weighed, self.BEGIN + CH * n + (-2, -1, 1, 2, 0)[c])
            r, bank = self.rows[c], self.TURN_BANK[c]
            full = min(c + 1, CH - 1)
            at = self.pT_at[c]
            last = nc.scalar.activation(self.pT[:, at:at + full * r], ps[:, bank, 0:full * r], ACT.Copy)
            if full < c + 1:
                last.then_inc(self.own, 1)
                last = nc.scalar.activation(self.pT[0:TAIL, at + c * r:at + (c + 1) * r], ps[0:TAIL, bank, c * r:(c + 1) * r], ACT.Copy)
                act.wait_ge(self.own, self.BEGIN + n + 1)
            last.then_inc(self.p_copied, 1)

        for c in range(CH):
            r, w = self.rows[c], self.width[c]
            act.wait_ge(self.peaked, self.BEGIN + CH * n + c + 1)
            nc.scalar.activation(self.probs[0:r, self.prob_at[c]:self.prob_at[c] + w], self.probs[0:r, self.prob_at[c]:self.prob_at[c] + w], ACT.Exp, bias=stat[0:r, u, c, 1:2],
                                 scale=self.scale, accum_out=stat[0:r, u, c, 2:3]).then_inc(self.exped, 1)
            if c >= 1:
                copy(c - 1)
        copy(CH - 1)

    def dve_norm(self, dve, steps, n, u, out_of):
        nc, ps, d = self.nc, self.core.psum, self.d
        parts = ((0, CH - 1, P), (CH - 1, CH, TAIL))
        dve.wait_ge(self.weighed, self.BEGIN + CH * n + CH)
        for lo, hi, r in parts:
            steps.add(nc.vector.reciprocal(self.stat[0:r, u, lo:hi, 3], self.stat[0:r, u, lo:hi, 2]))
        steps.settle()
        for lo, hi, r in parts:
            nc.vector.tensor_tensor(out_of(lo, hi, r), ps[0:r, 1, lo * d:hi * d].rearrange("p (c d) -> p c d", d=d),
                                    over(self.stat[0:r, u, lo:hi, 3], d), ALU.mult).then_inc(self.normed, 1)

    STEPS = CH + 2

    def dve_start(self, dve, n, u):
        for tail in (False, True):
            self.dve_turn(dve, n, u, tail)

    def dve_head(self, dve, steps, n, u, more, carry, out_of, out_before=None):
        nc, ps, stat = self.nc, self.core.psum, self.stat
        flat = ps[:, :, :].rearrange("p b n -> p (b n)")
        for c in range(CH):
            r, w, at = self.rows[c], self.width[c], self.SCORE_BANK[c] * BANK
            dve.wait_ge(self.scored, self.BEGIN + CH * n + c + 1)
            dve.wait_ge(self.p_turned, self.BEGIN + CH * n + c - CH + 1)
            wait_apart(dve, self.passed_dve)
            steps.do(nc.vector.tensor_tensor_reduce(
                self.probs[0:r, self.prob_at[c]:self.prob_at[c] + w], flat[0:r, at:at + w], self.mask[0:r, PAD - P - c * P:PAD - P - c * P + w],
                1.0, -3e38, ALU.add, ALU.max, stat[0:r, u, c, 0:1]))
            nc.vector.tensor_scalar(stat[0:r, u, c, 1:2], stat[0:r, u, c, 0:1], -self.scale, None, ALU.mult
                                    ).then_inc(self.peaked, 1)
            if c == 1 and carry:
                self.dve_norm(dve, steps, n - 1, 1 - u, out_before)
            if more and c in (1, 2):
                self.dve_turn(dve, n + 1, 1 - u, c == 2)
        if not more:
            self.dve_norm(dve, steps, n, u, out_of)


def causal_attention_stage(nc, core, name, sources, out, heads, d, scale, parts=None):
    with Stage(nc, name) as st:
        A = CausalAttention(nc, core, st, d, scale, parts=parts)
        widths = (A.dq, A.dq, d)
        vec = st.sem("vector_steps")
        A.begin()
        pairs = heads // 2
        views = lambda b, h: [of[:, bass.ds(b * CH, CH), bass.ds(h * stride + start, w)]
                              for (of, stride, start), w in zip(sources, widths)]
        out_of = lambda b, h: (lambda lo, hi, r: out[0:r, bass.ds(b * CH + lo, hi - lo), bass.ds(h * d, d)])

        def walk(engine, pair):
            def sequence(b, first=False, last=False):
                for j in range(pairs):
                    pair(b, j, first and j == 0, last and j == pairs - 1)

            sequence(0, first=True)
            with engine.Fori(1, B - 1) as b:
                sequence(b)
            sequence(B - 1, last=True)

        with nc.Block() as block:
            @block.gpsimd
            def _(pool):
                with pool.Fori(0, B) as b:
                    with pool.Fori(0, pairs) as j:
                        for u in range(2):
                            A.pool_fetch(pool, b * heads + j * 2 + u, u, *views(b, j * 2 + u))

            @block.tensor
            def _(pe):
                A.pe_start(pe, 0, 0)
                with pe.Fori(0, B * pairs - 1) as m:
                    for u in range(2):
                        A.pe_head(pe, m, u, True)
                for u in range(2):
                    A.pe_head(pe, B * pairs - 1, u, u == 0)

            @block.scalar
            def _(act):
                with act.Fori(0, B * pairs) as m:
                    for u in range(2):
                        A.act_head(act, 2 * m + u, u)

            @block.vector
            def _(dve):
                steps = Steps(dve, vec)

                def pair(b, j, first, last):
                    n, h = b * heads + j * 2, j * 2
                    steps.before, steps.count = A.STEPS * n - (0 if first else 2), 0
                    if first:
                        A.dve_start(dve, n, 0)
                    before = None if first else out_of(b, h - 1) if h else out_of(b - 1, heads - 1)
                    A.dve_head(dve, steps, n, 0, True, not first, out_of(b, h), before)
                    A.dve_head(dve, steps, n + 1, 1, not last, True, out_of(b, h + 1), out_of(b, h))

                walk(dve, pair)


KEYS = 64
HEADS = 8
TOP = 16
SLOTS = 4
LOWEST = -3e38


def retrieval_stage(nc, core, I, norm):
    with Stage(nc, "peer") as st:
        O = st.sb("O", [P, T, HEADS * D])
        w_o = st.sb("w_o", [P, HEADS * D // P, D])
        with Stage(nc, "pk") as at:
            w_pk = at.sb("w_pk", [D, 2 * HEADS * D // 2])
            keys = at.sb("keys", [P, 4, 4 * KEYS])
            w_q = at.sb("w_q", [D, HEADS * D])
            loads = Loads(nc, at, "landed", [(w_pk[:, :], I["w_pk"]), (keys[:, :, :], I["pk_blocks"]), (w_q[:, :], I["w_q"]),
                                              (w_o[:, :, :], I["w_o"].rearrange("(k p) n -> p k n", p=P))])
            set_stage(nc, "peer_padding", [(O[TAIL:P, CH - 1::CH, :], 0.0)])
            norm()
            loads.arrive()
            xt = at.sb("xt", [D, P])
            pkT = at.sb("pkT", [P, 4, P])
            sim = at.sb("sim", [P, 2 * HEADS, KEYS])
            vals = at.sb("vals", [P, 2 * HEADS, TOP])
            ids = at.sb("ids", [P, 2 * HEADS, TOP], U32)
            idf = at.sb("idf", [P, 2 * HEADS, TOP])
            cand = at.sb("cand", [P, HEADS, TOP * TOP])
            fvals = at.sb("fvals", [P, HEADS, TOP])
            fids = at.sb("fids", [P, HEADS * TOP], U32)
            half = at.sb("half", [P, HEADS * TOP], U32)
            halff = at.sb("halff", [P, HEADS * TOP])
            found = at.sb("found", [P, 2, HEADS * TOP])
            index = at.sb("index", [P, 3, HEADS * TOP], U32)
            weight = at.sb("weight", [P, 3, HEADS, TOP])
            sums = at.sb("sums", [P, 2, HEADS])
            count16 = at.sb("count16", [P, TOP])
            base = at.sb("base", [P, HEADS, TOP])
            rows = at.sb("rows", [P, SLOTS, TOP, 2 * D])
            made_tile = at.sb("made_tile", [P, 3, HEADS, 3 * D])
            kept = nc.dram_tensor("peer_kept", (T, P, HEADS, 3 * D), F32, kind="Internal").ap()
            (consts, fetched, pk_made, pk_copied, sims_made, sims_copied, q_made, q_copied, sim_used, shifted, exped,
             index_ready, weighed, vec, attn_vec) = (at.sem(n) for n in (
                "consts", "fetched", "pk_made", "pk_copied", "sims_made", "sims_copied", "q_made", "q_copied",
                "sim_used", "shifted", "exped", "index_ready", "weighed", "vector_steps", "attention_steps"))
            passed, passed_pool, passed_sp = at.sem("passed"), at.sem("passed_by_pool"), at.sem("passed_by_sync")
            gathered = [at.sem(f"gathered{s}") for s in range(SLOTS)]
            stored = [at.sem(f"stored{u}") for u in range(3)]
            start_loop(nc, [fetched, pk_made, pk_copied, sims_made, sims_copied, q_made, q_copied, sim_used, shifted,
                            exped, index_ready])
            A = CausalAttention(nc, core, at, D, 1.0, fetches=(32, 32))
            A.begin()
            o1 = at.sb("o1", [P, 2, HEADS * D])
            o_turned, o_copied, o_projected, o_added = (
                at.sem(n) for n in ("o_turned", "o_copied", "o_projected", "o_added"))
            EARLY = (B - 1) * CH
            early_tiles = lambda p: range((p - 1) * CH, p * CH) if 1 <= p < B else []
            ps = core.psum
            TAILS = B // 2
            TILES = TAILS + 4 * B
            PAIRS = HEADS // 2

            class Step:

                def __init__(self, t, u, round_, tails=None, tile=None, following=None, beside=()):
                    self.t, self.u, self.round, self.tails, self.tile, self.next = t, u, round_, tails, tile, following
                    self.beside, self.second = beside, False

            def turn(s, half, attend):
                for i in range(2):
                    yield Step(TAILS + 4 * s + 2 * half + i, i, 1 + 2 * s + half, tile=s * CH + 2 * half + i,
                               following=("tile", s * CH + 2 * half + 1 if i == 0 else s * CH + 2 + 3 * half),
                               beside=[(s - 1, 2 * half + i)] if attend else [])

            def walk(engine, step):
                step(Step(0, 0, 0, tails=0, following=("tails", 1)))
                step(Step(1, 1, 0, tails=1, following=("tile", 0)))
                with engine.Fori(0, 2) as half:
                    for x in turn(0, half, False):
                        step(x)
                with engine.Fori(1, B - 1) as s:
                    with engine.Fori(0, 2) as half:
                        for x in turn(s, half, True):
                            step(x)
                for x in turn(B - 1, 0, True):
                    x.beside = [(B - 2, 0), (B - 2, 1)] if x.u == 0 else [(B - 2, 2)]
                    x.second = x.u == 1
                    step(x)

            LAST = TILES - 2
            beside = [[(B - 2, 3)], [(B - 1, 0)], [(B - 1, 1)], [(B - 1, 2)], [(B - 1, 3)]]
            fetch_order = lambda p: [(u, 2 * p + k) for u in (0, 2) for k in range(2)]

            out_of = lambda b, h: (lambda lo, hi, r: O[0:r, bass.ds(b * CH + lo, hi - lo), bass.ds(h * D, D)])

            with nc.Block() as block:
                @block.sync
                def _(sp):
                    def load(m, u, b, h):
                        n = 2 * m + u
                        for sem, to, lo, hi, free, at_least in (
                                (A.fetched[u], A.qk1, 0, 2 * D, A.turned, A.BEGIN + 2 * n - 2),
                                (A.v_fetched[u], A.v1, 2 * D, 3 * D, A.weighed, A.BEGIN + CH * n - CH)):
                            sp.wait_ge(free, at_least)
                            wait_apart(sp, passed_sp)
                            sp.dma_start(to[:, u, 0:CH - 1, :].unsqueeze(2),
                                         kept.rearrange("t p h f -> p t h f")[:, bass.ds(b * CH, CH - 1), bass.ds(h, 1), lo:hi]
                                         ).then_inc(sem, 16)
                            sp.dma_start(to[0:TAIL, u, CH - 1, :].unsqueeze(1).unsqueeze(1),
                                         kept.rearrange("t p h f -> p t h f")[0:TAIL, bass.ds(b * CH + CH - 1, 1), bass.ds(h, 1), lo:hi]
                                         ).then_inc(sem, 16)

                    def step(x):
                        if x.beside:
                            sp.wait_ge(stored[0], 16 * (x.round + 1 + x.u))
                            wait_apart(sp, passed_sp)
                            sp.wait_ge(stored[1], 16 * (x.round + 1))
                            wait_apart(sp, passed_sp)
                        for b, j in x.beside:
                            for u in range(2):
                                load(b * PAIRS + j, u, b, 2 * j + u)
                        sp.wait_ge(weighed, SLOTS + HEADS * (x.t + 1))
                        wait_apart(sp, passed_sp)
                        sp.wait_ge(q_copied, START + x.t + 1)
                        wait_apart(sp, passed_sp)
                        if x.tails is None:
                            sp.dma_start(kept[bass.ds(x.tile, 1), :, :, :].rearrange("o p h f -> p (o h) f"), made_tile[:, x.u, :, :]
                                         ).then_inc(stored[x.u], 16)
                        else:
                            for k in range(2):
                                sp.dma_start(kept[(2 * x.tails + k) * CH + CH - 1, 0:TAIL, :, :],
                                             made_tile[k * TAIL:(k + 1) * TAIL, x.u, :, :]).then_inc(stored[x.u], 16)

                    walk(sp, step)
                    for p in range(PAIRS + 1):
                        for b, j in beside[p]:
                            for u, before in enumerate((LAST // 2 + 1, LAST // 2 + 1, 0)):
                                if u != 1 and before + p:
                                    sp.wait_ge(stored[u], 16 * (before + p))
                                elif u == 1:
                                    sp.wait_ge(stored[u], 16 * before)
                            for u in range(2):
                                load(b * PAIRS + j, u, b, 2 * j + u)
                        if p == 0:
                            sp.wait_ge(q_copied, START + TILES)
                        if p < PAIRS:
                            sp.wait_ge(weighed, SLOTS + HEADS * LAST + 4 * (p + 1))
                            for i, u in enumerate((0, 2)):
                                sp.dma_start(kept[(B - 1) * CH + CH - 3 + i, :, 2 * p:2 * p + 2, :],
                                             made_tile[:, u, 2 * p:2 * p + 2, :]).then_inc(stored[u], 16)

                @block.gpsimd
                def _(pool):
                    nc.gpsimd.iota(count16[:, :], [[1, TOP]], base=0, channel_multiplier=0,
                                   allow_small_or_imprecise_dtypes=True).then_inc(consts, 1)
                    nc.gpsimd.iota(base[:, :, :], [[KEYS * KEYS // 2, HEADS], [0, TOP]], base=0, channel_multiplier=0,
                                   allow_small_or_imprecise_dtypes=True).then_inc(consts, 1)

                    def fetch(u, h, slot):
                        for k in range(TOP):
                            pool.indirect_dma_start(
                                out=rows[:, slot, k, :], out_offset=None, in_=I["table"],
                                in_offset=bass.IndirectOffsetOnAxis(ap=index[:, u, h * TOP + k:h * TOP + k + 1], axis=0)
                            ).then_inc(gathered[slot], 16)

                    def gather(x):
                        pool.wait_ge(index_ready, START + x.t + 1)
                        for h in range(HEADS):
                            pool.wait_ge(weighed, HEADS * x.t + h + 1)
                            wait_apart(pool, passed_pool)
                            fetch(x.u, h, h % SLOTS)

                    walk(pool, gather)
                    for p in range(PAIRS):
                        for n, (u, h) in enumerate(fetch_order(p)):
                            pool.wait_ge(index_ready, START + LAST + u // 2 + 1)
                            pool.wait_ge(weighed, HEADS * LAST + 4 * p + n + 1)
                            fetch(u, h, n)

                @block.tensor
                def _(pe):
                    def project(t):
                        pe.wait_ge(fetched, START + t + 1)
                        pe.wait_ge(pk_copied, START + t)
                        for c in range(4):
                            last = nc.tensor.matmul(ps[:, 0, c * P:(c + 1) * P], w_pk[:, c * P:(c + 1) * P], xt[:, :],
                                                    start=True, stop=True)
                        last.then_inc(pk_made, 1)
                        pe.wait_ge(q_copied, START + t)
                        nc.tensor.matmul(ps[:, 3, :], xt[:, :], w_q[:, :], start=True, stop=True).then_inc(q_made, 1)
                        pe.wait_ge(pk_copied, START + t + 1)
                        pe.wait_ge(sims_copied, START + t)
                        for c in range(4):
                            last = nc.tensor.matmul(ps[:, 1 + c // 2, c % 2 * 256:(c % 2 + 1) * 256], pkT[:, c, :],
                                                    keys[:, c, :], start=True, stop=True)
                        last.then_inc(sims_made, 1)

                    def attend(m, projected):
                        for copied in (pk_copied, q_copied, sims_copied):
                            pe.wait_ge(copied, START + projected)
                        wait_apart(pe, A.passed_pe)
                        A.pe_start(pe, m, 0)
                        A.pe_head(pe, m, 0, True)
                        A.pe_head(pe, m, 1, False)
                        pe.wait_ge(A.normed, A.BEGIN + 2 * (2 * m + 2))
                        wait_apart(pe, A.passed_pe)

                    def step(x):
                        project(x.t + 1)
                        for b, j in x.beside:
                            attend(b * PAIRS + j, x.t + 2)
                        if x.second:
                            project(TILES - 1)

                    project(0)
                    walk(pe, step)
                    for p in range(PAIRS + 1):
                        for b, j in beside[p]:
                            attend(b * PAIRS + j, TILES)
                        for t in early_tiles(p):
                            if t >= 2:
                                pe.wait_ge(o_copied, t - 1)
                            for k in range(HEADS * D // P):
                                last = nc.tensor.transpose(ps[:, 6 + t % 2, k * P:(k + 1) * P], O[:, t, k * P:(k + 1) * P],
                                                           core.ident[:, :])
                            last.then_inc(o_turned, 1)
                            for done in ([t - 1] if t % CH else []) + ([t] if t % CH == CH - 1 else []):
                                pe.wait_ge(o_copied, done + 1)
                                if done >= 2:
                                    pe.wait_ge(o_added, done - 1)
                                for k in range(HEADS * D // P):
                                    last = nc.tensor.matmul(ps[:, 4 + done % 2, 0:D], o1[:, done % 2, k * P:(k + 1) * P], w_o[:, k, :],
                                                            start=(k == 0), stop=(k == HEADS * D // P - 1))
                                last.then_inc(o_projected, 1)
                        if early_tiles(p):
                            pe.wait_ge(o_added, p * CH)

                @block.scalar
                def _(act):
                    def prepare(t, u, tile, stores):
                        act.wait_ge(q_made, START + t)
                        if tile[0] == "tails":
                            lo = (2 * tile[1] + 1) * CH - 1
                            tails = core.xnT[0:D, :].rearrange("d (t n) -> d t n", n=P)[:, lo:lo + CH + 1:CH, 0:TAIL]
                            nc.scalar.activation(xt[:, :].rearrange("d (t n) -> d t n", n=TAIL), tails, ACT.Copy
                                                 ).then_inc(fetched, 1)
                        else:
                            nc.scalar.activation(xt[:, :], core.xnT[0:D, bass.ds(tile[1] * P, P)], ACT.Copy).then_inc(fetched, 1)
                        act.wait_ge(pk_made, START + t + 1)
                        act.wait_ge(sims_made, START + t)
                        nc.scalar.activation(pkT[:, :, :], ps[:, 0, :].rearrange("p (c n) -> p c n", n=P), ACT.Copy
                                             ).then_inc(pk_copied, 1)
                        act.wait_ge(q_made, START + t + 1)
                        if stores is not None:
                            act.wait_ge(stored[u], stores)
                        nc.scalar.activation(made_tile[:, u, :, 0:D], ps[:, 3, :].rearrange("p (h d) -> p h d", d=D),
                                             ACT.Copy, scale=0.125).then_inc(q_copied, 1)
                        act.wait_ge(sims_made, START + t + 1)
                        act.wait_ge(sim_used, START + t)
                        nc.scalar.activation(sim[:, :, :], ps[:, 1:3, :].rearrange("p b (q n) -> p (b q) n", n=KEYS),
                                             ACT.Copy).then_inc(sims_copied, 1)
                        act.wait_ge(shifted, START + t + 1)
                        nc.scalar.activation(fvals[:, :, :], fvals[:, :, :], ACT.Exp).then_inc(exped, 1)

                    def step(x):
                        first = isinstance(x.t, int) and x.t == 0
                        prepare(x.t + 1, 1 - x.u, x.next, None if first else 16 * (x.round + 1 + x.u))
                        for b, j in x.beside:
                            for u in range(2):
                                A.act_head(act, 2 * (b * PAIRS + j) + u, u)
                        if x.second:
                            prepare(TILES - 1, 2, ("tile", (B - 1) * CH + CH - 2), None)

                    prepare(0, 0, ("tails", 0), None)
                    walk(act, step)
                    for p in range(PAIRS + 1):
                        for b, j in beside[p]:
                            for u in range(2):
                                A.act_head(act, 2 * (b * PAIRS + j) + u, u)
                        for t in early_tiles(p):
                            act.wait_ge(o_turned, t + 1)
                            if t >= 2:
                                act.wait_ge(o_projected, t - 1)
                            nc.scalar.activation(o1[:, t % 2, :], ps[:, 6 + t % 2, :], ACT.Copy).then_inc(o_copied, 1)

                @block.vector
                def _(dve):
                    steps, attn_steps = Steps(dve, vec), Steps(dve, attn_vec)

                    def select(t, u):
                        dve.wait_ge(sims_copied, START + t + 1)
                        wait_apart(dve, passed)
                        for lo in (0, 8):
                            for q in range(2 * HEADS):
                                steps.add(nc.vector.max(vals[:, q, lo:lo + 8], sim[:, q, :]))
                            steps.settle(passed)
                            for q in range(2 * HEADS):
                                steps.add(nc.vector.max_index(ids[:, q, lo:lo + 8], vals[:, q, lo:lo + 8], sim[:, q, :]))
                            steps.settle(passed)
                            if lo == 0:
                                for q in range(2 * HEADS):
                                    steps.add(nc.vector.match_replace(sim[:, q, :], vals[:, q, 0:8], sim[:, q, :], LOWEST))
                                steps.settle(passed)
                        nc.vector.tensor_copy(idf[:, :, :], ids[:, :, :]).then_inc(sim_used, 1)
                        dve.wait_ge(sim_used, START + t + 1)
                        steps.add(nc.vector.tensor_scalar(idf[:, HEADS:, :], idf[:, HEADS:, :], float(KEYS), None, ALU.mult))
                        steps.add(nc.vector.scalar_tensor_tensor(idf[:, 0:HEADS, :], base[:, :, :], 2.0, idf[:, 0:HEADS, :],
                                                                 ALU.mult, ALU.add))
                        steps.do(nc.vector.tensor_tensor(
                            cand[:, :, :].rearrange("p h (a b) -> p h a b", a=TOP),
                            vals[:, 0:HEADS, :].unsqueeze(3).to_broadcast([P, HEADS, TOP, TOP]),
                            vals[:, HEADS:, :].unsqueeze(2).to_broadcast([P, HEADS, TOP, TOP]), ALU.add))
                        wait_apart(dve, passed)
                        for lo in (0, 8):
                            for h in range(HEADS):
                                steps.add(nc.vector.max(fvals[:, h, lo:lo + 8], cand[:, h, :]))
                            steps.settle(passed)
                            for h in range(HEADS):
                                steps.add(nc.vector.max_index(fids[:, h * TOP + lo:h * TOP + lo + 8],
                                                              fvals[:, h, lo:lo + 8], cand[:, h, :]))
                            steps.settle(passed)
                            if lo == 0:
                                for h in range(HEADS):
                                    steps.add(nc.vector.match_replace(cand[:, h, :], fvals[:, h, 0:8], cand[:, h, :], LOWEST))
                                steps.settle(passed)
                        onehot = cand[:, :, :].rearrange("p h (k a) -> p h k a", a=TOP)
                        for part, (op, by) in enumerate(((ALU.logical_shift_right, 4), (ALU.bitwise_and, 15))):
                            steps.do(nc.vector.tensor_scalar(half[:, :], fids[:, :], by, None, op))
                            steps.do(nc.vector.tensor_copy(halff[:, :], half[:, :]))
                            steps.do(nc.vector.tensor_tensor(cand[:, :, :].rearrange("p h (k a) -> p (h k) a", a=TOP),
                                                             over(halff[:, :], TOP), rows_of(count16[:, :], HEADS * TOP),
                                                             ALU.is_equal))
                            steps.do(nc.vector.tensor_tensor(
                                onehot, onehot,
                                idf[:, part * HEADS:(part + 1) * HEADS, :].unsqueeze(2).to_broadcast([P, HEADS, TOP, TOP]),
                                ALU.mult))
                            steps.do(nc.vector.tensor_reduce(found[:, part, :],
                                                             cand[:, :, :].rearrange("p h (k a) -> p (h k) a", a=TOP),
                                                             AX.X, ALU.add))
                        steps.add(nc.vector.tensor_copy(sums[:, 0, :], fvals[:, :, 0]))
                        nc.vector.tensor_tensor(index[:, u, :], found[:, 0, :], found[:, 1, :], ALU.add
                                                ).then_inc(index_ready, 1)
                        steps.settle()
                        nc.vector.tensor_tensor(fvals[:, :, :], fvals[:, :, :], over(sums[:, 0, :], TOP), ALU.subtract
                                                ).then_inc(shifted, 1)
                        dve.wait_ge(exped, START + t + 1)
                        steps.do(nc.vector.tensor_reduce(sums[:, 1, :], fvals[:, :, :], AX.X, ALU.add))
                        steps.do(nc.vector.reciprocal(sums[:, 0, :], sums[:, 1, :]))
                        steps.do(nc.vector.tensor_tensor(weight[:, u, :, :], fvals[:, :, :], over(sums[:, 0, :], TOP), ALU.mult))

                    def weigh_rows(u, h, slot):
                        steps.do(nc.vector.tensor_tensor(rows[:, slot, :, :], rows[:, slot, :, :],
                                                         over(weight[:, u, h, :], 2 * D), ALU.mult))
                        nc.vector.tensor_reduce(made_tile[:, u, h, D:3 * D], rows[:, slot, :, :].rearrange("p k d -> p d k"),
                                                AX.X, ALU.add).then_inc(weighed, 1)

                    def weigh(x, heads):
                        for h in heads:
                            uses = HEADS // SLOTS
                            dve.wait_ge(gathered[h % SLOTS], 16 * TOP * (uses * x.t + h // SLOTS + 1))
                            weigh_rows(x.u, h, h % SLOTS)

                    def attend(b, j, u):
                        m = b * PAIRS + j
                        if u == 0:
                            attn_steps.before, attn_steps.count = 2 * A.STEPS * m, 0
                            A.dve_start(dve, 2 * m, 0)
                        A.dve_head(dve, attn_steps, 2 * m + u, u, u == 0, u == 1, out_of(b, 2 * j + u),
                                   out_of(b, 2 * j) if u else None)

                    dve.sem_inc(weighed, SLOTS)
                    dve.wait_ge(consts, 2)
                    select(0, 0)
                    per_select = steps.count

                    def step(x):
                        steps.before, steps.count = per_select * (x.t + 1) + HEADS * x.t, 0
                        select(x.t + 1, 1 - x.u)
                        if x.tails is None:
                            dve.wait_ge(stored[x.u], 16 * (x.round + 1))
                            wait_apart(dve, passed)
                        if not x.beside:
                            weigh(x, range(HEADS))
                        for n, (b, j) in enumerate(x.beside):
                            share = HEADS // len(x.beside)
                            heads = range(n * share, (n + 1) * share)
                            weigh(x, heads[:share // 4])
                            attend(b, j, 0)
                            weigh(x, heads[share // 4:share // 2 + 1])
                            attend(b, j, 1)
                            if x.second:
                                steps.before, steps.count = per_select * (LAST + 1) + HEADS * (LAST - 1) + share // 2 + 1, 0
                                select(TILES - 1, 2)
                            weigh(x, heads[share // 2 + 1:])

                    walk(dve, step)
                    steps.before, steps.count = per_select * (LAST + 2) + HEADS * LAST, 0
                    dve.wait_ge(stored[0], 16 * (LAST // 2 + 1))
                    for p in range(PAIRS + 1):
                        for b, j in beside[p]:
                            for u in range(2):
                                attend(b, j, u)
                                if p < PAIRS:
                                    for n in (2 * u, 2 * u + 1):
                                        dve.wait_ge(gathered[n], 16 * TOP * (HEADS // SLOTS * LAST + p + 1))
                                        weigh_rows(*fetch_order(p)[n], n)
                        for t in early_tiles(p):
                            dve.wait_ge(o_projected, t + 1)
                            nc.vector.tensor_tensor(core.h[:, t, :], core.h[:, t, :], ps[:, 4 + t % 2, 0:D], ALU.add
                                                    ).then_inc(o_added, 1)
        with Stage(nc, "peer_out") as at:
            TERMS = HEADS * D // P
            oT = at.sb("oT", [P, TERMS, CH * P])
            turn_stage(nc, core, "peer_turn", [(oT[:, k, :], P, lambda t, k=k: O[:, T - CH + t, k * P:(k + 1) * P])
                                               for k in range(TERMS)], tiles=CH)
            product_stage(nc, core, "peer_proj",
                          [(lambda t, k=k: oT[:, k, t * P:(t + 1) * P], w_o[:, k, :]) for k in range(TERMS)], D,
                          lambda t0, t1, made: nc.vector.tensor_tensor(core.h[:, T - CH + t0:T - CH + t1, :],
                                                                       core.h[:, T - CH + t0:T - CH + t1, :], made, ALU.add),
                          tiles=CH)


CHANNELS = 3 * D
RPE = 8
RPE_LAYERS = 3
SPAN = 2 * SEQ
LAGS = SPAN // P
FREQ = SEQ + 1
FCH = (FREQ + P - 1) // P
FREQ_ROWS = [min(P, FREQ - P * k) for k in range(FCH)]
TOKEN_ROWS = [min(P, SEQ - P * c) for c in range(CH)]


def root_stage(nc, core, name, x, sq, stat, scale, eps, ones=None):
    with Stage(nc, name) as st:
        vec, squared, rooted = st.sem("vector_steps"), st.sem("squared"), st.sem("rooted")
        with nc.Block() as block:
            @block.vector
            def _(dve):
                steps = Steps(dve, vec)
                steps.do(nc.vector.tensor_tensor(sq, x, x, ALU.mult))
                nc.vector.tensor_reduce(stat[:, 0, :], sq, AX.X, ALU.add).then_inc(squared, 1)
                dve.wait_ge(rooted, 1)
                steps.do(nc.vector.tensor_scalar(stat[:, 0, :], stat[:, 0, :], scale, eps, ALU.mult, ALU.add))
                steps.do(nc.vector.reciprocal(stat[:, 1, :], stat[:, 0, :]))
                steps.do(nc.vector.tensor_tensor(x, x, over(stat[:, 1, :], D), ALU.mult))

            @block.scalar
            def _(act):
                act.wait_ge(squared, 1)
                nc.scalar.activation(stat[:, 0, :], stat[:, 0, :], ACT.Sqrt).then_inc(rooted, 1)


def lag_network_stage(nc, core, lags, w_pos, w_mid, w_out, a):
    with Stage(nc, "rpe") as st:
        x, sq = st.sb("x", [P, LAGS, RPE]), st.sb("sq", [P, LAGS, RPE])
        stat = st.sb("stat", [P, 3, LAGS])
        act_in = st.sb("act_in", [RPE + 1, SPAN])
        made, squared, rooted, ready, vec, turned, turned_copied, copied, ones = (
            st.sem(n) for n in ("made", "squared", "rooted", "ready", "vector_steps", "turned", "turned_copied",
                                "copied", "ones"))
        ps, third = core.psum, SPAN // 3
        per = LAGS // 3
        rounds = RPE_LAYERS + 1
        with nc.Block() as block:
            @block.gpsimd
            def _(pool):
                nc.gpsimd.memset(act_in[:, :], 1.0).then_inc(ones, 1)

            @block.tensor
            def _(pe):
                for r in range(rounds):
                    if r:
                        pe.wait_ge(turned_copied, r)
                    for t in range(LAGS):
                        weights = w_pos[:, :] if r == 0 else w_mid[:, r - 1, :]
                        moving = lags if r == 0 else act_in
                        last = nc.tensor.matmul(ps[:, 0, t * RPE:(t + 1) * RPE], moving[:, t * P:(t + 1) * P], weights,
                                                start=True, stop=True)
                    last.then_inc(made, 1)
                    pe.wait_ge(ready, r + 1)
                    for t in range(LAGS):
                        last = nc.tensor.transpose(ps[0:RPE, 1 + t // per, t % per * P:(t % per + 1) * P], x[:, t, :],
                                                   core.ident[:, :])
                    last.then_inc(turned, 1)
                pe.wait_ge(turned_copied, rounds)
                for t in range(LAGS):
                    if t == 4:
                        pe.wait_ge(copied, 1)
                    bank = 4 + t % 4 if t < 8 else 0
                    nc.tensor.matmul(ps[:, bank, 0:CHANNELS], act_in[:, t * P:(t + 1) * P], w_out[:, :],
                                     start=True, stop=True).then_inc(made, 1)

            @block.vector
            def _(dve):
                steps = Steps(dve, vec)
                for r in range(rounds):
                    dve.wait_ge(made, r + 1)
                    steps.do(nc.vector.tensor_copy(x[:, :, :], ps[:, 0, 0:LAGS * RPE].rearrange("p (t f) -> p t f", f=RPE)))
                    steps.do(nc.vector.tensor_tensor(sq[:, :, :], x[:, :, :], x[:, :, :], ALU.mult))
                    nc.vector.tensor_reduce(stat[:, 0, :], sq[:, :, :], AX.X, ALU.add).then_inc(squared, 1)
                    dve.wait_ge(rooted, r + 1)
                    steps.do(nc.vector.tensor_scalar(stat[:, 1, :], stat[:, 1, :], RPE ** -0.5, 1e-8, ALU.mult, ALU.add))
                    steps.do(nc.vector.reciprocal(stat[:, 2, :], stat[:, 1, :]))
                    steps.do(nc.vector.tensor_tensor(x[:, :, :], x[:, :, :], over(stat[:, 2, :], RPE), ALU.mult))
                    nc.vector.tensor_scalar(x[:, :, :], x[:, :, :], 0.0, None, ALU.max).then_inc(ready, 1)
                dve.wait_ge(made, rounds + 4)
                nc.vector.tensor_copy(a[:, 0:4, :], ps[:, 4:8, 0:CHANNELS]).then_inc(copied, 1)
                dve.wait_ge(made, rounds + LAGS)
                nc.vector.tensor_copy(a[:, 4:8, :], ps[:, 4:8, 0:CHANNELS]).then_inc(copied, 1)
                nc.vector.tensor_copy(a[:, 8, :], ps[:, 0, 0:CHANNELS]).then_inc(copied, 1)

            @block.scalar
            def _(act):
                act.wait_ge(ones, 1)
                for r in range(rounds):
                    act.wait_ge(squared, r + 1)
                    nc.scalar.activation(stat[:, 1, :], stat[:, 0, :], ACT.Sqrt).then_inc(rooted, 1)
                    act.wait_ge(turned, r + 1)
                    nc.scalar.activation(act_in[0:RPE, :].rearrange("p (k n) -> p k n", k=3), ps[0:RPE, 1:4, 0:third], ACT.Copy
                                         ).then_inc(turned_copied, 1)


def toeplitz_stage(nc, core, I, norm):
    with Stage(nc, "tnn") as st:
        w_uv = st.sb("w_uv", [D + 1, 2 * CHANNELS])
        uv = st.sb("uv", [P, T, 2 * CHANNELS])
        lags = st.sb("lags", [2, SPAN])
        w_pos = st.sb("w_pos", [2, RPE])
        w_mid = st.sb("w_mid", [RPE + 1, RPE_LAYERS, RPE])
        w_out = st.sb("w_out", [RPE + 1, CHANNELS])
        small_loads = Loads(nc, st, "landed", [
            (w_uv[:, :], I["uv_aug"]), (lags[:, :], I["lags"]), (w_pos[:, :], I["pos_aug"]),
            (w_mid[:, :, :], I["rpe_aug"]), (w_out[:, :], I["out_aug"])])
        uv_b = uv[:, :, :].rearrange("p (b c) w -> p b c w", c=CH)
        with Stage(nc, "dft") as at:
            a = at.sb("a", [P, LAGS, CHANNELS])
            cos, sin = at.sb("cos", [P, LAGS, FREQ]), at.sb("sin", [P, LAGS, FREQ])
            icos, isin = at.sb("icos", [P, FCH, SEQ]), at.sb("isin", [P, FCH, SEQ])
            af = at.sb("af", [P, 2, CHANNELS])
            vf = at.sb("vf", [P, 2, B, CHANNELS])
            t1, t2, t3, t4 = (at.sb(f"t{k}", [P, B, CHANNELS]) for k in range(4))
            y = at.sb("y", [P, FCH, 2, B, CHANNELS])
            loads = [(to[:, :, :], I[n].rearrange("(k p) f -> p k f", p=P)) for to, n in ((cos, "cos"), (sin, "sin"))]
            for to, n in ((icos, "icos"), (isin, "isin")):
                loads += [(to[:, 0:FCH - 1, :], I[n][0:(FCH - 1) * P, :].rearrange("(k p) f -> p k f", p=P)),
                          (to[0:FREQ_ROWS[-1], FCH - 1, :], I[n][(FCH - 1) * P:FREQ, :])]
            loads = Loads(nc, at, "landed", loads)
            norm()
            product_stage(nc, core, "tnn_uv", [(lambda t: core.xnT[:, t * P:(t + 1) * P], w_uv[:, :])], 2 * CHANNELS,
                          lambda t0, t1, made: nc.scalar.activation(uv[:, t0:t1, :], made, ACT.Silu), engine="scalar", loads=small_loads)
            lag_network_stage(nc, core, lags, w_pos, w_mid, w_out, a)
            loads.arrive()
            made, copied, multiplied, vec, gps, crossed = (
                at.sem(n) for n in ("made", "copied", "multiplied", "vector_steps", "pool_steps", "crossed"))
            ps = core.psum
            with nc.Block() as block:
                @block.tensor
                def _(pe):
                    for f in range(FCH):
                        m = FREQ_ROWS[f]
                        if f:
                            pe.wait_ge(copied, f)
                        for part, table in enumerate((cos, sin)):
                            for k in range(LAGS):
                                nc.tensor.matmul(ps[0:m, part, 0:CHANNELS], table[:, k, f * P:f * P + m], a[:, k, :],
                                                 start=(k == 0), stop=(k == LAGS - 1))
                            for pair in range(2):
                                for c in range(CH):
                                    r = TOKEN_ROWS[c]
                                    last = nc.tensor.matmul(
                                        ps[0:m, 2 + 2 * part + pair, 0:2 * CHANNELS].rearrange("p (b w) -> p b w", b=2),
                                        table[0:r, c, f * P:f * P + m],
                                        uv_b[0:r, 2 * pair:2 * pair + 2, c, CHANNELS:2 * CHANNELS],
                                        start=(c == 0), stop=(c == CH - 1))
                        last.then_inc(made, 1)

                @block.scalar
                def _(act):
                    for f in range(FCH):
                        m = FREQ_ROWS[f]
                        act.wait_ge(made, f + 1)
                        if f:
                            act.wait_ge(multiplied, f)
                            act.wait_ge(crossed, f)
                        nc.scalar.activation(af[0:m, :, :], ps[0:m, 0:2, 0:CHANNELS], ACT.Copy)
                        nc.scalar.activation(
                            vf[0:m, :, :, :].rearrange("p s (q b) w -> p (s q) (b w)", b=2),
                            ps[0:m, 2:6, 0:2 * CHANNELS], ACT.Copy).then_inc(copied, 1)

                def cross(eng, engine, steps, f, out, parts, temps, op, done):
                    m = FREQ_ROWS[f]
                    for k in range(2):
                        steps.add(engine.tensor_tensor(temps[k][0:m, :, :], vf[0:m, parts[2 * k], :, :],
                                                       rows_of(af[0:m, parts[2 * k + 1], :], B), ALU.mult))
                    steps.settle()
                    engine.tensor_tensor(out[0:m, :, :], temps[0][0:m, :, :], temps[1][0:m, :, :], op).then_inc(done, 1)

                @block.vector
                def _(dve):
                    steps = Steps(dve, vec)
                    for f in range(FCH):
                        dve.wait_ge(copied, f + 1)
                        if f:
                            dve.wait_ge(multiplied, f)
                        cross(dve, nc.vector, steps, f, y[:, f, 0, :, :], (0, 0, 1, 1), (t1, t2), ALU.subtract, multiplied)

                @block.gpsimd
                def _(pool):
                    steps = Steps(pool, gps)
                    for f in range(FCH):
                        pool.wait_ge(copied, f + 1)
                        if f:
                            pool.wait_ge(crossed, f)
                        cross(pool, nc.gpsimd, steps, f, y[:, f, 1, :, :], (1, 0, 0, 1), (t3, t4), ALU.add, crossed)

            jobs = [(c, pair) for c in range(CH) for pair in range(2)]
            inverted, gated = at.sem("inverted"), at.sem("gated")
            with nc.Block() as block:
                @block.tensor
                def _(pe):
                    for n, (c, pair) in enumerate(jobs):
                        if n >= 8:
                            pe.wait_ge(gated, n - 7)
                        m = TOKEN_ROWS[c]
                        for k in range(2 * FCH):
                            f, part = k // 2, k % 2
                            r = FREQ_ROWS[f]
                            last = nc.tensor.matmul(
                                ps[0:m, n % 8, 0:2 * CHANNELS].rearrange("p (b w) -> p b w", b=2),
                                (icos, isin)[part][0:r, f, c * P:c * P + m], y[0:r, f, part, 2 * pair:2 * pair + 2, :],
                                start=(k == 0), stop=(k == 2 * FCH - 1))
                        last.then_inc(inverted, 1)

                @block.vector
                def _(dve):
                    for n, (c, pair) in enumerate(jobs):
                        m = TOKEN_ROWS[c]
                        dve.wait_ge(inverted, n + 1)
                        u = uv_b[0:m, 2 * pair:2 * pair + 2, c, 0:CHANNELS]
                        nc.vector.tensor_tensor(u, u, ps[0:m, n % 8, 0:2 * CHANNELS].rearrange("p (b w) -> p b w", b=2),
                                                ALU.mult).then_inc(gated, 1)
        with Stage(nc, "tnn_out") as at:
            g0, g1 = at.sb("g0", [P, COLS]), at.sb("g1", [D + 1, COLS])
            w_o0, w_o1, w_t = at.sb("w_o0", [P, D]), at.sb("w_o1", [D + 1, D]), at.sb("w_t", [D + 1, D])
            r = at.sb("r", [P, T, D])
            sq, stat = at.sb("sq", [P, T, D]), at.sb("stat", [P, 2, T])
            set_stage(nc, "g1_ones", [(g1[:, :], 1.0)])
            loads = Loads(nc, at, "landed", [(w_o0[:, :], I["o_aug"][0:P, :]), (w_o1[:, :], I["o_aug"][P:CHANNELS + 1, :]),
                                            (w_t[:, :], I["t_aug"])])
            turn_stage(nc, core, "tnn_turn", [(g0, P, lambda t: uv[:, t, 0:P]), (g1, D, lambda t: uv[:, t, P:CHANNELS])])
            product_stage(nc, core, "tnn_o", [(lambda t: g0[:, t * P:(t + 1) * P], w_o0[:, :]),
                                              (lambda t: g1[:, t * P:(t + 1) * P], w_o1[:, :])], D,
                          lambda t0, t1, made: nc.vector.tensor_tensor(r[:, t0:t1, :], core.xn[:, t0:t1, :], made, ALU.subtract), loads=loads)
            turn_stage(nc, core, "tnn_turn_r", [(core.xnT, D, lambda t: r[:, t, :])])
            product_stage(nc, core, "tnn_t", [(lambda t: core.xnT[:, t * P:(t + 1) * P], w_t[:, :])], D,
                          lambda t0, t1, made: nc.vector.tensor_copy(r[:, t0:t1, :], made))
            root_stage(nc, core, "tnn_root", r[:, :, :], sq[:, :, :], stat, CHANNELS ** -0.5, 1e-8)
            silu_stage(nc, core, "tnn_silu", r[:, :, :])
            add_stage(nc, core, "tnn_add", (core.h[:, :, :], core.h[:, :, :], core.xn[:, :, :]),
                      (core.h[:, :, :], core.h[:, :, :], r[:, :, :]))


def silu_stage(nc, core, name, x):
    with nc.Block() as block:
        @block.scalar
        def _(act):
            nc.scalar.activation(x, x, ACT.Silu)


def top_two_stage(nc, core, name, scores, weight, experts, renorm):
    E = experts
    with Stage(nc, name) as st:
        peak, total = st.sb("peak", [P, T]), st.sb("total", [P, T])
        above = st.sb("above", [P, T, E, E])
        same = st.sb("same", [P, T, E, E])
        before = st.sb("before", [P, E, E])
        rank = st.sb("rank", [P, T, E])
        vec, shifted, exped, consts = (st.sem(n) for n in ("vector_steps", "shifted", "exped", "consts"))
        with nc.Block() as block:
            @block.gpsimd
            def _(pool):
                nc.gpsimd.memset(before[:, :, :], 1.0).then_inc(consts, 1)
                pool.wait_ge(consts, 1)
                nc.gpsimd.affine_select(out=before[:, :, :], in_=before[:, :, :], compare_op=ALU.is_gt, fill=0.0,
                                        base=0, pattern=[[1, E], [-1, E]], channel_multiplier=0).then_inc(consts, 1)

            @block.scalar
            def _(act):
                act.wait_ge(shifted, 1)
                nc.scalar.activation(scores, scores, ACT.Exp).then_inc(exped, 1)
                if renorm == "softmax":
                    act.wait_ge(shifted, 2)
                    nc.scalar.activation(weight, weight, ACT.Exp).then_inc(exped, 1)

            @block.vector
            def _(dve):
                steps = Steps(dve, vec)
                steps.do(nc.vector.tensor_reduce(peak[:, :], scores, AX.X, ALU.max))
                nc.vector.tensor_tensor(scores, scores, over(peak[:, :], E), ALU.subtract).then_inc(shifted, 1)
                dve.wait_ge(exped, 1)
                steps.do(nc.vector.tensor_reduce(total[:, :], scores, AX.X, ALU.add))
                steps.do(nc.vector.reciprocal(total[:, :], total[:, :]))
                steps.do(nc.vector.tensor_tensor(scores, scores, over(total[:, :], E), ALU.mult))
                of_f = scores.unsqueeze(2).to_broadcast([P, T, E, E])
                of_e = scores.unsqueeze(3).to_broadcast([P, T, E, E])
                steps.add(nc.vector.tensor_tensor(above[:, :, :, :], of_f, of_e, ALU.is_gt))
                steps.do(nc.vector.tensor_tensor(same[:, :, :, :], of_f, of_e, ALU.is_equal))
                dve.wait_ge(consts, 2)
                flat = lambda a: a[:, :, :, :].rearrange("p t e f -> p t (e f)")
                steps.do(nc.vector.tensor_tensor(flat(same), flat(same),
                                                 rows_of(before[:, :, :].rearrange("p e f -> p (e f)"), T), ALU.mult))
                steps.do(nc.vector.tensor_tensor(flat(above), flat(above), flat(same), ALU.add))
                steps.do(nc.vector.tensor_reduce(rank[:, :, :], above[:, :, :, :], AX.X, ALU.add))
                steps.do(nc.vector.tensor_scalar(rank[:, :, :], rank[:, :, :], 2.0, None, ALU.is_lt))
                if renorm == "softmax":
                    steps.do(nc.vector.tensor_reduce(peak[:, :], scores, AX.X, ALU.max))
                    nc.vector.tensor_tensor(weight, scores, over(peak[:, :], E), ALU.subtract).then_inc(shifted, 1)
                    dve.wait_ge(exped, 2)
                    steps.do(nc.vector.tensor_tensor(weight, weight, rank[:, :, :], ALU.mult))
                else:
                    steps.do(nc.vector.tensor_tensor(weight, scores, rank[:, :, :], ALU.mult))
                steps.do(nc.vector.tensor_reduce(total[:, :], weight, AX.X, ALU.add))
                if renorm != "softmax":
                    steps.do(nc.vector.tensor_scalar(total[:, :], total[:, :], 1e-9, None, ALU.add))
                steps.do(nc.vector.reciprocal(total[:, :], total[:, :]))
                steps.do(nc.vector.tensor_tensor(weight, weight, over(total[:, :], E), ALU.mult))


Q_HEADS = 4
HD = D // Q_HEADS
EXPERTS = 8
HIDDEN = 170
HALF = HIDDEN // 2


def gated_experts_stage(nc, core, I, weight, acc, x, loads_x):
    with Stage(nc, "moe") as st:
        WIDE = EXPERTS * HIDDEN
        w11, w22, w31 = (st.sb(n, [P, 2 * WIDE], BF16) for n in ("w11", "w22", "w31"))
        x12, x13 = st.sb("x12", [P, COLS], BF16), st.sb("x13", [P, COLS], BF16)
        w2 = st.sb("w2", [HALF, 2 * EXPERTS, D])
        loads = Loads(nc, st, "landed", [(w2[:, :, :], I["moe_w2"].rearrange("(u p) d -> p u d", p=HALF))])
        loads_x.arrive()
        split_tokens_stage(nc, "moe_split", x[:, :], x12, x13)
        split_weights_stage(nc, "moe_weights", I["moe_w13"], w11, w22, w31, WIDE // 2)
        products = ((w11, x12), (w22, x12), (w31, x13))
        act1 = st.sb("act1", [HALF, 3, BANK])
        hid = st.sb("hid", [HALF, 4, BANK])
        part = st.sb("part", [P, 2, 4, D])
        loads.arrive()
        raised, activated, gated, lowered, scaled, added, passed = (
            st.sem(n) for n in ("raised", "activated", "gated", "lowered", "scaled", "added", "passed"))
        start_loop(nc, [raised, activated, gated, lowered, scaled, added])
        ps = core.psum
        U = 2 * EXPERTS
        with nc.Block() as block:
            @block.tensor
            def _(pe):
                with pe.Fori(0, GROUPS) as g:
                    def raise_(e):
                        for u in (2 * e, 2 * e + 1):
                            pe.wait_ge(gated, START + U * g + max(u - 2, 0))
                            wait_apart(pe, passed)
                            for which in range(2):
                                lo = which * WIDE + u * HALF
                                for k, (w, x) in enumerate(products):
                                    last = nc.tensor.matmul(ps[0:HALF, 3 * which + u % 3, :], w[:, lo:lo + HALF],
                                                            x[:, bass.ds(g * BANK, BANK)], start=(k == 0), stop=(k == 2))
                            last.then_inc(raised, 1)

                    raise_(0)
                    for e in range(EXPERTS):
                        if e + 1 < EXPERTS:
                            raise_(e + 1)
                        pe.wait_ge(gated, START + U * g + 2 * e + 2)
                        pe.wait_ge(scaled, START + EXPERTS * g + max(e - 1, 0))
                        wait_apart(pe, passed)
                        for k in range(4):
                            for half in range(2):
                                last = nc.tensor.matmul(ps[:, 6 + e % 2, k * D:(k + 1) * D],
                                                        hid[:, (2 * e + half) % 4, k * P:(k + 1) * P], w2[:, 2 * e + half, :],
                                                        start=(half == 0), stop=(half == 1))
                        last.then_inc(lowered, 1)

            @block.scalar
            def _(act):
                with act.Fori(0, GROUPS) as g:
                    for u in range(U):
                        act.wait_ge(raised, START + U * g + u + 1)
                        act.wait_ge(gated, START + U * g + max(u - 2, 0))
                        nc.scalar.activation(act1[:, u % 3, :], ps[0:HALF, u % 3, :], ACT.Silu).then_inc(activated, 1)

            @block.vector
            def _(dve):
                with dve.Fori(0, GROUPS) as g:
                    def gate(e):
                        for u in (2 * e, 2 * e + 1):
                            dve.wait_ge(activated, START + U * g + u + 1)
                            dve.wait_ge(lowered, START + EXPERTS * g + max(e - 1, 0))
                            nc.vector.tensor_tensor(hid[:, u % 4, :], act1[:, u % 3, :], ps[0:HALF, 3 + u % 3, :],
                                                    ALU.mult).then_inc(gated, 1)

                    gate(0)
                    for e in range(EXPERTS):
                        if e + 1 < EXPERTS:
                            gate(e + 1)
                        n = EXPERTS * g + e
                        dve.wait_ge(lowered, START + n + 1)
                        nc.vector.tensor_tensor(part[:, e % 2, :, :], ps[:, 6 + e % 2, 0:4 * D].rearrange("p (t d) -> p t d", d=D),
                                                over(weight[:, bass.ds(4 * g, 4), e], D), ALU.mult).then_inc(scaled, 1)
                        dve.wait_ge(scaled, START + n + 1)
                        dve.wait_ge(added, START + n)
                        nc.vector.tensor_tensor(acc[:, bass.ds(4 * g, 4), :], acc[:, bass.ds(4 * g, 4), :],
                                                part[:, e % 2, :, :], ALU.add).then_inc(added, 1)


PARTS = 6 * HD


def stack_parts_stage(nc, qkv, q_parts, k_parts):
    with Stage(nc, "parts") as st:
        part = [st.sb(f"part{k}", [P, T, 2 * D], BF16) for k in range(3)]
        rest = st.sb("rest", [P, T, 2 * D])
        cast, less = st.sem("cast"), st.sem("less")
        x = qkv[:, :, 0:2 * D]
        head = lambda a: a.rearrange("p t (h d) -> p t h d", h=Q_HEADS)

        def place(copy, to, column, k, which):
            copy(head(to[:, :, :])[:, :, :, column * HD:(column + 1) * HD], head(part[k][:, :, which * D:(which + 1) * D]))

        with nc.Block() as block:
            @block.scalar
            def _(act):
                copy = lambda to, of: nc.scalar.activation(to, of, ACT.Copy)
                copy(part[0][:, :, :], x).then_inc(cast, 1)
                act.wait_ge(cast, 1)
                for column in (0, 1):
                    place(copy, q_parts, column, 0, 0)
                act.wait_ge(less, 1)
                copy(part[1][:, :, :], rest[:, :, :]).then_inc(cast, 1)
                act.wait_ge(cast, 2)
                for column in (2, 3):
                    place(copy, q_parts, column, 1, 0)
                place(copy, k_parts, 1, 1, 1)

            @block.gpsimd
            def _(pool):
                pool.wait_ge(cast, 1)
                place(nc.gpsimd.tensor_copy, q_parts, 4, 0, 0)
                for column in (0, 2, 5):
                    place(nc.gpsimd.tensor_copy, k_parts, column, 0, 1)

            @block.vector
            def _(dve):
                dve.wait_ge(cast, 1)
                nc.vector.tensor_tensor(rest[:, :, :], x, part[0][:, :, :], ALU.subtract).then_inc(less, 1)
                dve.wait_ge(cast, 2)
                dve.wait_ge(less, 1)
                nc.vector.tensor_tensor(part[2][:, :, :], rest[:, :, :], part[1][:, :, :], ALU.subtract).then_inc(less, 1)
                place(nc.vector.tensor_copy, k_parts, 3, 1, 1)
                dve.wait_ge(less, 2)
                place(nc.vector.tensor_copy, q_parts, 5, 2, 0)
                place(nc.vector.tensor_copy, k_parts, 4, 2, 1)


def rotary_experts_stage(nc, core, I, norm):
    with Stage(nc, "rot") as st:
        spare = st.sb("spare", [P, T, D])
        with Stage(nc, "rot_attn") as at:
            width = 5 * D
            w_in = at.sb("w_in", [D, width])
            w_out = at.sb("w_out", [D, D])
            cos, sin = at.sb("cos", [P, CH, HD]), at.sb("sin", [P, CH, HD])
            qkv = at.sb("qkv", [P, T, width])
            yT = at.sb("yT", [D, COLS])
            loads = Loads(nc, at, "landed", [(w_in[:, :], I["rot_in"]), (w_out[:, :], I["rot_out"]),
                                        (cos[:, :, :], I["rot_cos"].rearrange("(c p) d -> p c d", p=P)),
                                        (sin[:, :, :], I["rot_sin"].rearrange("(c p) d -> p c d", p=P))])
            norm()
            norm_stage(nc, core, "rot_rms1", core.xn, eps=1e-6, use_mean=False, gain=I["rms1_w"], dst=spare)
            product_stage(nc, core, "rot_qkv", [(lambda t: core.xnT[0:D, t * P:(t + 1) * P], w_in[:, :])], width,
                          lambda t0, t1, made: nc.scalar.activation(qkv[:, t0:t1, :], made, ACT.Copy), engine="scalar", loads=loads)
            with Stage(nc, "rope") as rt:
                vec = rt.sem("vector_steps")
                with nc.Block() as block:
                    @block.vector
                    def _(dve):
                        steps = Steps(dve, vec)
                        parts = [(lo, table) for lo, table in ((0, cos), (2 * D, sin))]
                        view = lambda b, lo: qkv[:, b * CH:(b + 1) * CH, lo:lo + 2 * D].rearrange("p c (h d) -> p c h d", d=HD)
                        for b in range(B):
                            for lo, table in parts:
                                steps.add(nc.vector.tensor_tensor(
                                    view(b, lo), view(b, lo),
                                    table[:, :, :].unsqueeze(2).to_broadcast([P, CH, 2 * Q_HEADS, HD]), ALU.mult))
                        steps.settle()
                        steps.do(nc.vector.tensor_tensor(qkv[:, :, 0:2 * D], qkv[:, :, 0:2 * D], qkv[:, :, 2 * D:4 * D], ALU.add))
            q_parts, k_parts = (at.sb(n, [P, T, Q_HEADS * PARTS], BF16) for n in ("q_parts", "k_parts"))
            stack_parts_stage(nc, qkv, q_parts, k_parts)
            causal_attention_stage(nc, core, "rot_soft", [(q_parts, PARTS, 0), (k_parts, PARTS, 0), (qkv, HD, 4 * D)], qkv,
                                   Q_HEADS, HD, HD ** -0.5, parts=PARTS)
            turn_stage(nc, core, "rot_turn", [(yT, D, lambda t: qkv[:, t, 0:D])])
            product_stage(nc, core, "rot_proj", [(lambda t: yT[:, t * P:(t + 1) * P], w_out[:, :])], D,
                          lambda t0, t1, made: nc.vector.tensor_tensor(core.xn[:, t0:t1, :], core.xn[:, t0:t1, :], made, ALU.add))
        router, weight = st.sb("router", [P, T, EXPERTS]), st.sb("weight", [P, T, EXPERTS])
        w_r = st.sb("w_r", [D, EXPERTS])
        loads = Loads(nc, st, "landed", [(w_r[:, :], I["router"])])
        norm_stage(nc, core, "rot_rms2", core.xn, eps=1e-6, use_mean=False, gain=I["rms2_w"], dst=spare)
        loads.arrive()
        x = st.sb("x_twice", [P, COLS])
        loads_x = Loads(nc, st, "x_landed", [(x[half * D:(half + 1) * D, :], core.xnT[0:D, :]) for half in range(2)])
        product_stage(nc, core, "router_p", [(lambda t: core.xnT[0:D, t * P:(t + 1) * P], w_r[:, :])], EXPERTS,
                      lambda t0, t1, made: nc.vector.tensor_copy(router[:, t0:t1, :], made))
        top_two_stage(nc, core, "router_top", router[:, :, :], weight[:, :, :], EXPERTS, "sum")
        gated_experts_stage(nc, core, I, weight, core.xn, x, loads_x)
        add_stage(nc, core, "rot_residual", (core.h[:, :, :], core.h[:, :, :], core.xn[:, :, :]))


KEEP = SEQ // 10
SLOT = 64
S_HEADS = 8
S_HD = D // S_HEADS


def sparse_attention_stage(nc, core, I, norm):
    with Stage(nc, "sparse") as st:
        w_qkv, w_g1, w_g2, w_o = (st.sb(n, s) for n, s in (
            ("w_qkv", [D + 1, 3 * D]), ("w_g1", [D + 1, 16]), ("w_g2", [17, 1]), ("w_o", [D + 1, D])))
        qkv = st.sb("qkv", [P, T, 3 * D])
        gT = st.sb("gT", [17, COLS])
        imp = st.sb("imp", [P, T])
        diag = st.sb("diag", [P, T, P])
        row = st.sb("row", [P, COLS])
        square = st.sb("square", [P, P])
        earlier = st.sb("earlier", [P, 2 * PAD - P])
        junk = st.sb("junk", [P, 4, SEQ])
        col, larger, ties = st.sb("col", [P, T]), st.sb("larger", [P, T]), st.sb("ties", [P, T])
        slots = st.sb("slots", [P, SLOT])
        pick = st.sb("pick", [P, T, 2, SLOT])
        k_mask, v_mask = st.sb("k_mask", [D, S_HEADS]), st.sb("v_mask", [P, S_HEADS // 2, 2, S_HD])
        kB = st.sb("kB", [D, B, S_HEADS * SLOT])
        vB = st.sb("vB", [P, B, D])
        qT = st.sb("qT", [D, COLS])
        attn = st.sb("attn", [P, T, D])
        loads = Loads(nc, st, "landed", [(w_qkv[:, :], I["s_qkv"]), (w_g1[:, :], I["s_g1"]), (w_g2[:, :], I["s_g2"]),
                                       (w_o[:, :], I["s_out"])])
        consts = st.sem("consts")
        with nc.Block() as block:
            @block.gpsimd
            def _(pool):
                steps = Steps(pool, consts)
                steps.do(nc.gpsimd.memset(gT[:, :], 1.0))
                steps.do(nc.gpsimd.memset(square[:, :], 1.0))
                steps.do(nc.gpsimd.memset(earlier[:, :], 1.0))
                steps.do(nc.gpsimd.memset(k_mask[:, :], 1.0))
                steps.do(nc.gpsimd.memset(v_mask[:, :, :, :], 0.0))
                steps.do(nc.gpsimd.iota(slots[:, :], [[1, SLOT]], base=0, channel_multiplier=0,
                                        allow_small_or_imprecise_dtypes=True))
                steps.do(nc.gpsimd.memset(slots[:, KEEP:SLOT], -1.0))
                steps.do(nc.gpsimd.memset(v_mask[0:D, :, 0, :], 1.0))
                steps.do(nc.gpsimd.memset(v_mask[D:P, :, 1, :], 1.0))
                steps.do(nc.gpsimd.affine_select(out=earlier[:, :], in_=earlier[:, :], compare_op=ALU.is_gt, fill=0.0,
                                                 base=PAD - P, pattern=[[-1, 2 * PAD - P]], channel_multiplier=1))
                steps.do(nc.gpsimd.affine_select(out=k_mask[:, :], in_=k_mask[:, :], compare_op=ALU.is_ge, fill=0.0,
                                                 base=0, pattern=[[-S_HD, S_HEADS]], channel_multiplier=1))
                steps.do(nc.gpsimd.affine_select(out=k_mask[:, :], in_=k_mask[:, :], compare_op=ALU.is_ge, fill=0.0,
                                                 base=S_HD - 1, pattern=[[S_HD, S_HEADS]], channel_multiplier=-1))
        norm()
        product_stage(nc, core, "sparse_qkv", [(lambda t: core.xnT[:, t * P:(t + 1) * P], w_qkv[:, :])], 3 * D,
                      lambda t0, t1, made: nc.scalar.activation(qkv[:, t0:t1, :], made, ACT.Copy), engine="scalar", loads=loads)
        wide_product_stage(nc, core, "sparse_g1", [(16, [(w_g1[:, :], lambda c0, c1: core.xnT[:, c0:c1])])],
                           lambda c0, c1, _, made: nc.scalar.activation(gT[0:16, c0:c1], made, ACT.Relu))
        product_stage(nc, core, "sparse_g2", [(lambda t: gT[:, t * P:(t + 1) * P], w_g2[:, :])], 1,
                      lambda t0, t1, made: nc.scalar.activation(imp[:, t0:t1], made.rearrange("p t w -> p (t w)"), ACT.Sigmoid),
                      engine="scalar")
        ps = core.psum
        vec, dg, spread, rowed, picked, made, done = (
            st.sem(n) for n in ("vector_steps", "diag_ready", "spread", "rowed", "picked", "made", "done"))
        with nc.Block() as block:
            @block.tensor
            def _(pe):
                pe.wait_ge(dg, 1)
                for g in range(GROUPS):
                    nc.tensor.matmul(ps[:, g, :], square[:, :], diag[:, 4 * g:4 * g + 4, :].rearrange("p t n -> p (t n)"),
                                     start=True, stop=True).then_inc(spread, 1)
                pe.wait_ge(picked, 1)
                pe.wait_ge(rowed, GROUPS)
                for b in range(B):
                    for c in range(CH):
                        t, r = b * CH + c, TOKEN_ROWS[c]
                        nc.tensor.matmul(ps[0:D, b, 0:SLOT], qkv[0:r, t, D:2 * D], pick[0:r, t, 0, :],
                                         start=(c == 0), stop=(c == CH - 1))
                    for c in range(CH):
                        t, r = b * CH + c, TOKEN_ROWS[c]
                        last = nc.tensor.matmul(ps[:, 4 + b, 0:D], pick[0:r, t, :, :].rearrange("p s n -> p (s n)"),
                                                qkv[0:r, t, 2 * D:3 * D], start=(c == 0), stop=(c == CH - 1))
                    last.then_inc(made, 1)

            @block.scalar
            def _(act):
                for g in range(GROUPS):
                    act.wait_ge(spread, g + 1)
                    nc.scalar.activation(row[:, g * BANK:(g + 1) * BANK], ps[:, g, :], ACT.Copy).then_inc(rowed, 1)

            @block.vector
            def _(dve):
                steps = Steps(dve, vec)
                nc.vector.tensor_tensor(diag[:, :, :], rows_of(core.ident[:, :], T), over(imp[:, :], P), ALU.mult
                                        ).then_inc(dg, 1)
                dve.wait_ge(rowed, GROUPS)
                steps.do(nc.vector.tensor_tensor(diag[:, :, :], row[:, :].rearrange("p (t n) -> p t n", n=P),
                                                 rows_of(core.ident[:, :], T), ALU.mult))
                steps.do(nc.vector.tensor_reduce(col[:, :], diag[:, :, :], AX.X, ALU.add))
                for b in range(B):
                    for c in range(CH):
                        t = b * CH + c
                        seq = row[:, b * PAD:b * PAD + SEQ]
                        shift = PAD - P - c * P
                        at = t % 2 * 2
                        if t % 2 == 0:
                            steps.settle()
                        steps.add(nc.vector.tensor_scalar(junk[:, at, :], seq, col[:, t:t + 1], 0.0, ALU.is_gt, ALU.add,
                                                          accum_out=larger[:, t:t + 1]))
                        steps.add(nc.vector.scalar_tensor_tensor(junk[:, at + 1, :], seq, col[:, t:t + 1],
                                                                 earlier[:, shift:shift + SEQ], ALU.is_equal, ALU.mult,
                                                                 accum_out=ties[:, t:t + 1]))
                steps.settle()
                steps.do(nc.vector.tensor_tensor(larger[:, :], larger[:, :], ties[:, :], ALU.add))
                for s in range(2):
                    steps.add(nc.vector.tensor_tensor(pick[:, :, s, :], over(larger[:, :], SLOT), rows_of(slots[:, :], T),
                                                      ALU.is_equal))
                steps.settle()
                dve.sem_inc(picked, 1)
                for b in range(B):
                    dve.wait_ge(made, b + 1)
                    nc.vector.tensor_tensor(kB[:, b, :].rearrange("p (h s) -> p h s", s=SLOT),
                                            ps[0:D, b, 0:SLOT].unsqueeze(1).to_broadcast([D, S_HEADS, SLOT]),
                                            over(k_mask[:, :], SLOT), ALU.mult).then_inc(done, 1)
                    nc.vector.tensor_tensor(vB[:, b, :], ps[:, 4 + b, 0:D],
                                            v_mask[:, :, :, :].rearrange("p a s d -> p (a s d)"), ALU.mult).then_inc(done, 1)
        turn_stage(nc, core, "sparse_turn_q", [(qT, D, lambda t: qkv[:, t, 0:D])])
        with Stage(nc, "sparse_soft") as at:
            q1 = at.sb("q1", [D, PAD])
            probs = at.sb("probs", [P, CH, S_HEADS, SLOT])
            pT = at.sb("pT", [P, 2, 4, P])
            stat = at.sb("stat", [P, CH, 3, S_HEADS])
            (fetched, scored, shifted, exped, normed, turned, copied, weighed, kept, vec, passed) = (
                at.sem(n) for n in ("fetched", "scored", "shifted", "exped", "normed", "turned", "copied", "weighed",
                                    "kept", "vector_steps", "passed"))
            BEGIN = CH
            start_loop(nc, [fetched, scored, shifted, exped, normed, turned, copied, weighed, kept], BEGIN)
            kB_flat, vB_flat = kB[:, :, :].rearrange("p b n -> p (b n)"), vB[:, :, :].rearrange("p b n -> p (b n)")
            real = lambda x: x[:, :, 0:KEEP]
            of_three, of_two = (-1, 0, -2, 1, 2), (0, -1, 1, 2, 3)
            with nc.Block() as block:
                @block.tensor
                def _(pe):
                    def score(b, c):
                        if c == 0:
                            pe.wait_ge(fetched, BEGIN + b + 1)
                        pe.wait_ge(shifted, BEGIN + CH * b + of_three[c])
                        wait_apart(pe, passed)
                        nc.tensor.matmul(ps[:, c % 3, :], q1[:, c * P:(c + 1) * P], kB_flat[:, bass.ds(b * S_HEADS * SLOT, BANK)],
                                         start=True, stop=True).then_inc(scored, 1)

                    def turn(b, c):
                        pe.wait_ge(normed, BEGIN + CH * b + c + 1)
                        pe.wait_ge(copied, BEGIN + CH * b + of_two[c])
                        wait_apart(pe, passed)
                        for k in range(4):
                            last = nc.tensor.transpose(ps[:, 3 + c % 2, k * P:(k + 1) * P],
                                                       probs[:, c, 2 * k:2 * k + 2, :].rearrange("p h s -> p (h s)"),
                                                       core.ident[:, :])
                        last.then_inc(turned, 1)

                    def weigh(b, c):
                        pe.wait_ge(copied, BEGIN + CH * b + c + 1)
                        pe.wait_ge(kept, BEGIN + CH * b + of_two[c])
                        wait_apart(pe, passed)
                        for k in range(4):
                            last = nc.tensor.matmul(ps[:, 5 + c % 2, k * 2 * S_HD:(k + 1) * 2 * S_HD], pT[:, c % 2, k, :],
                                                    vB_flat[:, bass.ds(b * D + k * 2 * S_HD, 2 * S_HD)],
                                                    start=True, stop=True)
                        last.then_inc(weighed, 1)

                    with pe.Fori(0, B) as b:
                        for c in range(3):
                            score(b, c)
                        for c in range(CH):
                            turn(b, c)
                            if c + 3 < CH:
                                score(b, c + 3)
                            if c >= 1:
                                weigh(b, c - 1)
                        weigh(b, CH - 1)

                @block.scalar
                def _(act):
                    def exp(b, c):
                        act.wait_ge(shifted, BEGIN + CH * b + c + 1)
                        nc.scalar.activation(real(probs[:, c]), real(probs[:, c]), ACT.Exp, scale=S_HD ** -0.5).then_inc(exped, 1)

                    def copy(b, c):
                        act.wait_ge(turned, BEGIN + CH * b + c + 1)
                        act.wait_ge(weighed, BEGIN + CH * b + of_two[c])
                        nc.scalar.activation(pT[:, c % 2, :, :], ps[:, 3 + c % 2, :].rearrange("p (k n) -> p k n", n=P), ACT.Copy
                                             ).then_inc(copied, 1)

                    def keep(b, c):
                        act.wait_ge(weighed, BEGIN + CH * b + c + 1)
                        nc.scalar.activation(attn[:, bass.ds(b * CH + c, 1), :], ps[:, 5 + c % 2, 0:D].unsqueeze(1), ACT.Copy
                                             ).then_inc(kept, 1)

                    with act.Fori(0, B) as b:
                        act.wait_ge(scored, BEGIN + CH * b)
                        nc.scalar.activation(q1[:, :], qT[:, bass.ds(b * PAD, PAD)], ACT.Copy).then_inc(fetched, 1)
                        exp(b, 0)
                        for c in range(CH):
                            if c + 1 < CH:
                                exp(b, c + 1)
                            copy(b, c)
                            if c >= 1:
                                keep(b, c - 1)
                        keep(b, CH - 1)

                @block.vector
                def _(dve):
                    steps = Steps(dve, vec)
                    steps.do(nc.vector.memset(probs[:, :, :, :], 0.0))

                    def shift(b, c):
                        s = ps[:, c % 3, :].rearrange("p (h s) -> p h s", s=SLOT)
                        dve.wait_ge(scored, BEGIN + CH * b + c + 1)
                        steps.do(nc.vector.tensor_reduce(stat[:, c, 0, :], real(s), AX.X, ALU.max))
                        dve.wait_ge(turned, BEGIN + CH * b + c - CH + 1)
                        nc.vector.tensor_tensor(real(probs[:, c]), real(s), over(stat[:, c, 0, :], KEEP), ALU.subtract
                                                ).then_inc(shifted, 1)

                    def norm(b, c):
                        dve.wait_ge(exped, BEGIN + CH * b + c + 1)
                        steps.do(nc.vector.tensor_reduce(stat[:, c, 1, :], real(probs[:, c]), AX.X, ALU.add))
                        steps.do(nc.vector.reciprocal(stat[:, c, 2, :], stat[:, c, 1, :]))
                        nc.vector.tensor_tensor(real(probs[:, c]), real(probs[:, c]), over(stat[:, c, 2, :], KEEP), ALU.mult
                                                ).then_inc(normed, 1)

                    with dve.Fori(0, B) as b:
                        steps.enter_loop(b, 3 * CH)
                        shift(b, 0)
                        for c in range(CH):
                            if c + 1 < CH:
                                shift(b, c + 1)
                            norm(b, c)
        turn_stage(nc, core, "sparse_turn_o", [(core.xnT, D, lambda t: attn[:, t, :])])
        product_stage(nc, core, "sparse_out", [(lambda t: core.xnT[:, t * P:(t + 1) * P], w_o[:, :])], D,
                      lambda t0, t1, made: nc.vector.tensor_tensor(core.h[:, t0:t1, :], core.h[:, t0:t1, :], made, ALU.add))


DEPTH = 7
NODES = 2 ** (DEPTH + 1)
CHUNK = BANK // D
LEVELS = DEPTH + 1 - 3
PAIR = 2 * CH - 1
DENSE = B // 2 * PAIR


def tree_stage(nc, core, I, norm):
    with Stage(nc, "tree") as st:
        w_b = st.sb("w_b", [P, 2, D])
        logit = st.sb("logit", [P, DENSE, NODES])
        on = st.sb("on", [P, DENSE, NODES])
        gate = st.sb("gate", [P, DENSE, DEPTH + 1])
        x12, x13 = st.sb("x12", [P, DENSE * P], BF16), st.sb("x13", [P, DENSE * P], BF16)
        with Stage(nc, "path") as at:
            w_n, b_n = at.sb("w_n", [D, NODES]), at.sb("b_n", [1, NODES])
            right = at.sb("right", [P, DENSE, NODES])
            twice = at.sb("twice", [P, DENSE, 2, D])
            xT2 = at.sb("xT2", [P, DENSE * P])
            loads = Loads(nc, at, "landed", [(w_n[:, :], I["tree_w1"]), (b_n[:, :], I["tree_b1"]),
                                         (w_b[:, :, :], I["tree_b2"].rearrange("(k p) d -> p k d", p=P))])
            norm(turn=False)
            moved = at.sem("moved")
            with nc.Block() as block:
                @block.vector
                def _(dve):
                    for pair in range(2):
                        lo, of = pair * PAIR, pair * 2 * CH
                        nc.vector.tensor_copy(twice[:, lo:lo + PAIR, :, :],
                                              core.xn[:, of:of + PAIR, :].unsqueeze(2).to_broadcast([P, PAIR, 2, D])
                                              ).then_inc(moved, 1)
                    dve.wait_ge(moved, 2)
                    nc.vector.tensor_copy(twice[TAIL:P, CH - 1::PAIR, :, :],
                                          core.xn[0:TAIL, 2 * CH - 1::2 * CH, :].unsqueeze(2).to_broadcast([TAIL, 2, 2, D]))
            turn_stage(nc, core, "tree_turn", [(xT2, P, lambda t: twice[:, t, :, :].rearrange("p s d -> p (s d)"))], tiles=DENSE)
            product_stage(nc, core, "tree_logits", [(lambda t: xT2[0:D, t * P:(t + 1) * P], w_n[:, :]),
                                                      (lambda t: core.ones[:, :], b_n[:, :])], NODES,
                          lambda t0, t1, made: nc.scalar.activation(logit[:, t0:t1, :], made, ACT.Copy), engine="scalar", tiles=DENSE, loads=loads)
            vec, gelu, absed = (at.sem(n) for n in ("vector_steps", "gelu", "absed"))
            with nc.Block() as block:
                @block.vector
                def _(dve):
                    steps = Steps(dve, vec)
                    steps.add(nc.vector.tensor_scalar(right[:, :, :], logit[:, :, :], 0.0, None, ALU.is_gt))
                    steps.add(nc.vector.memset(on[:, :, 0:1], 0.0))
                    steps.do(nc.vector.memset(on[:, :, 1:2], 1.0))
                    dve.sem_inc(absed, 1)
                    for level in range(DEPTH):
                        lo, n = 2 ** level, 2 ** level
                        child = on[:, :, 2 * lo:4 * lo].rearrange("p t (n s) -> p t n s", s=2)
                        steps.do(nc.vector.tensor_tensor(child[:, :, :, 1], on[:, :, lo:lo + n], right[:, :, lo:lo + n], ALU.mult))
                        steps.do(nc.vector.tensor_tensor(child[:, :, :, 0], on[:, :, lo:lo + n], child[:, :, :, 1], ALU.subtract))
                    dve.wait_ge(gelu, 2)
                    steps.do(nc.vector.tensor_tensor(logit[:, :, :], logit[:, :, :], on[:, :, :], ALU.mult))
                    for level in range(DEPTH + 1):
                        lo = 2 ** level
                        steps.add(nc.vector.tensor_reduce(gate[:, :, level], logit[:, :, lo:2 * lo], AX.X, ALU.add))

                @block.scalar
                def _(act):
                    act.wait_ge(absed, 1)
                    nc.scalar.activation(logit[:, :, :], logit[:, :, :], ACT.Abs).then_inc(gelu, 1)
                    act.wait_ge(gelu, 1)
                    nc.scalar.activation(logit[:, :, :], logit[:, :, :], ACT.Gelu).then_inc(gelu, 1)
            split_tokens_stage(nc, "tree_split", xT2[:, :], x12, x13)
        w11, w22, w31 = (st.sb(n, [P, NODES * D], BF16) for n in ("w11", "w22", "w31"))
        split_weights_stage(nc, "tree_weights", I["tree_w2"], w11, w22, w31, 2 * BANK)
        tree_sum_stage(nc, core, logit, on, gate, ((x12, w11), (x12, w22), (x13, w31)), w_b)


def tree_sum_stage(nc, core, weight, on, gate, products, w_b):
    with Stage(nc, "leaf") as st:
        ws = st.sb("ws", [P, NODES])
        path = st.sb("path", [P, 2, NODES])
        of_level = st.sb("of_level", [P, 2, DEPTH + 1])
        wT = st.sb("wT", [P, 2, P])
        acc = st.sb("acc", [P, 2, LEVELS + 1, CHUNK, D])
        total = st.sb("total", [P, D])
        y = st.sb("y", [P, DENSE, D])
        across = st.sb("across", [TAIL, 2, D])
        passed_v, passed_p = st.sem("passed_by_vector"), st.sem("passed_by_pool")
        fetched, masked, made, taken, turned, turned_copied, biased, scaled, vec, passed, added = (
            st.sem(n) for n in ("fetched", "masked", "made", "taken", "turned", "turned_copied", "biased", "scaled",
                                "vector_steps", "passed", "added"))
        start_loop(nc, [fetched, masked, made, taken, turned, turned_copied, biased, added])
        SCALED = START + 2 * LEVELS
        start_loop(nc, [scaled], SCALED)
        ps = core.psum
        C = NODES // CHUNK
        BANKS = 6
        first = {2 ** (3 + k) // CHUNK: k for k in range(LEVELS)}
        order = [c for pair in zip(range(C // 2), range(C // 2, C)) for c in pair]
        with nc.Block() as block:
            @block.tensor
            def _(pe):
                def bias(t):
                    pe.wait_ge(turned_copied, START + t + 1)
                    pe.wait_ge(added, START + t)
                    wait_apart(pe, passed)
                    for k in range(2):
                        last = nc.tensor.matmul(ps[:, 7, 0:D], wT[:, k, :], w_b[:, k, :], start=(k == 0), stop=(k == 1))
                    last.then_inc(biased, 1)

                def tile(t, before):
                    for n, c in enumerate(order):
                        pe.wait_ge(taken, START + C * t + n - BANKS + 1 if n >= BANKS else START + C * t)
                        wait_apart(pe, passed)
                        for k, (x, w) in enumerate(products):
                            last = nc.tensor.matmul(ps[:, n % BANKS, :], x[:, bass.ds(t * P, P)], w[:, c * BANK:(c + 1) * BANK],
                                                    start=(k == 0), stop=(k == len(products) - 1))
                        last.then_inc(made, 1)
                        if before and n == BANKS:
                            bias(t - 1)
                        if n == 2 * BANKS:
                            pe.wait_ge(fetched, START + t + 1)
                            pe.wait_ge(turned_copied, START + t)
                            wait_apart(pe, passed)
                            for k in range(2):
                                last = nc.tensor.transpose(ps[:, 6, k * P:(k + 1) * P], ws[:, k * P:(k + 1) * P], core.ident[:, :])
                            last.then_inc(turned, 1)

                tile(0, False)
                with pe.Fori(1, DENSE) as t:
                    tile(t, True)
                bias(DENSE - 1)

            @block.scalar
            def _(act):
                with act.Fori(0, DENSE // 2) as j:
                    for u in range(2):
                        t = 2 * j + u
                        act.wait_ge(turned, START + t)
                        nc.scalar.activation(ws[:, :].unsqueeze(1), weight[:, bass.ds(t, 1), :], ACT.Copy).then_inc(fetched, 1)
                        act.wait_ge(taken, START + C * t)
                        nc.scalar.activation(path[:, u, :].unsqueeze(1), on[:, bass.ds(t, 1), :], ACT.Copy).then_inc(masked, 1)
                        act.wait_ge(scaled, SCALED + 2 * LEVELS * (t - 1))
                        nc.scalar.activation(of_level[:, u, :].unsqueeze(1), gate[:, bass.ds(t, 1), :], ACT.Copy).then_inc(masked, 1)
                        act.wait_ge(turned, START + t + 1)
                        act.wait_ge(biased, START + t)
                        nc.scalar.activation(wT[:, :, :], ps[:, 6, 0:2 * P].rearrange("p (k n) -> p k n", n=P), ACT.Copy
                                             ).then_inc(turned_copied, 1)

            @block.gpsimd
            def _(pool):
                with pool.Fori(0, DENSE // 2) as j:
                    for u in range(2):
                        t = 2 * j + u
                        pool.wait_ge(taken, START + C * (t + 1))
                        pool.wait_ge(masked, START + 2 * (t + 1))
                        sums = lambda l: acc[:, u, l, :, :].rearrange("p c d -> p (c d)")
                        for k in range(LEVELS):
                            nc.gpsimd.tensor_tensor(sums(k + 1), sums(k + 1), of_level[:, u, k + 3:k + 4].to_broadcast([P, CHUNK * D]),
                                                    ALU.mult).then_inc(scaled, 1)
                        for k in range(LEVELS):
                            pool.wait_ge(scaled, SCALED + 2 * LEVELS * t + LEVELS + k)
                            wait_apart(pool, passed_p)
                            nc.gpsimd.tensor_tensor(sums(0), sums(0), sums(k + 1), ALU.add).then_inc(scaled, 1)

            @block.vector
            def _(dve):
                steps = Steps(dve, vec)

                def take(t, u):
                    dve.wait_ge(masked, START + 2 * t + 1)
                    for n, c in enumerate(order):
                        dve.wait_ge(made, START + C * t + n + 1)
                        if n >= 2:
                            dve.wait_ge(taken, START + C * t + n - 1)
                        wait_apart(dve, passed_v)
                        bank = ps[:, n % BANKS, :].rearrange("p (c d) -> p c d", d=D)
                        if c == 0:
                            ins = nc.vector.tensor_tensor(acc[:, u, 0, :, :], bank,
                                                          over(weight[:, bass.ds(t, 1), 0:CHUNK].rearrange("p t n -> p (t n)"), D), ALU.mult)
                        else:
                            level = max(k for f, k in first.items() if f <= c)
                            mask = path[:, u, c * CHUNK:(c + 1) * CHUNK]
                            if c in first:
                                ins = nc.vector.tensor_tensor(acc[:, u, level + 1, :, :], bank, over(mask, D), ALU.mult)
                            else:
                                ins = nc.vector.copy_predicated(acc[:, u, level + 1, :, :], over(mask.bitcast(U32), D), bank)
                        ins.then_inc(taken, 1)

                def finish(t, u):
                    steps.before, steps.count = t, 0
                    dve.wait_ge(scaled, SCALED + 2 * LEVELS * (t + 1))
                    dve.wait_ge(added, START + t)
                    steps.do(nc.vector.tensor_reduce(total[:, :], acc[:, u, 0, :, :].rearrange("p c d -> p d c"), AX.X, ALU.add))
                    dve.wait_ge(biased, START + t + 1)
                    nc.vector.tensor_tensor(y[:, bass.ds(t, 1), :], ps[:, 7, 0:D].unsqueeze(1), total[:, :].unsqueeze(1), ALU.add
                                            ).then_inc(added, 1)

                take(0, 0)
                take(1, 1)
                finish(0, 0)
                with dve.Fori(1, DENSE // 2) as j:
                    take(2 * j, 0)
                    finish(2 * j - 1, 1)
                    take(2 * j + 1, 1)
                    finish(2 * j, 0)
                finish(DENSE - 1, 1)
                dve.wait_ge(added, START + DENSE)
                nc.vector.tensor_copy(across[:, :, :], y[TAIL:P, CH - 1::PAIR, :]).then_inc(added, 1)
                for pair in range(2):
                    lo, at = pair * PAIR, pair * 2 * CH
                    for rows, c0, c1 in ((P, 0, CH - 1), (TAIL, CH - 1, CH), (P, CH, PAIR)):
                        nc.vector.tensor_tensor(core.h[0:rows, at + c0:at + c1, :], core.h[0:rows, at + c0:at + c1, :],
                                                y[0:rows, lo + c0:lo + c1, :], ALU.add)
                dve.wait_ge(added, START + DENSE + 1)
                tails = core.h[0:TAIL, 2 * CH - 1::2 * CH, :]
                nc.vector.tensor_tensor(tails, tails, across[:, :, :], ALU.add)


def sigmoid_attention_stage(nc, core, I, norm):
    with Stage(nc, "sig") as st:
        w = st.sb("w", [D, D])
        qT = st.sb("qT", [D, COLS])
        keys = st.sb("keys", [D, 2, PAD])
        att = st.sb("att", [P, 2, CH, PAD])
        loads = Loads(nc, st, "landed", [(w[:, :], I["sig_w"])])
        norm()
        wide_product_stage(nc, core, "sig_q", [(D, [(w[:, :], lambda c0, c1: core.xnT[0:D, c0:c1])])],
                           lambda c0, c1, _, made: nc.scalar.activation(qT[:, c0:c1], made, ACT.Copy), loads=loads)
        set_stage(nc, "att_zero", [(att[:, :, :, SEQ:PAD], 0.0)])
        fetched, scored, attended, weighed, added, passed = (
            st.sem(n) for n in ("fetched", "scored", "attended", "weighed", "added", "passed"))
        BEGIN = CH + 1
        start_loop(nc, [fetched, scored, weighed, added], BEGIN)
        start_loop(nc, [attended])
        ps = core.psum
        side = SEQ // 2
        with nc.Block() as block:
            @block.tensor
            def _(pe):
                def score(b, u):
                    pe.wait_ge(fetched, BEGIN + b + 1)
                    for m in range(CH):
                        n = CH * u + m
                        pe.wait_ge(attended, START + CH * (b - u) + (n - 1 if n >= 2 else 0))
                        wait_apart(pe, passed)
                        for s in range(2):
                            last = nc.tensor.matmul(ps[:, 2 * (n % 2) + s, 0:side], keys[:, u, m * P:(m + 1) * P],
                                                    qT[:, bass.ds(b * PAD + s * side, side)], start=True, stop=True)
                        last.then_inc(scored, 1)

                def weigh(b, u):
                    pe.wait_ge(attended, START + CH * b + CH)
                    pe.wait_ge(added, BEGIN + b - 1)
                    wait_apart(pe, passed)
                    for c in range(CH):
                        for m in range(CH):
                            r = TOKEN_ROWS[m]
                            last = nc.tensor.matmul(ps[:, 4 + u, c * D:(c + 1) * D], att[0:r, u, m, c * P:(c + 1) * P],
                                                    core.xn[0:r, bass.ds(b * CH + m, 1), :].rearrange("p t d -> p (t d)"),
                                                    start=(m == 0), stop=(m == CH - 1))
                    last.then_inc(weighed, 1)

                with pe.Fori(0, B // 2) as j:
                    for u in range(2):
                        score(2 * j + u, u)
                    for u in range(2):
                        weigh(2 * j + u, u)

            @block.scalar
            def _(act):
                with act.Fori(0, B // 2) as j:
                    for u in range(2):
                        b = 2 * j + u
                        act.wait_ge(scored, BEGIN + CH * (b - 1))
                        nc.scalar.activation(keys[:, u, :], core.xnT[0:D, bass.ds(b * PAD, PAD)], ACT.Copy).then_inc(fetched, 1)
                    for u in range(2):
                        b = 2 * j + u
                        act.wait_ge(weighed, BEGIN + b - 1)
                        for m in range(CH):
                            r, n = TOKEN_ROWS[m], CH * u + m
                            act.wait_ge(scored, BEGIN + CH * b + m + 1)
                            nc.scalar.activation(att[0:r, u, m, 0:SEQ].rearrange("p (s n) -> p s n", s=2),
                                                 ps[0:r, 2 * (n % 2):2 * (n % 2) + 2, 0:side], ACT.Sigmoid).then_inc(attended, 1)

            @block.vector
            def _(dve):
                with dve.Fori(0, B // 2) as j:
                    for u in range(2):
                        b = 2 * j + u
                        dve.wait_ge(weighed, BEGIN + b + 1)
                        full = core.h[:, bass.ds(b * CH, CH - 1), :]
                        nc.vector.tensor_tensor(full, full, ps[:, 4 + u, 0:(CH - 1) * D].rearrange("p (c d) -> p c d", d=D), ALU.add)
                        tail = core.h[0:TAIL, bass.ds(b * CH + CH - 1, 1), :]
                        nc.vector.tensor_tensor(tail, tail, ps[0:TAIL, 4 + u, (CH - 1) * D:CH * D].unsqueeze(1), ALU.add
                                                ).then_inc(added, 1)


R_EXPERTS = 4


def relu_experts_stage(nc, core, I, norm):
    with Stage(nc, "mlp") as st:
        E = R_EXPERTS
        w_g = st.sb("w_g", [D + 1, E])
        router, weight = st.sb("router", [P, T, E]), st.sb("weight", [P, T, E])
        s1, s2, s3 = st.sb("s1", [D + 1, D]), st.sb("s2", [D + 1, P]), st.sb("s3", [P, D])
        s3b = st.sb("s3b", [1, D])
        e1, e2, e3 = st.sb("e1", [D + 1, E, P]), st.sb("e2", [P, E, D]), st.sb("e3", [D + 1, E, D])
        e2b = st.sb("e2b", [D, E])
        h1, h2 = st.sb("h1", [P, 2, BANK]), st.sb("h2", [P, 2, BANK])
        g1, g2 = st.sb("g1", [D + 1, BANK]), st.sb("g2", [P, BANK])
        part = st.sb("part", [P, 2, 4, D])
        loads = Loads(nc, st, "landed", [(w_g[:, :], I["m_gate"]), (s1[:, :], I["m_s1"]), (s2[:, :], I["m_s2"]),
                                    (s3[:, :], I["m_s3"]), (s3b[:, :], I["m_s3b"]), (e1[:, :, :], I["m_e1"]),
                                    (e2[:, :, :], I["m_e2"]), (e3[:, :, :], I["m_e3"]), (e2b[:, :], I["m_e2b"])])
        set_stage(nc, "mlp_ones", [(h2[:, :, :], 1.0), (g1[:, :], 1.0)])
        norm()
        loads.arrive()
        product_stage(nc, core, "mlp_gate", [(lambda t: core.xnT[:, t * P:(t + 1) * P], w_g[:, :])], E,
                      lambda t0, t1, made: nc.vector.tensor_copy(router[:, t0:t1, :], made))
        top_two_stage(nc, core, "mlp_top", router[:, :, :], weight[:, :, :], E, "softmax")
        up1, act1, up2, act2, down, taken, added, passed = (
            st.sem(n) for n in ("up1", "act1", "up2", "act2", "down", "taken", "added", "passed"))
        start_loop(nc, [up1, act1, up2, act2, down, taken, added])
        ps = core.psum
        N = E + 1
        with nc.Block() as block:
            @block.tensor
            def _(pe):
                with pe.Fori(0, GROUPS) as g:
                    cols = core.xnT[:, bass.ds(g * BANK, BANK)]

                    def first_layer(e):
                        pe.wait_ge(act1, START + N * g + max(e - 1, 0))
                        wait_apart(pe, passed)
                        rows = P if e < E else D
                        nc.tensor.matmul(ps[0:rows, e % 2, :], e1[:, e, :] if e < E else s1[:, :], cols,
                                         start=True, stop=True).then_inc(up1, 1)

                    def second_layer(e):
                        pe.wait_ge(act1, START + N * g + e + 1)
                        pe.wait_ge(act2, START + N * g + max(e - 1, 0))
                        wait_apart(pe, passed)
                        if e < E:
                            last = nc.tensor.matmul(ps[0:D, 2 + e % 2, :], e2[:, e, :], h1[:, e % 2, :], start=True, stop=True)
                        else:
                            last = nc.tensor.matmul(ps[:, 2 + e % 2, :], s2[:, :], g1[:, :], start=True, stop=True)
                        last.then_inc(up2, 1)

                    def third_layer(e):
                        pe.wait_ge(act2, START + N * g + e + 1)
                        pe.wait_ge(taken, START + N * g + max(e - 1, 0))
                        wait_apart(pe, passed)
                        for k in range(4):
                            out = ps[:, 4 + e % 2, k * D:(k + 1) * D]
                            if e < E:
                                last = nc.tensor.matmul(out, h2[0:D + 1, e % 2, k * P:(k + 1) * P], e3[:, e, :],
                                                        start=True, stop=True)
                            else:
                                nc.tensor.matmul(out, g2[:, k * P:(k + 1) * P], s3[:, :], start=True, stop=False)
                                last = nc.tensor.matmul(out, core.ones[:, :], s3b[:, :], start=False, stop=True)
                        last.then_inc(down, 1)

                    first_layer(0)
                    for e in range(N):
                        if e + 1 < N:
                            first_layer(e + 1)
                        if e >= 1:
                            third_layer(e - 1)
                        second_layer(e)
                    third_layer(N - 1)

            @block.scalar
            def _(act):
                with act.Fori(0, GROUPS) as g:
                    def first(e):
                        act.wait_ge(up1, START + N * g + e + 1)
                        act.wait_ge(up2, START + N * g + max(e - 1, 0))
                        if e < E:
                            ins = nc.scalar.activation(h1[:, e % 2, :], ps[:, e % 2, :], ACT.Relu)
                        else:
                            ins = nc.scalar.activation(g1[0:D, :], ps[0:D, e % 2, :], ACT.Relu)
                        ins.then_inc(act1, 1)

                    def second(e):
                        act.wait_ge(up2, START + N * g + e + 1)
                        act.wait_ge(down, START + N * g + max(e - 1, 0))
                        if e < E:
                            ins = nc.scalar.activation(h2[0:D, e % 2, :], ps[0:D, 2 + e % 2, :], ACT.Relu, bias=e2b[:, e:e + 1])
                        else:
                            ins = nc.scalar.activation(g2[:, :], ps[:, 2 + e % 2, :], ACT.Relu)
                        ins.then_inc(act2, 1)

                    first(0)
                    for e in range(N):
                        if e + 1 < N:
                            first(e + 1)
                        second(e)

            @block.vector
            def _(dve):
                with dve.Fori(0, GROUPS) as g:
                    tiles = core.h[:, bass.ds(4 * g, 4), :]
                    for e in range(N):
                        n = N * g + e
                        dve.wait_ge(down, START + n + 1)
                        dve.wait_ge(added, START + N * g + max(e - 1, 0))
                        made = ps[:, 4 + e % 2, 0:4 * D].rearrange("p (t d) -> p t d", d=D)
                        if e < E:
                            ins = nc.vector.tensor_tensor(part[:, e % 2, :, :], made,
                                                          over(weight[:, bass.ds(4 * g, 4), e], D), ALU.mult)
                        else:
                            ins = nc.vector.tensor_copy(part[:, e % 2, :, :], made)
                        ins.then_inc(taken, 1)
                        dve.wait_ge(taken, START + n + 1)
                        dve.wait_ge(added, START + n)
                        nc.vector.tensor_tensor(tiles, tiles, part[:, e % 2, :, :], ALU.add).then_inc(added, 1)


def store_stage(nc, core, out):
    with Stage(nc, "store") as st:
        stored = st.sem("stored")
        h_b = core.h[:, :, :].rearrange("p (b c) d -> p b c d", c=CH)
        with nc.Block() as block:
            @block.sync
            def _(sp):
                for b in range(B):
                    sp.dma_start(out[b, 0:4 * P, :].rearrange("(c p) d -> p c d", p=P), h_b[:, b, 0:4, :]).then_inc(stored, 16)
                    sp.dma_start(out[b, 4 * P:SEQ, :], h_b[0:TAIL, b, 4, :]).then_inc(stored, 16)
                sp.wait_ge(stored, 16 * 2 * B)


def build(nc, I, out):
    core = Core()
    Stage.spent.clear()
    with ExitStack() as stack:
        sb = lambda name, shape: stack.enter_context(nc.sbuf_tensor(name, shape, F32))
        core.h = sb("h", [P, T, D])
        core.xn = sb("xn", [P, T, D])
        core.xnT = sb("xnT", [D + 1, COLS])
        core.ident = sb("ident", [P, P])
        core.ones = sb("ones", [1, P])
        core.psum = stack.enter_context(nc.psum_tensor("psum", [P, 8, BANK], F32))
        set_stage(nc, "ones", [(core.ones[:, :], 1.0)])
        embed_stage(nc, core, I["x_patches"], I["txt"], I["tok_aug"])
        layers = [linear_attention_stage, retrieval_stage, toeplitz_stage, rotary_experts_stage,
                  sparse_attention_stage, tree_stage, sigmoid_attention_stage, relu_experts_stage]
        for n, layer in enumerate(layers):
            layer(nc, core, I, lambda turn=True: norm_stage(nc, core, f"norm{n}", core.h, turn=turn))
        store_stage(nc, core, out)


def transform_tables():
    lag = np.concatenate([np.arange(SEQ), [0], np.arange(1 - SEQ, 0)]).astype(np.float32)
    n, f = np.arange(SPAN), np.arange(FREQ)
    angle = 2 * np.pi * (np.outer(n, f) % SPAN) / SPAN
    twice = np.where((f == 0) | (f == SEQ), 1.0, 2.0)[:, None] / SPAN
    back = angle[:SEQ].T
    tables = {"cos": np.cos(angle), "sin": -np.sin(angle), "icos": twice * np.cos(back), "isin": -twice * np.sin(back)}
    return {"lags": np.stack([lag, np.ones_like(lag)]), **{k: v.astype(np.float32) for k, v in tables.items()}}


def rotary_weights(wq, wk, wv):
    q = wq.T.reshape(D, Q_HEADS, HD)
    k, v = (w.T.reshape(D, Q_HEADS // 2, HD).repeat(2, axis=1) for w in (wk, wv))
    swap = np.roll(np.arange(HD), HD // 2)
    return np.concatenate([q, k, q[:, :, swap], k[:, :, swap], v], axis=1).reshape(D, 5 * D)


def rotary_tables():
    frequency = 1.0 / 10000.0 ** (np.arange(0, HD, 2, dtype=np.float32) / HD)
    angle = np.outer(np.arange(PAD, dtype=np.float32), frequency)
    angle = np.concatenate([angle, angle], axis=-1)
    sign = np.where(np.arange(HD) < HD // 2, -1.0, 1.0)
    return {"rot_cos": np.cos(angle).astype(np.float32), "rot_sin": (np.sin(angle) * sign).astype(np.float32)}


def tree_weights(w1, b1, w2, b2):
    first = lambda a: np.concatenate([np.zeros_like(a[:1]), a], axis=0)
    w1, b1, w2, b2 = (first(a) for a in (w1, b1, w2, b2))
    return {"tree_w1": w1.T, "tree_b1": b1[None], "tree_w2": w2.transpose(1, 0, 2).reshape(D, NODES * D),
            "tree_b2": b2}


def pk_blocks(keys):
    k = keys.reshape(2, KEYS, 2, 4, D // 2)
    blocks = np.zeros((4, D // 2, 2, 2, 4, KEYS), keys.dtype)
    for h in range(4):
        blocks[h, :, :, :, h, :] = k[:, :, :, h, :].transpose(3, 0, 2, 1)
    return blocks.reshape(P, 4, 4 * KEYS)


def lay_out(a):
    g = {k: np.asarray(v) for k, v in a.items()}
    join = lambda w, b: np.concatenate([w, b.reshape(1, -1)], axis=0)
    x = g["x"].reshape(B, 8, 8, 8, 8)
    return {
        "x_patches": x.transpose(2, 4, 0, 1, 3).reshape(D, B * PATCHES),
        "txt": g["txt"],
        "tok_aug": join(g["L0_tok_W"].T, g["L0_tok_b"]),
        "qkv_aug": join(g["L0_attn_qkv_w"], g["L0_attn_qkv_b"]),
        "proj_aug": join(g["L0_attn_proj_w"], g["L0_attn_proj_b"]),
        "ln1_g": g["L0_attn_ln1_g"], "ln1_b": g["L0_attn_ln1_b"],
        "ln2_g": g["L0_attn_ln2_g"], "ln2_b": g["L0_attn_ln2_b"],
        "w1_aug": join(g["L0_attn_w1"], g["L0_attn_b1"]),
        "w2": g["L0_attn_w2"], "b2": g["L0_attn_b2"],
        "uv_aug": np.concatenate([join(g["L1_attn_u_w"].T, g["L1_attn_u_b"]), join(g["L1_attn_v_w"].T, g["L1_attn_v_b"])], axis=1),
        "o_aug": join(g["L1_attn_o_w"].T, g["L1_attn_o_b"]),
        "t_aug": join(g["L1_attn_t_w"].T, g["L1_attn_t_b"]),
        "pos_aug": join(g["L1_attn_pos_w"].T, g["L1_attn_pos_b"]),
        "rpe_aug": np.concatenate([g["L1_attn_rpe_lw"].transpose(2, 0, 1), g["L1_attn_rpe_lb"][None]], axis=0),
        "out_aug": join(g["L1_attn_out_w"].T, g["L1_attn_out_b"]),
        **transform_tables(),
        "rms1_w": g["L1_ffn_ln1_w"], "rms2_w": g["L1_ffn_ln2_w"],
        "rot_in": rotary_weights(g["L1_ffn_wq"], g["L1_ffn_wk"], g["L1_ffn_wv"]),
        "rot_out": g["L1_ffn_wo"].T,
        **rotary_tables(),
        "router": g["L1_ffn_router_w"].T,
        "moe_w13": np.concatenate([g[k].reshape(EXPERTS * HIDDEN, D).T for k in ("L1_ffn_w1", "L1_ffn_w3")], axis=1),
        "moe_w2": g["L1_ffn_w2"].transpose(0, 2, 1).reshape(EXPERTS * HIDDEN, D),
        "s_qkv": join(g["L2_attn_w_in"].T, g["L2_attn_b_in"]),
        "s_g1": join(g["L2_attn_gate_w1"].T, g["L2_attn_gate_b1"]),
        "s_g2": join(g["L2_attn_gate_w2"].T, g["L2_attn_gate_b2"]),
        "s_out": join(g["L2_attn_w_out"].T, g["L2_attn_b_out"]),
        **tree_weights(g["L2_ffn_w1s"], g["L2_ffn_b1s"], g["L2_ffn_w2s"], g["L2_ffn_b2s"]),
        "sig_w": g["L3_attn_q_weight"],
        "m_gate": join(g["L3_ffn_gW"], g["L3_ffn_gb"]),
        "m_s1": join(g["L3_ffn_sW1"], g["L3_ffn_sb1"]), "m_s2": join(g["L3_ffn_sW2"], g["L3_ffn_sb2"]),
        "m_s3": g["L3_ffn_sW3"], "m_s3b": g["L3_ffn_sb3"].reshape(1, D),
        "m_e1": np.concatenate([g["L3_ffn_eW1"].transpose(1, 0, 2), g["L3_ffn_eb1"][None]], axis=0),
        "m_e2": g["L3_ffn_eW2"].transpose(1, 0, 2), "m_e2b": g["L3_ffn_eb2"].T,
        "m_e3": np.concatenate([g["L3_ffn_eW3"].transpose(1, 0, 2), g["L3_ffn_eb3"][None]], axis=0),
        "w_pk": g["L0_ffn_Wq_pk"], "w_q": g["L0_ffn_Wq"], "w_o": g["L0_ffn_Wo"],
        "pk_blocks": pk_blocks(g["L0_ffn_pk_keys"]),
        "table": np.concatenate([g["L0_ffn_keys_table"], g["L0_ffn_values_table"]], axis=1),
    }


def kernel(**inputs):
    import concourse.bacc as _bacc
    from concourse.bass_utils import run_bass_kernel_spmd as _run

    nc = _bacc.Bacc("TRN2", target_bir_lowering=False, num_devices=1)
    arrays = {f"in_{k}": np.ascontiguousarray(v) for k, v in lay_out(inputs).items()}
    I = {k[3:]: nc.dram_tensor(k, v.shape, mybir.dt.from_np(v.dtype), kind="ExternalInput").ap() for k, v in arrays.items()}
    out = nc.dram_tensor("out", (B, SEQ, D), F32, kind="ExternalOutput").ap()
    build(nc, I, out)
    return _run(nc, [arrays], core_ids=[0]).results[0]["out"]
```
